# Optimizing a Trainium2 kernel written in Bass

```python
import numpy as np
import jax
import jax.numpy as jnp

def _softmax(x, axis=-1):
    return jax.nn.softmax(x, axis=axis)

def _gelu(x):
    return jax.nn.gelu(x, approximate=True)

def _silu(x):
    return jax.nn.silu(x)

def _sigmoid(x):
    return jax.nn.sigmoid(x)

def _layernorm(x, axis=-1, eps=1e-05):
    m = jnp.mean(x, axis=axis, keepdims=True)
    v = jnp.var(x, axis=axis, keepdims=True)
    return (x - m) / jnp.sqrt(v + eps)

def _scatter_add(tgt, idx, src, axis=0):
    return tgt.at[idx].add(src)

def _segment_sum(src, seg, n):
    return jax.ops.segment_sum(src, seg, n)
kernel_name = 'mk_xattn_ffn_d4_seqx_r8_59984b'

def setup_inputs(seed: int=0):
    np.random.seed(seed)
    _w = jnp.asarray

    def _rec_inputs():
        import jax
        import jax.numpy as jnp
        _rk = jax.random.key(seed)
        x = 7.22e-05 + 1 * jax.random.normal(jax.random.fold_in(_rk, 1), (8, 128, 512), jnp.float32)
        _lenS = 128 - jax.random.randint(jax.random.fold_in(_rk, 7), (8,), 0, max(1, 128 // 4) + 1, jnp.int32)
        _lenS2 = 128 - jax.random.randint(jax.random.fold_in(_rk, 8), (8,), 0, max(1, 128 // 4) + 1, jnp.int32)
        _ctx_4096P = jax.random.normal(jax.random.fold_in(_rk, 11), (8, 16, 512), jnp.float32)
        _ctx_4096c = jax.random.dirichlet(jax.random.fold_in(_rk, 511), 0.3 * jnp.ones((16,), jnp.float32), (8, 128))
        _ctx_4096t = jnp.einsum('bsk,bkd->bsd', _ctx_4096c, _ctx_4096P)
        _ctx_4096t = _ctx_4096t * jax.lax.rsqrt(jnp.mean(jnp.square(_ctx_4096t)) + 1e-12) * 0.953939
        ctx_4096 = 4.13588e-05 + 0.999923 * (_ctx_4096t + 0.3 * jax.random.normal(jax.random.fold_in(_rk, 611), (8, 128, 512), jnp.float32))
        pos_BxS2 = jnp.broadcast_to(jnp.arange(128, dtype=jnp.int32), (8, 128))
        _validS = jnp.arange(128)[None, :] < _lenS[:, None]
        _validS2 = jnp.arange(128)[None, :] < _lenS2[:, None]
        _causal = jnp.tril(jnp.ones((128, 128), dtype=bool))
        mask_BxSxS2_bk0 = jnp.logical_not(jnp.broadcast_to(_validS2[:, None, :], (8, 128, 128)))
        mask_Bx1x4096_ff1 = jnp.where(jnp.ones((8, 1, 512), dtype=bool), 1.0, 0.0).astype(jnp.float32)
        mask_BxSxS2_ik0 = jnp.where(jnp.broadcast_to(_validS2[:, None, :], (8, 128, 128)), 0, 1).astype(jnp.int32)
        return (x, ctx_4096, pos_BxS2, mask_BxSxS2_bk0, mask_Bx1x4096_ff1, mask_BxSxS2_ik0)
    x, ctx_4096, pos_BxS2, mask_BxSxS2_bk0, mask_Bx1x4096_ff1, mask_BxSxS2_ik0 = _rec_inputs()

    def _L0_xattn_setup():
        import jax, jax.numpy as jnp
        import numpy as np
        B, LQ, LK, D, H, DH = (2, 128, 128, 512, 32, 128)
        EPS = 1e-05

        def _rmsnorm(x, weight):
            var = jnp.mean(jnp.square(x), axis=-1, keepdims=True)
            return x * jax.lax.rsqrt(var + EPS) * weight
        key = jax.random.key(seed)
        ks = jax.random.split(key, 8)
        scale = 0.02
        return {'hidden_states': jax.random.normal(ks[0], (B, LQ, D), jnp.float32), 'key_value_states': jax.random.normal(ks[1], (B, LK, D), jnp.float32), 'attention_mask': jax.random.randint(ks[2], (B, LQ, LK), 0, 2) > 0, 'position_bias': jax.random.normal(ks[3], (H, LQ, LK), jnp.float32), 'ln_weight': jnp.ones((D,), jnp.float32), 'w_q': jax.random.normal(ks[4], (H * DH, D), jnp.float32) * scale, 'w_k': jax.random.normal(ks[5], (H * DH, D), jnp.float32) * scale, 'w_v': jax.random.normal(ks[6], (H * DH, D), jnp.float32) * scale, 'w_out': jax.random.normal(ks[7], (D, H * DH), jnp.float32) * scale}
    _L0_xattn_all = _L0_xattn_setup()
    _L0_xattn_in = {k: v for k, v in _L0_xattn_all.items() if k in ('position_bias', 'ln_weight', 'w_q', 'w_k', 'w_v', 'w_out')}
    del _L0_xattn_all

    def _L0_ffn_setup():
        import jax, jax.numpy as jnp
        import numpy as np

        def sparsemax(z):
            E = z.shape[-1]
            z_sorted = -jnp.sort(-z, axis=-1)
            z_cum = jnp.cumsum(z_sorted, axis=-1)
            k = jnp.arange(1, E + 1, dtype=z.dtype)
            support = 1.0 + k * z_sorted > z_cum
            k_z = jnp.sum(support, axis=-1, keepdims=True)
            tau_sum = jnp.take_along_axis(z_cum, k_z.astype(jnp.int32) - 1, axis=-1)
            tau = (tau_sum - 1.0) / k_z.astype(z.dtype)
            return jnp.maximum(z - tau, 0.0)
        key = jax.random.key(seed)
        ks = jax.random.split(key, 6)
        B, S, D_IN, D_OUT, E, R = (8, 256, 512, 512, 8, 16)
        x = jax.random.normal(ks[0], (B, S, D_IN), dtype=jnp.float32)
        W_base = jax.random.normal(ks[1], (D_OUT, D_IN), dtype=jnp.float32) * D_IN ** (-0.5)
        b_base = jax.random.normal(ks[2], (D_OUT,), dtype=jnp.float32) * 0.01
        W_router = jax.random.normal(ks[3], (E, D_IN), dtype=jnp.float32) * D_IN ** (-0.5)
        b_router = jnp.zeros((E,), dtype=jnp.float32)
        lora_A = jax.random.normal(ks[4], (E, D_IN, R), dtype=jnp.float32) * D_IN ** (-0.5)
        lora_B = jnp.zeros((E, R, D_OUT), dtype=jnp.float32)
        return {'x': x, 'W_base': W_base, 'b_base': b_base, 'W_router': W_router, 'b_router': b_router, 'lora_A': lora_A, 'lora_B': lora_B}
    _L0_ffn_all = _L0_ffn_setup()
    _L0_ffn_in = {k: v for k, v in _L0_ffn_all.items() if k in ('W_base', 'b_base', 'W_router', 'b_router', 'lora_A', 'lora_B')}
    del _L0_ffn_all

    def _L1_xattn_setup():
        import jax, jax.numpy as jnp
        import numpy as np
        W = 128
        H = 8
        D = 128
        DK = D // 2

        def _to_patches(x):
            b, d, s = x.shape
            np_ = s // W
            return x.reshape(b, d, np_, W).transpose(0, 2, 1, 3).reshape(b * np_, d, W)
        key = jax.random.key(seed)
        ks = jax.random.split(key, 10)
        B, S = (8, 512)
        qk = jax.random.normal(ks[0], (B, D, S), dtype=jnp.float32)
        v = jax.random.normal(ks[1], (B, D, S), dtype=jnp.float32)
        masks = jnp.ones((B, 1, S), dtype=jnp.float32)
        sc = 1.0 / np.sqrt(D)
        Wq = jax.random.normal(ks[2], (DK, D), dtype=jnp.float32) * sc
        bq = jnp.zeros((DK,), dtype=jnp.float32)
        Wk = jax.random.normal(ks[3], (DK, D), dtype=jnp.float32) * sc
        bk = jnp.zeros((DK,), dtype=jnp.float32)
        Wv = jax.random.normal(ks[4], (DK, D), dtype=jnp.float32) * sc
        bv = jnp.zeros((DK,), dtype=jnp.float32)
        Wo = jax.random.normal(ks[5], (D, DK), dtype=jnp.float32) * (1.0 / np.sqrt(DK))
        bo = jnp.zeros((D,), dtype=jnp.float32)
        return dict(qk=qk, v=v, masks=masks, Wq=Wq, bq=bq, Wk=Wk, bk=bk, Wv=Wv, bv=bv, Wo=Wo, bo=bo)
    _L1_xattn_all = _L1_xattn_setup()
    _L1_xattn_in = {k: v for k, v in _L1_xattn_all.items() if k in ('Wq', 'bq', 'Wk', 'bk', 'Wv', 'bv', 'Wo', 'bo')}
    del _L1_xattn_all

    def _L1_ffn_setup():
        import jax, jax.numpy as jnp
        import numpy as np
        IN_FEATURES = 512
        OUT_FEATURES = 512
        key = jax.random.key(seed)
        k_x, k_w, k_ws, k_b = jax.random.split(key, 4)
        x = jax.random.normal(k_x, (4, 256, IN_FEATURES), dtype=jnp.float16)
        weight = jax.random.randint(k_w, (OUT_FEATURES, IN_FEATURES), -127, 128, dtype=jnp.int32).astype(jnp.int8)
        weight_scales = (jax.random.uniform(k_ws, (OUT_FEATURES,), dtype=jnp.float32) * 0.02 + 0.001).astype(jnp.float16)
        bias = (jax.random.normal(k_b, (1, OUT_FEATURES), dtype=jnp.float32) * 0.01).astype(jnp.float16)
        return {'x': x, 'weight': weight, 'weight_scales': weight_scales, 'bias': bias}
    _L1_ffn_all = _L1_ffn_setup()
    _L1_ffn_in = {k: v for k, v in _L1_ffn_all.items() if k in ('weight', 'weight_scales', 'bias')}
    del _L1_ffn_all

    def _L2_xattn_setup():
        import jax, jax.numpy as jnp
        import numpy as np
        B, S, E = (2, 256, 512)
        H, KVH, D = (32, 8, 128)
        GROUPS = H // KVH
        MAX_POS = 512
        ROPE_THETA = 10000.0

        def _rope_tables(max_pos, dim, theta):
            inv_freq = 1.0 / theta ** (jnp.arange(0, dim, 2, dtype=jnp.float32) / dim)
            t = jnp.arange(max_pos, dtype=jnp.float32)
            freqs = jnp.einsum('i,j->ij', t, inv_freq)
            emb = jnp.concatenate([freqs, freqs], axis=-1)
            return (jnp.cos(emb), jnp.sin(emb))

        def _rotate_half(x):
            x1, x2 = (x[..., :x.shape[-1] // 2], x[..., x.shape[-1] // 2:])
            return jnp.concatenate([-x2, x1], axis=-1)
        key = jax.random.key(seed)
        ks = jax.random.split(key, 8)
        scale_w = 1.0 / np.sqrt(E)
        query = jax.random.normal(ks[0], (B, S, E), dtype=jnp.float32)
        k_in = jax.random.normal(ks[1], (B, S, E), dtype=jnp.float32)
        v_in = jax.random.normal(ks[2], (B, S, E), dtype=jnp.float32)
        position_ids = jnp.broadcast_to(jnp.arange(S, dtype=jnp.int64), (B, S))
        src_mask = jnp.tril(jnp.ones((S, S), dtype=jnp.int32))
        src_mask = jnp.broadcast_to(src_mask, (B, S, S))
        Wq = jax.random.normal(ks[3], (E, H * D), dtype=jnp.float32) * scale_w
        Wk = jax.random.normal(ks[4], (E, KVH * D), dtype=jnp.float32) * scale_w
        Wv = jax.random.normal(ks[5], (E, KVH * D), dtype=jnp.float32) * scale_w
        Wo = jax.random.normal(ks[6], (H * D, E), dtype=jnp.float32) * scale_w
        return {'query': query, 'key': k_in, 'value': v_in, 'position_ids': position_ids, 'src_mask': src_mask, 'Wq': Wq, 'Wk': Wk, 'Wv': Wv, 'Wo': Wo}
    _L2_xattn_all = _L2_xattn_setup()
    _L2_xattn_in = {k: v for k, v in _L2_xattn_all.items() if k in ('Wq', 'Wk', 'Wv', 'Wo')}
    del _L2_xattn_all

    def _L2_ffn_setup():
        import jax, jax.numpy as jnp
        import numpy as np
        NF4_CODE = jnp.array([-1.0, -0.6961928009986877, -0.5250730514526367, -0.39491748809814453, -0.28444138169288635, -0.18477343022823334, -0.09105003625154495, 0.0, 0.07958029955625534, 0.16093020141124725, 0.24611230194568634, 0.33791524171829224, 0.44070982933044434, 0.5626170039176941, 0.7229568362236023, 1.0], dtype=jnp.float32)
        BLOCKSIZE = 64

        def nf4_quant_dequant(w):
            shape = w.shape
            flat = w.reshape(-1, BLOCKSIZE)
            absmax = jnp.max(jnp.abs(flat), axis=1, keepdims=True)
            normalized = flat / jnp.where(absmax == 0, 1.0, absmax)
            bounds = (NF4_CODE[:-1] + NF4_CODE[1:]) * 0.5
            idx = jnp.searchsorted(bounds, normalized)
            return (NF4_CODE[idx] * absmax).reshape(shape)
        key = jax.random.key(seed)
        k1, k2, k3, kx = jax.random.split(key, 4)
        D, H = (512, 1376)
        scale = 0.02
        w1 = jax.random.normal(k1, (H, D), jnp.float32) * scale
        w2 = jax.random.normal(k2, (H, D), jnp.float32) * scale
        w3 = jax.random.normal(k3, (D, H), jnp.float32) * scale
        x = jax.random.normal(kx, (2, 256, D), jnp.float32)
        return {'x': x, 'w1': w1, 'w2': w2, 'w3': w3}
    _L2_ffn_all = _L2_ffn_setup()
    _L2_ffn_in = {k: v for k, v in _L2_ffn_all.items() if k in ('w1', 'w2', 'w3')}
    del _L2_ffn_all

    def _L3_xattn_setup():
        import jax, jax.numpy as jnp
        import numpy as np
        HEADS = 32
        KV_HEADS = 8
        HEAD_DIM = 128
        EPS = 1e-06

        def rms_norm(x, w):
            var = jnp.mean(jnp.square(x.astype(jnp.float32)), axis=-1, keepdims=True)
            return (x.astype(jnp.float32) * jax.lax.rsqrt(var + EPS)).astype(x.dtype) * w
        key = jax.random.key(seed)
        ks = jax.random.split(key, 6)
        bsz, n_lat, seq, hidden = (8, 64, 512, 512)
        return {'latents': jax.random.normal(ks[0], (bsz, n_lat, hidden), jnp.float32), 'context': jax.random.normal(ks[1], (bsz, seq, hidden), jnp.float32), 'Wq': jax.random.normal(ks[2], (hidden, HEADS * HEAD_DIM), jnp.float32) * 0.02, 'Wk': jax.random.normal(ks[3], (hidden, KV_HEADS * HEAD_DIM), jnp.float32) * 0.02, 'Wv': jax.random.normal(ks[4], (hidden, KV_HEADS * HEAD_DIM), jnp.float32) * 0.02, 'Wo': jax.random.normal(ks[5], (HEADS * HEAD_DIM, hidden), jnp.float32) * 0.02, 'q_norm_w': jnp.ones((HEAD_DIM,), jnp.float32), 'k_norm_w': jnp.ones((HEAD_DIM,), jnp.float32)}
    _L3_xattn_all = _L3_xattn_setup()
    _L3_xattn_in = {k: v for k, v in _L3_xattn_all.items() if k in ('Wq', 'Wk', 'Wv', 'Wo', 'q_norm_w', 'k_norm_w')}
    del _L3_xattn_all

    def _L3_ffn_setup():
        import jax, jax.numpy as jnp
        import numpy as np
        IN_F = 512
        OUT_F = 512
        RANK = 8
        NUM_EXPERTS = 64
        TOP_K = 16
        ROUTER_DIM = 16
        ALPHA = 32
        SCALING = ALPHA / TOP_K
        BOTTLENECK = NUM_EXPERTS * RANK
        key = jax.random.key(seed)
        ks = jax.random.split(key, 5)
        x = jax.random.normal(ks[0], (4, 512, IN_F), dtype=jnp.float32)
        bound_a = float(np.sqrt(6.0 / IN_F))
        A_w = jax.random.uniform(ks[1], (BOTTLENECK, IN_F), jnp.float32, -bound_a, bound_a)
        B_w = jax.random.normal(ks[2], (OUT_F, BOTTLENECK), dtype=jnp.float32) * 0.02
        Wq_w = jax.random.normal(ks[3], (ROUTER_DIM, IN_F), dtype=jnp.float32) * 0.02
        keys = jax.random.normal(ks[4], (NUM_EXPERTS, ROUTER_DIM), dtype=jnp.float32) * 0.01
        return {'x': x, 'A_w': A_w, 'B_w': B_w, 'Wq_w': Wq_w, 'keys': keys}
    _L3_ffn_all = _L3_ffn_setup()
    _L3_ffn_in = {k: v for k, v in _L3_ffn_all.items() if k in ('A_w', 'B_w', 'Wq_w', 'keys')}
    del _L3_ffn_all
    return {'x': x, 'ctx_4096': ctx_4096, 'pos_BxS2': pos_BxS2, 'mask_BxSxS2_bk0': mask_BxSxS2_bk0, 'mask_Bx1x4096_ff1': mask_Bx1x4096_ff1, 'mask_BxSxS2_ik0': mask_BxSxS2_ik0, 'L0_xattn_position_bias': _L0_xattn_in['position_bias'], 'L0_xattn_ln_weight': _L0_xattn_in['ln_weight'], 'L0_xattn_w_q': _L0_xattn_in['w_q'], 'L0_xattn_w_k': _L0_xattn_in['w_k'], 'L0_xattn_w_v': _L0_xattn_in['w_v'], 'L0_xattn_w_out': _L0_xattn_in['w_out'], 'L0_ffn_W_base': _L0_ffn_in['W_base'], 'L0_ffn_b_base': _L0_ffn_in['b_base'], 'L0_ffn_W_router': _L0_ffn_in['W_router'], 'L0_ffn_b_router': _L0_ffn_in['b_router'], 'L0_ffn_lora_A': _L0_ffn_in['lora_A'], 'L0_ffn_lora_B': _L0_ffn_in['lora_B'], 'L1_xattn_Wq': _L1_xattn_in['Wq'], 'L1_xattn_bq': _L1_xattn_in['bq'], 'L1_xattn_Wk': _L1_xattn_in['Wk'], 'L1_xattn_bk': _L1_xattn_in['bk'], 'L1_xattn_Wv': _L1_xattn_in['Wv'], 'L1_xattn_bv': _L1_xattn_in['bv'], 'L1_xattn_Wo': _L1_xattn_in['Wo'], 'L1_xattn_bo': _L1_xattn_in['bo'], 'L1_ffn_weight': _L1_ffn_in['weight'], 'L1_ffn_weight_scales': _L1_ffn_in['weight_scales'], 'L1_ffn_bias': _L1_ffn_in['bias'], 'L2_xattn_Wq': _L2_xattn_in['Wq'], 'L2_xattn_Wk': _L2_xattn_in['Wk'], 'L2_xattn_Wv': _L2_xattn_in['Wv'], 'L2_xattn_Wo': _L2_xattn_in['Wo'], 'L2_ffn_w1': _L2_ffn_in['w1'], 'L2_ffn_w2': _L2_ffn_in['w2'], 'L2_ffn_w3': _L2_ffn_in['w3'], 'L3_xattn_Wq': _L3_xattn_in['Wq'], 'L3_xattn_Wk': _L3_xattn_in['Wk'], 'L3_xattn_Wv': _L3_xattn_in['Wv'], 'L3_xattn_Wo': _L3_xattn_in['Wo'], 'L3_xattn_q_norm_w': _L3_xattn_in['q_norm_w'], 'L3_xattn_k_norm_w': _L3_xattn_in['k_norm_w'], 'L3_ffn_A_w': _L3_ffn_in['A_w'], 'L3_ffn_B_w': _L3_ffn_in['B_w'], 'L3_ffn_Wq_w': _L3_ffn_in['Wq_w'], 'L3_ffn_keys': _L3_ffn_in['keys']}

def reference(x, ctx_4096, pos_BxS2, mask_BxSxS2_bk0, mask_Bx1x4096_ff1, mask_BxSxS2_ik0, L0_xattn_position_bias, L0_xattn_ln_weight, L0_xattn_w_q, L0_xattn_w_k, L0_xattn_w_v, L0_xattn_w_out, L0_ffn_W_base, L0_ffn_b_base, L0_ffn_W_router, L0_ffn_b_router, L0_ffn_lora_A, L0_ffn_lora_B, L1_xattn_Wq, L1_xattn_bq, L1_xattn_Wk, L1_xattn_bk, L1_xattn_Wv, L1_xattn_bv, L1_xattn_Wo, L1_xattn_bo, L1_ffn_weight, L1_ffn_weight_scales, L1_ffn_bias, L2_xattn_Wq, L2_xattn_Wk, L2_xattn_Wv, L2_xattn_Wo, L2_ffn_w1, L2_ffn_w2, L2_ffn_w3, L3_xattn_Wq, L3_xattn_Wk, L3_xattn_Wv, L3_xattn_Wo, L3_xattn_q_norm_w, L3_xattn_k_norm_w, L3_ffn_A_w, L3_ffn_B_w, L3_ffn_Wq_w, L3_ffn_keys):
    import jax
    import jax.numpy as jnp

    def _L0_xattn_ref(hidden_states, key_value_states, attention_mask, position_bias, ln_weight, w_q, w_k, w_v, w_out):
        import jax, jax.numpy as jnp
        import numpy as np
        B, LQ, LK, D, H, DH = (2, 128, 128, 512, 32, 128)
        EPS = 1e-05

        def _rmsnorm(x, weight):
            var = jnp.mean(jnp.square(x), axis=-1, keepdims=True)
            return x * jax.lax.rsqrt(var + EPS) * weight
        x = _rmsnorm(hidden_states, ln_weight)
        b, lq, _ = x.shape
        lk = key_value_states.shape[1]
        h_q = (x @ w_q.T).reshape(b, lq, H, DH)
        h_k = (key_value_states @ w_k.T).reshape(b, lk, H, DH)
        h_v = (key_value_states @ w_v.T).reshape(b, lk, H, DH)
        score = jnp.einsum('bqhd,bkhd->bhqk', h_q, h_k)
        score = score + position_bias[None]
        m = attention_mask[:, None]
        score = jnp.where(m, score, -jnp.inf)
        score = jax.nn.softmax(score, axis=-1)
        score = jnp.where(m, score, 0.0)
        attn = jnp.einsum('bhqk,bkhd->bqhd', score, h_v).reshape(b, lq, H * DH)
        out = attn @ w_out.T
        return hidden_states + out

    def _L0_ffn_ref(x, W_base, b_base, W_router, b_router, lora_A, lora_B):
        import jax, jax.numpy as jnp
        import numpy as np

        def sparsemax(z):
            E = z.shape[-1]
            z_sorted = -jnp.sort(-z, axis=-1)
            z_cum = jnp.cumsum(z_sorted, axis=-1)
            k = jnp.arange(1, E + 1, dtype=z.dtype)
            support = 1.0 + k * z_sorted > z_cum
            k_z = jnp.sum(support, axis=-1, keepdims=True)
            tau_sum = jnp.take_along_axis(z_cum, k_z.astype(jnp.int32) - 1, axis=-1)
            tau = (tau_sum - 1.0) / k_z.astype(z.dtype)
            return jnp.maximum(z - tau, 0.0)
        base_out = jnp.einsum('bsd,od->bso', x, W_base) + b_base
        logits = jnp.einsum('bsd,ed->bse', x, W_router) + b_router
        weights = sparsemax(logits)
        h = jnp.einsum('bsd,edr->bser', x, lora_A)
        expert_out = jnp.einsum('bser,bse,ero->bso', h, weights, lora_B)
        return base_out + expert_out

    def _L1_xattn_ref(qk, v, masks, Wq, bq, Wk, bk, Wv, bv, Wo, bo):
        import jax, jax.numpy as jnp
        import numpy as np
        W = 128
        H = 8
        D = 128
        DK = D // 2

        def _to_patches(x):
            b, d, s = x.shape
            np_ = s // W
            return x.reshape(b, d, np_, W).transpose(0, 2, 1, 3).reshape(b * np_, d, W)
        B, _, S = qk.shape
        np_ = S // W
        qp = _to_patches(qk)
        vp = _to_patches(v)
        mp = _to_patches(masks)
        q = jnp.einsum('ed,bdw->bew', Wq, qp) + bq[:, None]
        k = jnp.einsum('ed,bdw->bew', Wk, qp) + bk[:, None]
        val = jnp.einsum('ed,bdw->bew', Wv, vp) + bv[:, None]
        BN = q.shape[0]
        dh = DK // H
        qh = q.reshape(BN, H, dh, W)
        kh = k.reshape(BN, H, dh, W)
        vh = val.reshape(BN, H, dh, W)
        scores = jnp.einsum('bhdi,bhdj->bhij', qh, kh) / jnp.sqrt(jnp.asarray(dh, qh.dtype))
        scores = jnp.where(mp[:, :, None, :] > 0, scores, jnp.asarray(-1000000000.0, scores.dtype))
        attn = jax.nn.softmax(scores, axis=-1)
        o = jnp.einsum('bhij,bhdj->bhdi', attn, vh).reshape(BN, DK, W)
        o = jax.nn.gelu(o, approximate=False)
        out = jnp.einsum('de,bew->bdw', Wo, o) + bo[:, None]
        out = out.reshape(B, np_, D, W).transpose(0, 2, 1, 3).reshape(B, D, S)
        out = out * masks
        return out

    def _L1_ffn_ref(x, weight, weight_scales, bias):
        import jax, jax.numpy as jnp
        import numpy as np
        IN_FEATURES = 512
        OUT_FEATURES = 512
        x_shape = x.shape
        xf = x.reshape(-1, x_shape[-1]).astype(jnp.float32)
        x_scale = jnp.max(jnp.abs(xf), axis=-1, keepdims=True) / 127.0
        q_x = jnp.clip(jnp.round(xf / x_scale), -128, 127).astype(jnp.int8)
        q_y = jnp.matmul(q_x.astype(jnp.int32), weight.T.astype(jnp.int32))
        y = q_y.astype(jnp.float32) * weight_scales.astype(jnp.float32)[None, :] * x_scale
        y = y.astype(jnp.float16).reshape(*x_shape[:-1], -1)
        y = y + bias
        return y

    def _L2_xattn_ref(query, key, value, position_ids, src_mask, Wq, Wk, Wv, Wo):
        import jax, jax.numpy as jnp
        import numpy as np
        B, S, E = (2, 256, 512)
        H, KVH, D = (32, 8, 128)
        GROUPS = H // KVH
        MAX_POS = 512
        ROPE_THETA = 10000.0

        def _rope_tables(max_pos, dim, theta):
            inv_freq = 1.0 / theta ** (jnp.arange(0, dim, 2, dtype=jnp.float32) / dim)
            t = jnp.arange(max_pos, dtype=jnp.float32)
            freqs = jnp.einsum('i,j->ij', t, inv_freq)
            emb = jnp.concatenate([freqs, freqs], axis=-1)
            return (jnp.cos(emb), jnp.sin(emb))

        def _rotate_half(x):
            x1, x2 = (x[..., :x.shape[-1] // 2], x[..., x.shape[-1] // 2:])
            return jnp.concatenate([-x2, x1], axis=-1)
        nb, q_len, _ = query.shape
        q = (query @ Wq).reshape(nb, q_len, H, D).transpose(0, 2, 1, 3)
        k = (key @ Wk).reshape(nb, q_len, KVH, D).transpose(0, 2, 1, 3)
        v = (value @ Wv).reshape(nb, q_len, KVH, D).transpose(0, 2, 1, 3)
        cos_t, sin_t = _rope_tables(MAX_POS, D, ROPE_THETA)
        cos = cos_t[position_ids][:, None]
        sin = sin_t[position_ids][:, None]
        q = q * cos + _rotate_half(q) * sin
        k = k * cos + _rotate_half(k) * sin
        k = jnp.repeat(k, GROUPS, axis=1)
        v = jnp.repeat(v, GROUPS, axis=1)
        scores = jnp.einsum('bhqd,bhkd->bhqk', q, k) / jnp.sqrt(jnp.float32(D))
        mask = src_mask[:, None]
        scores = jnp.where(mask == 0, jnp.float32(-1000000000.0), scores)
        attn = jax.nn.softmax(scores, axis=-1)
        x = jnp.einsum('bhqk,bhkd->bhqd', attn, v)
        x = x.transpose(0, 2, 1, 3).reshape(nb, q_len, H * D)
        return x @ Wo

    def _L2_ffn_ref(x, w1, w2, w3):
        import jax, jax.numpy as jnp
        import numpy as np
        NF4_CODE = jnp.array([-1.0, -0.6961928009986877, -0.5250730514526367, -0.39491748809814453, -0.28444138169288635, -0.18477343022823334, -0.09105003625154495, 0.0, 0.07958029955625534, 0.16093020141124725, 0.24611230194568634, 0.33791524171829224, 0.44070982933044434, 0.5626170039176941, 0.7229568362236023, 1.0], dtype=jnp.float32)
        BLOCKSIZE = 64

        def nf4_quant_dequant(w):
            shape = w.shape
            flat = w.reshape(-1, BLOCKSIZE)
            absmax = jnp.max(jnp.abs(flat), axis=1, keepdims=True)
            normalized = flat / jnp.where(absmax == 0, 1.0, absmax)
            bounds = (NF4_CODE[:-1] + NF4_CODE[1:]) * 0.5
            idx = jnp.searchsorted(bounds, normalized)
            return (NF4_CODE[idx] * absmax).reshape(shape)
        dq1 = nf4_quant_dequant(w1)
        dq2 = nf4_quant_dequant(w2)
        dq3 = nf4_quant_dequant(w3)
        gate = jnp.einsum('bsd,hd->bsh', x, dq1)
        up = jnp.einsum('bsd,hd->bsh', x, dq2)
        h = jax.nn.silu(gate) * up
        return jnp.einsum('bsh,dh->bsd', h, dq3)

    def _L3_xattn_ref(latents, context, Wq, Wk, Wv, Wo, q_norm_w, k_norm_w):
        import jax, jax.numpy as jnp
        import numpy as np
        HEADS = 32
        KV_HEADS = 8
        HEAD_DIM = 128
        EPS = 1e-06

        def rms_norm(x, w):
            var = jnp.mean(jnp.square(x.astype(jnp.float32)), axis=-1, keepdims=True)
            return (x.astype(jnp.float32) * jax.lax.rsqrt(var + EPS)).astype(x.dtype) * w
        bsz, q_len, hidden = latents.shape
        kv = jnp.concatenate([context, latents], axis=1)
        kv_len = kv.shape[1]
        groups = HEADS // KV_HEADS
        q = (latents @ Wq).reshape(bsz, q_len, HEADS, HEAD_DIM).transpose(0, 2, 1, 3)
        k = (kv @ Wk).reshape(bsz, kv_len, KV_HEADS, HEAD_DIM).transpose(0, 2, 1, 3)
        v = (kv @ Wv).reshape(bsz, kv_len, KV_HEADS, HEAD_DIM).transpose(0, 2, 1, 3)
        q = rms_norm(q, q_norm_w)
        k = rms_norm(k, k_norm_w)
        qg = q.reshape(bsz, KV_HEADS, groups, q_len, HEAD_DIM)
        scale = 1.0 / np.sqrt(HEAD_DIM)
        scores = jnp.einsum('bhgqd,bhkd->bhgqk', qg, k) * scale
        probs = jax.nn.softmax(scores.astype(jnp.float32), axis=-1).astype(q.dtype)
        out = jnp.einsum('bhgqk,bhkd->bhgqd', probs, v)
        out = out.reshape(bsz, HEADS, q_len, HEAD_DIM).transpose(0, 2, 1, 3)
        out = out.reshape(bsz, q_len, HEADS * HEAD_DIM)
        return out @ Wo

    def _L3_ffn_ref(x, A_w, B_w, Wq_w, keys):
        import jax, jax.numpy as jnp
        import numpy as np
        IN_F = 512
        OUT_F = 512
        RANK = 8
        NUM_EXPERTS = 64
        TOP_K = 16
        ROUTER_DIM = 16
        ALPHA = 32
        SCALING = ALPHA / TOP_K
        BOTTLENECK = NUM_EXPERTS * RANK
        q = jnp.einsum('bsd,rd->bsr', x, Wq_w)
        scores = jnp.einsum('bsr,er->bse', q, keys)
        top_vals, top_idx = jax.lax.top_k(scores, TOP_K)
        top_w = jax.nn.softmax(top_vals, axis=-1)
        gate = jnp.sum(jax.nn.one_hot(top_idx, NUM_EXPERTS, dtype=top_w.dtype) * top_w[..., None], axis=-2)
        z = jnp.einsum('bsd,nd->bsn', x, A_w)
        z = z.reshape(*z.shape[:-1], NUM_EXPERTS, RANK)
        z_gated = (z * gate[..., None]).reshape(*z.shape[:-2], BOTTLENECK)
        out = jnp.einsum('bsn,on->bso', z_gated, B_w) * SCALING
        return out
    x = x + _L0_xattn_ref(_layernorm(x, axis=-1), ctx_4096, mask_BxSxS2_bk0, L0_xattn_position_bias, L0_xattn_ln_weight, L0_xattn_w_q, L0_xattn_w_k, L0_xattn_w_v, L0_xattn_w_out)
    x = x + _L0_ffn_ref(_layernorm(x, axis=-1), L0_ffn_W_base, L0_ffn_b_base, L0_ffn_W_router, L0_ffn_b_router, L0_ffn_lora_A, L0_ffn_lora_B)
    x = x + _L1_xattn_ref(_layernorm(x, axis=-1), ctx_4096, mask_Bx1x4096_ff1, L1_xattn_Wq, L1_xattn_bq, L1_xattn_Wk, L1_xattn_bk, L1_xattn_Wv, L1_xattn_bv, L1_xattn_Wo, L1_xattn_bo)
    x = x + _L1_ffn_ref(_layernorm(x, axis=-1), L1_ffn_weight, L1_ffn_weight_scales, L1_ffn_bias)
    x = x + _L2_xattn_ref(_layernorm(x, axis=-1), ctx_4096, ctx_4096, pos_BxS2, mask_BxSxS2_ik0, L2_xattn_Wq, L2_xattn_Wk, L2_xattn_Wv, L2_xattn_Wo)
    x = x + _L2_ffn_ref(_layernorm(x, axis=-1), L2_ffn_w1, L2_ffn_w2, L2_ffn_w3)
    x = x + _L3_xattn_ref(_layernorm(x, axis=-1), ctx_4096, L3_xattn_Wq, L3_xattn_Wk, L3_xattn_Wv, L3_xattn_Wo, L3_xattn_q_norm_w, L3_xattn_k_norm_w)
    x = x + _L3_ffn_ref(_layernorm(x, axis=-1), L3_ffn_A_w, L3_ffn_B_w, L3_ffn_Wq_w, L3_ffn_keys)
    return x

_drawn_inputs = setup_inputs


def setup_inputs(seed=0):
    import zlib

    import numpy as np

    out = dict(_drawn_inputs(seed))
    spreads = {'L0_xattn_ln_weight': (1.0, 0.2),
     'L0_ffn_b_router': (0.0, 0.464),
     'L0_ffn_lora_B': (0.0, 0.1),
     'L1_xattn_bq': (0.0, 0.771),
     'L1_xattn_bk': (0.0, 2.0),
     'L1_xattn_bv': (0.0, 0.518),
     'L1_xattn_bo': (0.0, 0.488),
     'L3_xattn_q_norm_w': (1.0, 0.6),
     'L3_xattn_k_norm_w': (1.0, 0.6)}
    factors = {'L0_ffn_b_base': 5.475,
     'L1_ffn_bias': 64.0,
     'L2_ffn_w1': 8.0,
     'L2_ffn_w2': 8.0,
     'L2_ffn_w3': 8.0,
     'L3_xattn_Wq': 8.0,
     'L3_xattn_Wk': 8.0,
     'L3_xattn_Wv': 6.875,
     'L3_xattn_Wo': 6.755,
     'L3_ffn_A_w': 8.0,
     'L3_ffn_B_w': 8.0,
     'L3_ffn_Wq_w': 8.0,
     'L3_ffn_keys': 8.0}
    for name, (base, spread) in spreads.items():
        noise = np.random.default_rng([zlib.crc32(name.encode()), seed]).standard_normal(out[name].shape)
        drawn = base * np.exp(spread * noise) if base else spread * noise
        out[name] = jnp.asarray(drawn.astype(out[name].dtype))
    for name, factor in factors.items():
        out[name] = (out[name] * factor).astype(out[name].dtype)
    return out
```

```python
import math
from contextlib import ExitStack

import numpy as np

import concourse.bass as bass
from concourse import mybir

F32 = mybir.dt.float32
F32R = mybir.dt.float32r
BF16 = mybir.dt.bfloat16
F16 = mybir.dt.float16
I32 = mybir.dt.int32
I8 = mybir.dt.int8
U8 = mybir.dt.uint8
ALU = mybir.AluOpType
ACT = mybir.ActivationFunctionType
AX = mybir.AxisListType

P = 128
NB = 8
D = 512
DC = D // P
NT = NB * P
BANK = 512
H = 32
HI, LO = 0, 1
PASSES = ((HI, HI), (HI, LO), (LO, HI))
NEG = -1.0e30
NH2 = 1376
HC2 = -(-NH2 // P)
NF4_COLS = 2752
NF4_BLOCK = 64
NF4_CODE = [-1.0, -0.6961928009986877, -0.5250730514526367, -0.39491748809814453,
            -0.28444138169288635, -0.18477343022823334, -0.09105003625154495, 0.0,
            0.07958029955625534, 0.16093020141124725, 0.24611230194568634, 0.33791524171829224,
            0.44070982933044434, 0.5626170039176941, 0.7229568362236023, 1.0]


class Steps:

    def __init__(self, engine, sem, base=0):
        self.engine, self.sem, self.base, self.n = engine, sem, base, 0

    def mark(self, ins):
        ins.then_inc(self.sem, 1)
        self.n += 1

    def wait(self):
        self.engine.wait_ge(self.sem, self.base + self.n)


class Stage:

    def __init__(self, nc, name):
        self.nc, self.name, self.ctx, self.sems = nc, name, ExitStack(), []

    def sem(self, name):
        s = self.nc.alloc_semaphore(name=f"{self.name}_{name}")
        self.sems.append(s)
        return s

    def sb(self, name, shape, dt=F32):
        return self.ctx.enter_context(self.nc.sbuf_tensor(f"{self.name}_{name}", shape, dt))

    def ps(self, name, shape, dt=F32):
        return self.ctx.enter_context(self.nc.psum_tensor(f"{self.name}_{name}", shape, dt))

    def close(self):
        self.ctx.close()
        self.nc.clear_and_free_semaphores(self.sems)
        self.nc.all_engine_barrier()


def mm3(nc, out, lhs, rhs, first=True, last=True):
    for i, (a, b) in enumerate(PASSES):
        ins = nc.tensor.matmul(out, lhs(a), rhs(b), start=first and i == 0, stop=last and i == 2)
    return ins



def load_stage(nc, x, ident, ctx_t, x_in, ident_in, ctxt_in):
    st = Stage(nc, "load")
    raw = st.sb("ctx_raw", [P, DC, NT])
    loaded, ctx_loaded = st.sem("loaded"), st.sem("ctx_loaded")
    hi_done, lo_done = st.sem("hi_done"), st.sem("lo_done")
    with nc.Block() as block:
        @block.sync
        def _(sp):
            sp.dma_start(raw[:, :, :], ctxt_in.rearrange("(c p) t -> p c t", p=P)).then_inc(ctx_loaded, 16)
            sp.dma_start(x[:, :, :], x_in.rearrange("b t d -> t b d")).then_inc(loaded, 16)
            sp.dma_start(ident[:, :], ident_in).then_inc(loaded, 16)
            sp.wait_ge(loaded, 32)

        @block.scalar
        def _(act):
            act.wait_ge(ctx_loaded, 16)
            for c in range(DC):
                nc.scalar.activation(ctx_t[:, HI, c, :], raw[:, c, :], ACT.Copy).then_inc(hi_done, 1)

        @block.vector
        def _(dve):
            for c in range(DC):
                dve.wait_ge(hi_done, c + 1)
                nc.vector.tensor_tensor(ctx_t[:, LO, c, :], raw[:, c, :],
                                        ctx_t[:, HI, c, :].bitcast(F32), ALU.subtract).then_inc(lo_done, 1)
            dve.wait_ge(lo_done, DC)
    st.close()



class Norm:

    def __init__(self, st):
        self.stats = st.sb("stats", [P, NB, 6])
        self.mv = st.sb("mv", [P, NB, 2])
        self.var = st.sb("var", [P, NB])
        self.rstd = st.sb("rstd", [P, NB])
        self.half = st.sb("half", [P, 16])
        self.var_ready, self.rstd_ready = st.sem("var_ready"), st.sem("rstd_ready")
        self.half_set = st.sem("half_set")

    def stats_on_vector(self, nc, steps, x):
        for b in range(NB):
            steps.mark(nc.vector.bn_stats(self.stats[:, b, :], x[:, b, :]))
        steps.wait()
        for b in range(NB):
            steps.mark(nc.vector.bn_aggr(self.mv[:, b, :], self.stats[:, b, :]))
        steps.wait()
        nc.vector.tensor_scalar(self.var[:, :], self.mv[:, :, 1], 1e-5, None, ALU.add).then_inc(self.var_ready, 1)

    def set_half(self, nc):
        nc.gpsimd.memset(self.half[:, :], -0.5).then_inc(self.half_set, 1)

    def rstd_on_gpsimd(self, nc, pool):
        pool.wait_ge(self.half_set, 1)
        pool.wait_ge(self.var_ready, 1)
        nc.gpsimd.tensor_tensor(self.rstd[:, :], self.var[:, :], self.half[:, 0:NB], ALU.pow).then_inc(self.rstd_ready, 1)

    def apply(self, nc, b, out, x):
        return nc.vector.tensor_scalar(out, x[:, b, :], self.mv[:, b, 0:1], self.rstd[:, b:b + 1],
                                       ALU.subtract, ALU.mult)


def norm_stage(nc, name, x, ident, h_t, lnw_in=None):
    st = Stage(nc, name)
    rms = lnw_in is not None
    norm = Norm(st)
    h = st.sb("h", [P, NB, D])
    tp = st.ps("tp", [P, 4, DC, P])
    h_ready, tp_ready, hi_done, lo_done, own = (st.sem(n) for n in ("h_ready", "tp_ready", "hi_done", "lo_done", "own"))
    if rms:
        sq = st.sb("sq", [P, 2, D])
        ssq = st.sb("ssq", [P, NB])
        ms = st.sb("ms", [P, NB])
        r2 = st.sb("r2", [P, NB])
        h2 = st.sb("h2", [P, NB, D])
        lnw = st.sb("lnw", [P, DC])
        lnw_loaded, ssq_ready, ms_ready, r2_ready, ln_ready = (
            st.sem(n) for n in ("lnw_loaded", "ssq_ready", "ms_ready", "r2_ready", "ln_ready"))
    src = h2 if rms else h
    with nc.Block() as block:
        if rms:
            @block.sync
            def _(sp):
                with nc.allow_non_contiguous_dma(reason="512 weights"):
                    sp.dma_start(lnw[:, :], lnw_in).then_inc(lnw_loaded, 16)

        @block.gpsimd
        def _(pool):
            norm.set_half(nc)
            norm.rstd_on_gpsimd(nc, pool)
            if rms:
                pool.wait_ge(ms_ready, 1)
                nc.gpsimd.tensor_tensor(r2[:, :], ms[:, :], norm.half[:, 0:NB], ALU.pow).then_inc(r2_ready, 1)

        @block.vector
        def _(dve):
            steps = Steps(dve, own)
            norm.stats_on_vector(nc, steps, x)
            dve.wait_ge(norm.rstd_ready, 1)
            if rms:
                for b in range(NB):
                    norm.apply(nc, b, h[:, b, :], x).then_inc(ln_ready, 1)
                dve.wait_ge(ssq_ready, NB)
                nc.vector.tensor_scalar(ms[:, :], ssq[:, :], 1.0 / D, 1e-5, ALU.mult, ALU.add).then_inc(ms_ready, 1)
                for b in range(NB):
                    dve.wait_ge(ln_ready, b + 1)
                    nc.vector.tensor_tensor(x[:, b, :], x[:, b, :], h[:, b, :], ALU.add)
                dve.wait_ge(r2_ready, 1)
                for b in range(NB):
                    nc.vector.tensor_scalar(h2[:, b, :], h[:, b, :], r2[:, b:b + 1], None, ALU.mult).then_inc(h_ready, 1)
                dve.wait_ge(lnw_loaded, 16)
            else:
                for b in range(NB):
                    norm.apply(nc, b, h[:, b, :], x).then_inc(h_ready, 1)
            for b in range(NB):
                dve.wait_ge(hi_done, b + 1)
                dst = h_t[:, LO, :, b * P:(b + 1) * P]
                hi = h_t[:, HI, :, b * P:(b + 1) * P].bitcast(F32)
                if rms:
                    for c in range(DC):
                        ins = nc.vector.scalar_tensor_tensor(dst[:, c, :], tp[:, b % 4, c, :], lnw[:, c:c + 1],
                                                             hi[:, c, :], ALU.mult, ALU.subtract)
                else:
                    ins = nc.vector.tensor_tensor(dst, tp[:, b % 4, :, :], hi, ALU.subtract)
                ins.then_inc(lo_done, 1)
            dve.wait_ge(lo_done, NB)

        @block.tensor
        def _(pe):
            for b in range(NB):
                pe.wait_ge(h_ready, b + 1)
                if b >= 4:
                    pe.wait_ge(lo_done, b - 3)
                for c in range(DC):
                    ins = nc.tensor.transpose(tp[:, b % 4, c, :], src[:, b, c * P:(c + 1) * P], ident[:, :])
                ins.then_inc(tp_ready, 1)

        @block.scalar
        def _(act):
            if rms:
                for b in range(NB):
                    act.wait_ge(ln_ready, b + 1)
                    if b >= 2:
                        act.wait_ge(ssq_ready, b - 1)
                    nc.scalar.activation(sq[:, b % 2, :], h[:, b, :], ACT.Square,
                                         accum_out=ssq[:, b:b + 1]).then_inc(ssq_ready, 1)
                act.wait_ge(lnw_loaded, 16)
            for b in range(NB):
                act.wait_ge(tp_ready, b + 1)
                dst = h_t[:, HI, :, b * P:(b + 1) * P]
                if rms:
                    for c in range(DC):
                        ins = nc.scalar.activation(dst[:, c, :], tp[:, b % 4, c, :], ACT.Copy, scale=lnw[:, c:c + 1])
                else:
                    ins = nc.scalar.activation(dst, tp[:, b % 4, :, :], ACT.Copy)
                ins.then_inc(hi_done, 1)
    st.close()



class Place:

    def __init__(self, g, per, n):
        self.before = g * per + n if n or not isinstance(g, int) else g * per
        self.through = g * per + (n + 1)
        self.slot = n % 2
        self.turn = g * (per // 2) + (n // 2 + 1)
        self.filled = n >= 2 or not isinstance(g, int) or g > 0
        self.last_but_one = g * per + (n - 1) if self.filled else None


class Plan:

    def __init__(self, name, hpg, own_kv=False, kvb=1, rope=False, qknorm=False, out_every=2, scale=1.0):
        self.name, self.hpg, self.own_kv, self.kvb = name, hpg, own_kv, kvb
        self.rope, self.qknorm, self.out_every, self.scale = rope, qknorm, out_every, scale
        self.groups = H // hpg
        self.kvh = hpg if own_kv else 1
        self.keys = kvb * P
        self.vcols = self.kvh * P
        self.v_per = BANK // self.vcols
        self.v_tiles = NB * kvb // self.v_per
        self.s_tiles = NB * self.keys // BANK
        self.b_per_s = NB // self.s_tiles

    def q_keys(self, head):
        return [("q", head, 0), ("q", head, 1)]

    def k_keys(self):
        if self.qknorm:
            return [(k, t) for u in (0, 2) for k in ("kn", "kt") for t in (u, u + 1)]
        return [("k", h, half) for h in range(self.kvh) for half in range(2)]

    def v_keys(self):
        return [("v", t) for t in range(self.v_tiles)]

    def in_segment(self, j, last):
        return not (last and j + 2 >= self.hpg), not (last and j == self.hpg - 1), not last and j == self.hpg - 1

    def first_a(self):
        order = []
        for head in (0, 1):
            order += self.q_keys(head) + ([("ss", head)] if self.qknorm else [])
        return order + self.k_keys() + self.v_keys()

    def a_order(self, last=False):
        order = []
        for j in range(self.hpg):
            q_next, _, kv_next = self.in_segment(j, last)
            order += self.q_keys(j + 2) if q_next else []
            order += self.k_keys() if kv_next else []
            order += [("ss", j + 2)] if q_next and self.qknorm else []
            if (j + 1) % self.out_every == 0:
                order += [("o", j, b) for b in range(NB)]
            order += self.v_keys() if kv_next else []
        return order

    def hi_of(self, order):
        return [k for k in order if k[0] not in ("o", "ss") and not (self.rope and k[0] in "qk")]

    def ms_of(self, order):
        return [k for k in order if k[0] in ("ss", "kn")]

    def rot_of(self, order):
        return [k for k in order if k[0] in ("q", "k")]

    def first_rot_parts(self):
        return self.rot_of(self.first_a())

    def rot_parts_order(self, last=False):
        order = []
        for j in range(self.hpg):
            q_next, _, kv_next = self.in_segment(j, last)
            order += (self.k_keys() if kv_next else []) + (self.q_keys(j + 2) if q_next else [])
        return order

    def first_w(self):
        kv = [(kind, 0, i) for kind in "kv" for i in range(self.kvh)]
        return [("q", 0), ("q", 1)] + kv + [("q", 2)]

    def segment_w(self, j, last=False):
        out = [("q", j + 3)] if not (last and j + 3 >= self.hpg) else []
        out.append(("o", j))
        if not last and j < 2:
            out += [("kv"[j], 1, i) for i in range(self.kvh)]
        return out

    def w_order(self, last=False):
        return [w for j in range(self.hpg) for w in self.segment_w(j, last)]

    def all_w(self):
        order = self.first_w()
        for g in range(self.groups):
            for kind, n, *slot in self.w_order(g == self.groups - 1):
                order.append((kind, g + n, *slot) if slot else (kind, g * self.hpg + n))
        return order


def attention_stage(nc, plan, x, ident, ctx_t, h_t, pieces_in, mask_in=None, bias_in=None, rope_sb=None, kq_norm_in=None):
    st = Stage(nc, plan.name)
    hpg, keys, kvh, kvb = plan.hpg, plan.keys, plan.kvh, plan.kvb
    rope, qknorm = plan.rope, plan.qknorm
    masked, biased = mask_in is not None, bias_in is not None
    bps, NS, NG = plan.b_per_s, plan.s_tiles, plan.groups

    raw = st.sb("raw", [P, 2, D])
    wq = st.sb("wq", [P, 2, 2, DC, P], F32R)
    wo = st.sb("wo", [P, 2, 2, D], F32R)
    wk = st.sb("wk", [P, kvh, 2, DC, P], F32R)
    wv = st.sb("wv", [P, 2, DC, kvh, P], F32R)
    qt = st.sb("qt", [P, 2, 2, NT], F32R)
    kt = st.sb("kt", [P, kvh, 2, NB * keys], F32R)
    v = st.sb("v", [P, 2, NB * kvb, plan.vcols], F32R)
    prob = st.sb("prob", [P, 2, NB, keys])
    pt = st.sb("pt", [P, 2, 2, BANK], F32R)
    ot = st.sb("ot", [P, plan.out_every, 2, NT], F32R)
    top = st.sb("top", [P, 2, NB])
    shift = st.sb("shift", [P, 2, NB])
    total = st.sb("total", [P, 2, NB])
    inv = st.sb("inv", [P, 2, NB])
    if masked:
        neg = st.sb("neg", [P, NB, P])
        words = st.sb("words", [P, NB, mask_in.shape[2]], I32)
        mask = words[:, :, :] if mask_in.shape[2] == P else words[:, :, :].bitcast(U8)
        mask_loaded, s_used = st.sem("mask_loaded"), st.sem("s_used")
    if biased:
        bias_raw = st.sb("bias_raw", [P, 2, P])
        bias = st.sb("bias", [P, NB, P])
        valid = st.sb("valid", [P, 2, NB])
        bias_loaded = [st.sem("bias_loaded0"), st.sem("bias_loaded1")]
        bias_ready = st.sem("bias_ready")
    if rope:
        cos, sin = rope_sb
        rot = st.sb("rot", [P, 4, 2, BANK])
        rot_ready, rot_sum, rot_hi, rot_lo = (st.sem(n) for n in ("rot_ready", "rot_sum", "rot_hi", "rot_lo"))
    if qknorm:
        q2 = st.sb("q2", [P, NT])
        k2 = st.sb("k2", [P, 2, BANK])
        kn = st.sb("kn", [P, 2, 4, P])
        kss = st.sb("kss", [P, 4, 4])
        kms = st.sb("kms", [P, 4, 4])
        krs = st.sb("krs", [P, 4, 4])
        qms = st.sb("qms", [P, 2, NB])
        qsc = st.sb("qsc", [P, 2, NB])
        half_ = st.sb("half", [P, NB])
        ones = st.sb("ones", [P, 1])
        kqw = st.sb("kqw", [P, 2])
        kw = st.sb("kw", [P, 1])
        kqw_loaded, sq_done, ms_ready, rs_ready, kn_ready = (
            st.sem(n) for n in ("kqw_loaded", "sq_done", "ms_ready", "rs_ready", "kn_ready"))
    pa = st.ps("pa", [P, 2, BANK])
    pscore = st.ps("pscore", [P, 2, BANK])
    ptr = st.ps("ptr", [P, 2, BANK])
    pout = st.ps("pout", [P, 2, BANK])

    raw_loaded = [st.sem("raw_loaded0"), st.sem("raw_loaded1")]
    (split_done, a_ready, a_hi, a_used, s_ready, shift_ready, exp_done, inv_ready, norm_done,
     t_ready, t_hi, t_used, o_ready, o_hi, o_used, own, pool_set, pool_own) = (st.sem(n) for n in (
         "split_done", "a_ready", "a_hi", "a_used", "s_ready", "shift_ready", "exp_done",
         "inv_ready", "norm_done", "t_ready", "t_hi", "t_used", "o_ready", "o_hi", "o_used", "own",
         "pool_set", "pool_own"))
    piece_seen = st.sem("piece_seen")
    s_free = s_used if masked else exp_done
    n_first_a, n_group_a = len(plan.first_a()), len(plan.a_order())
    assert n_first_a % 2 == 0 and n_group_a % 2 == 0 and len(plan.w_order()) % 2 == 0
    n_first_w, n_group_w = len(plan.first_w()), len(plan.w_order())
    n_set = 1 + (3 if qknorm else 0)

    class Orders:

        def __init__(self, g=None, last=False):
            first = g is None
            self.a_keys = plan.first_a() if first else plan.a_order(last)
            w_keys = plan.first_w() if first else plan.w_order(last)
            parts = plan.first_rot_parts() if first else plan.rot_parts_order(last)
            at = 0 if first else g

            def places(keys, first_n, group_n):
                return {k: Place(at, group_n, i + (0 if first else first_n)) for i, k in enumerate(keys)}

            fa, ga = plan.first_a(), plan.a_order()
            self.a = places(self.a_keys, len(fa), len(ga))
            self.hi = places(plan.hi_of(self.a_keys), len(plan.hi_of(fa)), len(plan.hi_of(ga)))
            self.ms = places(plan.ms_of(self.a_keys), len(plan.ms_of(fa)), len(plan.ms_of(ga)))
            self.rot = places(plan.rot_of(self.a_keys), len(plan.rot_of(fa)), len(plan.rot_of(ga)))
            self.part = places(parts, len(plan.rot_of(fa)), len(plan.rot_of(ga)))
            self.w = places(w_keys, n_first_w, n_group_w)

    def body(engine, emit):
        with engine.Fori(0, NG - 1) as g:
            emit(g, False)
        emit(NG - 1, True)

    with nc.Block() as block:
        @block.sync
        def _(sp):
            if qknorm:
                with nc.allow_non_contiguous_dma(reason="256 weights"):
                    sp.dma_start(kqw[:, :], kq_norm_in).then_inc(kqw_loaded, 16)
            if masked:
                sp.dma_start(words[:, :, :], mask_in.rearrange("b q k -> q b k")).then_inc(mask_loaded, 16)

            def load_piece(place):
                if place.filled:
                    sp.wait_ge(split_done, place.last_but_one)
                sp.dma_start(raw[:, place.slot, :], pieces_in[bass.ds(place.before, 1), :, :].rearrange("o p n -> p (o n)")
                             ).then_inc(raw_loaded[place.slot], 16)

            def load_bias(head, slot):
                sp.dma_start(bias_raw[:, slot, :], bias_in[bass.ds(head, 1), :, :].rearrange("o q k -> q (o k)")
                             ).then_inc(bias_loaded[slot], 16)

            for place in Orders().w.values():
                load_piece(place)
            if biased:
                load_bias(0, 0)
                load_bias(1, 1)

            def group(g, last):
                w = Orders(g, last).w
                for j in range(hpg):
                    for key in plan.segment_w(j, last):
                        load_piece(w[key])
                    if biased and plan.in_segment(j, last)[0]:
                        sp.wait_ge(bias_ready, g * hpg + (j + 1))
                        load_bias(g * hpg + (j + 2), j % 2)

            body(sp, group)

        @block.gpsimd
        def _(pool):
            def split_piece(key, place, steps):
                src = raw[:, place.slot, :]
                kind, n = key[0], key[-1]
                dst = {"q": lambda p: wq[:, n % 2, p, :, :], "o": lambda p: wo[:, n % 2, p, :],
                       "k": lambda p: wk[:, n, p, :, :], "v": lambda p: wv[:, p, :, n, :]}[kind]
                if kind != "o":
                    src = src.rearrange("p (c n) -> p c n", c=DC)
                pool.wait_ge(raw_loaded[place.slot], place.turn * 16)
                pool.sem_inc(piece_seen, 1)
                steps.mark(nc.gpsimd.tensor_scalar(dst(HI), src, 1.0, 0.0, ALU.mult, ALU.add))
                steps.wait()
                nc.gpsimd.tensor_tensor(dst(LO), src, dst(HI).bitcast(F32), ALU.subtract).then_inc(split_done, 1)

            def make_bias(slot, turn, used=None):
                pool.wait_ge(bias_loaded[slot], turn * 16)
                if used is not None:
                    pool.wait_ge(s_used, used)
                nc.gpsimd.tensor_tensor(bias[:, :, :], neg[:, :, :],
                                        bias_raw[:, slot, None, :].broadcast_to([P, NB, P]),
                                        ALU.add).then_inc(bias_ready, 1)

            def sum_rotated(key, place):
                tile = key[2] + (2 if key[0] == "k" else 0)
                pool.wait_ge(rot_ready, place.through)
                nc.gpsimd.tensor_tensor(rot[:, tile, 0, :], rot[:, tile, 0, :], rot[:, tile, 1, :],
                                        ALU.add).then_inc(rot_sum, 1)

            def inverse_root(key, place):
                pool.wait_ge(ms_ready, place.through)
                if key[0] == "ss":
                    src, dst = qms[:, key[1] % 2, :], qsc[:, key[1] % 2, :]
                    nc.gpsimd.tensor_tensor(dst, src, half_[:, :], ALU.pow).then_inc(rs_ready, 1)
                else:
                    src, dst = kms[:, key[1], :], krs[:, key[1], :]
                    nc.gpsimd.tensor_tensor(dst, src, half_[:, 0:4], ALU.pow).then_inc(rs_ready, 1)

            if qknorm:
                nc.gpsimd.memset(half_[:, :], -0.5).then_inc(pool_set, 1)
                nc.gpsimd.memset(ones[:, :], 1.0).then_inc(pool_set, 1)
                pool.wait_ge(kqw_loaded, 16)
                nc.gpsimd.tensor_tensor(kw[:, :], kqw[:, 0:1], kqw[:, 1:2], ALU.mult).then_inc(pool_set, 1)
            if not masked:
                nc.gpsimd.memset(inv[:, :, :], 0.0).then_inc(pool_set, 1)
            else:
                pool.wait_ge(mask_loaded, 16)
                nc.gpsimd.tensor_scalar(neg[:, :, :], mask, 0.0, NEG, ALU.is_equal, ALU.mult).then_inc(pool_set, 1)
            pool.wait_ge(pool_set, n_set)
            steps = Steps(pool, pool_own)
            o = Orders()
            for key, place in o.w.items():
                if key == ("q", 2):
                    pool.wait_ge(a_ready, o.a["q", 0, 1].through)
                split_piece(key, place, steps)
            if biased:
                make_bias(0, 1)
                make_bias(1, 1, NS)
            if rope:
                for key, place in o.rot.items():
                    sum_rotated(key, place)
            if qknorm:
                for key, place in o.ms.items():
                    inverse_root(key, place)

            def group(g, last):
                o = Orders(g, last)
                steps = Steps(pool, pool_own, g * n_group_w + n_first_w)
                for j in range(hpg):
                    q_next, _, kv_next = plan.in_segment(j, last)
                    pool.wait_ge(inv_ready, g * hpg + (j + 1))
                    nc.gpsimd.tensor_tensor(prob[:, j % 2, :, :], prob[:, j % 2, :, :],
                                            inv[:, j % 2, :, None].broadcast_to([P, NB, keys]),
                                            ALU.mult).then_inc(norm_done, 1)
                    if rope:
                        for key in (plan.q_keys(j + 2) if q_next else []) + (plan.k_keys() if kv_next else []):
                            sum_rotated(key, o.rot[key])
                    if qknorm:
                        for key in ([k for k in plan.k_keys() if k[0] == "kn"] if kv_next else []) + (
                                [("ss", j + 2)] if q_next else []):
                            inverse_root(key, o.ms[key])
                    for key in plan.segment_w(j, last):
                        if key[0] == "o" and plan.out_every == 2 and j % 2 == 0:
                            if j > 0:
                                pool.wait_ge(a_ready, o.a["o", j - 1, NB - 1].through)
                            elif not (isinstance(g, int) and g == 0):
                                pool.wait_ge(a_ready, g * n_group_a + (n_first_a - plan.v_tiles))
                        split_piece(key, o.w[key], steps)
                    if biased and q_next:
                        make_bias(j % 2, g * (hpg // 2) + (j // 2 + 2), (g * hpg + (j + 2)) * NS)

            body(pool, group)

        @block.tensor
        def _(pe):
            def tile_of_a(place):
                if place.filled:
                    pe.wait_ge(a_used, place.last_but_one)
                return pa[:, place.slot, :]

            def queries(o, head):
                for half in range(2):
                    out = tile_of_a(o.a["q", head, half])
                    for c in range(DC):
                        ins = mm3(nc, out, lambda p: wq[:, head % 2, p, c, :],
                                  lambda p: h_t[:, p, c, half * BANK:(half + 1) * BANK], c == 0, c == DC - 1)
                    ins.then_inc(a_ready, 1)

            def query_squares(o, head, count):
                out = tile_of_a(o.a["ss", head])
                pe.wait_ge(sq_done, count)
                for b in range(NB):
                    ins = nc.tensor.matmul(out[:, b:b + 1], q2[:, b * P:(b + 1) * P], ones[:, :], start=True, stop=True)
                ins.then_inc(a_ready, 1)

            def keys_of(o, kn_before):
                for key in plan.k_keys():
                    out = tile_of_a(o.a[key])
                    if key[0] == "k":
                        _, h, half = key
                        for c in range(DC):
                            ins = mm3(nc, out, lambda p: wk[:, h, p, c, :],
                                      lambda p: ctx_t[:, p, c, half * BANK:(half + 1) * BANK], c == 0, c == DC - 1)
                    elif key[0] == "kn":
                        for i in range(4):
                            b, src = 2 * key[1] + i // 2, (ctx_t, h_t)[i % 2]
                            for c in range(DC):
                                ins = mm3(nc, out[:, i * P:(i + 1) * P], lambda p: src[:, p, c, b * P:(b + 1) * P],
                                          lambda p: wk[:, 0, p, c, :], c == 0, c == DC - 1)
                    else:
                        pe.wait_ge(kn_ready, kn_before + (key[1] + 1))
                        for i in range(4):
                            ins = nc.tensor.transpose(out[:, i * P:(i + 1) * P], kn[:, key[1] % 2, i, :], ident[:, :])
                    ins.then_inc(a_ready, 1)

            def values(o):
                for key in plan.v_keys():
                    out = tile_of_a(o.a[key])
                    for i in range(plan.v_per):
                        n = key[1] * plan.v_per + i
                        b, src = n // kvb, (ctx_t, h_t)[n % kvb]
                        for c in range(DC):
                            ins = mm3(nc, out[:, i * plan.vcols:(i + 1) * plan.vcols],
                                      lambda p: src[:, p, c, b * P:(b + 1) * P],
                                      lambda p: wv[:, p, c, :, :], c == 0, c == DC - 1)
                    ins.then_inc(a_ready, 1)

            def scores(slot, kv_head, head):
                for t in range(NS):
                    if not (isinstance(head, int) and head * NS + t < 2):
                        pe.wait_ge(s_free, head * NS + (t - 1))
                    for i in range(bps):
                        b = t * bps + i
                        ins = mm3(nc, pscore[:, t % 2, i * keys:(i + 1) * keys],
                                  lambda p: qt[:, slot, p, b * P:(b + 1) * P],
                                  lambda p: kt[:, kv_head, p, b * keys:(b + 1) * keys])
                    ins.then_inc(s_ready, 1)

            def weigh(j, head):
                pe.wait_ge(norm_done, head + 1)
                col = (j if plan.own_kv else 0) * P
                flat = prob[:, j % 2, :, :].rearrange("p b k -> p (b k)")

                def transpose(t):
                    pe.wait_ge(t_used, head * NS + (t + 1))
                    for i in range(4):
                        ins = nc.tensor.transpose(ptr[:, t % 2, i * P:(i + 1) * P],
                                                  flat[:, t * BANK + i * P:t * BANK + (i + 1) * P], ident[:, :])
                    ins.then_inc(t_ready, 1)

                def weighed(n):
                    pe.wait_ge(o_used, head * 2 + (n + 1))
                    for t in range(n * NS // 2, (n + 1) * NS // 2):
                        pe.wait_ge(t_used, head * NS + (t + 3))
                        for i in range(bps):
                            b = t * bps + i
                            for s in range(kvb):
                                cols = slice((i * kvb + s) * P, (i * kvb + s + 1) * P)
                                ins = mm3(nc, pout[:, n, (b % 4) * P:(b % 4 + 1) * P],
                                          lambda p: v[:, p, b * kvb + s, col:col + P],
                                          lambda p: pt[:, t % 2, p, cols], s == 0, s == kvb - 1)
                    ins.then_inc(o_ready, 1)

                transpose(0)
                transpose(1)
                weighed(0)
                if NS == 4:
                    transpose(2)
                    transpose(3)
                weighed(1)

            def output(o, j, head):
                pe.wait_ge(split_done, o.w["o", j].through)
                pe.wait_ge(o_used, (head + 1) * 2 + 2)
                heads = range(j - plan.out_every + 1, j + 1)
                for b in range(NB):
                    out = tile_of_a(o.a["o", j, b])
                    for i in heads:
                        ins = mm3(nc, out, lambda p: ot[:, i % plan.out_every, p, b * P:(b + 1) * P],
                                  lambda p: wo[:, i % 2, p, :], i == heads[0], i == heads[-1])
                    ins.then_inc(a_ready, 1)

            def parts_ready(o, key):
                if rope:
                    pe.wait_ge(rot_lo, o.part[key].through)
                else:
                    pe.wait_ge(a_used, o.a[key].through)

            o = Orders()
            if qknorm:
                pe.wait_ge(pool_set, n_set)
            for head in (0, 1):
                pe.wait_ge(split_done, o.w["q", head].through)
                queries(o, head)
                if qknorm:
                    query_squares(o, head, 2 * (head + 1))
            pe.wait_ge(split_done, o.w["k", 0, kvh - 1].through)
            keys_of(o, 0)
            parts_ready(o, plan.k_keys()[-1])
            scores(0, 0, 0)
            pe.wait_ge(split_done, o.w["v", 0, kvh - 1].through)
            values(o)

            def group(g, last):
                o = Orders(g, last)
                pieces = 0
                for j in range(hpg):
                    head = g * hpg + j
                    q_next, score_next, kv_next = plan.in_segment(j, last)
                    if q_next:
                        pe.wait_ge(split_done, g * n_group_w + (n_first_w + pieces))
                        queries(o, j + 2)
                    if kv_next:
                        keys_of(o, (g + 1) * 4)
                        parts_ready(o, plan.k_keys()[-1])
                    elif score_next and j > 0:
                        parts_ready(o, ("q", j + 1, 1))
                    if score_next:
                        scores((j + 1) % 2, (j + 1) % hpg if plan.own_kv else 0, head + 1)
                    if qknorm and q_next:
                        query_squares(o, j + 2, g * (2 * hpg) + (4 + 2 * (j + 1)))
                    if j == 0:
                        pe.wait_ge(a_used, g * n_group_a + n_first_a)
                    weigh(j, head)
                    pieces += len(plan.segment_w(j, last))
                    if (j + 1) % plan.out_every == 0:
                        output(o, j, head)
                    if kv_next:
                        pe.wait_ge(split_done, o.w["v", 1, kvh - 1].through)
                        values(o)

            body(pe, group)

        @block.scalar
        def _(act):
            def hi(o, key, dst, **scale):
                act.wait_ge(a_ready, o.a[key].through)
                nc.scalar.activation(dst, pa[:, o.a[key].slot, :], ACT.Copy, **scale).then_inc(a_hi, 1)

            def query_hi(o, head):
                for half in range(2):
                    cols, key = slice(half * BANK, (half + 1) * BANK), ("q", head, half)
                    if qknorm:
                        act.wait_ge(a_ready, o.a[key].through)
                        nc.scalar.activation(q2[:, cols], pa[:, o.a[key].slot, :], ACT.Square).then_inc(sq_done, 1)
                    hi(o, key, qt[:, head % 2, HI, cols])

            def rotated_hi(o, key, dst):
                tile = key[2] + (2 if key[0] == "k" else 0)
                act.wait_ge(rot_sum, o.rot[key].through)
                nc.scalar.activation(dst, rot[:, tile, 0, :], ACT.Copy).then_inc(rot_hi, 1)

            def rotated_query_hi(o, head):
                for half in range(2):
                    rotated_hi(o, ("q", head, half), qt[:, head % 2, HI, half * BANK:(half + 1) * BANK])

            def keys_hi(o):
                for key in plan.k_keys():
                    if key[0] == "k":
                        dst = kt[:, key[1], HI, key[2] * BANK:(key[2] + 1) * BANK]
                        (rotated_hi if rope else hi)(o, key, dst)
                    elif key[0] == "kn":
                        act.wait_ge(a_ready, o.a[key].through)
                        nc.scalar.activation(k2[:, key[1] % 2, :], pa[:, o.a[key].slot, :], ACT.Square).then_inc(a_hi, 1)
                    else:
                        hi(o, key, kt[:, 0, HI, key[1] * BANK:(key[1] + 1) * BANK], scale=kw[:, :])

            def values_hi(o):
                for key in plan.v_keys():
                    blocks = slice(key[1] * plan.v_per, (key[1] + 1) * plan.v_per)
                    hi(o, key, v[:, HI, blocks, :].rearrange("p b n -> p (b n)"))

            def exps(slot, head):
                if masked:
                    act.wait_ge(shift_ready, head + 1)
                for t in range(NS):
                    if not masked:
                        act.wait_ge(shift_ready, head * NS + (t + 1))
                    for i in range(bps):
                        b = t * bps + i
                        src, scale = prob[:, slot, b, :], plan.scale
                        if not masked:
                            src, scale = pscore[:, t % 2, i * keys:(i + 1) * keys], qsc[:, slot, b:b + 1]
                        ins = nc.scalar.activation(prob[:, slot, b, :], src, ACT.Exp, bias=shift[:, slot, b:b + 1],
                                                   scale=scale, accum_out=total[:, slot, b:b + 1])
                    if not masked or t == NS - 1:
                        ins.then_inc(exp_done, 1)

            def weights_hi(j, head):
                def weight(t):
                    act.wait_ge(t_ready, head * NS + (t + 1))
                    nc.scalar.activation(pt[:, t % 2, HI, :], ptr[:, t % 2, :], ACT.Copy).then_inc(t_hi, 1)

                def weighed(n):
                    act.wait_ge(o_ready, head * 2 + (n + 1))
                    nc.scalar.activation(ot[:, j % plan.out_every, HI, n * BANK:(n + 1) * BANK], pout[:, n, :],
                                         ACT.Copy).then_inc(o_hi, 1)

                weight(0)
                weight(1)
                weighed(0)
                if NS == 4:
                    weight(2)
                    weight(3)
                weighed(1)

            if qknorm:
                act.wait_ge(pool_set, n_set)
            o = Orders()
            if not rope:
                query_hi(o, 0)
                query_hi(o, 1)
            else:
                rotated_query_hi(o, 0)
                rotated_query_hi(o, 1)
            keys_hi(o)
            exps(0, 0)
            values_hi(o)

            def group(g, last):
                o = Orders(g, last)
                for j in range(hpg):
                    head = g * hpg + j
                    q_next, score_next, kv_next = plan.in_segment(j, last)
                    if q_next and not rope:
                        query_hi(o, j + 2)
                    if kv_next:
                        keys_hi(o)
                    if score_next and not masked:
                        exps((j + 1) % 2, head + 1)
                    weights_hi(j, head)
                    if q_next and rope:
                        rotated_query_hi(o, j + 2)
                    if score_next and masked:
                        exps((j + 1) % 2, head + 1)
                    if kv_next:
                        values_hi(o)

            body(act, group)

        @block.vector
        def _(dve):
            def lo(o, key, dst, hi_part, scale=None):
                dve.wait_ge(a_hi, o.hi[key].through)
                src = pa[:, o.a[key].slot, :]
                if scale is None:
                    nc.vector.tensor_tensor(dst, src, hi_part.bitcast(F32), ALU.subtract).then_inc(a_used, 1)
                else:
                    nc.vector.scalar_tensor_tensor(dst, src, scale, hi_part.bitcast(F32), ALU.mult,
                                                   ALU.subtract).then_inc(a_used, 1)

            def rotate(o, key):
                half = key[2]
                tile, cols = half + (2 if key[0] == "k" else 0), slice(half * BANK, (half + 1) * BANK)
                src = pa[:, o.a[key].slot, :]
                dve.wait_ge(a_ready, o.a[key].through)
                with_keys = key[0] == "k" or (key[1] == hpg + 1 and plan.k_keys()[0] in o.part)
                parts = o.part[plan.k_keys()[0] if with_keys else (key[0], key[1], 0)].before
                if not isinstance(parts, int) or parts:
                    dve.wait_ge(rot_lo, parts)
                nc.vector.tensor_tensor(rot[:, tile, 0, :], src, cos[:, cols], ALU.mult)
                nc.vector.tensor_tensor(rot[0:64, tile, 1, :], src[64:128, :], sin[0:64, cols], ALU.mult)
                ins = nc.vector.tensor_tensor(rot[64:128, tile, 1, :], src[0:64, :], sin[64:128, cols], ALU.mult)
                ins.then_inc(rot_ready, 1)
                dve.wait_ge(rot_ready, o.rot[key].through)
                dve.sem_inc(a_used, 1)

            def rotated_lo(o, key, dst, hi_part):
                tile = key[2] + (2 if key[0] == "k" else 0)
                dve.wait_ge(rot_hi, o.part[key].through)
                nc.vector.tensor_tensor(dst, rot[:, tile, 0, :], hi_part.bitcast(F32), ALU.subtract).then_inc(rot_lo, 1)

            def query_lo(o, head):
                for half in range(2):
                    if rope:
                        rotate(o, ("q", head, half))
                    else:
                        cols = slice(half * BANK, (half + 1) * BANK)
                        lo(o, ("q", head, half), qt[:, head % 2, LO, cols], qt[:, head % 2, HI, cols])

            def rotated_query_lo(o, head):
                for half in range(2):
                    cols = slice(half * BANK, (half + 1) * BANK)
                    rotated_lo(o, ("q", head, half), qt[:, head % 2, LO, cols], qt[:, head % 2, HI, cols])

            def keys_lo(o, steps):
                if rope:
                    for key in plan.k_keys():
                        rotate(o, key)
                for key in plan.k_keys():
                    if key[0] == "k":
                        cols = slice(key[2] * BANK, (key[2] + 1) * BANK)
                        (rotated_lo if rope else lo)(o, key, kt[:, key[1], LO, cols], kt[:, key[1], HI, cols])
                    elif key[0] == "kn":
                        t = key[1]
                        dve.wait_ge(a_hi, o.hi[key].through)
                        steps.mark(nc.vector.reduce_sum(kss[:, t, :], k2[:, t % 2, :].rearrange("p (i d) -> p i d", d=P), AX.X))
                        steps.wait()
                        nc.vector.tensor_scalar(kms[:, t, :], kss[:, t, :], 1.0 / P, 1e-6, ALU.mult, ALU.add).then_inc(ms_ready, 1)
                        dve.wait_ge(rs_ready, o.ms[key].through)
                        steps.mark(nc.vector.tensor_tensor(
                            kn[:, t % 2, :, :], pa[:, o.a[key].slot, :].rearrange("p (i d) -> p i d", d=P),
                            krs[:, t, :, None].broadcast_to([P, 4, P]), ALU.mult))
                        steps.wait()
                        dve.sem_inc(kn_ready, 1)
                        dve.sem_inc(a_used, 1)
                    else:
                        cols = slice(key[1] * BANK, (key[1] + 1) * BANK)
                        lo(o, key, kt[:, 0, LO, cols], kt[:, 0, HI, cols], kw[:, :])

            def values_lo(o):
                for key in plan.v_keys():
                    blocks = slice(key[1] * plan.v_per, (key[1] + 1) * plan.v_per)
                    lo(o, key, v[:, LO, blocks, :].rearrange("p b n -> p (b n)"),
                       v[:, HI, blocks, :].rearrange("p b n -> p (b n)"))

            def shifts(slot, head, steps):
                if not masked:
                    for t in range(NS):
                        bs = slice(t * bps, (t + 1) * bps)
                        dve.wait_ge(s_ready, head * NS + (t + 1))
                        steps.mark(nc.vector.reduce_max(top[:, slot, bs], pscore[:, t % 2, :].rearrange("p (b k) -> p b k", k=keys), AX.X))
                        steps.wait()
                        nc.vector.scalar_tensor_tensor(shift[:, slot, bs], top[:, slot, bs], -1.0, qsc[:, slot, bs],
                                                       ALU.mult, ALU.mult).then_inc(shift_ready, 1)
                    return
                if biased:
                    dve.wait_ge(bias_ready, head + 1)
                for t in range(NS):
                    bs = slice(t * bps, (t + 1) * bps)
                    dve.wait_ge(s_ready, head * NS + (t + 1))
                    add = bias[:, bs, :] if biased else neg[:, bs, :]
                    nc.vector.tensor_tensor(prob[:, slot, bs, :], pscore[:, t % 2, :].rearrange("p (b k) -> p b k", k=keys),
                                            add, ALU.add).then_inc(s_used, 1)
                dve.wait_ge(s_used, head * NS + NS)
                steps.mark(nc.vector.reduce_max(top[:, slot, :], prob[:, slot, :, :], AX.X))
                steps.wait()
                if biased:
                    steps.mark(nc.vector.tensor_scalar(valid[:, slot, :], top[:, slot, :], NEG / 2, None, ALU.is_gt))
                nc.vector.tensor_scalar(shift[:, slot, :], top[:, slot, :], -plan.scale, None, ALU.mult).then_inc(shift_ready, 1)

            def inverse(slot, head, steps):
                dve.wait_ge(exp_done, head + 1 if masked else head * NS + NS)
                if not biased:
                    nc.vector.reciprocal(inv[:, slot, :], total[:, slot, :]).then_inc(inv_ready, 1)
                    return
                steps.mark(nc.vector.reciprocal(inv[:, slot, :], total[:, slot, :]))
                steps.wait()
                nc.vector.tensor_tensor(inv[:, slot, :], inv[:, slot, :], valid[:, slot, :], ALU.mult).then_inc(inv_ready, 1)

            def weights_lo(j, head):
                def weight(t):
                    dve.wait_ge(t_hi, head * NS + (t + 1))
                    nc.vector.tensor_tensor(pt[:, t % 2, LO, :], ptr[:, t % 2, :], pt[:, t % 2, HI, :].bitcast(F32),
                                            ALU.subtract).then_inc(t_used, 1)

                def weighed(n):
                    dve.wait_ge(o_hi, head * 2 + (n + 1))
                    cols = slice(n * BANK, (n + 1) * BANK)
                    nc.vector.tensor_tensor(ot[:, j % plan.out_every, LO, cols], pout[:, n, :],
                                            ot[:, j % plan.out_every, HI, cols].bitcast(F32),
                                            ALU.subtract).then_inc(o_used, 1)

                weight(0)
                weight(1)
                weighed(0)
                if NS == 4:
                    weight(2)
                    weight(3)
                weighed(1)

            def query_scale(o, head):
                key = ("ss", head)
                dve.wait_ge(a_ready, o.a[key].through)
                nc.vector.tensor_scalar(qms[:, head % 2, :], pa[:, o.a[key].slot, 0:NB], P * 1e-6, None, ALU.add
                                        ).then_inc(ms_ready, 1)
                dve.wait_ge(ms_ready, o.ms[key].through)
                dve.sem_inc(a_used, 1)

            dve.sem_inc(t_used, 2)
            dve.sem_inc(o_used, 2)
            if masked or qknorm:
                dve.wait_ge(pool_set, n_set)
            o = Orders()
            steps = Steps(dve, own)
            for head in (0, 1):
                query_lo(o, head)
                if rope:
                    rotated_query_lo(o, head)
                if qknorm:
                    query_scale(o, head)
            keys_lo(o, steps)
            if qknorm:
                dve.wait_ge(rs_ready, len(plan.ms_of(plan.first_a())))
            shifts(0, 0, steps)
            inverse(0, 0, steps)
            values_lo(o)
            own_first = steps.n
            own_group = hpg * ((3 if biased else 1) if masked else NS) + (8 if qknorm else 0)

            def group(g, last):
                o = Orders(g, last)
                steps = Steps(dve, own, g * own_group + own_first)
                for j in range(hpg):
                    head = g * hpg + j
                    q_next, score_next, kv_next = plan.in_segment(j, last)
                    if q_next:
                        query_lo(o, j + 2)
                    if kv_next:
                        keys_lo(o, steps)
                    if score_next:
                        shifts((j + 1) % 2, head + 1, steps)
                    if q_next and qknorm:
                        query_scale(o, j + 2)
                    weights_lo(j, head)
                    if q_next and rope:
                        rotated_query_lo(o, j + 2)
                    out_now = (j + 1) % plan.out_every == 0
                    if score_next and not out_now:
                        inverse((j + 1) % 2, head + 1, steps)
                    if out_now:
                        dve.wait_ge(a_used, o.a["o", j, 0].before)
                        for b in range(NB):
                            dve.wait_ge(a_ready, o.a["o", j, b].through)
                            nc.vector.tensor_tensor(x[:, b, :], pa[:, o.a["o", j, b].slot, :], x[:, b, :],
                                                    ALU.add).then_inc(a_used, 1)
                            if b == 3 and score_next:
                                inverse((j + 1) % 2, head + 1, steps)
                    if kv_next:
                        values_lo(o)
                assert last or steps.n == own_group, (steps.n, own_group)

            body(dve, group)
            dve.wait_ge(a_used, (NG - 1) * n_group_a + n_first_a + len(plan.a_order(True)))
    st.close()



MAX_POS = 512
ROOT_SCALE = float(P) ** -0.25


def rope_stage(nc, cos, sin, pos_in, iota_in, tables_in):
    st = Stage(nc, "rope")
    pos_i = st.sb("pos_i", [P, NT], I32)
    pos = st.sb("pos", [P, NT])
    below = st.sb("below", [P, NT])
    iota = st.sb("iota", [P, DC])
    hot = st.sb("hot", [P, DC, NT], F32R)
    tab = st.sb("tab", [P, DC, 2, P])
    pair = st.sb("pair", [P, 2, DC, 2, P], F32R)
    acc = st.ps("acc", [P, 2, 2, BANK])
    loaded, own, split_done, hot_ready, made, copied = (
        st.sem(n) for n in ("loaded", "own", "split_done", "hot_ready", "made", "copied"))
    with nc.Block() as block:
        @block.sync
        def _(sp):
            sp.dma_start(pos_i[:, :], pos_in.rearrange("(o b) t -> o (b t)", o=1).broadcast_to([P, NT])
                         ).then_inc(loaded, 16)
            sp.dma_start(iota[:, :], iota_in).then_inc(loaded, 16)
            for w in range(2):
                sp.dma_start(tab[:, :, w, :], tables_in[w].rearrange("(c p) d -> p c d", p=P)).then_inc(loaded, 16)

        @block.vector
        def _(dve):
            steps = Steps(dve, own)
            dve.wait_ge(loaded, 64)
            steps.mark(nc.vector.tensor_scalar(below[:, :], pos_i[:, :], 0.0, float(MAX_POS), ALU.is_lt, ALU.mult))
            steps.mark(nc.vector.tensor_copy(pos[:, :], pos_i[:, :]))
            steps.wait()
            steps.mark(nc.vector.tensor_tensor(pos[:, :], pos[:, :], below[:, :], ALU.add))
            steps.wait()
            steps.mark(nc.vector.tensor_scalar(pos[:, :], pos[:, :], 0.0, MAX_POS - 1.0, ALU.max, ALU.min))
            steps.mark(nc.vector.tensor_copy(pair[:, HI, :, :, :], tab[:, :, :, :]))
            steps.wait()
            nc.vector.tensor_tensor(pair[:, LO, :, :, :], tab[:, :, :, :], pair[:, HI, :, :, :].bitcast(F32),
                                    ALU.subtract).then_inc(split_done, 1)
            for c in range(DC):
                nc.vector.tensor_scalar(hot[:, c, :], pos[:, :], iota[:, c:c + 1], None,
                                        ALU.is_equal).then_inc(hot_ready, 1)
            for w, dst in enumerate((cos, sin)):
                for half in range(2):
                    dve.wait_ge(made, 2 * w + half + 1)
                    nc.vector.tensor_scalar(dst[:, half * BANK:(half + 1) * BANK], acc[:, w, half, :], ROOT_SCALE, None,
                                            ALU.mult).then_inc(copied, 1)
            dve.wait_ge(copied, 4)

        @block.tensor
        def _(pe):
            pe.wait_ge(split_done, 1)
            pe.wait_ge(hot_ready, DC)
            for w in range(2):
                for half in range(2):
                    for c in range(DC):
                        for part in (HI, LO):
                            ins = nc.tensor.matmul(acc[:, w, half, :], pair[:, part, c, w, :],
                                                   hot[:, c, half * BANK:(half + 1) * BANK],
                                                   start=c == 0 and part == HI, stop=c == DC - 1 and part == LO)
                    ins.then_inc(made, 1)
    st.close()



E0, R0 = 8, 16


def ffn0_stage(nc, x, ident, h_t, base_in, side_in, lora_b_in, b_base_in, b_router_in):
    st = Stage(nc, "f0")
    SIDE = E0 * R0 + E0
    raw = st.sb("raw", [P, DC, D])
    base = st.sb("base", [P, 2, DC, D], F32R)
    raw_side = st.sb("raw_side", [P, DC, SIDE])
    side = st.sb("side", [P, 2, DC, SIDE], F32R)
    raw_b = st.sb("raw_b", [P, D])
    lora_b = st.sb("lora_b", [P, 2, D], F32R)
    b_base = st.sb("b_base", [P, D])
    b_router = st.sb("b_router", [P, E0])
    low = st.sb("low", [P, NB, E0 * R0])
    z = st.sb("z", [P, NB, E0])
    zs = st.sb("zs", [P, NB, E0])
    cum = st.sb("cum", [P, NB, E0])
    rank = st.sb("rank", [P, E0])
    sup = st.sb("sup", [P, NB, E0])
    count = st.sb("count", [P, NB])
    tau = st.sb("tau", [P, NB])
    rcount = st.sb("rcount", [P, NB])
    gated = st.sb("gated", [P, 2, NB, P], F32R)
    p_side = st.ps("p_side", [P, 2, BANK])
    p_tr = st.ps("p_tr", [P, 2, BANK])
    p_out = st.ps("p_out", [P, 2, BANK])
    (loaded, loaded_side, side_split, base_split, side_ready, side_used, own, gate_ready, tr_ready, tr_hi, tr_lo,
     out_ready, out_used, ranked) = (st.sem(n) for n in (
         "loaded", "loaded_side", "side_split", "base_split", "side_ready", "side_used", "own", "gate_ready",
         "tr_ready", "tr_hi", "tr_lo", "out_ready", "out_used", "ranked"))
    with nc.Block() as block:
        @block.sync
        def _(sp):
            sp.dma_start(raw_side[:, :, :], side_in.rearrange("(c p) n -> p c n", p=P)).then_inc(loaded_side, 16)
            sp.dma_start(b_router[:, :], b_router_in.rearrange("(o n) -> o n", o=1).broadcast_to([P, E0])
                         ).then_inc(loaded_side, 16)
            sp.dma_start(raw[:, :, :], base_in.rearrange("(c p) n -> p c n", p=P)).then_inc(loaded, 16)
            sp.dma_start(raw_b[:, :], lora_b_in).then_inc(loaded, 16)
            sp.dma_start(b_base[:, :], b_base_in.rearrange("(o n) -> o n", o=1).broadcast_to([P, D])).then_inc(loaded, 16)

        @block.gpsimd
        def _(pool):
            for e in range(E0):
                nc.gpsimd.memset(rank[:, e:e + 1], float(e + 1)).then_inc(ranked, 1)
            pool.wait_ge(loaded, 48)
            nc.gpsimd.tensor_scalar(base[:, HI, :, :], raw[:, :, :], 1.0, 0.0, ALU.mult, ALU.add).then_inc(base_split, 1)
            nc.gpsimd.tensor_scalar(lora_b[:, HI, :], raw_b[:, :], 1.0, 0.0, ALU.mult, ALU.add).then_inc(base_split, 1)
            pool.wait_ge(base_split, 2)
            nc.gpsimd.tensor_tensor(base[:, LO, :, :], raw[:, :, :], base[:, HI, :, :].bitcast(F32),
                                    ALU.subtract).then_inc(base_split, 1)
            nc.gpsimd.tensor_tensor(lora_b[:, LO, :], raw_b[:, :], lora_b[:, HI, :].bitcast(F32),
                                    ALU.subtract).then_inc(base_split, 1)

        @block.tensor
        def _(pe):
            pe.wait_ge(side_split, 1)
            for b in range(NB):
                if b >= 2:
                    pe.wait_ge(side_used, b - 1)
                for c in range(DC):
                    ins = mm3(nc, p_side[:, b % 2, 0:SIDE], lambda p: h_t[:, p, c, b * P:(b + 1) * P],
                              lambda p: side[:, p, c, :], c == 0, c == DC - 1)
                ins.then_inc(side_ready, 1)
            pe.wait_ge(base_split, 4)
            for b in range(NB):
                if b >= 2:
                    pe.wait_ge(out_used, b - 1)
                for c in range(DC):
                    mm3(nc, p_out[:, b % 2, :], lambda p: h_t[:, p, c, b * P:(b + 1) * P],
                        lambda p: base[:, p, c, :], c == 0, False)
                if b % 4 == 0:
                    pe.wait_ge(gate_ready, 1)
                    for i in range(4):
                        ins = nc.tensor.transpose(p_tr[:, b // 4, i * P:(i + 1) * P], low[:, b + i, :], ident[:, :])
                    ins.then_inc(tr_ready, 1)
                    pe.wait_ge(tr_lo, b // 4 + 1)
                ins = mm3(nc, p_out[:, b % 2, :], lambda p: gated[:, p, b, :], lambda p: lora_b[:, p, :], False, True)
                ins.then_inc(out_ready, 1)

        @block.scalar
        def _(act):
            for t in range(2):
                act.wait_ge(tr_ready, t + 1)
                nc.scalar.activation(gated[:, HI, 4 * t:4 * t + 4, :].rearrange("p b n -> p (b n)"), p_tr[:, t, :],
                                     ACT.Copy).then_inc(tr_hi, 1)

        @block.vector
        def _(dve):
            steps = Steps(dve, own)
            dve.wait_ge(loaded_side, 32)
            steps.mark(nc.vector.tensor_copy(side[:, HI, :, :], raw_side[:, :, :]))
            steps.wait()
            nc.vector.tensor_tensor(side[:, LO, :, :], raw_side[:, :, :], side[:, HI, :, :].bitcast(F32),
                                    ALU.subtract).then_inc(side_split, 1)
            for b in range(NB):
                dve.wait_ge(side_ready, b + 1)
                steps.mark(nc.vector.tensor_tensor(z[:, b, :], p_side[:, b % 2, E0 * R0:SIDE], b_router[:, :], ALU.add))
                nc.vector.tensor_copy(low[:, b, :], p_side[:, b % 2, 0:E0 * R0]).then_inc(side_used, 1)
            steps.wait()
            for b in range(NB):
                steps.mark(nc.vector.max(zs[:, b, :], z[:, b, :]))
            steps.wait()
            steps.mark(nc.vector.tensor_copy(cum[:, :, 0:1], zs[:, :, 0:1]))
            for e in range(1, E0):
                steps.wait()
                steps.mark(nc.vector.tensor_tensor(cum[:, :, e:e + 1], cum[:, :, e - 1:e], zs[:, :, e:e + 1], ALU.add))
            dve.wait_ge(ranked, E0)
            ranks = rank[:, None, :].broadcast_to([P, NB, E0])
            steps.mark(nc.vector.tensor_tensor(sup[:, :, :], zs[:, :, :], ranks, ALU.mult))
            steps.wait()
            steps.mark(nc.vector.tensor_scalar(sup[:, :, :], sup[:, :, :], 1.0, None, ALU.add))
            steps.wait()
            steps.mark(nc.vector.tensor_tensor(sup[:, :, :], sup[:, :, :], cum[:, :, :], ALU.is_gt))
            steps.wait()
            steps.mark(nc.vector.reduce_sum(count[:, :], sup[:, :, :], AX.X))
            steps.wait()
            steps.mark(nc.vector.tensor_tensor(sup[:, :, :], ranks, count[:, :, None].broadcast_to([P, NB, E0]), ALU.is_equal))
            steps.mark(nc.vector.reciprocal(rcount[:, :], count[:, :]))
            steps.wait()
            steps.mark(nc.vector.tensor_tensor(sup[:, :, :], sup[:, :, :], cum[:, :, :], ALU.mult))
            steps.wait()
            steps.mark(nc.vector.reduce_sum(tau[:, :], sup[:, :, :], AX.X))
            steps.wait()
            steps.mark(nc.vector.scalar_tensor_tensor(tau[:, :], tau[:, :], -1.0, rcount[:, :], ALU.add, ALU.mult))
            steps.wait()
            steps.mark(nc.vector.tensor_tensor(z[:, :, :], z[:, :, :], tau[:, :, None].broadcast_to([P, NB, E0]), ALU.subtract))
            steps.wait()
            steps.mark(nc.vector.tensor_scalar(z[:, :, :], z[:, :, :], 0.0, None, ALU.max))
            steps.wait()
            dve.wait_ge(side_used, NB)
            lowr = low[:, :, :].rearrange("p b (e r) -> p (b e) r", r=R0)
            gate = z[:, :, :].rearrange("p b e -> p (b e)")[:, :, None].broadcast_to([P, NB * E0, R0])
            nc.vector.tensor_tensor(lowr, lowr, gate, ALU.mult).then_inc(gate_ready, 1)
            dve.wait_ge(loaded, 48)
            for b in range(NB):
                steps.mark(nc.vector.tensor_tensor(x[:, b, :], x[:, b, :], b_base[:, :], ALU.add))
            for t in range(2):
                dve.wait_ge(tr_hi, t + 1)
                dst = gated[:, LO, 4 * t:4 * t + 4, :].rearrange("p b n -> p (b n)")
                hi = gated[:, HI, 4 * t:4 * t + 4, :].rearrange("p b n -> p (b n)")
                nc.vector.tensor_tensor(dst, p_tr[:, t, :], hi.bitcast(F32), ALU.subtract).then_inc(tr_lo, 1)
                steps.wait()
                for b in range(4 * t, 4 * t + 4):
                    dve.wait_ge(out_ready, b + 1)
                    nc.vector.tensor_tensor(x[:, b, :], p_out[:, b % 2, :], x[:, b, :], ALU.add).then_inc(out_used, 1)
            dve.wait_ge(out_used, NB)
    st.close()



DK = 64
PH = 8
DH = DK // PH
ROWS = 32
VC = 10


def norm_natural_stage(nc, name, x, h):
    st = Stage(nc, name)
    norm = Norm(st)
    own, done = st.sem("own"), st.sem("done")
    with nc.Block() as block:
        @block.gpsimd
        def _(pool):
            norm.set_half(nc)
            norm.rstd_on_gpsimd(nc, pool)

        @block.vector
        def _(dve):
            norm.stats_on_vector(nc, Steps(dve, own), x)
            dve.wait_ge(norm.rstd_ready, 1)
            for b in range(NB):
                norm.apply(nc, b, h[:, b, :], x).then_inc(done, 1)
            dve.wait_ge(done, NB)
    st.close()


def patch_attention_stage(nc, x, h, ident, ctx_in, mask_in, wqk_in, wv_in, wo_in, bqk_in, flag_in, bv_in, bo_in):
    st = Stage(nc, "a1")
    NP = D // P
    raw_w = st.sb("raw_w", [P, 4 * P + DK])
    w = st.sb("w", [P, 2, 4 * P + DK], F32R)
    raw_o = st.sb("raw_o", [DK, P])
    wo = st.sb("wo", [DK, 2, P], F32R)
    bqk = st.sb("bqk", [P, 4])
    flag = st.sb("flag", [P, 1])
    bv = st.sb("bv", [P, DK])
    bo = st.sb("bo", [P, 1])
    mask = st.sb("mask", [P, 2, D])
    keep = st.sb("keep", [P, D])
    gone = st.sb("gone", [P, D])
    hp = st.sb("hp", [P, 2, D], F32R)
    ctx = st.sb("ctx", [P, 2, D])
    cp = st.sb("cp", [P, 2, D], F32R)
    q32 = st.sb("q32", [P, 4, D])
    qp = st.sb("qp", [P, 2, 2, D], F32R)
    kd = st.sb("kd", [P, 2, 2, NP, 4, P], F32R)
    v32 = st.sb("v32", [P, NP, DK])
    vp = st.sb("vp", [P, 2, NP, PH, VC], F32R)
    top = st.sb("top", [P, 2, PH])
    e = st.sb("e", [P, 2, PH, P])
    ep = st.sb("ep", [P, 2, 2, 4, P], F32R)
    rs = st.sb("rs", [P, PH])
    o32 = st.sb("o32", [P, 2, DK])
    g32 = st.sb("g32", [DK, D])
    gp = st.sb("gp", [DK, 2, D], F32R)
    y = st.sb("y", [P, D])
    pj = st.ps("pj", [P, 2, BANK])
    psc = st.ps("psc", [P, 2, BANK])
    ptr = st.ps("ptr", [P, 2, BANK])
    pov = st.ps("pov", [P, BANK])
    pot = st.ps("pot", [P, BANK])
    (w_loaded, w_split, own, split, pj_ready, pj_used, qkv_ready, sc_ready, sc_used, e_ready, exp_done, tr_ready,
     tr_hi, tr_used, pv_ready, o_ready, ot_ready, g_ready, gs_ready, y_ready, x_done, ones_set, gone_ready, pool_own, o_seen) = (
        st.sem(n) for n in (
            "w_loaded", "w_split", "own", "split", "pj_ready", "pj_used", "qkv_ready", "sc_ready", "sc_used", "e_ready",
            "exp_done", "tr_ready", "tr_hi", "tr_used", "pv_ready", "o_ready", "ot_ready", "g_ready", "gs_ready",
            "y_ready", "x_done", "ones_set", "gone_ready", "pool_own", "o_seen"))
    loaded = [st.sem("loaded0"), st.sem("loaded1")]
    INV = 1.0 / math.sqrt(DH)

    with nc.Block() as block:
        @block.sync
        def _(sp):
            sp.dma_start(raw_w[:, 0:4 * P], wqk_in).then_inc(w_loaded, 16)
            sp.dma_start(raw_w[:, 4 * P:], wv_in).then_inc(w_loaded, 16)
            sp.dma_start(raw_o[:, :], wo_in).then_inc(w_loaded, 16)
            with nc.allow_non_contiguous_dma(reason="a few columns"):
                sp.dma_start(bqk[:, :], bqk_in).then_inc(w_loaded, 16)
                sp.dma_start(flag[:, :], flag_in).then_inc(w_loaded, 16)
                sp.dma_start(bo[:, :], bo_in.rearrange("(p o) -> p o", o=1)).then_inc(w_loaded, 16)
            sp.dma_start(bv[:, :], bv_in.rearrange("(o n) -> o n", o=1).broadcast_to([P, DK])).then_inc(w_loaded, 16)

            def load(b, slot):
                sp.dma_start(mask[:, slot, :], mask_in[bass.ds(b, 1), :].broadcast_to([P, D])).then_inc(loaded[slot], 16)
                sp.dma_start(ctx[:, slot, :], ctx_in[bass.ds(b, 1), :, :].rearrange("o p n -> p (o n)")
                             ).then_inc(loaded[slot], 16)

            load(0, 0)
            load(1, 1)
            with sp.Fori(0, NB // 2 - 1) as g:
                for slot in range(2):
                    sp.wait_ge(x_done, g * 2 + (slot + 1))
                    load(g * 2 + (slot + 2), slot)

        @block.gpsimd
        def _(pool):
            nc.gpsimd.memset(kd[:, :, :, :, :, :].bitcast(F32), 0.0).then_inc(ones_set, 1)
            nc.gpsimd.memset(vp[:, HI, :, :, DH:VC].bitcast(F32), 1.0).then_inc(ones_set, 1)
            nc.gpsimd.memset(vp[:, LO, :, :, DH:VC].bitcast(F32), 0.0).then_inc(ones_set, 1)

        @block.tensor
        def _(pe):
            pe.wait_ge(w_split, 2)
            pe.wait_ge(ones_set, 3)
            with pe.Fori(0, NB) as b:
                pe.wait_ge(split, b * 2 + 2)
                for t in range(4):
                    if t >= 2:
                        pe.wait_ge(pj_used, b * 6 + (t - 1))
                    mm3(nc, pj[:, t % 2, :], lambda p: w[:, p, t * P:(t + 1) * P], lambda p: hp[:, p, :]).then_inc(pj_ready, 1)
                pe.wait_ge(pj_used, b * 6 + 3)
                for s in range(NP):
                    ins = mm3(nc, pj[:, 0, s * DK:(s + 1) * DK], lambda p: cp[:, p, s * P:(s + 1) * P],
                              lambda p: w[:, p, 4 * P:])
                ins.then_inc(pj_ready, 1)
                pe.wait_ge(qkv_ready, b * 1 + 1)

                def scores(s):
                    for t in range(2):
                        if s > 0:
                            pe.wait_ge(sc_used, b * (2 * NP) + (2 * s + t - 1))
                        ins = mm3(nc, psc[:, t, :], lambda p: qp[:, p, t, s * P:(s + 1) * P],
                                  lambda p: kd[:, p, t, s, :, :].rearrange("p i j -> p (i j)"))
                        ins.then_inc(sc_ready, 1)

                scores(0)
                for s in range(NP):
                    if s + 1 < NP:
                        scores(s + 1)
                    pe.wait_ge(exp_done, b * NP + (s + 1))
                    for t in range(2):
                        pe.wait_ge(tr_used, b * (2 * NP) + (2 * s + t + 1))
                        for i in range(4):
                            ins = nc.tensor.transpose(ptr[:, t, i * P:(i + 1) * P], e[:, s % 2, 4 * t + i, :], ident[:, :])
                        ins.then_inc(tr_ready, 1)
                    if s > 0:
                        pe.wait_ge(o_ready, b * NP + s)
                    for t in range(2):
                        pe.wait_ge(tr_used, b * (2 * NP) + (2 * s + t + 3))
                        for i in range(4):
                            head = 4 * t + i
                            ins = mm3(nc, pov[:, head * VC:(head + 1) * VC], lambda p: ep[:, p, t, i, :],
                                      lambda p: vp[:, p, s, head, :])
                    ins.then_inc(pv_ready, 1)
                    pe.wait_ge(o_ready, b * NP + (s + 1))
                    pe.sem_inc(o_seen, 1)
                    ins = nc.tensor.transpose(pot[0:DK, s * P:(s + 1) * P], o32[:, s % 2, :], ident[:, :])
                    if s == NP - 1:
                        ins.then_inc(ot_ready, 1)
                pe.wait_ge(gs_ready, b + 1)
                mm3(nc, pj[:, 1, :], lambda p: wo[:, p, :], lambda p: gp[:, p, :]).then_inc(pj_ready, 1)
                pe.wait_ge(x_done, b + 1)

        @block.scalar
        def _(act):
            with act.Fori(0, NB) as b:
                for t in range(4):
                    act.wait_ge(pj_ready, b * 6 + (t + 1))
                    nc.scalar.activation(q32[:, t, :], pj[:, t % 2, :], ACT.Identity, bias=bqk[:, t:t + 1]).then_inc(pj_used, 1)
                for s in range(NP):
                    act.wait_ge(e_ready, b * NP + (s + 1))
                    sl = e[:, s % 2, :, :].rearrange("p h j -> p (h j)")
                    nc.scalar.activation(sl, sl, ACT.Exp, scale=INV).then_inc(exp_done, 1)
                    for t in range(2):
                        act.wait_ge(tr_ready, b * (2 * NP) + (2 * s + t + 1))
                        nc.scalar.activation(ep[:, HI, t, :, :].rearrange("p i j -> p (i j)"), ptr[:, t, :],
                                             ACT.Copy).then_inc(tr_hi, 1)
                act.wait_ge(ot_ready, b + 1)
                nc.scalar.activation(g32[:, :], pot[0:DK, :], ACT.Gelu).then_inc(g_ready, 1)

        @block.vector
        def _(dve):
            dve.sem_inc(tr_used, 2)
            steps = Steps(dve, own)
            dve.wait_ge(w_loaded, 7 * 16)
            steps.mark(nc.vector.tensor_copy(w[:, HI, :], raw_w[:, :]))
            steps.mark(nc.vector.tensor_copy(wo[:, HI, :], raw_o[:, :]))
            steps.mark(nc.vector.tensor_scalar(bqk[:, 0:2], bqk[:, 0:2], flag[:, 0:1], None, ALU.add))
            steps.wait()
            nc.vector.tensor_tensor(w[:, LO, :], raw_w[:, :], w[:, HI, :].bitcast(F32), ALU.subtract).then_inc(w_split, 1)
            nc.vector.tensor_tensor(wo[:, LO, :], raw_o[:, :], wo[:, HI, :].bitcast(F32), ALU.subtract).then_inc(w_split, 1)
            first = steps.n
            PER = 24 + 2 * NP
            dve.wait_ge(ones_set, 3)

            def batch(b, slot, turn):
                steps = Steps(dve, own, b * PER + first)
                dve.wait_ge(loaded[slot], turn * 32)
                steps.mark(nc.vector.tensor_copy(hp[:, HI, :], h[:, bass.ds(b, 1), :].rearrange("p o n -> p (o n)")))
                steps.mark(nc.vector.tensor_copy(cp[:, HI, :], ctx[:, slot, :]))
                steps.mark(nc.vector.tensor_scalar(keep[:, :], mask[:, slot, :], 0.0, None, ALU.is_gt))
                steps.wait()
                nc.vector.tensor_tensor(hp[:, LO, :], h[:, bass.ds(b, 1), :].rearrange("p o n -> p (o n)"),
                                        hp[:, HI, :].bitcast(F32), ALU.subtract).then_inc(split, 1)
                nc.vector.tensor_tensor(cp[:, LO, :], ctx[:, slot, :], cp[:, HI, :].bitcast(F32), ALU.subtract).then_inc(split, 1)
                steps.mark(nc.vector.tensor_scalar(gone[:, :], keep[:, :], 0.0, NEG, ALU.is_equal, ALU.mult))
                steps.wait()
                steps.mark(nc.vector.tensor_scalar(gone[:, :], gone[:, :], flag[:, 0:1], None, ALU.mult))
                dve.wait_ge(pj_used, b * 6 + 4)
                for t in (2, 3):
                    steps.mark(nc.vector.tensor_tensor(q32[:, t, :], q32[:, t, :], keep[:, :], ALU.mult))
                steps.wait()
                for t in (2, 3):
                    steps.mark(nc.vector.tensor_tensor(q32[:, t, :], q32[:, t, :], gone[:, :], ALU.add))
                steps.wait()
                steps.mark(nc.vector.tensor_copy(qp[:, HI, :, :], q32[:, 0:2, :]))
                for i in range(4):
                    rows = slice(ROWS * i, ROWS * (i + 1))
                    steps.mark(nc.vector.tensor_copy(kd[rows, HI, :, :, i, :].rearrange("p t s j -> p (t s) j"),
                                                     q32[rows, 2:4, :].rearrange("p t (s j) -> p (t s) j", j=P)))
                dve.wait_ge(pj_ready, b * 6 + 5)
                vt = pj[:, 0, 0:NP * DK].rearrange("p (s n) -> p s n", n=DK)
                steps.mark(nc.vector.tensor_tensor(v32[:, :, :], vt, bv[:, None, :].broadcast_to([P, NP, DK]), ALU.add))
                steps.wait()
                dve.sem_inc(pj_used, 1)
                v32h = v32[:, :, :].rearrange("p s (h d) -> p (s h) d", d=DH)
                steps.mark(nc.vector.tensor_copy(vp[:, HI, :, :, 0:DH].rearrange("p s h d -> p (s h) d"), v32h))
                steps.mark(nc.vector.tensor_tensor(qp[:, LO, :, :], q32[:, 0:2, :], qp[:, HI, :, :].bitcast(F32), ALU.subtract))
                for i in range(4):
                    rows = slice(ROWS * i, ROWS * (i + 1))
                    steps.mark(nc.vector.tensor_tensor(
                        kd[rows, LO, :, :, i, :].rearrange("p t s j -> p (t s) j"),
                        q32[rows, 2:4, :].rearrange("p t (s j) -> p (t s) j", j=P),
                        kd[rows, HI, :, :, i, :].rearrange("p t s j -> p (t s) j").bitcast(F32), ALU.subtract))
                steps.wait()
                steps.mark(nc.vector.tensor_tensor(
                    vp[:, LO, :, :, 0:DH].rearrange("p s h d -> p (s h) d"), v32h,
                    vp[:, HI, :, :, 0:DH].rearrange("p s h d -> p (s h) d").bitcast(F32), ALU.subtract))
                steps.wait()
                dve.sem_inc(qkv_ready, 1)

                def shifted(s):
                    for t in range(2):
                        dve.wait_ge(sc_ready, b * (2 * NP) + (2 * s + t + 1))
                        ins = nc.vector.reduce_max(top[:, s % 2, 4 * t:4 * t + 4],
                                                   psc[:, t, :].rearrange("p (i j) -> p i j", j=P), AX.X)
                    steps.mark(ins)
                    steps.wait()
                    for t in range(2):
                        ins = nc.vector.tensor_tensor(e[:, s % 2, 4 * t:4 * t + 4, :],
                                                      psc[:, t, :].rearrange("p (i j) -> p i j", j=P),
                                                      top[:, s % 2, 4 * t:4 * t + 4, None].broadcast_to([P, 4, P]),
                                                      ALU.subtract)
                        ins.then_inc(sc_used, 1)
                    dve.wait_ge(sc_used, b * (2 * NP) + (2 * s + 2))
                    dve.sem_inc(e_ready, 1)

                shifted(0)
                for s in range(NP):
                    if s + 1 < NP:
                        shifted(s + 1)
                    for t in range(2):
                        dve.wait_ge(tr_hi, b * (2 * NP) + (2 * s + t + 1))
                        nc.vector.tensor_tensor(ep[:, LO, t, :, :].rearrange("p i j -> p (i j)"), ptr[:, t, :],
                                                ep[:, HI, t, :, :].rearrange("p i j -> p (i j)").bitcast(F32),
                                                ALU.subtract).then_inc(tr_used, 1)
                    dve.wait_ge(pv_ready, b * NP + (s + 1))
                    ov = pov[:, 0:PH * VC].rearrange("p (h c) -> p h c", c=VC)
                    steps.mark(nc.vector.reciprocal(rs[:, :], ov[:, :, DH]))
                    steps.wait()
                    nc.vector.tensor_tensor(o32[:, s % 2, :].rearrange("p (h d) -> p h d", d=DH), ov[:, :, 0:DH],
                                            rs[:, :, None].broadcast_to([P, PH, DH]), ALU.mult).then_inc(o_ready, 1)
                dve.wait_ge(g_ready, b + 1)
                steps.mark(nc.vector.tensor_copy(gp[:, HI, :], g32[:, :]))
                steps.wait()
                nc.vector.tensor_tensor(gp[:, LO, :], g32[:, :], gp[:, HI, :].bitcast(F32), ALU.subtract).then_inc(gs_ready, 1)
                dve.wait_ge(pj_ready, b * 6 + 6)
                steps.mark(nc.vector.scalar_tensor_tensor(y[:, :], pj[:, 1, :], bo[:, 0:1], mask[:, slot, :], ALU.add, ALU.mult))
                steps.wait()
                dve.sem_inc(pj_used, 1)
                xb = x[:, bass.ds(b, 1), :].rearrange("p o n -> p (o n)")
                nc.vector.tensor_tensor(xb, xb, y[:, :], ALU.add).then_inc(x_done, 1)
                assert steps.n == PER, steps.n

            with dve.Fori(0, NB // 2) as g:
                for slot in range(2):
                    batch(g * 2 + slot, slot, g + 1)
            dve.wait_ge(x_done, NB)
    st.close()



ROUND = 1.5 * 2.0 ** 23


def ffn1_stage(nc, x, h, ident_bf, weight_in, scales_in, bias_in):
    st = Stage(nc, "f1")
    words = st.sb("words", [P, DC, D // 4], I32)
    w = st.sb("w", [P, DC, D], BF16)
    ws = st.sb("ws", [P, D], F16)
    bias = st.sb("bias", [P, D], F16)
    top = st.sb("top", [P, NB])
    scale = st.sb("scale", [P, NB])
    inv = st.sb("inv", [P, NB])
    step = st.sb("step", [P, 2, D])
    q = st.sb("q", [P, NB, D], BF16)
    qt = st.sb("qt", [P, 2, DC, P], BF16)
    y32 = st.sb("y32", [P, 2, D])
    y16 = st.sb("y16", [P, 2, D], F16)
    tp = st.ps("tp", [P, 2, 2 * BANK], BF16)
    acc = st.ps("acc", [P, 2, BANK])
    (loaded, w_ready, own, q_ready, tp_ready, qt_ready, acc_ready, y_ready, x_done) = (st.sem(n) for n in (
        "loaded", "w_ready", "own", "q_ready", "tp_ready", "qt_ready", "acc_ready", "y_ready", "x_done"))
    with nc.Block() as block:
        @block.sync
        def _(sp):
            sp.dma_start(words[:, :, :], weight_in.rearrange("(c p) n -> p c n", p=P)).then_inc(loaded, 16)
            sp.dma_start(ws[:, :], scales_in.rearrange("(o n) -> o n", o=1).broadcast_to([P, D])).then_inc(loaded, 16)
            sp.dma_start(bias[:, :], bias_in.broadcast_to([P, D])).then_inc(loaded, 16)

        @block.scalar
        def _(act):
            act.wait_ge(loaded, 48)
            nc.scalar.activation(w[:, :, :], words[:, :, :].bitcast(I8), ACT.Copy).then_inc(w_ready, 1)
            for b in range(NB):
                act.wait_ge(tp_ready, b + 1)
                if b >= 2:
                    act.wait_ge(acc_ready, b - 1)
                nc.scalar.activation(qt[:, b % 2, :, :].rearrange("p c t -> p (c t)"), tp[:, b % 2, 0:D],
                                     ACT.Copy).then_inc(qt_ready, 1)

        @block.tensor
        def _(pe):
            def transposes(b):
                pe.wait_ge(q_ready, b + 1)
                if b >= 2:
                    pe.wait_ge(qt_ready, b - 1)
                for c in range(DC):
                    ins = nc.tensor.transpose(tp[:, b % 2, c * P:(c + 1) * P], q[:, b, c * P:(c + 1) * P], ident_bf[:, :])
                ins.then_inc(tp_ready, 1)

            transposes(0)
            pe.wait_ge(w_ready, 1)
            for b in range(NB):
                if b + 1 < NB:
                    transposes(b + 1)
                pe.wait_ge(qt_ready, b + 1)
                if b >= 2:
                    pe.wait_ge(y_ready, b - 1)
                for c in range(DC):
                    ins = nc.tensor.matmul(acc[:, b % 2, :], qt[:, b % 2, c, :], w[:, c, :], start=c == 0, stop=c == DC - 1)
                ins.then_inc(acc_ready, 1)

        @block.vector
        def _(dve):
            steps = Steps(dve, own)
            for b in range(NB):
                steps.mark(nc.vector.tensor_reduce(top[:, b:b + 1], h[:, b, :], AX.X, ALU.max, apply_absolute_value=True))
            steps.wait()
            steps.mark(nc.vector.tensor_scalar(scale[:, :], top[:, :], 1.0 / 127.0, 1e-37, ALU.mult, ALU.max))
            steps.wait()
            steps.mark(nc.vector.reciprocal(inv[:, :], scale[:, :]))
            steps.wait()
            for b in range(NB):
                steps.mark(nc.vector.tensor_scalar(step[:, b % 2, :], h[:, b, :], inv[:, b:b + 1], ROUND, ALU.mult, ALU.add))
                steps.wait()
                steps.mark(nc.vector.tensor_scalar(step[:, b % 2, :], step[:, b % 2, :], ROUND, 127.0, ALU.subtract, ALU.min))
                steps.wait()
                nc.vector.tensor_scalar(q[:, b, :], step[:, b % 2, :], -128.0, None, ALU.max).then_inc(q_ready, 1)
            dve.wait_ge(loaded, 48)
            for b in range(NB):
                dve.wait_ge(acc_ready, b + 1)
                nc.vector.tensor_tensor(y32[:, b % 2, :], acc[:, b % 2, :], ws[:, :], ALU.mult).then_inc(y_ready, 1)
                dve.wait_ge(y_ready, b + 1)
                steps.mark(nc.vector.tensor_scalar(y16[:, b % 2, :], y32[:, b % 2, :], scale[:, b:b + 1], None, ALU.mult))
                steps.wait()
                steps.mark(nc.vector.tensor_tensor(y16[:, b % 2, :], y16[:, b % 2, :], bias[:, :], ALU.add))
                steps.wait()
                nc.vector.tensor_tensor(x[:, b, :], x[:, b, :], y16[:, b % 2, :], ALU.add).then_inc(x_done, 1)
            dve.wait_ge(x_done, NB)
    st.close()



NF4_PIECES = 3 * NH2 * D // (P * NF4_COLS)


def nf4_stage(nc, flat_in, rounded):
    st = Stage(nc, "nf4")
    blocks = NF4_COLS // NF4_BLOCK
    code = np.array(NF4_CODE, np.float32)
    bounds = ((code[:-1] + code[1:]) * np.float32(0.5)).astype(np.float32)
    above = np.nextafter(bounds, np.float32(np.inf))
    BIG = 2.0 ** 60
    zero = NF4_CODE.index(0.0)
    negative = [(float(above[i]), float(code[i])) for i in range(zero)]
    positive = [(float(bounds[i]), float(code[i + 1])) for i in range(zero, len(bounds))]
    terms = negative + positive
    w = st.sb("w", [P, 2, NF4_COLS])
    top = st.sb("top", [P, blocks])
    empty = st.sb("empty", [P, blocks])
    inv = st.sb("inv", [P, blocks])
    v = st.sb("v", [P, NF4_COLS])
    t = st.sb("t", [P, 4, NF4_COLS])
    acc = st.sb("acc", [P, 2, 2, NF4_COLS])
    res = st.sb("res", [P, 2, NF4_COLS])
    shifts = st.sb("shifts", [P, len(terms)])
    loaded = [st.sem("loaded0"), st.sem("loaded1")]
    stored = [st.sem("stored0"), st.sem("stored1")]
    own, v_ready, t_ready, t_used, done, shifts_set = (
        st.sem(n) for n in ("own", "v_ready", "t_ready", "t_used", "done", "shifts_set"))
    NT_ = len(terms)
    with nc.Block() as block:
        @block.sync
        def _(sp):
            def load(n, slot):
                sp.dma_start(w[:, slot, :], flat_in[bass.ds(n, 1), :, :].rearrange("o p n -> p (o n)")
                             ).then_inc(loaded[slot], 16)

            def store(n, slot):
                sp.dma_start(rounded[bass.ds(n, 1), :, :].rearrange("o p n -> p (o n)"), res[:, slot, :]
                             ).then_inc(stored[slot], 16)

            load(0, 0)
            load(1, 1)
            with sp.Fori(0, NF4_PIECES // 2 - 1) as g:
                for slot in range(2):
                    sp.wait_ge(done, g * 2 + (slot + 1))
                    store(g * 2 + slot, slot)
                    load(g * 2 + (slot + 2), slot)
            for slot in range(2):
                sp.wait_ge(done, NF4_PIECES - 1 + slot)
                store(NF4_PIECES - 2 + slot, slot)
            for slot in range(2):
                sp.wait_ge(stored[slot], NF4_PIECES // 2 * 16)

        @block.gpsimd
        def _(pool):
            for i, (bound, _) in enumerate(terms):
                nc.gpsimd.memset(shifts[:, i:i + 1], -bound * BIG).then_inc(shifts_set, 1)

        @block.scalar
        def _(act):
            act.wait_ge(shifts_set, NT_)
            with act.Fori(0, NF4_PIECES) as n:
                act.wait_ge(v_ready, n + 1)
                for i in range(NT_):
                    act.wait_ge(t_used, n * NT_ + (i + (2 if i < NT_ % 4 else 1)))
                    nc.scalar.activation(t[:, i % 4, :], v[:, :], ACT.Identity, bias=shifts[:, i:i + 1], scale=BIG
                                         ).then_inc(t_ready, 1)

        @block.vector
        def _(dve):
            dve.sem_inc(t_used, 4)

            def piece(n, slot, turn, wait_store, after_first=True):
                steps = Steps(dve, own, n * 5)
                wb = w[:, slot, :].rearrange("p (b i) -> p b i", i=NF4_BLOCK)
                vb = v[:, :].rearrange("p (b i) -> p b i", i=NF4_BLOCK)
                dve.wait_ge(loaded[slot], turn * 16)
                if after_first:
                    dve.wait_ge(done, n)
                steps.mark(nc.vector.tensor_reduce(top[:, :], wb, AX.X, ALU.max, apply_absolute_value=True))
                steps.wait()
                steps.mark(nc.vector.tensor_scalar(empty[:, :], top[:, :], 0.0, None, ALU.is_equal))
                steps.wait()
                steps.mark(nc.vector.tensor_tensor(empty[:, :], empty[:, :], top[:, :], ALU.add))
                steps.wait()
                steps.mark(nc.vector.reciprocal(inv[:, :], empty[:, :]))
                steps.wait()
                nc.vector.tensor_tensor(vb, wb, inv[:, :, None].broadcast_to([P, blocks, NF4_BLOCK]),
                                        ALU.mult).then_inc(v_ready, 1)
                for i, (_, c) in enumerate(terms):
                    below = i < zero
                    acc_i, prev = acc[:, 0 if below else 1, i % 2, :], acc[:, 0 if below else 1, (i + 1) % 2, :]
                    dve.wait_ge(t_ready, n * NT_ + (i + 1))
                    if i in (0, zero):
                        ins = nc.vector.tensor_scalar(acc_i, t[:, i % 4, :], c, 0.0, ALU.max if below else ALU.min,
                                                      ALU.min if below else ALU.max)
                    else:
                        dve.wait_ge(t_used, n * NT_ + (i + 4))
                        ins = nc.vector.scalar_tensor_tensor(acc_i, t[:, i % 4, :], c, prev,
                                                             ALU.max if below else ALU.min, ALU.min if below else ALU.max)
                    ins.then_inc(t_used, 1)
                dve.wait_ge(t_used, n * NT_ + (NT_ + 4))
                steps.mark(nc.vector.tensor_tensor(v[:, :], acc[:, 0, (zero - 1) % 2, :], acc[:, 1, (NT_ - 1) % 2, :], ALU.add))
                steps.wait()
                if wait_store is not None:
                    dve.wait_ge(stored[slot], wait_store)
                nc.vector.tensor_tensor(res[:, slot, :].rearrange("p (b i) -> p b i", i=NF4_BLOCK), vb,
                                        top[:, :, None].broadcast_to([P, blocks, NF4_BLOCK]), ALU.mult).then_inc(done, 1)

            piece(0, 0, 1, None, after_first=False)
            piece(1, 1, 1, None)
            with dve.Fori(1, NF4_PIECES // 2) as g:
                for slot in range(2):
                    piece(g * 2 + slot, slot, g + 1, g * 16)
    st.close()


def ffn2_stage(nc, x, ident, h_t, rounded):
    st = Stage(nc, "f2")
    w1, w2 = (rounded[i * NH2:(i + 1) * NH2, :] for i in range(2))
    w3 = rounded[2 * NH2:3 * NH2, :].rearrange("r c -> (r c)").rearrange("(d h) -> d h", h=NH2)
    REST = NH2 - (HC2 - 1) * P
    rows = st.sb("rows", [P, 2, 2, D])
    cols = st.sb("cols", [P, 2, DC, P])
    wt = st.sb("wt", [P, 2, 2, DC, P], F32R)
    w3t = st.sb("w3t", [P, 2, 2, D], F32R)
    gate = st.sb("gate", [P, 2, BANK])
    a32 = st.sb("a32", [P, 2, BANK])
    a = st.sb("a", [P, 2, 2, NT], F32R)
    ptr = st.ps("ptr", [P, 2, BANK])
    pg = st.ps("pg", [P, 2, BANK])
    pd = st.ps("pd", [P, 2, BANK])
    loaded = [st.sem("loaded0"), st.sem("loaded1")]
    (tr_ready, tr_hi, tr_used, g_ready, silu_done, a_done, g_used, a_hi, a_lo, d_ready, d_used, own) = (
        st.sem(n) for n in ("tr_ready", "tr_hi", "tr_used", "g_ready", "silu_done", "a_done", "g_used",
                            "a_hi", "a_lo", "d_ready", "d_used", "own"))
    turns = [(n, min(n * P, NH2 - P)) for n in range(HC2)]
    with nc.Block() as block:
        @block.sync
        def _(sp):
            def load(start, slot):
                sp.dma_start(rows[:, slot, 0, :], w1[bass.ds(start, P), :]).then_inc(loaded[slot], 16)
                sp.dma_start(rows[:, slot, 1, :], w2[bass.ds(start, P), :]).then_inc(loaded[slot], 16)
                sp.dma_start(cols[:, slot, :, :], w3[:, bass.ds(start, P)].rearrange("(c p) h -> p c h", p=P)
                             ).then_inc(loaded[slot], 16)

            load(0, 0)
            load(P, 1)
            for n, start in turns[2:]:
                sp.wait_ge(tr_ready, 3 * (n - 1))
                load(start, n % 2)

        @block.tensor
        def _(pe):
            def down(n):
                pe.wait_ge(a_lo, 2 * (n + 1))
                for b in range(NB):
                    k = n * NB + b
                    if k >= 2:
                        pe.wait_ge(d_used, k - 1)
                    ins = mm3(nc, pd[:, b % 2, :], lambda p: a[:, n % 2, p, b * P:(b + 1) * P],
                              lambda p: w3t[:, n % 2, p, :])
                    ins.then_inc(d_ready, 1)

            for n, start in turns:
                pe.wait_ge(loaded[n % 2], (n // 2 + 1) * 48)
                for which in range(3):
                    k = 3 * n + which
                    if k >= 2:
                        pe.wait_ge(tr_used, k - 1)
                    for c in range(DC):
                        src = rows[:, n % 2, which, c * P:(c + 1) * P] if which < 2 else cols[:, n % 2, c, :]
                        ins = nc.tensor.transpose(ptr[:, k % 2, c * P:(c + 1) * P], src, ident[:, :])
                    ins.then_inc(tr_ready, 1)
                if n > 0:
                    down(n - 1)
                for half in range(2):
                    k = 2 * n + half
                    if k >= 1:
                        pe.wait_ge(g_used, k)
                    pe.wait_ge(tr_used, 3 * n + 2)
                    for which in range(2):
                        for c in range(DC):
                            ins = mm3(nc, pg[:, which, :], lambda p: wt[:, which, p, c, :],
                                      lambda p: h_t[:, p, c, half * BANK:(half + 1) * BANK], c == 0, c == DC - 1)
                    ins.then_inc(g_ready, 1)
            down(HC2 - 1)

        def tr_dst(n, which, part):
            if which < 2:
                return wt[:, which, part, :, :].rearrange("p c h -> p (c h)")
            return w3t[:, n % 2, part, :]

        @block.scalar
        def _(act):
            for n, start in turns:
                for which in range(3):
                    k = 3 * n + which
                    act.wait_ge(tr_ready, k + 1)
                    if which < 2 and n > 0:
                        act.wait_ge(g_ready, 2 * n)
                    if which == 2 and n >= 2:
                        act.wait_ge(d_ready, NB * (n - 1))
                    nc.scalar.activation(tr_dst(n, which, HI), ptr[:, k % 2, :], ACT.Copy).then_inc(tr_hi, 1)
                for half in range(2):
                    k = 2 * n + half
                    act.wait_ge(g_ready, k + 1)
                    if k >= 2:
                        act.wait_ge(a_done, k - 1)
                    nc.scalar.activation(gate[:, half, :], pg[:, 0, :], ACT.Silu).then_inc(silu_done, 1)
                    act.wait_ge(a_done, k + 1)
                    if n >= 2:
                        act.wait_ge(d_ready, NB * (n - 1))
                    nc.scalar.activation(a[:, n % 2, HI, half * BANK:(half + 1) * BANK], a32[:, half, :],
                                         ACT.Copy).then_inc(a_hi, 1)

        @block.vector
        def _(dve):
            def down(n):
                for b in range(NB):
                    k = n * NB + b
                    dve.wait_ge(d_ready, k + 1)
                    if k >= NB:
                        dve.wait_ge(d_used, k - NB + 1)
                    nc.vector.tensor_tensor(x[:, b, :], pd[:, b % 2, :], x[:, b, :], ALU.add).then_inc(d_used, 1)

            for n, start in turns:
                for which in range(3):
                    k = 3 * n + which
                    dve.wait_ge(tr_hi, k + 1)
                    ins = nc.vector.tensor_tensor(tr_dst(n, which, LO), ptr[:, k % 2, :],
                                                  tr_dst(n, which, HI).bitcast(F32), ALU.subtract)
                    if which == 2 and n == HC2 - 1:
                        for part in (HI, LO):
                            ins.then_inc(own, 1)
                            dve.wait_ge(own, part + 1)
                            ins = nc.vector.memset(w3t[0:P - REST, n % 2, part, :].bitcast(F32), 0.0)
                    ins.then_inc(tr_used, 1)
                if n > 0:
                    down(n - 1)
                for half in range(2):
                    k = 2 * n + half
                    dve.wait_ge(silu_done, k + 1)
                    if n > 0:
                        dve.wait_ge(a_lo, k - 1)
                    nc.vector.tensor_tensor(a32[:, half, :], pg[:, 1, :], gate[:, half, :], ALU.mult).then_inc(a_done, 1)
                    dve.wait_ge(a_done, k + 1)
                    dve.sem_inc(g_used, 1)
                    dve.wait_ge(a_hi, k + 1)
                    cols_ = slice(half * BANK, (half + 1) * BANK)
                    nc.vector.tensor_tensor(a[:, n % 2, LO, cols_], a32[:, half, :], a[:, n % 2, HI, cols_].bitcast(F32),
                                            ALU.subtract).then_inc(a_lo, 1)
            down(HC2 - 1)
            dve.wait_ge(d_used, NB * HC2)
    st.close()



E3, R3, RD3 = 64, 8, 16
TAKEN = -3.0e38


def ffn3_stage(nc, x, ident, h_t, a_in, b_in, router_in, keys_in):
    st = Stage(nc, "f3")
    raw = st.sb("raw", [P, 2, DC, D])
    wa = st.sb("wa", [P, 2, DC, D], F32R)
    wb = st.sb("wb", [P, 2, DC, D], F32R)
    raw_r = st.sb("raw_r", [P, DC, RD3])
    router = st.sb("router", [P, 2, DC, RD3], F32R)
    raw_k = st.sb("raw_k", [RD3, E3])
    keys = st.sb("keys", [RD3, 2, E3], F32R)
    q = st.sb("q", [RD3, 2, NT], F32R)
    s = st.sb("s", [P, NB, E3])
    left = st.sb("left", [P, NB, E3])
    left2 = st.sb("left2", [P, NB, E3])
    best = st.sb("best", [P, NB, 16])
    shift = st.sb("shift", [P, NB])
    total = st.sb("total", [P, NB])
    inv = st.sb("inv", [P, NB])
    zg = st.sb("zg", [P, 2, D])
    zt = st.sb("zt", [P, 2, 2, DC, P], F32R)
    pq = st.ps("pq", [P, BANK])
    ps_ = st.ps("ps", [P, BANK])
    pz = st.ps("pz", [P, 2, BANK])
    ptr = st.ps("ptr", [P, 2, BANK])
    po = st.ps("po", [P, 2, BANK])
    (small_loaded, a_loaded, b_loaded, own, small_split, a_split, b_split, q_ready, q_hi, q_lo, s_ready, shift_ready,
     exp_done, z_ready, z_used, tr_ready, tr_hi, tr_used, o_ready, x_done) = (st.sem(n) for n in (
         "small_loaded", "a_loaded", "b_loaded", "own", "small_split", "a_split", "b_split", "q_ready", "q_hi", "q_lo",
         "s_ready", "shift_ready", "exp_done", "z_ready", "z_used", "tr_ready", "tr_hi", "tr_used", "o_ready", "x_done"))
    with nc.Block() as block:
        @block.sync
        def _(sp):
            with nc.allow_non_contiguous_dma(reason="small weights"):
                sp.dma_start(raw_r[:, :, :], router_in.rearrange("(c p) n -> p c n", p=P)).then_inc(small_loaded, 16)
            sp.dma_start(raw_k[:, :], keys_in).then_inc(small_loaded, 16)
            sp.dma_start(raw[:, 0, :, :], a_in.rearrange("(c p) n -> p c n", p=P)).then_inc(a_loaded, 16)
            sp.dma_start(raw[:, 1, :, :], b_in.rearrange("(c p) n -> p c n", p=P)).then_inc(b_loaded, 16)

        @block.gpsimd
        def _(pool):
            for i, (w, loaded, split) in enumerate(((wa, a_loaded, a_split), (wb, b_loaded, b_split))):
                pool.wait_ge(loaded, 16)
                nc.gpsimd.tensor_scalar(w[:, HI, :, :], raw[:, i, :, :], 1.0, 0.0, ALU.mult, ALU.add).then_inc(split, 1)
                pool.wait_ge(split, 1)
                nc.gpsimd.tensor_tensor(w[:, LO, :, :], raw[:, i, :, :], w[:, HI, :, :].bitcast(F32),
                                        ALU.subtract).then_inc(split, 1)

        @block.tensor
        def _(pe):
            pe.wait_ge(small_split, 2)
            for half in range(2):
                if half:
                    pe.wait_ge(q_lo, 1)
                for c in range(DC):
                    ins = mm3(nc, pq[0:RD3, :], lambda p: router[:, p, c, :],
                              lambda p: h_t[:, p, c, half * BANK:(half + 1) * BANK], c == 0, c == DC - 1)
                ins.then_inc(q_ready, 1)
            pe.wait_ge(q_lo, 2)
            for b in range(NB):
                ins = mm3(nc, ps_[:, b * E3:(b + 1) * E3], lambda p: q[:, p, b * P:(b + 1) * P], lambda p: keys[:, p, :])
            ins.then_inc(s_ready, 1)

            def low(b):
                if b >= 2:
                    pe.wait_ge(z_used, b - 1)
                for c in range(DC):
                    ins = mm3(nc, pz[:, b % 2, :], lambda p: h_t[:, p, c, b * P:(b + 1) * P],
                              lambda p: wa[:, p, c, :], c == 0, c == DC - 1)
                ins.then_inc(z_ready, 1)

            pe.wait_ge(a_split, 2)
            low(0)
            low(1)
            for b in range(NB):
                pe.wait_ge(z_used, b + 1)
                if b >= 2:
                    pe.wait_ge(tr_used, b - 1)
                for c in range(DC):
                    ins = nc.tensor.transpose(ptr[:, b % 2, c * P:(c + 1) * P], zg[:, b % 2, c * P:(c + 1) * P], ident[:, :])
                ins.then_inc(tr_ready, 1)
                if b + 2 < NB:
                    low(b + 2)
                if b == 0:
                    pe.wait_ge(b_split, 2)
                pe.wait_ge(tr_used, b + 1)
                if b >= 2:
                    pe.wait_ge(x_done, b - 1)
                for c in range(DC):
                    ins = mm3(nc, po[:, b % 2, :], lambda p: zt[:, b % 2, p, c, :], lambda p: wb[:, p, c, :],
                              c == 0, c == DC - 1)
                ins.then_inc(o_ready, 1)

        @block.scalar
        def _(act):
            for half in range(2):
                act.wait_ge(q_ready, half + 1)
                nc.scalar.activation(q[:, HI, half * BANK:(half + 1) * BANK], pq[0:RD3, :], ACT.Copy).then_inc(q_hi, 1)
            act.wait_ge(shift_ready, 1)
            for b in range(NB):
                nc.scalar.activation(s[:, b, :], s[:, b, :], ACT.Exp, bias=shift[:, b:b + 1]).then_inc(exp_done, 1)
            for b in range(NB):
                act.wait_ge(tr_ready, b + 1)
                if b >= 2:
                    act.wait_ge(o_ready, b - 1)
                nc.scalar.activation(zt[:, b % 2, HI, :, :].rearrange("p c t -> p (c t)"), ptr[:, b % 2, :],
                                     ACT.Copy).then_inc(tr_hi, 1)

        @block.vector
        def _(dve):
            steps = Steps(dve, own)
            dve.wait_ge(small_loaded, 32)
            steps.mark(nc.vector.tensor_copy(router[:, HI, :, :], raw_r[:, :, :]))
            steps.mark(nc.vector.tensor_copy(keys[:, HI, :], raw_k[:, :]))
            steps.wait()
            nc.vector.tensor_tensor(router[:, LO, :, :], raw_r[:, :, :], router[:, HI, :, :].bitcast(F32),
                                    ALU.subtract).then_inc(small_split, 1)
            nc.vector.tensor_tensor(keys[:, LO, :], raw_k[:, :], keys[:, HI, :].bitcast(F32), ALU.subtract).then_inc(small_split, 1)
            for half in range(2):
                dve.wait_ge(q_hi, half + 1)
                cols = slice(half * BANK, (half + 1) * BANK)
                nc.vector.tensor_tensor(q[:, LO, cols], pq[0:RD3, :], q[:, HI, cols].bitcast(F32), ALU.subtract).then_inc(q_lo, 1)
            dve.wait_ge(s_ready, 1)
            steps.mark(nc.vector.tensor_copy(s[:, :, :].rearrange("p b e -> p (b e)"), ps_[:, :]))
            steps.wait()
            for b in range(NB):
                steps.mark(nc.vector.max(best[:, b, 0:8], s[:, b, :]))
            steps.wait()
            for b in range(NB):
                steps.mark(nc.vector.match_replace(left[:, b, :], best[:, b, 0:8], s[:, b, :], TAKEN))
            steps.mark(nc.vector.tensor_scalar(shift[:, :], best[:, :, 0], -1.0, None, ALU.mult))
            steps.wait()
            for b in range(NB):
                steps.mark(nc.vector.max(best[:, b, 8:16], left[:, b, :]))
            steps.wait()
            for b in range(NB):
                steps.mark(nc.vector.match_replace(left2[:, b, :], best[:, b, 8:16], left[:, b, :], TAKEN))
            steps.wait()
            steps.mark(nc.vector.tensor_scalar(left[:, :, :], left2[:, :, :], TAKEN, None, ALU.is_equal))
            steps.wait()
            dve.sem_inc(shift_ready, 1)
            dve.wait_ge(exp_done, NB)
            steps.mark(nc.vector.tensor_tensor(s[:, :, :], s[:, :, :], left[:, :, :], ALU.mult))
            steps.wait()
            steps.mark(nc.vector.reduce_sum(total[:, :], s[:, :, :], AX.X))
            steps.wait()
            steps.mark(nc.vector.tensor_scalar(total[:, :], total[:, :], 0.5, None, ALU.mult))
            steps.wait()
            steps.mark(nc.vector.reciprocal(inv[:, :], total[:, :]))
            steps.wait()
            steps.mark(nc.vector.tensor_tensor(s[:, :, :], s[:, :, :], inv[:, :, None].broadcast_to([P, NB, E3]), ALU.mult))
            steps.wait()

            def gated(b):
                dve.wait_ge(z_ready, b + 1)
                if b >= 2:
                    dve.wait_ge(tr_ready, b - 1)
                nc.vector.tensor_tensor(zg[:, b % 2, :].rearrange("p (e r) -> p e r", r=R3),
                                        pz[:, b % 2, :].rearrange("p (e r) -> p e r", r=R3),
                                        s[:, b, :, None].broadcast_to([P, E3, R3]), ALU.mult).then_inc(z_used, 1)

            gated(0)
            gated(1)
            for b in range(NB):
                dve.wait_ge(tr_hi, b + 1)
                nc.vector.tensor_tensor(zt[:, b % 2, LO, :, :].rearrange("p c t -> p (c t)"), ptr[:, b % 2, :],
                                        zt[:, b % 2, HI, :, :].rearrange("p c t -> p (c t)").bitcast(F32),
                                        ALU.subtract).then_inc(tr_used, 1)
                if b + 2 < NB:
                    gated(b + 2)
                dve.wait_ge(o_ready, b + 1)
                nc.vector.tensor_tensor(x[:, b, :], po[:, b % 2, :], x[:, b, :], ALU.add).then_inc(x_done, 1)
            dve.wait_ge(x_done, NB)
    st.close()


def store_stage(nc, x, out):
    st = Stage(nc, "store")
    stored = st.sem("stored")
    with nc.Block() as block:
        @block.sync
        def _(sp):
            sp.dma_start(out.rearrange("b t d -> t b d"), x[:, :, :]).then_inc(stored, 16)
            sp.wait_ge(stored, 16)
    st.close()


PLAN0 = Plan("a0", hpg=2, own_kv=True)
PLAN2 = Plan("a2", hpg=4, rope=True)
PLAN3 = Plan("a3", hpg=4, kvb=2, qknorm=True, out_every=1)


def pieces(plan, wq_t, wk_t, wv_t, wo_t):
    def columns(w, n):
        return w[:, n * P:(n + 1) * P].reshape(DC, P, P).transpose(1, 0, 2).reshape(P, D)

    out = []
    for key in plan.all_w():
        kind, n = key[0], key[1]
        if kind == "q":
            out.append(columns(wq_t, n % H))
        elif kind == "o":
            out.append(wo_t[n * P:(n + 1) * P, :])
        else:
            out.append(columns(wk_t if kind == "k" else wv_t, n * plan.kvh + key[2]))
    return np.stack(out)


def rope_tables():
    inv_freq = (1.0 / np.float32(10000.0) ** (np.arange(0, P, 2, dtype=np.float32) / np.float32(P))).astype(np.float32)
    freqs = np.arange(MAX_POS, dtype=np.float32)[:, None] * inv_freq[None, :]
    both = np.concatenate([freqs, freqs], axis=1)
    sin = np.sin(both)
    sin[:, :P // 2] *= -1
    return np.stack([np.cos(both), sin]).astype(np.float32)


def program(nc, ins, out):
    rounded = nc.dram_tensor("nf4_rounded", (NF4_PIECES, P, NF4_COLS), F32, kind="Internal").ap()
    rounded_rows = rounded.rearrange("a p n -> (a p n)").rearrange("(r c) -> r c", c=D)
    with ExitStack() as ctx:
        def sb(name, shape, dt=F32):
            return ctx.enter_context(nc.sbuf_tensor(name, shape, dt))

        x = sb("x", [P, NB, D])
        ident = sb("ident", [P, P])
        nf4_stage(nc, ins["nf4"], rounded)
        ctx_t = sb("ctx_t", [P, 2, DC, NT], F32R)
        load_stage(nc, x, ident, ctx_t, ins["x"], ins["ident"], ins["ctxt"])
        with nc.sbuf_tensor("h_t0", [P, 2, DC, NT], F32R) as h_t:
            norm_stage(nc, "n0", x, ident, h_t, ins["ln_w"])
            attention_stage(nc, PLAN0, x, ident, ctx_t, h_t, ins["a0_w"], ins["mask_bool"], ins["pos_bias"])
            norm_stage(nc, "n1", x, ident, h_t)
            ffn0_stage(nc, x, ident, h_t, ins["w_base"], ins["f0_side"], ins["lora_b"], ins["b_base"], ins["b_router"])
        with nc.sbuf_tensor("h_nat", [P, NB, D], F32) as h:
            norm_natural_stage(nc, "n2", x, h)
            patch_attention_stage(nc, x, h, ident, ins["ctx"], ins["mask_f"], ins["a1_wqk"], ins["a1_wv"], ins["a1_wo"],
                                  ins["a1_bqk"], ins["a1_flag"], ins["a1_bv"], ins["a1_bo"])
            norm_natural_stage(nc, "n3", x, h)
            with nc.sbuf_tensor("ident_bf", [P, P], BF16) as ident_bf:
                made = Stage(nc, "ib")
                done = made.sem("done")
                with nc.Block() as block:
                    @block.vector
                    def _(dve):
                        nc.vector.tensor_copy(ident_bf[:, :], ident[:, :]).then_inc(done, 1)
                        dve.wait_ge(done, 1)
                made.close()
                ffn1_stage(nc, x, h, ident_bf, ins["f1_w"], ins["f1_scale"], ins["f1_bias"])
        with nc.sbuf_tensor("h_t1", [P, 2, DC, NT], F32R) as h_t:
            with nc.sbuf_tensor("cos", [P, NT], F32) as cos, nc.sbuf_tensor("sin", [P, NT], F32) as sin:
                rope_stage(nc, cos, sin, ins["pos"], ins["iota"], ins["rope"])
                norm_stage(nc, "n4", x, ident, h_t)
                attention_stage(nc, PLAN2, x, ident, ctx_t, h_t, ins["a2_w"], ins["mask_i"], rope_sb=(cos, sin))
            norm_stage(nc, "n5", x, ident, h_t)
            ffn2_stage(nc, x, ident, h_t, rounded_rows)
            norm_stage(nc, "n6", x, ident, h_t)
            attention_stage(nc, PLAN3, x, ident, ctx_t, h_t, ins["a3_w"], kq_norm_in=ins["a3_norm"])
            norm_stage(nc, "n7", x, ident, h_t)
            ffn3_stage(nc, x, ident, h_t, ins["f3_a"], ins["f3_b"], ins["f3_router"], ins["f3_keys"])
        store_stage(nc, x, out)


def host_layout(i):
    c = np.ascontiguousarray

    def spread(w):
        out = np.zeros((w.shape[1], 2, 4, ROWS), w.dtype)
        out[:, :, :, :DH] = w.T.reshape(w.shape[1], 2, 4, DH)
        return out.reshape(w.shape[1], 2 * P)

    flag = np.zeros((4, ROWS), np.float32)
    flag[:, DH] = 1
    bqk = np.concatenate([spread(i["L1_xattn_bq"][:, None]), spread(i["L1_xattn_bk"][:, None])], 1)
    lora_a = i["L0_ffn_lora_A"].transpose(1, 0, 2).reshape(D, E0 * R0)
    return {
        "x": i["x"], "ctx": i["ctx_4096"], "ctxt": c(i["ctx_4096"].reshape(NT, D).T), "ident": np.eye(P, dtype=np.float32),
        "mask_bool": c(i["mask_BxSxS2_bk0"]).view(np.int32), "mask_i": i["mask_BxSxS2_ik0"],
        "mask_f": c(i["mask_Bx1x4096_ff1"].reshape(NB, D)), "pos": i["pos_BxS2"],
        "pos_bias": i["L0_xattn_position_bias"], "ln_w": c(i["L0_xattn_ln_weight"].reshape(DC, P).T),
        "a0_w": pieces(PLAN0, i["L0_xattn_w_q"].T, i["L0_xattn_w_k"].T, i["L0_xattn_w_v"].T, i["L0_xattn_w_out"].T),
        "w_base": c(i["L0_ffn_W_base"].T), "f0_side": np.concatenate([lora_a, i["L0_ffn_W_router"].T], 1),
        "lora_b": c(i["L0_ffn_lora_B"].reshape(E0 * R0, D)), "b_base": i["L0_ffn_b_base"], "b_router": i["L0_ffn_b_router"],
        "a1_wqk": np.concatenate([spread(i["L1_xattn_Wq"]), spread(i["L1_xattn_Wk"])], 1),
        "a1_wv": c(i["L1_xattn_Wv"].T), "a1_wo": c(i["L1_xattn_Wo"].T), "a1_bqk": c(bqk.reshape(4, P).T),
        "a1_flag": c(flag.reshape(P, 1)), "a1_bv": i["L1_xattn_bv"], "a1_bo": i["L1_xattn_bo"],
        "f1_w": c(i["L1_ffn_weight"].T).view(np.int32), "f1_scale": i["L1_ffn_weight_scales"], "f1_bias": i["L1_ffn_bias"],
        "iota": c(np.arange(MAX_POS, dtype=np.float32).reshape(DC, P).T), "rope": rope_tables(),
        "a2_w": pieces(PLAN2, i["L2_xattn_Wq"], i["L2_xattn_Wk"], i["L2_xattn_Wv"], i["L2_xattn_Wo"]),
        "nf4": np.concatenate([i[f"L2_ffn_w{n}"].reshape(-1, P, NF4_COLS) for n in (1, 2, 3)]),
        "a3_w": pieces(PLAN3, i["L3_xattn_Wq"], i["L3_xattn_Wk"], i["L3_xattn_Wv"], i["L3_xattn_Wo"]),
        "a3_norm": np.stack([i["L3_xattn_q_norm_w"], i["L3_xattn_k_norm_w"]], 1),
        "f3_a": c(i["L3_ffn_A_w"].T), "f3_b": c(i["L3_ffn_B_w"].T), "f3_router": c(i["L3_ffn_Wq_w"].T),
        "f3_keys": c(i["L3_ffn_keys"].T),
    }


def kernel(**inputs):
    import concourse.bacc as bacc
    from concourse.bass_utils import run_bass_kernel_spmd

    nc = bacc.Bacc("TRN2", target_bir_lowering=False, num_devices=1)
    arrays, ins = {}, {}
    for name, a in host_layout({k: np.asarray(v) for k, v in inputs.items()}).items():
        arrays[f"in_{name}"] = np.ascontiguousarray(a)
        ins[name] = nc.dram_tensor(f"in_{name}", a.shape, mybir.dt.from_np(a.dtype), kind="ExternalInput").ap()
    out = nc.dram_tensor("out", (NB, P, D), F32, kind="ExternalOutput").ap()
    program(nc, ins, out)
    return run_bass_kernel_spmd(nc, [arrays], core_ids=[0]).results[0]["out"]
```

```python
import math
from contextlib import ExitStack

import numpy as np

import concourse.bass as bass
from concourse import mybir

F32 = mybir.dt.float32
F32R = mybir.dt.float32r
BF16 = mybir.dt.bfloat16
F16 = mybir.dt.float16
I32 = mybir.dt.int32
I8 = mybir.dt.int8
U8 = mybir.dt.uint8
ALU = mybir.AluOpType
ACT = mybir.ActivationFunctionType
AX = mybir.AxisListType

P = 128
NB = 8
D = 512
DC = D // P
NT = NB * P
BANK = 512
H = 32
HI, LO = 0, 1
PASSES = ((HI, HI), (HI, LO), (LO, HI))
NEG = -1.0e30
NH2 = 1376
HC2 = -(-NH2 // P)
NF4_COLS = 2752
NF4_BLOCK = 64
NF4_CODE = [-1.0, -0.6961928009986877, -0.5250730514526367, -0.39491748809814453,
            -0.28444138169288635, -0.18477343022823334, -0.09105003625154495, 0.0,
            0.07958029955625534, 0.16093020141124725, 0.24611230194568634, 0.33791524171829224,
            0.44070982933044434, 0.5626170039176941, 0.7229568362236023, 1.0]


class Steps:

    def __init__(self, engine, sem, base=0):
        self.engine, self.sem, self.base, self.n = engine, sem, base, 0

    def mark(self, ins):
        ins.then_inc(self.sem, 1)
        self.n += 1

    def wait(self):
        self.engine.wait_ge(self.sem, self.base + self.n)


class Stage:

    def __init__(self, nc, name):
        self.nc, self.name, self.ctx, self.sems = nc, name, ExitStack(), []

    def sem(self, name):
        s = self.nc.alloc_semaphore(name=f"{self.name}_{name}")
        self.sems.append(s)
        return s

    def sb(self, name, shape, dt=F32):
        return self.ctx.enter_context(self.nc.sbuf_tensor(f"{self.name}_{name}", shape, dt))

    def ps(self, name, shape, dt=F32):
        return self.ctx.enter_context(self.nc.psum_tensor(f"{self.name}_{name}", shape, dt))

    def close(self):
        self.ctx.close()
        self.nc.clear_and_free_semaphores(self.sems)
        self.nc.all_engine_barrier()


def mm3(nc, out, lhs, rhs, first=True, last=True):
    for i, (a, b) in enumerate(PASSES):
        ins = nc.tensor.matmul(out, lhs(a), rhs(b), start=first and i == 0, stop=last and i == 2)
    return ins



def load_stage(nc, x, ident, ctx_t, x_in, ident_in, ctxt_in):
    st = Stage(nc, "load")
    raw = st.sb("ctx_raw", [P, DC, NT])
    loaded, ctx_loaded = st.sem("loaded"), st.sem("ctx_loaded")
    hi_done, lo_done = st.sem("hi_done"), st.sem("lo_done")
    with nc.Block() as block:
        @block.sync
        def _(sp):
            sp.dma_start(raw[:, :, :], ctxt_in.rearrange("(c p) t -> p c t", p=P)).then_inc(ctx_loaded, 16)
            sp.dma_start(x[:, :, :], x_in.rearrange("b t d -> t b d")).then_inc(loaded, 16)
            sp.dma_start(ident[:, :], ident_in).then_inc(loaded, 16)
            sp.wait_ge(loaded, 32)

        @block.scalar
        def _(act):
            act.wait_ge(ctx_loaded, 16)
            for c in range(DC):
                nc.scalar.activation(ctx_t[:, HI, c, :], raw[:, c, :], ACT.Copy).then_inc(hi_done, 1)

        @block.vector
        def _(dve):
            for c in range(DC):
                dve.wait_ge(hi_done, c + 1)
                nc.vector.tensor_tensor(ctx_t[:, LO, c, :], raw[:, c, :],
                                        ctx_t[:, HI, c, :].bitcast(F32), ALU.subtract).then_inc(lo_done, 1)
            dve.wait_ge(lo_done, DC)
    st.close()



class Norm:

    def __init__(self, st):
        self.stats = st.sb("stats", [P, NB, 6])
        self.mv = st.sb("mv", [P, NB, 2])
        self.var = st.sb("var", [P, NB])
        self.rstd = st.sb("rstd", [P, NB])
        self.half = st.sb("half", [P, 16])
        self.var_ready, self.rstd_ready = st.sem("var_ready"), st.sem("rstd_ready")
        self.half_set = st.sem("half_set")

    def stats_on_vector(self, nc, steps, x):
        for b in range(NB):
            steps.mark(nc.vector.bn_stats(self.stats[:, b, :], x[:, b, :]))
        steps.wait()
        for b in range(NB):
            steps.mark(nc.vector.bn_aggr(self.mv[:, b, :], self.stats[:, b, :]))
        steps.wait()
        nc.vector.tensor_scalar(self.var[:, :], self.mv[:, :, 1], 1e-5, None, ALU.add).then_inc(self.var_ready, 1)

    def set_half(self, nc):
        nc.gpsimd.memset(self.half[:, :], -0.5).then_inc(self.half_set, 1)

    def rstd_on_gpsimd(self, nc, pool):
        pool.wait_ge(self.half_set, 1)
        pool.wait_ge(self.var_ready, 1)
        nc.gpsimd.tensor_tensor(self.rstd[:, :], self.var[:, :], self.half[:, 0:NB], ALU.pow).then_inc(self.rstd_ready, 1)

    def apply(self, nc, b, out, x):
        return nc.vector.tensor_scalar(out, x[:, b, :], self.mv[:, b, 0:1], self.rstd[:, b:b + 1],
                                       ALU.subtract, ALU.mult)


def norm_stage(nc, name, x, ident, h_t, lnw_in=None):
    st = Stage(nc, name)
    rms = lnw_in is not None
    norm = Norm(st)
    h = st.sb("h", [P, NB, D])
    tp = st.ps("tp", [P, 4, DC, P])
    h_ready, tp_ready, hi_done, lo_done, own = (st.sem(n) for n in ("h_ready", "tp_ready", "hi_done", "lo_done", "own"))
    if rms:
        sq = st.sb("sq", [P, 2, D])
        ssq = st.sb("ssq", [P, NB])
        ms = st.sb("ms", [P, NB])
        r2 = st.sb("r2", [P, NB])
        h2 = st.sb("h2", [P, NB, D])
        lnw = st.sb("lnw", [P, DC])
        lnw_loaded, ssq_ready, ms_ready, r2_ready, ln_ready = (
            st.sem(n) for n in ("lnw_loaded", "ssq_ready", "ms_ready", "r2_ready", "ln_ready"))
    src = h2 if rms else h
    with nc.Block() as block:
        if rms:
            @block.sync
            def _(sp):
                with nc.allow_non_contiguous_dma(reason="512 weights"):
                    sp.dma_start(lnw[:, :], lnw_in).then_inc(lnw_loaded, 16)

        @block.gpsimd
        def _(pool):
            norm.set_half(nc)
            norm.rstd_on_gpsimd(nc, pool)
            if rms:
                pool.wait_ge(ms_ready, 1)
                nc.gpsimd.tensor_tensor(r2[:, :], ms[:, :], norm.half[:, 0:NB], ALU.pow).then_inc(r2_ready, 1)

        @block.vector
        def _(dve):
            steps = Steps(dve, own)
            norm.stats_on_vector(nc, steps, x)
            dve.wait_ge(norm.rstd_ready, 1)
            if rms:
                for b in range(NB):
                    norm.apply(nc, b, h[:, b, :], x).then_inc(ln_ready, 1)
                dve.wait_ge(ssq_ready, NB)
                nc.vector.tensor_scalar(ms[:, :], ssq[:, :], 1.0 / D, 1e-5, ALU.mult, ALU.add).then_inc(ms_ready, 1)
                for b in range(NB):
                    dve.wait_ge(ln_ready, b + 1)
                    nc.vector.tensor_tensor(x[:, b, :], x[:, b, :], h[:, b, :], ALU.add)
                dve.wait_ge(r2_ready, 1)
                for b in range(NB):
                    nc.vector.tensor_scalar(h2[:, b, :], h[:, b, :], r2[:, b:b + 1], None, ALU.mult).then_inc(h_ready, 1)
                dve.wait_ge(lnw_loaded, 16)
            else:
                for b in range(NB):
                    norm.apply(nc, b, h[:, b, :], x).then_inc(h_ready, 1)
            for b in range(NB):
                dve.wait_ge(hi_done, b + 1)
                dst = h_t[:, LO, :, b * P:(b + 1) * P]
                hi = h_t[:, HI, :, b * P:(b + 1) * P].bitcast(F32)
                if rms:
                    for c in range(DC):
                        ins = nc.vector.scalar_tensor_tensor(dst[:, c, :], tp[:, b % 4, c, :], lnw[:, c:c + 1],
                                                             hi[:, c, :], ALU.mult, ALU.subtract)
                else:
                    ins = nc.vector.tensor_tensor(dst, tp[:, b % 4, :, :], hi, ALU.subtract)
                ins.then_inc(lo_done, 1)
            dve.wait_ge(lo_done, NB)

        @block.tensor
        def _(pe):
            for b in range(NB):
                pe.wait_ge(h_ready, b + 1)
                if b >= 4:
                    pe.wait_ge(lo_done, b - 3)
                for c in range(DC):
                    ins = nc.tensor.transpose(tp[:, b % 4, c, :], src[:, b, c * P:(c + 1) * P], ident[:, :])
                ins.then_inc(tp_ready, 1)

        @block.scalar
        def _(act):
            if rms:
                for b in range(NB):
                    act.wait_ge(ln_ready, b + 1)
                    if b >= 2:
                        act.wait_ge(ssq_ready, b - 1)
                    nc.scalar.activation(sq[:, b % 2, :], h[:, b, :], ACT.Square,
                                         accum_out=ssq[:, b:b + 1]).then_inc(ssq_ready, 1)
                act.wait_ge(lnw_loaded, 16)
            for b in range(NB):
                act.wait_ge(tp_ready, b + 1)
                dst = h_t[:, HI, :, b * P:(b + 1) * P]
                if rms:
                    for c in range(DC):
                        ins = nc.scalar.activation(dst[:, c, :], tp[:, b % 4, c, :], ACT.Copy, scale=lnw[:, c:c + 1])
                else:
                    ins = nc.scalar.activation(dst, tp[:, b % 4, :, :], ACT.Copy)
                ins.then_inc(hi_done, 1)
    st.close()



class Place:

    def __init__(self, g, per, n):
        self.before = g * per + n if n or not isinstance(g, int) else g * per
        self.through = g * per + (n + 1)
        self.slot = n % 2
        self.turn = g * (per // 2) + (n // 2 + 1)
        self.filled = n >= 2 or not isinstance(g, int) or g > 0
        self.last_but_one = g * per + (n - 1) if self.filled else None


class Plan:

    def __init__(self, name, hpg, own_kv=False, kvb=1, rope=False, qknorm=False, out_every=2, scale=1.0):
        self.name, self.hpg, self.own_kv, self.kvb = name, hpg, own_kv, kvb
        self.rope, self.qknorm, self.out_every, self.scale = rope, qknorm, out_every, scale
        self.groups = H // hpg
        self.kvh = hpg if own_kv else 1
        self.keys = kvb * P
        self.vcols = self.kvh * P
        self.v_per = BANK // self.vcols
        self.v_tiles = NB * kvb // self.v_per
        self.s_tiles = NB * self.keys // BANK
        self.b_per_s = NB // self.s_tiles

    def q_keys(self, head):
        return [("q", head, 0), ("q", head, 1)]

    def k_keys(self):
        if self.qknorm:
            return [("kt", t) for t in range(4)]
        return [("k", h, half) for h in range(self.kvh) for half in range(2)]

    def v_keys(self):
        return [] if self.qknorm else [("v", t) for t in range(self.v_tiles)]

    def joint_keys(self, ss=()):
        kv, kt = [("kv", n) for n in range(8)], [("kt", t) for t in range(4)]
        return list(ss) + kv[0:4] + kt[0:1] + kv[4:6] + kt[1:2] + kv[6:8] + kt[2:3] + kt[3:4]

    def in_segment(self, j, last):
        return not (last and j + 2 >= self.hpg), not (last and j == self.hpg - 1), not last and j == self.hpg - 1

    def first_a(self):
        order = []
        for head in (0, 1):
            order += self.q_keys(head) + ([("ss", head)] if self.qknorm else [])
        return order + (self.joint_keys() if self.qknorm else self.k_keys() + self.v_keys())

    def segment_a(self, j, last=False):
        q_next, _, kv_next = self.in_segment(j, last)
        q = self.q_keys(j + 2) if q_next else []
        out = [("o", j, b) for b in range(NB)] if (j + 1) % self.out_every == 0 else []
        ss = [("ss", j + 2)] if q_next and self.qknorm else []
        if not kv_next:
            return q + ss + out
        if self.qknorm:
            return q + self.joint_keys(ss)[:-1] + out[:2] + self.joint_keys()[-1:] + out[2:]
        return q[:1] + self.k_keys() + q[1:] + out + self.v_keys()

    def a_order(self, last=False):
        return [key for j in range(self.hpg) for key in self.segment_a(j, last)]

    def hi_of(self, order):
        return [k for k in order if k[0] not in ("o", "ss") and not (self.rope and k[0] in "qk")]

    def ms_of(self, order):
        return [("kn", k[1] // 2) if k[0] == "kv" else k for k in order
                if k[0] == "ss" or (k[0] == "kv" and k[1] % 2 == 1)]

    def rot_of(self, order):
        return [k for k in order if k[0] in ("q", "k")]

    def first_w(self):
        kv = [(kind, 0, i) for kind in "kv" for i in range(self.kvh)]
        return [("q", 0), ("q", 1)] + kv + [("q", 2)]

    def segment_w(self, j, last=False):
        q = [("q", j + 3)] if not (last and j + 3 >= self.hpg) else []
        out = [("o", j)] + q if (j + 1) % self.out_every == 0 else q + [("o", j)]
        if not last and j < 2:
            out += [("kv"[j], 1, i) for i in range(self.kvh)]
        return out

    def w_order(self, last=False):
        return [w for j in range(self.hpg) for w in self.segment_w(j, last)]

    def all_w(self):
        order = self.first_w()
        for g in range(self.groups):
            for kind, n, *slot in self.w_order(g == self.groups - 1):
                order.append((kind, g + n, *slot) if slot else (kind, g * self.hpg + n))
        return order


def attention_stage(nc, plan, x, ident, ctx_t, h_t, pieces_in, mask_in=None, bias_in=None, rope_sb=None, kq_norm_in=None):
    st = Stage(nc, plan.name)
    hpg, keys, kvh, kvb = plan.hpg, plan.keys, plan.kvh, plan.kvb
    rope, qknorm = plan.rope, plan.qknorm
    masked, biased = mask_in is not None, bias_in is not None
    bps, NS, NG = plan.b_per_s, plan.s_tiles, plan.groups

    raw = st.sb("raw", [P, 2, D])
    wq = st.sb("wq", [P, 2, 2, DC, P], F32R)
    wo = st.sb("wo", [P, 2, 2, D], F32R)
    if qknorm:
        wkv = st.sb("wkv", [P, 2, DC, 2, P], F32R)
    else:
        wk = st.sb("wk", [P, kvh, 2, DC, P], F32R)
        wv = st.sb("wv", [P, 2, DC, kvh, P], F32R)
    qt = st.sb("qt", [P, 2, 2, NT], F32R)
    kt = st.sb("kt", [P, kvh, 2, NB * keys], F32R)
    v = st.sb("v", [P, 2, NB * kvb, plan.vcols], F32R)
    prob = st.sb("prob", [P, 2, NB, keys])
    pt = st.sb("pt", [P, 2, 2, BANK], F32R)
    ot = st.sb("ot", [P, plan.out_every, 2, NT], F32R)
    top = st.sb("top", [P, 2, NB])
    shift = st.sb("shift", [P, 2, NB])
    total = st.sb("total", [P, 2, NB])
    inv = st.sb("inv", [P, 2, NB])
    if masked:
        neg = st.sb("neg", [P, NB, P])
        words = st.sb("words", [P, NB, mask_in.shape[2]], I32)
        mask = words[:, :, :] if mask_in.shape[2] == P else words[:, :, :].bitcast(U8)
        mask_loaded, s_used = st.sem("mask_loaded"), st.sem("s_used")
    if biased:
        bias_raw = st.sb("bias_raw", [P, 2, P])
        bias = st.sb("bias", [P, NB, P])
        valid = st.sb("valid", [P, 2, NB])
        bias_loaded = [st.sem("bias_loaded0"), st.sem("bias_loaded1")]
        bias_ready = st.sem("bias_ready")
    if rope:
        cos, sin = rope_sb
        rot = st.sb("rot", [P, 4, 2, BANK])
        rot_ready, rot_sum, rot_hi, rot_lo = (st.sem(n) for n in ("rot_ready", "rot_sum", "rot_hi", "rot_lo"))
    if qknorm:
        q2 = st.sb("q2", [P, NT])
        k2 = q2[:, 0:BANK].rearrange("p (t i n) -> p t i n", t=2, i=2)
        kn = st.sb("kn", [P, 2, 4, P])
        kss = st.sb("kss", [P, 4, 4])
        kms = st.sb("kms", [P, 4, 4])
        krs = st.sb("krs", [P, 4, 4])
        qms = st.sb("qms", [P, 2, NB])
        qsc = st.sb("qsc", [P, 2, NB])
        half_ = st.sb("half", [P, NB])
        ones = st.sb("ones", [P, 1])
        kqw = st.sb("kqw", [P, 2])
        kw = st.sb("kw", [P, 1])
        kqw_loaded, sq_done, ms_ready, rs_ready, kn_ready = (
            st.sem(n) for n in ("kqw_loaded", "sq_done", "ms_ready", "rs_ready", "kn_ready"))
    pa = st.ps("pa", [P, 2, BANK])
    pscore = st.ps("pscore", [P, 2, BANK])
    ptr = st.ps("ptr", [P, 2, BANK])
    pout = st.ps("pout", [P, 2, BANK])

    raw_loaded = [st.sem("raw_loaded0"), st.sem("raw_loaded1")]
    (split_done, a_ready, a_hi, a_used, s_ready, shift_ready, exp_done, inv_ready, norm_done,
     t_ready, t_hi, t_used, o_ready, o_hi, o_used, own, pool_set, pool_own) = (st.sem(n) for n in (
         "split_done", "a_ready", "a_hi", "a_used", "s_ready", "shift_ready", "exp_done",
         "inv_ready", "norm_done", "t_ready", "t_hi", "t_used", "o_ready", "o_hi", "o_used", "own",
         "pool_set", "pool_own"))
    piece_seen = st.sem("piece_seen")
    s_free = s_used if masked else exp_done
    n_first_a, n_group_a = len(plan.first_a()), len(plan.a_order())
    assert n_first_a % 2 == 0 and n_group_a % 2 == 0 and len(plan.w_order()) % 2 == 0
    n_first_w, n_group_w = len(plan.first_w()), len(plan.w_order())
    n_first_ms, n_group_ms = len(plan.ms_of(plan.first_a())), len(plan.ms_of(plan.a_order()))
    n_first_rot, n_group_rot = len(plan.rot_of(plan.first_a())), len(plan.rot_of(plan.a_order()))
    n_set = 1 + (3 if qknorm else 0)

    class Orders:

        def __init__(self, g=None, last=False):
            first = g is None
            self.a_keys = plan.first_a() if first else plan.a_order(last)
            w_keys = plan.first_w() if first else plan.w_order(last)
            at = 0 if first else g

            def places(keys, first_n, group_n):
                return {k: Place(at, group_n, i + (0 if first else first_n)) for i, k in enumerate(keys)}

            fa, ga = plan.first_a(), plan.a_order()
            self.a = places(self.a_keys, len(fa), len(ga))
            self.hi = places(plan.hi_of(self.a_keys), len(plan.hi_of(fa)), len(plan.hi_of(ga)))
            self.ms = places(plan.ms_of(self.a_keys), len(plan.ms_of(fa)), len(plan.ms_of(ga)))
            self.rot = places(plan.rot_of(self.a_keys), len(plan.rot_of(fa)), len(plan.rot_of(ga)))
            self.w = places(w_keys, n_first_w, n_group_w)

    def body(engine, emit):
        with engine.Fori(0, NG - 1) as g:
            emit(g, False)
        emit(NG - 1, True)

    with nc.Block() as block:
        @block.sync
        def _(sp):
            if qknorm:
                with nc.allow_non_contiguous_dma(reason="256 weights"):
                    sp.dma_start(kqw[:, :], kq_norm_in).then_inc(kqw_loaded, 16)
            if masked:
                sp.dma_start(words[:, :, :], mask_in.rearrange("b q k -> q b k")).then_inc(mask_loaded, 16)

            def load_piece(place):
                if place.filled:
                    sp.wait_ge(split_done, place.last_but_one)
                sp.dma_start(raw[:, place.slot, :], pieces_in[bass.ds(place.before, 1), :, :].rearrange("o p n -> p (o n)")
                             ).then_inc(raw_loaded[place.slot], 16)

            def load_bias(head, slot):
                sp.dma_start(bias_raw[:, slot, :], bias_in[bass.ds(head, 1), :, :].rearrange("o q k -> q (o k)")
                             ).then_inc(bias_loaded[slot], 16)

            for place in Orders().w.values():
                load_piece(place)
            if biased:
                load_bias(0, 0)
                load_bias(1, 1)

            def group(g, last):
                w = Orders(g, last).w
                for j in range(hpg):
                    for key in plan.segment_w(j, last):
                        load_piece(w[key])
                    if biased and plan.in_segment(j, last)[0]:
                        sp.wait_ge(bias_ready, g * hpg + (j + 1))
                        load_bias(g * hpg + (j + 2), j % 2)

            body(sp, group)

        @block.gpsimd
        def _(pool):
            def split_piece(key, place, steps):
                src = raw[:, place.slot, :]
                kind, n = key[0], key[-1]
                dst = {"q": lambda p: wq[:, n % 2, p, :, :], "o": lambda p: wo[:, n % 2, p, :],
                       "k": lambda p: wkv[:, p, :, 0, :] if qknorm else wk[:, n, p, :, :],
                       "v": lambda p: wkv[:, p, :, 1, :] if qknorm else wv[:, p, :, n, :]}[kind]
                if kind != "o":
                    src = src.rearrange("p (c n) -> p c n", c=DC)
                pool.wait_ge(raw_loaded[place.slot], place.turn * 16)
                pool.sem_inc(piece_seen, 1)
                steps.mark(nc.gpsimd.tensor_scalar(dst(HI), src, 1.0, 0.0, ALU.mult, ALU.add))
                steps.wait()
                nc.gpsimd.tensor_tensor(dst(LO), src, dst(HI).bitcast(F32), ALU.subtract).then_inc(split_done, 1)

            def make_bias(slot, turn, used=None):
                pool.wait_ge(bias_loaded[slot], turn * 16)
                if used is not None:
                    pool.wait_ge(s_used, used)
                nc.gpsimd.tensor_tensor(bias[:, :, :], neg[:, :, :],
                                        bias_raw[:, slot, None, :].broadcast_to([P, NB, P]),
                                        ALU.add).then_inc(bias_ready, 1)

            def norm_weights(slot, head, halves=(0, 1)):
                if NS == 2:
                    pool.wait_ge(inv_ready, head + 1)
                for half in halves:
                    if NS == 4:
                        pool.wait_ge(inv_ready, head * 2 + (half + 1))
                    bs = slice(half * NB // 2, (half + 1) * NB // 2)
                    nc.gpsimd.tensor_tensor(prob[:, slot, bs, :], prob[:, slot, bs, :],
                                            inv[:, slot, bs, None].broadcast_to([P, NB // 2, keys]),
                                            ALU.mult).then_inc(norm_done, 1)

            def sum_rotated(key, place):
                tile = key[2] + (2 if key[0] == "k" else 0)
                pool.wait_ge(rot_ready, place.through)
                nc.gpsimd.tensor_tensor(rot[:, tile, 0, :], rot[:, tile, 0, :], rot[:, tile, 1, :],
                                        ALU.add).then_inc(rot_sum, 1)

            def inverse_root(key, place):
                pool.wait_ge(ms_ready, place.through)
                if key[0] == "ss":
                    src, dst = qms[:, key[1] % 2, :], qsc[:, key[1] % 2, :]
                    nc.gpsimd.tensor_tensor(dst, src, half_[:, :], ALU.pow).then_inc(rs_ready, 1)
                else:
                    src, dst = kms[:, key[1], :], krs[:, key[1], :]
                    nc.gpsimd.tensor_tensor(dst, src, half_[:, 0:4], ALU.pow).then_inc(rs_ready, 1)

            if qknorm:
                nc.gpsimd.memset(half_[:, :], -0.5).then_inc(pool_set, 1)
                nc.gpsimd.memset(ones[:, :], 1.0).then_inc(pool_set, 1)
                pool.wait_ge(kqw_loaded, 16)
                nc.gpsimd.tensor_tensor(kw[:, :], kqw[:, 0:1], kqw[:, 1:2], ALU.mult).then_inc(pool_set, 1)
            if not masked:
                nc.gpsimd.memset(inv[:, :, :], 0.0).then_inc(pool_set, 1)
            else:
                pool.wait_ge(mask_loaded, 16)
                nc.gpsimd.tensor_scalar(neg[:, :, :], mask, 0.0, NEG, ALU.is_equal, ALU.mult).then_inc(pool_set, 1)
            pool.wait_ge(pool_set, n_set)
            steps = Steps(pool, pool_own)
            o = Orders()
            for key, place in o.w.items():
                if key == ("q", 2):
                    pool.wait_ge(a_ready, o.a["q", 0, 1].through)
                split_piece(key, place, steps)
            if biased:
                make_bias(0, 1)
                make_bias(1, 1, NS)
            if rope:
                for key, place in o.rot.items():
                    sum_rotated(key, place)
            if qknorm:
                for key, place in o.ms.items():
                    inverse_root(key, place)
            norm_weights(0, 0)

            def group(g, last):
                o = Orders(g, last)
                steps = Steps(pool, pool_own, g * n_group_w + n_first_w)
                for j in range(hpg):
                    q_next, score_next, kv_next = plan.in_segment(j, last)
                    tiles = plan.segment_a(j, last)
                    rotated = plan.rot_of(tiles) if rope else []
                    for key in rotated[:1]:
                        sum_rotated(key, o.rot[key])
                    early = score_next and NS == 2 and not kv_next
                    before = 1 if rope and (j + 1) % plan.out_every == 0 else 0 if rope else 2
                    pieces = plan.segment_w(j, last)
                    for n, key in enumerate(pieces + [None]):
                        if early and n == min(before, len(pieces)):
                            norm_weights((j + 1) % 2, g * hpg + (j + 1))
                        if n == min(before, len(pieces)):
                            for tile in rotated[1:]:
                                sum_rotated(tile, o.rot[tile])
                        if key is None:
                            break
                        if key[0] == "o" and plan.out_every == 2 and j % 2 == 0:
                            if j > 0:
                                pool.wait_ge(a_ready, o.a["o", j - 1, NB - 1].through)
                            elif not (isinstance(g, int) and g == 0):
                                pool.wait_ge(a_ready, g * n_group_a + (n_first_a - len(plan.v_keys())))
                        if key[0] == "q" and j > 0:
                            pool.wait_ge(a_ready, o.a["q", j + 1, 1].through)
                        split_piece(key, o.w[key], steps)
                    halves = (0, 1)
                    if score_next and NS == 4 and not kv_next:
                        norm_weights((j + 1) % 2, g * hpg + (j + 1), (0,))
                        halves = (1,)
                    for key in plan.ms_of(tiles):
                        inverse_root(key, o.ms[key])
                    if score_next and not early:
                        norm_weights((j + 1) % 2, g * hpg + (j + 1), halves)
                    if biased and q_next:
                        make_bias(j % 2, g * (hpg // 2) + (j // 2 + 2), (g * hpg + (j + 2)) * NS)

            body(pool, group)

        @block.tensor
        def _(pe):
            def tile_of_a(place):
                if place.filled:
                    pe.wait_ge(a_used, place.last_but_one)
                return pa[:, place.slot, :]

            def query_half(o, head, half):
                out = tile_of_a(o.a["q", head, half])
                for c in range(DC):
                    ins = mm3(nc, out, lambda p: wq[:, head % 2, p, c, :],
                              lambda p: h_t[:, p, c, half * BANK:(half + 1) * BANK], c == 0, c == DC - 1)
                ins.then_inc(a_ready, 1)

            def query_squares(o, head, count):
                out = tile_of_a(o.a["ss", head])
                pe.wait_ge(sq_done, count)
                for b in range(NB):
                    ins = nc.tensor.matmul(out[:, b:b + 1], q2[:, b * P:(b + 1) * P], ones[:, :], start=True, stop=True)
                ins.then_inc(a_ready, 1)

            def keys_of(o):
                for key in plan.k_keys():
                    out = tile_of_a(o.a[key])
                    _, h, half = key
                    for c in range(DC):
                        ins = mm3(nc, out, lambda p: wk[:, h, p, c, :],
                                  lambda p: ctx_t[:, p, c, half * BANK:(half + 1) * BANK], c == 0, c == DC - 1)
                    ins.then_inc(a_ready, 1)

            def keys_and_values(o, key):
                out = tile_of_a(o.a[key])
                for i, src in enumerate((ctx_t, h_t)):
                    for c in range(DC):
                        ins = mm3(nc, out[:, i * 2 * P:(i + 1) * 2 * P], lambda p: src[:, p, c, key[1] * P:(key[1] + 1) * P],
                                  lambda p: wkv[:, p, c, :, :].rearrange("p w n -> p (w n)"), c == 0, c == DC - 1)
                ins.then_inc(a_ready, 1)

            def turned_keys(o, key, kn_before):
                out = tile_of_a(o.a[key])
                pe.wait_ge(kn_ready, kn_before + (key[1] + 1))
                for i in range(4):
                    ins = nc.tensor.transpose(out[:, i * P:(i + 1) * P], kn[:, key[1] % 2, i, :], ident[:, :])
                ins.then_inc(a_ready, 1)

            def values(o):
                for key in plan.v_keys():
                    out = tile_of_a(o.a[key])
                    for i in range(plan.v_per):
                        n = key[1] * plan.v_per + i
                        b, src = n // kvb, (ctx_t, h_t)[n % kvb]
                        for c in range(DC):
                            ins = mm3(nc, out[:, i * plan.vcols:(i + 1) * plan.vcols],
                                      lambda p: src[:, p, c, b * P:(b + 1) * P],
                                      lambda p: wv[:, p, c, :, :], c == 0, c == DC - 1)
                    ins.then_inc(a_ready, 1)

            def score_tiles(slot, kv_head, head, tiles):
                for t in tiles:
                    if not (isinstance(head, int) and head * NS + t < 2):
                        pe.wait_ge(s_free, head * NS + (t - 1))
                    for i in range(bps):
                        b = t * bps + i
                        ins = mm3(nc, pscore[:, t % 2, i * keys:(i + 1) * keys],
                                  lambda p: qt[:, slot, p, b * P:(b + 1) * P],
                                  lambda p: kt[:, kv_head, p, b * keys:(b + 1) * keys])
                    ins.then_inc(s_ready, 1)

            def transpose(j, head, t):
                pe.wait_ge(norm_done, head * 2 + (t * 2 // NS + 1))
                flat = prob[:, j % 2, :, :].rearrange("p b k -> p (b k)")
                pe.wait_ge(t_used, head * NS + (t + 1))
                for i in range(4):
                    ins = nc.tensor.transpose(ptr[:, t % 2, i * P:(i + 1) * P],
                                              flat[:, t * BANK + i * P:t * BANK + (i + 1) * P], ident[:, :])
                ins.then_inc(t_ready, 1)

            def weighed(j, head, n):
                col = (j if plan.own_kv else 0) * P
                pe.wait_ge(o_used, head * 2 + (n + 1))
                for t in range(n * NS // 2, (n + 1) * NS // 2):
                    pe.wait_ge(t_used, head * NS + (t + 3))
                    for i in range(bps):
                        b = t * bps + i
                        for s in range(kvb):
                            cols = slice((i * kvb + s) * P, (i * kvb + s + 1) * P)
                            ins = mm3(nc, pout[:, n, (b % 4) * P:(b % 4 + 1) * P],
                                      lambda p: v[:, p, b * kvb + s, col:col + P],
                                      lambda p: pt[:, t % 2, p, cols], s == 0, s == kvb - 1)
                ins.then_inc(o_ready, 1)

            def output_tiles(o, j, batches):
                heads = range(j - plan.out_every + 1, j + 1)
                for b in batches:
                    out = tile_of_a(o.a["o", j, b])
                    for i in heads:
                        ins = mm3(nc, out, lambda p: ot[:, i % plan.out_every, p, b * P:(b + 1) * P],
                                  lambda p: wo[:, i % 2, p, :], i == heads[0], i == heads[-1])
                    ins.then_inc(a_ready, 1)

            def parts_ready(o, key):
                if rope:
                    pe.wait_ge(rot_lo, o.rot[key].through)
                else:
                    pe.wait_ge(a_used, o.a[key].through)

            o = Orders()
            if qknorm:
                pe.wait_ge(pool_set, n_set)
            for head in (0, 1):
                pe.wait_ge(split_done, o.w["q", head].through)
                query_half(o, head, 0)
                query_half(o, head, 1)
                if qknorm:
                    query_squares(o, head, 2 * (head + 1))
            pe.wait_ge(split_done, o.w["k", 0, kvh - 1].through)
            if qknorm:
                pe.wait_ge(split_done, o.w["v", 0, 0].through)
                for key in plan.joint_keys():
                    keys_and_values(o, key) if key[0] == "kv" else turned_keys(o, key, 0)
                for t in range(NS):
                    parts_ready(o, ("kt", t))
                    score_tiles(0, 0, 0, (t,))
            else:
                keys_of(o)
                parts_ready(o, plan.k_keys()[-1])
                score_tiles(0, 0, 0, range(NS))
                pe.wait_ge(split_done, o.w["v", 0, kvh - 1].through)
                values(o)

            def group(g, last):
                o = Orders(g, last)
                for j in range(hpg):
                    head = g * hpg + j
                    q_next, score_next, kv_next = plan.in_segment(j, last)
                    out_now = (j + 1) % plan.out_every == 0
                    early_half = rope and not out_now
                    kv_head = (j + 1) % hpg if plan.own_kv else 0

                    def scores(tiles):
                        score_tiles((j + 1) % 2, kv_head, head + 1, tiles)

                    transpose(j, head, 0)
                    transpose(j, head, 1)
                    if j == 0:
                        pe.wait_ge(a_used, g * n_group_a + n_first_a)
                        if rope:
                            pe.wait_ge(rot_lo, g * n_group_rot + n_first_rot)
                    if score_next and not kv_next:
                        if j > 0:
                            parts_ready(o, ("q", j + 1, 1))
                        scores((0, 1))
                    if q_next:
                        pe.wait_ge(split_done, o.w["q", j + 2].through if j else g * n_group_w + n_first_w)
                        query_half(o, j + 2, 0)
                        if early_half:
                            query_half(o, j + 2, 1)
                    weighed(j, head, 0)
                    if NS == 4:
                        transpose(j, head, 2)
                        transpose(j, head, 3)
                        if score_next and not kv_next:
                            scores((2, 3))
                        if q_next:
                            query_half(o, j + 2, 1)
                        weighed(j, head, 1)
                    else:
                        weighed(j, head, 1)
                        if kv_next:
                            pe.wait_ge(split_done, o.w["k", 1, kvh - 1].through)
                            keys_of(o)
                        if q_next and not early_half:
                            query_half(o, j + 2, 1)
                        if kv_next:
                            parts_ready(o, plan.k_keys()[-1])
                            scores((0, 1))
                    count = g * (2 * hpg) + (4 + 2 * (j + 1))
                    if qknorm and kv_next:
                        pe.wait_ge(split_done, o.w["v", 1, 0].through)
                        for key in plan.joint_keys([("ss", j + 2)])[:-1]:
                            if key[0] == "kv":
                                keys_and_values(o, key)
                            elif key[0] == "kt":
                                turned_keys(o, key, (g + 1) * 4)
                            else:
                                query_squares(o, j + 2, count)
                            if key == ("kt", 2):
                                parts_ready(o, ("kt", 1))
                                scores((0, 1))
                    elif qknorm and q_next:
                        query_squares(o, j + 2, count)
                    if out_now:
                        pe.wait_ge(split_done, o.w["o", j].through)
                        pe.wait_ge(o_used, (head + 1) * 2 + 2)
                        if qknorm and kv_next:
                            output_tiles(o, j, (0, 1))
                            turned_keys(o, ("kt", 3), (g + 1) * 4)
                            output_tiles(o, j, (2, 3))
                            parts_ready(o, ("kt", 3))
                            scores((2, 3))
                            output_tiles(o, j, range(4, NB))
                        else:
                            output_tiles(o, j, range(NB))
                    if kv_next and not qknorm:
                        pe.wait_ge(split_done, o.w["v", 1, kvh - 1].through)
                        values(o)

            body(pe, group)

        @block.scalar
        def _(act):
            def hi(o, key, dst, **scale):
                act.wait_ge(a_ready, o.a[key].through)
                nc.scalar.activation(dst, pa[:, o.a[key].slot, :], ACT.Copy, **scale).then_inc(a_hi, 1)

            def query_hi(o, head, half):
                cols, key = slice(half * BANK, (half + 1) * BANK), ("q", head, half)
                if rope:
                    rotated_hi(o, key, qt[:, head % 2, HI, cols])
                    return
                if qknorm:
                    act.wait_ge(a_ready, o.a[key].through)
                    nc.scalar.activation(q2[:, cols], pa[:, o.a[key].slot, :], ACT.Square).then_inc(sq_done, 1)
                hi(o, key, qt[:, head % 2, HI, cols])

            def rotated_hi(o, key, dst):
                tile = key[2] + (2 if key[0] == "k" else 0)
                act.wait_ge(rot_sum, o.rot[key].through)
                nc.scalar.activation(dst, rot[:, tile, 0, :], ACT.Copy).then_inc(rot_hi, 1)

            def keys_hi(o):
                for key in plan.k_keys():
                    dst = kt[:, key[1], HI, key[2] * BANK:(key[2] + 1) * BANK]
                    (rotated_hi if rope else hi)(o, key, dst)

            def joint_hi(o, key):
                n = key[1]
                if key[0] == "kt":
                    hi(o, key, kt[:, 0, HI, n * BANK:(n + 1) * BANK], scale=kw[:, :])
                    return
                act.wait_ge(a_ready, o.a[key].through)
                src = pa[:, o.a[key].slot, :].rearrange("p (i w n) -> p i w n", i=2, w=2)
                nc.scalar.activation(k2[:, n % 2], src[:, :, 0, :], ACT.Square)
                nc.scalar.activation(kn[:, n // 2 % 2, n % 2 * 2:n % 2 * 2 + 2, :], src[:, :, 0, :], ACT.Copy)
                nc.scalar.activation(v[:, HI, 2 * n:2 * n + 2, :], src[:, :, 1, :], ACT.Copy).then_inc(a_hi, 1)

            def values_hi(o):
                for key in plan.v_keys():
                    blocks = slice(key[1] * plan.v_per, (key[1] + 1) * plan.v_per)
                    hi(o, key, v[:, HI, blocks, :].rearrange("p b n -> p (b n)"))

            def exps(slot, head, tiles):
                if masked:
                    act.wait_ge(shift_ready, head + 1)
                for t in tiles:
                    if not masked:
                        act.wait_ge(shift_ready, head * NS + (t + 1))
                    for i in range(bps):
                        b = t * bps + i
                        src, scale = prob[:, slot, b, :], plan.scale
                        if not masked:
                            src, scale = pscore[:, t % 2, i * keys:(i + 1) * keys], qsc[:, slot, b:b + 1]
                        ins = nc.scalar.activation(prob[:, slot, b, :], src, ACT.Exp, bias=shift[:, slot, b:b + 1],
                                                   scale=scale, accum_out=total[:, slot, b:b + 1])
                    if not masked or t == NS - 1:
                        ins.then_inc(exp_done, 1)

            def weight_hi(head, t):
                act.wait_ge(t_ready, head * NS + (t + 1))
                nc.scalar.activation(pt[:, t % 2, HI, :], ptr[:, t % 2, :], ACT.Copy).then_inc(t_hi, 1)

            def weighed_hi(j, head, n):
                act.wait_ge(o_ready, head * 2 + (n + 1))
                nc.scalar.activation(ot[:, j % plan.out_every, HI, n * BANK:(n + 1) * BANK], pout[:, n, :],
                                     ACT.Copy).then_inc(o_hi, 1)

            if qknorm:
                act.wait_ge(pool_set, n_set)
            o = Orders()
            for head in (0, 1):
                query_hi(o, head, 0)
                query_hi(o, head, 1)
            if qknorm:
                for key in plan.joint_keys():
                    joint_hi(o, key)
            else:
                keys_hi(o)
            exps(0, 0, range(NS))
            values_hi(o)

            def group(g, last):
                o = Orders(g, last)
                for j in range(hpg):
                    head = g * hpg + j
                    q_next, score_next, kv_next = plan.in_segment(j, last)
                    weight_hi(head, 0)
                    weight_hi(head, 1)
                    if NS == 4:
                        if score_next and not kv_next:
                            exps((j + 1) % 2, head + 1, (0, 1))
                        if q_next:
                            query_hi(o, j + 2, 0)
                        weighed_hi(j, head, 0)
                        weight_hi(head, 2)
                        weight_hi(head, 3)
                        if score_next and not kv_next:
                            exps((j + 1) % 2, head + 1, (2, 3))
                        if q_next:
                            query_hi(o, j + 2, 1)
                        weighed_hi(j, head, 1)
                        if kv_next:
                            for key in plan.joint_keys():
                                joint_hi(o, key)
                                if key == ("kt", 2):
                                    exps((j + 1) % 2, head + 1, (0, 1))
                            exps((j + 1) % 2, head + 1, (2, 3))
                        continue
                    if score_next and not kv_next:
                        exps((j + 1) % 2, head + 1, (0, 1))
                    if q_next and (kv_next or not rope):
                        query_hi(o, j + 2, 0)
                    weighed_hi(j, head, 0)
                    weighed_hi(j, head, 1)
                    if q_next and rope and not kv_next:
                        query_hi(o, j + 2, 0)
                    if kv_next:
                        keys_hi(o)
                    if q_next:
                        query_hi(o, j + 2, 1)
                    if kv_next:
                        exps((j + 1) % 2, head + 1, (0, 1))
                        values_hi(o)

            body(act, group)

        @block.vector
        def _(dve):
            def lo(o, key, dst, hi_part, scale=None):
                dve.wait_ge(a_hi, o.hi[key].through)
                src = pa[:, o.a[key].slot, :]
                if scale is None:
                    nc.vector.tensor_tensor(dst, src, hi_part.bitcast(F32), ALU.subtract).then_inc(a_used, 1)
                else:
                    nc.vector.scalar_tensor_tensor(dst, src, scale, hi_part.bitcast(F32), ALU.mult,
                                                   ALU.subtract).then_inc(a_used, 1)

            def rotate(o, key):
                half = key[2]
                tile, cols = half + (2 if key[0] == "k" else 0), slice(half * BANK, (half + 1) * BANK)
                src = pa[:, o.a[key].slot, :]
                dve.wait_ge(a_ready, o.a[key].through)
                parts = o.rot[key[0], key[1], 0].before
                if not isinstance(parts, int) or parts:
                    dve.wait_ge(rot_lo, parts)
                nc.vector.tensor_tensor(rot[:, tile, 0, :], src, cos[:, cols], ALU.mult)
                nc.vector.tensor_tensor(rot[0:64, tile, 1, :], src[64:128, :], sin[0:64, cols], ALU.mult)
                ins = nc.vector.tensor_tensor(rot[64:128, tile, 1, :], src[0:64, :], sin[64:128, cols], ALU.mult)
                ins.then_inc(rot_ready, 1)
                dve.wait_ge(rot_ready, o.rot[key].through)
                dve.sem_inc(a_used, 1)

            def rotated_lo(o, key, dst, hi_part):
                tile = key[2] + (2 if key[0] == "k" else 0)
                dve.wait_ge(rot_hi, o.rot[key].through)
                nc.vector.tensor_tensor(dst, rot[:, tile, 0, :], hi_part.bitcast(F32), ALU.subtract).then_inc(rot_lo, 1)

            def query_lo(o, head, half):
                if rope:
                    rotate(o, ("q", head, half))
                else:
                    cols = slice(half * BANK, (half + 1) * BANK)
                    lo(o, ("q", head, half), qt[:, head % 2, LO, cols], qt[:, head % 2, HI, cols])

            def rotated_query_lo(o, head, half):
                cols = slice(half * BANK, (half + 1) * BANK)
                rotated_lo(o, ("q", head, half), qt[:, head % 2, LO, cols], qt[:, head % 2, HI, cols])

            def keys_lo(o):
                if rope:
                    for key in plan.k_keys():
                        rotate(o, key)
                for key in plan.k_keys():
                    cols = slice(key[2] * BANK, (key[2] + 1) * BANK)
                    (rotated_lo if rope else lo)(o, key, kt[:, key[1], LO, cols], kt[:, key[1], HI, cols])

            def joint_lo(o, key, steps):
                n = key[1]
                if key[0] == "kt":
                    cols = slice(n * BANK, (n + 1) * BANK)
                    lo(o, key, kt[:, 0, LO, cols], kt[:, 0, HI, cols], kw[:, :])
                    return
                dve.wait_ge(a_hi, o.hi[key].through)
                steps.mark(nc.vector.reduce_sum(kss[:, n // 2, n % 2 * 2:n % 2 * 2 + 2], k2[:, n % 2], AX.X))
                src = pa[:, o.a[key].slot, :].rearrange("p (i w n) -> p i w n", i=2, w=2)
                nc.vector.tensor_tensor(v[:, LO, 2 * n:2 * n + 2, :], src[:, :, 1, :],
                                        v[:, HI, 2 * n:2 * n + 2, :].bitcast(F32), ALU.subtract).then_inc(a_used, 1)
                if n % 2 == 1:
                    t = n // 2
                    steps.wait()
                    nc.vector.tensor_scalar(kms[:, t, :], kss[:, t, :], 1.0 / P, 1e-6, ALU.mult, ALU.add).then_inc(ms_ready, 1)

            def norm_keys(o, t):
                dve.wait_ge(rs_ready, o.ms["kn", t].through)
                nc.vector.tensor_tensor(kn[:, t % 2, :, :], kn[:, t % 2, :, :],
                                        krs[:, t, :, None].broadcast_to([P, 4, P]), ALU.mult).then_inc(kn_ready, 1)

            def values_lo(o):
                for key in plan.v_keys():
                    blocks = slice(key[1] * plan.v_per, (key[1] + 1) * plan.v_per)
                    lo(o, key, v[:, LO, blocks, :].rearrange("p b n -> p (b n)"),
                       v[:, HI, blocks, :].rearrange("p b n -> p (b n)"))

            def shifts(slot, head, tiles, steps):
                if not masked:
                    for t in tiles:
                        bs = slice(t * bps, (t + 1) * bps)
                        dve.wait_ge(s_ready, head * NS + (t + 1))
                        steps.mark(nc.vector.reduce_max(top[:, slot, bs], pscore[:, t % 2, :].rearrange("p (b k) -> p b k", k=keys), AX.X))
                        steps.wait()
                        nc.vector.scalar_tensor_tensor(shift[:, slot, bs], top[:, slot, bs], -1.0, qsc[:, slot, bs],
                                                       ALU.mult, ALU.mult).then_inc(shift_ready, 1)
                    return
                if biased:
                    dve.wait_ge(bias_ready, head + 1)
                for t in range(NS):
                    bs = slice(t * bps, (t + 1) * bps)
                    dve.wait_ge(s_ready, head * NS + (t + 1))
                    add = bias[:, bs, :] if biased else neg[:, bs, :]
                    nc.vector.tensor_tensor(prob[:, slot, bs, :], pscore[:, t % 2, :].rearrange("p (b k) -> p b k", k=keys),
                                            add, ALU.add).then_inc(s_used, 1)
                dve.wait_ge(s_used, head * NS + NS)
                steps.mark(nc.vector.reduce_max(top[:, slot, :], prob[:, slot, :, :], AX.X))
                steps.wait()
                if biased:
                    steps.mark(nc.vector.tensor_scalar(valid[:, slot, :], top[:, slot, :], NEG / 2, None, ALU.is_gt))
                nc.vector.tensor_scalar(shift[:, slot, :], top[:, slot, :], -plan.scale, None, ALU.mult).then_inc(shift_ready, 1)

            def inverse(slot, head, steps, halves=(0, 1)):
                if NS == 4:
                    for half in halves:
                        bs = slice(half * 4, half * 4 + 4)
                        dve.wait_ge(exp_done, head * NS + 2 * (half + 1))
                        nc.vector.reciprocal(inv[:, slot, bs], total[:, slot, bs]).then_inc(inv_ready, 1)
                    return
                dve.wait_ge(exp_done, head + 1)
                if not biased:
                    nc.vector.reciprocal(inv[:, slot, :], total[:, slot, :]).then_inc(inv_ready, 1)
                    return
                steps.mark(nc.vector.reciprocal(inv[:, slot, :], total[:, slot, :]))
                steps.wait()
                nc.vector.tensor_tensor(inv[:, slot, :], inv[:, slot, :], valid[:, slot, :], ALU.mult).then_inc(inv_ready, 1)

            def weight_lo(head, t):
                dve.wait_ge(t_hi, head * NS + (t + 1))
                nc.vector.tensor_tensor(pt[:, t % 2, LO, :], ptr[:, t % 2, :], pt[:, t % 2, HI, :].bitcast(F32),
                                        ALU.subtract).then_inc(t_used, 1)

            def weighed_lo(j, head, n):
                dve.wait_ge(o_hi, head * 2 + (n + 1))
                cols = slice(n * BANK, (n + 1) * BANK)
                nc.vector.tensor_tensor(ot[:, j % plan.out_every, LO, cols], pout[:, n, :],
                                        ot[:, j % plan.out_every, HI, cols].bitcast(F32),
                                        ALU.subtract).then_inc(o_used, 1)

            def add_output(o, j, batches):
                for b in batches:
                    dve.wait_ge(a_ready, o.a["o", j, b].through)
                    nc.vector.tensor_tensor(x[:, b, :], pa[:, o.a["o", j, b].slot, :], x[:, b, :],
                                            ALU.add).then_inc(a_used, 1)

            def query_scale(o, head):
                key = ("ss", head)
                dve.wait_ge(a_ready, o.a[key].through)
                nc.vector.tensor_scalar(qms[:, head % 2, :], pa[:, o.a[key].slot, 0:NB], P * 1e-6, None, ALU.add
                                        ).then_inc(ms_ready, 1)
                dve.wait_ge(ms_ready, o.ms[key].through)
                dve.sem_inc(a_used, 1)

            NORMED_AFTER = {("kv", 2): 0, ("kv", 4): 1, ("kv", 6): 2, ("kt", 2): 3}

            dve.sem_inc(t_used, 2)
            dve.sem_inc(o_used, 2)
            if masked or qknorm:
                dve.wait_ge(pool_set, n_set)
            o = Orders()
            steps = Steps(dve, own)
            for head in (0, 1):
                for half in range(2):
                    query_lo(o, head, half)
                    if rope:
                        rotated_query_lo(o, head, half)
                if qknorm:
                    query_scale(o, head)
            if qknorm:
                for key in plan.joint_keys():
                    joint_lo(o, key, steps)
                    if key in NORMED_AFTER:
                        norm_keys(o, NORMED_AFTER[key])
                dve.wait_ge(rs_ready, n_first_ms)
            else:
                keys_lo(o)
            shifts(0, 0, range(NS), steps)
            inverse(0, 0, steps)
            values_lo(o)
            own_first = steps.n
            own_group = hpg * ((3 if biased else 1) if masked else NS) + (8 if qknorm else 0)

            def group(g, last):
                o = Orders(g, last)
                steps = Steps(dve, own, g * own_group + own_first)
                for j in range(hpg):
                    head = g * hpg + j
                    q_next, score_next, kv_next = plan.in_segment(j, last)
                    out_now = (j + 1) % plan.out_every == 0

                    def next_shifts(tiles):
                        shifts((j + 1) % 2, head + 1, tiles, steps)

                    weight_lo(head, 0)
                    weight_lo(head, 1)
                    if score_next and qknorm:
                        dve.wait_ge(rs_ready, o.ms["ss", j + 1].through if j else g * n_group_ms + n_first_ms)
                    if score_next and not kv_next:
                        next_shifts((0, 1))
                    if q_next and (rope or NS == 4 or kv_next):
                        query_lo(o, j + 2, 0)
                    if score_next and NS == 2 and not kv_next:
                        inverse((j + 1) % 2, head + 1, steps)
                    if q_next and not (rope or NS == 4 or kv_next):
                        query_lo(o, j + 2, 0)
                    if q_next and rope and not out_now:
                        query_lo(o, j + 2, 1)
                    weighed_lo(j, head, 0)
                    if NS == 4:
                        weight_lo(head, 2)
                        weight_lo(head, 3)
                        if score_next and not kv_next:
                            inverse((j + 1) % 2, head + 1, steps, (0,))
                            next_shifts((2, 3))
                        if q_next:
                            query_lo(o, j + 2, 1)
                        weighed_lo(j, head, 1)
                        if kv_next:
                            for key in plan.joint_keys([("ss", j + 2)])[:-1]:
                                query_scale(o, j + 2) if key[0] == "ss" else joint_lo(o, key, steps)
                                if key in NORMED_AFTER:
                                    norm_keys(o, NORMED_AFTER[key])
                            next_shifts((0, 1))
                            inverse((j + 1) % 2, head + 1, steps, (0,))
                        elif q_next:
                            query_scale(o, j + 2)
                        if score_next and not out_now:
                            inverse((j + 1) % 2, head + 1, steps, (1,))
                    else:
                        weighed_lo(j, head, 1)
                        if kv_next:
                            if rope:
                                rotated_query_lo(o, j + 2, 0)
                            keys_lo(o)
                        if q_next and not (rope and not out_now):
                            query_lo(o, j + 2, 1)
                        if kv_next:
                            next_shifts((0, 1))
                        elif q_next and rope:
                            rotated_query_lo(o, j + 2, 0)
                    if out_now:
                        dve.wait_ge(a_used, o.a["o", j, 0].before)
                        if NS == 4 and kv_next:
                            add_output(o, j, (0, 1))
                            joint_lo(o, ("kt", 3), steps)
                            add_output(o, j, (2, 3))
                            next_shifts((2, 3))
                        else:
                            add_output(o, j, range(4))
                        if q_next and rope:
                            rotated_query_lo(o, j + 2, 1)
                        if score_next and (NS == 4 or kv_next):
                            inverse((j + 1) % 2, head + 1, steps, (1,) if NS == 4 else (0, 1))
                        add_output(o, j, range(4, NB))
                    elif q_next and rope:
                        rotated_query_lo(o, j + 2, 1)
                    if kv_next:
                        values_lo(o)
                assert last or steps.n == own_group, (steps.n, own_group)

            body(dve, group)
            dve.wait_ge(a_used, (NG - 1) * n_group_a + n_first_a + len(plan.a_order(True)))
    st.close()



MAX_POS = 512
ROOT_SCALE = float(P) ** -0.25


def rope_stage(nc, cos, sin, pos_in, iota_in, tables_in):
    st = Stage(nc, "rope")
    pos_i = st.sb("pos_i", [P, NT], I32)
    pos = st.sb("pos", [P, NT])
    below = st.sb("below", [P, NT])
    iota = st.sb("iota", [P, DC])
    hot = st.sb("hot", [P, DC, NT], F32R)
    tab = st.sb("tab", [P, DC, 2, P])
    pair = st.sb("pair", [P, 2, DC, 2, P], F32R)
    acc = st.ps("acc", [P, 2, 2, BANK])
    loaded, own, split_done, hot_ready, made, copied = (
        st.sem(n) for n in ("loaded", "own", "split_done", "hot_ready", "made", "copied"))
    with nc.Block() as block:
        @block.sync
        def _(sp):
            sp.dma_start(pos_i[:, :], pos_in.rearrange("(o b) t -> o (b t)", o=1).broadcast_to([P, NT])
                         ).then_inc(loaded, 16)
            sp.dma_start(iota[:, :], iota_in).then_inc(loaded, 16)
            for w in range(2):
                sp.dma_start(tab[:, :, w, :], tables_in[w].rearrange("(c p) d -> p c d", p=P)).then_inc(loaded, 16)

        @block.vector
        def _(dve):
            steps = Steps(dve, own)
            dve.wait_ge(loaded, 64)
            steps.mark(nc.vector.tensor_scalar(below[:, :], pos_i[:, :], 0.0, float(MAX_POS), ALU.is_lt, ALU.mult))
            steps.mark(nc.vector.tensor_copy(pos[:, :], pos_i[:, :]))
            steps.wait()
            steps.mark(nc.vector.tensor_tensor(pos[:, :], pos[:, :], below[:, :], ALU.add))
            steps.wait()
            steps.mark(nc.vector.tensor_scalar(pos[:, :], pos[:, :], 0.0, MAX_POS - 1.0, ALU.max, ALU.min))
            steps.mark(nc.vector.tensor_copy(pair[:, HI, :, :, :], tab[:, :, :, :]))
            steps.wait()
            nc.vector.tensor_tensor(pair[:, LO, :, :, :], tab[:, :, :, :], pair[:, HI, :, :, :].bitcast(F32),
                                    ALU.subtract).then_inc(split_done, 1)
            for c in range(DC):
                nc.vector.tensor_scalar(hot[:, c, :], pos[:, :], iota[:, c:c + 1], None,
                                        ALU.is_equal).then_inc(hot_ready, 1)
            for w, dst in enumerate((cos, sin)):
                for half in range(2):
                    dve.wait_ge(made, 2 * w + half + 1)
                    nc.vector.tensor_scalar(dst[:, half * BANK:(half + 1) * BANK], acc[:, w, half, :], ROOT_SCALE, None,
                                            ALU.mult).then_inc(copied, 1)
            dve.wait_ge(copied, 4)

        @block.tensor
        def _(pe):
            pe.wait_ge(split_done, 1)
            pe.wait_ge(hot_ready, DC)
            for w in range(2):
                for half in range(2):
                    for c in range(DC):
                        for part in (HI, LO):
                            ins = nc.tensor.matmul(acc[:, w, half, :], pair[:, part, c, w, :],
                                                   hot[:, c, half * BANK:(half + 1) * BANK],
                                                   start=c == 0 and part == HI, stop=c == DC - 1 and part == LO)
                    ins.then_inc(made, 1)
    st.close()



E0, R0 = 8, 16


def ffn0_stage(nc, x, ident, h_t, base_in, side_in, lora_b_in, b_base_in, b_router_in):
    st = Stage(nc, "f0")
    SIDE = E0 * R0 + E0
    raw = st.sb("raw", [P, DC, D])
    base = st.sb("base", [P, 2, DC, D], F32R)
    raw_side = st.sb("raw_side", [P, DC, SIDE])
    side = st.sb("side", [P, 2, DC, SIDE], F32R)
    raw_b = st.sb("raw_b", [P, D])
    lora_b = st.sb("lora_b", [P, 2, D], F32R)
    b_base = st.sb("b_base", [P, D])
    b_router = st.sb("b_router", [P, E0])
    low = st.sb("low", [P, NB, E0 * R0])
    z = st.sb("z", [P, NB, E0])
    zs = st.sb("zs", [P, NB, E0])
    cum = st.sb("cum", [P, NB, E0])
    rank = st.sb("rank", [P, E0])
    sup = st.sb("sup", [P, NB, E0])
    count = st.sb("count", [P, NB])
    tau = st.sb("tau", [P, NB])
    rcount = st.sb("rcount", [P, NB])
    gated = st.sb("gated", [P, 2, NB, P], F32R)
    p_side = st.ps("p_side", [P, 2, BANK])
    p_tr = st.ps("p_tr", [P, 2, BANK])
    p_out = st.ps("p_out", [P, 2, BANK])
    (loaded, loaded_side, side_split, base_split, side_ready, side_used, own, gate_ready, tr_ready, tr_hi, tr_lo,
     out_ready, out_used, ranked) = (st.sem(n) for n in (
         "loaded", "loaded_side", "side_split", "base_split", "side_ready", "side_used", "own", "gate_ready",
         "tr_ready", "tr_hi", "tr_lo", "out_ready", "out_used", "ranked"))
    with nc.Block() as block:
        @block.sync
        def _(sp):
            sp.dma_start(raw_side[:, :, :], side_in.rearrange("(c p) n -> p c n", p=P)).then_inc(loaded_side, 16)
            sp.dma_start(b_router[:, :], b_router_in.rearrange("(o n) -> o n", o=1).broadcast_to([P, E0])
                         ).then_inc(loaded_side, 16)
            sp.dma_start(raw[:, :, :], base_in.rearrange("(c p) n -> p c n", p=P)).then_inc(loaded, 16)
            sp.dma_start(raw_b[:, :], lora_b_in).then_inc(loaded, 16)
            sp.dma_start(b_base[:, :], b_base_in.rearrange("(o n) -> o n", o=1).broadcast_to([P, D])).then_inc(loaded, 16)

        @block.gpsimd
        def _(pool):
            for e in range(E0):
                nc.gpsimd.memset(rank[:, e:e + 1], float(e + 1)).then_inc(ranked, 1)
            pool.wait_ge(loaded, 48)
            nc.gpsimd.tensor_scalar(base[:, HI, :, :], raw[:, :, :], 1.0, 0.0, ALU.mult, ALU.add).then_inc(base_split, 1)
            nc.gpsimd.tensor_scalar(lora_b[:, HI, :], raw_b[:, :], 1.0, 0.0, ALU.mult, ALU.add).then_inc(base_split, 1)
            pool.wait_ge(base_split, 2)
            nc.gpsimd.tensor_tensor(base[:, LO, :, :], raw[:, :, :], base[:, HI, :, :].bitcast(F32),
                                    ALU.subtract).then_inc(base_split, 1)
            nc.gpsimd.tensor_tensor(lora_b[:, LO, :], raw_b[:, :], lora_b[:, HI, :].bitcast(F32),
                                    ALU.subtract).then_inc(base_split, 1)

        @block.tensor
        def _(pe):
            pe.wait_ge(side_split, 1)
            for b in range(NB):
                if b >= 2:
                    pe.wait_ge(side_used, b - 1)
                for c in range(DC):
                    ins = mm3(nc, p_side[:, b % 2, 0:SIDE], lambda p: h_t[:, p, c, b * P:(b + 1) * P],
                              lambda p: side[:, p, c, :], c == 0, c == DC - 1)
                ins.then_inc(side_ready, 1)
            pe.wait_ge(base_split, 4)
            for b in range(NB):
                if b >= 2:
                    pe.wait_ge(out_used, b - 1)
                for c in range(DC):
                    mm3(nc, p_out[:, b % 2, :], lambda p: h_t[:, p, c, b * P:(b + 1) * P],
                        lambda p: base[:, p, c, :], c == 0, False)
                if b % 4 == 0:
                    pe.wait_ge(gate_ready, 1)
                    for i in range(4):
                        ins = nc.tensor.transpose(p_tr[:, b // 4, i * P:(i + 1) * P], low[:, b + i, :], ident[:, :])
                    ins.then_inc(tr_ready, 1)
                    pe.wait_ge(tr_lo, b // 4 + 1)
                ins = mm3(nc, p_out[:, b % 2, :], lambda p: gated[:, p, b, :], lambda p: lora_b[:, p, :], False, True)
                ins.then_inc(out_ready, 1)

        @block.scalar
        def _(act):
            for t in range(2):
                act.wait_ge(tr_ready, t + 1)
                nc.scalar.activation(gated[:, HI, 4 * t:4 * t + 4, :].rearrange("p b n -> p (b n)"), p_tr[:, t, :],
                                     ACT.Copy).then_inc(tr_hi, 1)

        @block.vector
        def _(dve):
            steps = Steps(dve, own)
            dve.wait_ge(loaded_side, 32)
            steps.mark(nc.vector.tensor_copy(side[:, HI, :, :], raw_side[:, :, :]))
            steps.wait()
            nc.vector.tensor_tensor(side[:, LO, :, :], raw_side[:, :, :], side[:, HI, :, :].bitcast(F32),
                                    ALU.subtract).then_inc(side_split, 1)
            for b in range(NB):
                dve.wait_ge(side_ready, b + 1)
                steps.mark(nc.vector.tensor_tensor(z[:, b, :], p_side[:, b % 2, E0 * R0:SIDE], b_router[:, :], ALU.add))
                nc.vector.tensor_copy(low[:, b, :], p_side[:, b % 2, 0:E0 * R0]).then_inc(side_used, 1)
            steps.wait()
            for b in range(NB):
                steps.mark(nc.vector.max(zs[:, b, :], z[:, b, :]))
            steps.wait()
            steps.mark(nc.vector.tensor_copy(cum[:, :, 0:1], zs[:, :, 0:1]))
            for e in range(1, E0):
                steps.wait()
                steps.mark(nc.vector.tensor_tensor(cum[:, :, e:e + 1], cum[:, :, e - 1:e], zs[:, :, e:e + 1], ALU.add))
            dve.wait_ge(ranked, E0)
            ranks = rank[:, None, :].broadcast_to([P, NB, E0])
            steps.mark(nc.vector.tensor_tensor(sup[:, :, :], zs[:, :, :], ranks, ALU.mult))
            steps.wait()
            steps.mark(nc.vector.tensor_scalar(sup[:, :, :], sup[:, :, :], 1.0, None, ALU.add))
            steps.wait()
            steps.mark(nc.vector.tensor_tensor(sup[:, :, :], sup[:, :, :], cum[:, :, :], ALU.is_gt))
            steps.wait()
            steps.mark(nc.vector.reduce_sum(count[:, :], sup[:, :, :], AX.X))
            steps.wait()
            steps.mark(nc.vector.tensor_tensor(sup[:, :, :], ranks, count[:, :, None].broadcast_to([P, NB, E0]), ALU.is_equal))
            steps.mark(nc.vector.reciprocal(rcount[:, :], count[:, :]))
            steps.wait()
            steps.mark(nc.vector.tensor_tensor(sup[:, :, :], sup[:, :, :], cum[:, :, :], ALU.mult))
            steps.wait()
            steps.mark(nc.vector.reduce_sum(tau[:, :], sup[:, :, :], AX.X))
            steps.wait()
            steps.mark(nc.vector.scalar_tensor_tensor(tau[:, :], tau[:, :], -1.0, rcount[:, :], ALU.add, ALU.mult))
            steps.wait()
            steps.mark(nc.vector.tensor_tensor(z[:, :, :], z[:, :, :], tau[:, :, None].broadcast_to([P, NB, E0]), ALU.subtract))
            steps.wait()
            steps.mark(nc.vector.tensor_scalar(z[:, :, :], z[:, :, :], 0.0, None, ALU.max))
            steps.wait()
            dve.wait_ge(side_used, NB)
            lowr = low[:, :, :].rearrange("p b (e r) -> p (b e) r", r=R0)
            gate = z[:, :, :].rearrange("p b e -> p (b e)")[:, :, None].broadcast_to([P, NB * E0, R0])
            nc.vector.tensor_tensor(lowr, lowr, gate, ALU.mult).then_inc(gate_ready, 1)
            dve.wait_ge(loaded, 48)
            for b in range(NB):
                steps.mark(nc.vector.tensor_tensor(x[:, b, :], x[:, b, :], b_base[:, :], ALU.add))
            for t in range(2):
                dve.wait_ge(tr_hi, t + 1)
                dst = gated[:, LO, 4 * t:4 * t + 4, :].rearrange("p b n -> p (b n)")
                hi = gated[:, HI, 4 * t:4 * t + 4, :].rearrange("p b n -> p (b n)")
                nc.vector.tensor_tensor(dst, p_tr[:, t, :], hi.bitcast(F32), ALU.subtract).then_inc(tr_lo, 1)
                steps.wait()
                for b in range(4 * t, 4 * t + 4):
                    dve.wait_ge(out_ready, b + 1)
                    nc.vector.tensor_tensor(x[:, b, :], p_out[:, b % 2, :], x[:, b, :], ALU.add).then_inc(out_used, 1)
            dve.wait_ge(out_used, NB)
    st.close()



DK = 64
PH = 8
DH = DK // PH
ROWS = 32
VC = 10


def norm_natural_stage(nc, name, x, h):
    st = Stage(nc, name)
    norm = Norm(st)
    own, done = st.sem("own"), st.sem("done")
    with nc.Block() as block:
        @block.gpsimd
        def _(pool):
            norm.set_half(nc)
            norm.rstd_on_gpsimd(nc, pool)

        @block.vector
        def _(dve):
            norm.stats_on_vector(nc, Steps(dve, own), x)
            dve.wait_ge(norm.rstd_ready, 1)
            for b in range(NB):
                norm.apply(nc, b, h[:, b, :], x).then_inc(done, 1)
            dve.wait_ge(done, NB)
    st.close()


def patch_attention_stage(nc, x, h, ident, ctx_in, mask_in, wqk_in, wv_in, wo_in, bqk_in, flag_in, bv_in, bo_in):
    st = Stage(nc, "a1")
    NP = D // P
    raw_w = st.sb("raw_w", [P, 4 * P + DK])
    w = st.sb("w", [P, 2, 4 * P + DK], F32R)
    raw_o = st.sb("raw_o", [DK, P])
    wo = st.sb("wo", [DK, 2, P], F32R)
    bqk = st.sb("bqk", [P, 4])
    flag = st.sb("flag", [P, 1])
    bv = st.sb("bv", [P, DK])
    bo = st.sb("bo", [P, 1])
    mask = st.sb("mask", [P, 2, D])
    keep = st.sb("keep", [P, D])
    gone = st.sb("gone", [P, D])
    hp = st.sb("hp", [P, 2, D], F32R)
    ctx = st.sb("ctx", [P, 2, D])
    cp = st.sb("cp", [P, 2, D], F32R)
    k32 = st.sb("k32", [P, 2, 2, D])
    qp = st.sb("qp", [P, 2, 2, 2, D], F32R)
    kd = st.sb("kd", [P, 2, 2, 2, 4, P], F32R)
    v32 = st.sb("v32", [P, NP, DK])
    vp = st.sb("vp", [P, 2, 2, NP, PH, VC], F32R)
    top = st.sb("top", [P, 2, PH])
    e = st.sb("e", [P, 2, PH, P])
    ep = st.sb("ep", [P, 2, 2, 4, P], F32R)
    rs = st.sb("rs", [P, PH])
    o32 = st.sb("o32", [P, 2, DK])
    o_all = st.sb("o_all", [DK, NB, D])
    gp = st.sb("gp", [DK, 2, 2, D], F32R)
    y = st.sb("y", [P, D])
    pj = st.ps("pj", [P, 2, BANK])
    psc = st.ps("psc", [P, 2, BANK])
    ptr = st.ps("ptr", [P, 2, BANK])
    pov = st.ps("pov", [P, BANK])
    pot = st.ps("pot", [P, BANK])
    names = ("w_loaded w_split own split_hi split pj_ready pj_used q_hi k_ready kd_hi kd_lo v_ready vp_hi vp_ready "
             "mask_ready sc_ready sc_used e_ready exp_done tr_ready tr_hi tr_used pv_ready o_ready o_seen ot_ready "
             "ot_copied g_ready g_hi g_lo y_ready y_used x_done zeros_set pool_own kd_part mask_seen").split()
    (w_loaded, w_split, own, split_hi, split, pj_ready, pj_used, q_hi, k_ready, kd_hi, kd_lo, v_ready, vp_hi, vp_ready,
     mask_ready, sc_ready, sc_used, e_ready, exp_done, tr_ready, tr_hi, tr_used, pv_ready, o_ready, o_seen, ot_ready,
     ot_copied, g_ready, g_hi, g_lo, y_ready, y_used, x_done, zeros_set, pool_own, kd_part, mask_seen) = (st.sem(n) for n in names)
    loaded = [st.sem("loaded0"), st.sem("loaded1")]
    mask_again = [st.sem("mask_again0"), st.sem("mask_again1")]
    INV = 1.0 / math.sqrt(DH)
    PJ = 5
    LAST = NB * NP - 1

    def wait(engine, sem, value):
        if not (isinstance(value, int) and value <= 0):
            engine.wait_ge(sem, value)

    def body(engine, patch):
        with engine.Fori(0, NB // 2 - 1) as g:
            for slot in range(2):
                for s in range(NP):
                    patch(g * 2 + slot, slot, s, True, True)
        for slot in range(2):
            for s in range(NP):
                patch(NB - 2 + slot, slot, s, slot == 0, False)

    def rows(i):
        return slice(ROWS * i, ROWS * (i + 1))

    def slots(slot, s, ahead):
        return (slot + (s + ahead) // NP) % 2, (s + ahead) % NP

    with nc.Block() as block:
        @block.sync
        def _(sp):
            sp.dma_start(raw_w[:, 0:4 * P], wqk_in).then_inc(w_loaded, 16)
            sp.dma_start(raw_w[:, 4 * P:], wv_in).then_inc(w_loaded, 16)
            sp.dma_start(raw_o[:, :], wo_in).then_inc(w_loaded, 16)
            with nc.allow_non_contiguous_dma(reason="a few columns"):
                sp.dma_start(bqk[:, :], bqk_in).then_inc(w_loaded, 16)
                sp.dma_start(flag[:, :], flag_in).then_inc(w_loaded, 16)
                sp.dma_start(bo[:, :], bo_in.rearrange("(p o) -> p o", o=1)).then_inc(w_loaded, 16)
            sp.dma_start(bv[:, :], bv_in.rearrange("(o n) -> o n", o=1).broadcast_to([P, DK])).then_inc(w_loaded, 16)

            def load_mask(b, slot, sem):
                sp.dma_start(mask[:, slot, :], mask_in[bass.ds(b, 1), :].broadcast_to([P, D])).then_inc(sem, 16)

            def load(b, slot):
                load_mask(b, slot, loaded[slot])
                sp.dma_start(ctx[:, slot, :], ctx_in[bass.ds(b, 1), :, :].rearrange("o p n -> p (o n)")
                             ).then_inc(loaded[slot], 16)

            load(0, 0)
            load(1, 1)
            with sp.Fori(0, NB // 2 - 1) as g:
                for slot in range(2):
                    sp.wait_ge(split, g * 4 + (2 * slot + 2))
                    sp.wait_ge(mask_ready, g * 2 + (slot + 1))
                    load(g * 2 + (slot + 2), slot)
            for b in range(NB):
                sp.wait_ge(mask_ready, NB)
                if b >= 2:
                    sp.wait_ge(y_used, b - 1)
                load_mask(b, b % 2, mask_again[b % 2])

        @block.gpsimd
        def _(pool):
            nc.gpsimd.memset(kd[:, :, :, :, :, :].bitcast(F32), 0.0).then_inc(zeros_set, 1)
            nc.gpsimd.memset(vp[:, :, HI, :, :, DH:VC].bitcast(F32), 1.0).then_inc(zeros_set, 1)
            nc.gpsimd.memset(vp[:, :, LO, :, :, DH:VC].bitcast(F32), 0.0).then_inc(zeros_set, 1)

            def masks(b, slot, turn):
                pool.wait_ge(loaded[slot], turn * 32)
                wait(pool, k_ready, b)
                pool.sem_inc(mask_seen, 1)
                steps = Steps(pool, pool_own, b * 2)
                steps.mark(nc.gpsimd.tensor_scalar(keep[:, :], mask[:, slot, :], 0.0, 1.0, ALU.is_gt, ALU.mult))
                steps.wait()
                pool.sem_inc(mask_seen, 1)
                steps.mark(nc.gpsimd.tensor_scalar(gone[:, :], keep[:, :], 0.0, NEG, ALU.is_equal, ALU.mult))
                steps.wait()
                nc.gpsimd.tensor_tensor(gone[:, :], gone[:, :], flag[:, 0:1].broadcast_to([P, D]),
                                        ALU.mult).then_inc(mask_ready, 1)

            def keys_lo(n, pslot, bslot, s):
                pool.wait_ge(kd_hi, n + 1)
                for i in range(4):
                    nc.gpsimd.tensor_tensor(
                        kd[rows(i), pslot, LO, :, i, :], k32[rows(i), bslot, :, s * P:(s + 1) * P],
                        kd[rows(i), pslot, HI, :, i, :].bitcast(F32), ALU.subtract).then_inc(kd_part, 1)
                    pool.wait_ge(kd_part, n * 4 + (i + 1))
                pool.sem_inc(kd_lo, 1)

            def values_lo(b, slot):
                pool.wait_ge(vp_hi, b + 1)
                nc.gpsimd.tensor_tensor(
                    vp[:, slot, LO, :, :, 0:DH].rearrange("p s h d -> p (s h) d"),
                    v32[:, :, :].rearrange("p s (h d) -> p (s h) d", d=DH),
                    vp[:, slot, HI, :, :, 0:DH].rearrange("p s h d -> p (s h) d").bitcast(F32),
                    ALU.subtract).then_inc(vp_ready, 1)

            pool.wait_ge(w_loaded, 7 * 16)
            masks(0, 0, 1)
            keys_lo(0, 0, 0, 0)
            keys_lo(1, 1, 0, 1)
            values_lo(0, 0)
            keys_lo(2, 0, 0, 2)
            masks(1, 1, 1)

            def patch(b, slot, s, has1):
                if has1 or s + 3 < NP:
                    bslot, ahead = slots(slot, s, 3)
                    keys_lo(b * NP + (s + 3), (s + 1) % 2, bslot, ahead)
                if s == 2 and has1:
                    values_lo(b + 1, 1 - slot)

            with pool.Fori(0, NB // 2 - 1) as g:
                for slot in range(2):
                    for s in range(NP):
                        patch(g * 2 + slot, slot, s, True)
                    masks(g * 2 + (slot + 2), slot, g + 2)
            for slot in range(2):
                for s in range(NP):
                    patch(NB - 2 + slot, slot, s, slot == 0)

        @block.tensor
        def _(pe):
            def project(b, slot, tiles):
                for i in tiles:
                    if i == 0:
                        pe.wait_ge(split, b * 2 + 2)
                    wait(pe, pj_used, b * PJ + (i - 1 if i else 0))
                    if i < 4:
                        t = (i + 2) % 4
                        mm3(nc, pj[:, i % 2, :], lambda p: w[:, p, t * P:(t + 1) * P], lambda p: hp[:, p, :]
                            ).then_inc(pj_ready, 1)
                        continue
                    for s in range(NP):
                        ins = mm3(nc, pj[:, 0, s * DK:(s + 1) * DK], lambda p: cp[:, p, s * P:(s + 1) * P],
                                  lambda p: w[:, p, 4 * P:])
                    ins.then_inc(pj_ready, 1)

            def scores(n, pslot, bslot, s):
                pe.wait_ge(kd_lo, n + 1)
                for t in range(2):
                    wait(pe, sc_used, n * 2 + (t - 1))
                    mm3(nc, psc[:, t, :], lambda p: qp[:, bslot, p, t, s * P:(s + 1) * P],
                        lambda p: kd[:, pslot, p, t, :, :].rearrange("p i j -> p (i j)")).then_inc(sc_ready, 1)

            def transposes(n, pslot):
                pe.wait_ge(exp_done, n + 1)
                for t in range(2):
                    pe.wait_ge(tr_used, n * 2 + (t + 1))
                    for i in range(4):
                        ins = nc.tensor.transpose(ptr[:, t, i * P:(i + 1) * P], e[:, pslot, 4 * t + i, :], ident[:, :])
                    ins.then_inc(tr_ready, 1)

            def patch(b, slot, s, has1, has2):
                n = b * NP + s
                if has1 or s + 2 < NP:
                    bslot, ahead = slots(slot, s, 2)
                    if ahead == 0:
                        pe.wait_ge(pj_used, b * PJ + (PJ + 4))
                    scores(n + 2, s % 2, bslot, ahead)
                if s == 0:
                    pe.wait_ge(vp_ready, b + 1)
                pe.wait_ge(o_ready, n + 1)
                for t in range(2):
                    pe.wait_ge(tr_used, n * 2 + (t + 3))
                    for i in range(4):
                        head = 4 * t + i
                        ins = mm3(nc, pov[:, head * VC:(head + 1) * VC], lambda p: ep[:, p, t, i, :],
                                  lambda p: vp[:, slot, p, s, head, :])
                ins.then_inc(pv_ready, 1)
                if has1 and s < 3:
                    project(b + 1, 1 - slot, ((0, 1), (2, 3), (4,))[s])
                if has1 or s + 1 < NP:
                    transposes(n + 1, (s + 1) % 2)
                if s == 0:
                    pe.wait_ge(ot_copied, b + 1)
                pe.wait_ge(o_ready, n + 2)
                pe.sem_inc(o_seen, 1)
                ins = nc.tensor.transpose(pot[0:DK, s * P:(s + 1) * P], o32[:, s % 2, :], ident[:, :])
                if s == NP - 1:
                    ins.then_inc(ot_ready, 1)

            pe.wait_ge(w_split, 2)
            pe.wait_ge(zeros_set, 3)
            project(0, 0, range(PJ))
            pe.wait_ge(pj_used, 4)
            scores(0, 0, 0, 0)
            scores(1, 1, 0, 1)
            transposes(0, 0)
            body(pe, patch)
            for b in range(NB):
                pe.wait_ge(g_lo, b + 1)
                if b >= 2:
                    pe.wait_ge(y_used, b - 1)
                mm3(nc, pj[:, b % 2, :], lambda p: wo[:, p, :], lambda p: gp[:, b % 2, p, :]).then_inc(y_ready, 1)

        @block.scalar
        def _(act):
            def split_his(b, slot):
                wait(act, pj_ready, b * PJ)
                nc.scalar.activation(hp[:, HI, :], h[:, bass.ds(b, 1), :].rearrange("p o n -> p (o n)"),
                                     ACT.Copy).then_inc(split_hi, 1)
                nc.scalar.activation(cp[:, HI, :], ctx[:, slot, :], ACT.Copy).then_inc(split_hi, 1)

            def queries_hi(b, slot):
                for t in range(2):
                    act.wait_ge(pj_ready, b * PJ + (t + 3))
                    nc.scalar.activation(qp[:, slot, HI, t, :], pj[:, t, :], ACT.Identity, bias=bqk[:, t:t + 1]).then_inc(q_hi, 1)

            def keys_hi(n, pslot, bslot, s, b):
                act.wait_ge(k_ready, b + 1)
                wait(act, sc_ready, n * 2 - 2)
                for i in range(4):
                    ins = nc.scalar.activation(kd[rows(i), pslot, HI, :, i, :], k32[rows(i), bslot, :, s * P:(s + 1) * P],
                                               ACT.Copy)
                ins.then_inc(kd_hi, 1)

            def values_hi(b, slot):
                act.wait_ge(v_ready, b + 1)
                nc.scalar.activation(vp[:, slot, HI, :, :, 0:DH].rearrange("p s h d -> p (s h) d"),
                                     v32[:, :, :].rearrange("p s (h d) -> p (s h) d", d=DH), ACT.Copy).then_inc(vp_hi, 1)

            def exp(n, pslot):
                act.wait_ge(e_ready, n + 1)
                sl = e[:, pslot, :, :].rearrange("p h j -> p (h j)")
                nc.scalar.activation(sl, sl, ACT.Exp, scale=INV).then_inc(exp_done, 1)

            def weights_hi(n):
                for t in range(2):
                    act.wait_ge(tr_ready, n * 2 + (t + 1))
                    nc.scalar.activation(ep[:, HI, t, :, :].rearrange("p i j -> p (i j)"), ptr[:, t, :], ACT.Copy).then_inc(tr_hi, 1)

            def patch(b, slot, s, has1, has2):
                n = b * NP + s
                if has1 or s + 3 < NP:
                    bslot, ahead = slots(slot, s, 3)
                    keys_hi(n + 3, (s + 1) % 2, bslot, ahead, b + (s + 3) // NP)
                if has1 or s + 2 < NP:
                    exp(n + 2, s % 2)
                if has1 and s == 1:
                    queries_hi(b + 1, 1 - slot)
                if has1 and s == 2:
                    values_hi(b + 1, 1 - slot)
                if has1 or s + 1 < NP:
                    weights_hi(n + 1)
                if s == 3:
                    if has2:
                        act.wait_ge(loaded[slot], load_turn[0] * 32)
                        split_his(b + 2, slot)
                    act.wait_ge(ot_ready, b + 1)
                    nc.scalar.activation(o_all[:, bass.ds(b, 1), :].rearrange("p o n -> p (o n)"), pot[0:DK, :],
                                         ACT.Copy).then_inc(ot_copied, 1)

            load_turn = [1]
            act.wait_ge(zeros_set, 3)
            act.wait_ge(loaded[0], 32)
            split_his(0, 0)
            act.wait_ge(w_split, 2)
            keys_hi(0, 0, 0, 0, 0)
            keys_hi(1, 1, 0, 1, 0)
            queries_hi(0, 0)
            values_hi(0, 0)
            exp(0, 0)
            keys_hi(2, 0, 0, 2, 0)
            exp(1, 1)
            weights_hi(0)
            act.wait_ge(loaded[1], 32)
            split_his(1, 1)
            with act.Fori(0, NB // 2 - 1) as g:
                load_turn[0] = g + 2
                for slot in range(2):
                    for s in range(NP):
                        patch(g * 2 + slot, slot, s, True, True)
            for slot in range(2):
                for s in range(NP):
                    patch(NB - 2 + slot, slot, s, slot == 0, False)
            act.wait_ge(ot_copied, NB + 1)
            for b in range(NB):
                nc.scalar.activation(o_all[:, b, :], o_all[:, b, :], ACT.Gelu).then_inc(g_ready, 1)
                if b >= 2:
                    act.wait_ge(y_ready, b - 1)
                act.wait_ge(g_ready, b + 1)
                nc.scalar.activation(gp[:, b % 2, HI, :], o_all[:, b, :], ACT.Copy).then_inc(g_hi, 1)

        @block.vector
        def _(dve):
            dve.sem_inc(tr_used, 2)
            dve.sem_inc(o_ready, 1)
            dve.sem_inc(ot_copied, 1)
            steps = Steps(dve, own)
            dve.wait_ge(w_loaded, 7 * 16)
            steps.mark(nc.vector.tensor_copy(w[:, HI, :], raw_w[:, :]))
            steps.mark(nc.vector.tensor_copy(wo[:, HI, :], raw_o[:, :]))
            steps.mark(nc.vector.tensor_scalar(bqk[:, 0:2], bqk[:, 0:2], flag[:, 0:1], None, ALU.add))
            steps.wait()
            nc.vector.tensor_tensor(w[:, LO, :], raw_w[:, :], w[:, HI, :].bitcast(F32), ALU.subtract).then_inc(w_split, 1)
            nc.vector.tensor_tensor(wo[:, LO, :], raw_o[:, :], wo[:, HI, :].bitcast(F32), ALU.subtract).then_inc(w_split, 1)

            def split_los(b, slot):
                for i, (dst, src) in enumerate(((hp, h[:, bass.ds(b, 1), :].rearrange("p o n -> p (o n)")), (cp, ctx[:, slot, :]))):
                    dve.wait_ge(split_hi, b * 2 + (i + 1))
                    nc.vector.tensor_tensor(dst[:, LO, :], src, dst[:, HI, :].bitcast(F32), ALU.subtract).then_inc(split, 1)

            def keys(b, slot, steps):
                dve.wait_ge(mask_ready, b + 1)
                wait(dve, kd_lo, b * NP - NP)
                for t in range(2):
                    dve.wait_ge(pj_ready, b * PJ + (t + 1))
                    ins = nc.vector.scalar_tensor_tensor(k32[:, slot, t, :], pj[:, t, :], bqk[:, 2 + t:3 + t], keep[:, :],
                                                         ALU.add, ALU.mult)
                    ins.then_inc(pj_used, 1)
                dve.wait_ge(pj_used, b * PJ + 2)
                nc.vector.tensor_tensor(k32[:, slot, :, :], k32[:, slot, :, :], gone[:, None, :].broadcast_to([P, 2, D]),
                                        ALU.add).then_inc(k_ready, 1)

            def queries_lo(b, slot):
                for t in range(2):
                    dve.wait_ge(q_hi, b * 2 + (t + 1))
                    nc.vector.scalar_tensor_tensor(qp[:, slot, LO, t, :], pj[:, t, :], bqk[:, t:t + 1],
                                                   qp[:, slot, HI, t, :].bitcast(F32), ALU.add, ALU.subtract).then_inc(pj_used, 1)

            def values(b):
                dve.wait_ge(pj_ready, b * PJ + 5)
                wait(dve, vp_ready, b)
                vt = pj[:, 0, 0:NP * DK].rearrange("p (s n) -> p s n", n=DK)
                nc.vector.tensor_tensor(v32[:, :, :], vt, bv[:, None, :].broadcast_to([P, NP, DK]), ALU.add).then_inc(v_ready, 1)
                dve.wait_ge(v_ready, b + 1)
                dve.sem_inc(pj_used, 1)

            def shifted(n, pslot, steps):
                for t in range(2):
                    dve.wait_ge(sc_ready, n * 2 + (t + 1))
                    ins = nc.vector.reduce_max(top[:, pslot, 4 * t:4 * t + 4],
                                               psc[:, t, :].rearrange("p (i j) -> p i j", j=P), AX.X)
                steps.mark(ins)
                steps.wait()
                for t in range(2):
                    nc.vector.tensor_tensor(e[:, pslot, 4 * t:4 * t + 4, :],
                                            psc[:, t, :].rearrange("p (i j) -> p i j", j=P),
                                            top[:, pslot, 4 * t:4 * t + 4, None].broadcast_to([P, 4, P]),
                                            ALU.subtract).then_inc(sc_used, 1)
                dve.wait_ge(sc_used, n * 2 + 2)
                dve.sem_inc(e_ready, 1)

            def weights_lo(n):
                for t in range(2):
                    dve.wait_ge(tr_hi, n * 2 + (t + 1))
                    nc.vector.tensor_tensor(ep[:, LO, t, :, :].rearrange("p i j -> p (i j)"), ptr[:, t, :],
                                            ep[:, HI, t, :, :].rearrange("p i j -> p (i j)").bitcast(F32),
                                            ALU.subtract).then_inc(tr_used, 1)

            split_los(0, 0)
            keys(0, 0, steps)
            queries_lo(0, 0)
            values(0)
            shifted(0, 0, steps)
            shifted(1, 1, steps)
            weights_lo(0)
            split_los(1, 1)
            first = steps.n
            PER = 2 * NP

            def patch(b, slot, s, has1, has2):
                n = b * NP + s
                steps = Steps(dve, own, b * PER + (first + 2 * s - (1 if not has1 and s == NP - 1 else 0)))
                if has1 or s + 2 < NP:
                    shifted(n + 2, s % 2, steps)
                dve.wait_ge(pv_ready, n + 1)
                ov = pov[:, 0:PH * VC].rearrange("p (h c) -> p h c", c=VC)
                steps.mark(nc.vector.reciprocal(rs[:, :], ov[:, :, DH]))
                steps.wait()
                nc.vector.tensor_tensor(o32[:, s % 2, :].rearrange("p (h d) -> p h d", d=DH), ov[:, :, 0:DH],
                                        rs[:, :, None].broadcast_to([P, PH, DH]), ALU.mult).then_inc(o_ready, 1)
                if has1 and s == 0:
                    keys(b + 1, 1 - slot, steps)
                if has1 and s == 1:
                    queries_lo(b + 1, 1 - slot)
                if has1 and s == 2:
                    values(b + 1)
                if has1 or s + 1 < NP:
                    weights_lo(n + 1)
                if has2 and s == 3:
                    split_los(b + 2, slot)

            body(dve, patch)
            for b in range(NB):
                dve.wait_ge(g_hi, b + 1)
                nc.vector.tensor_tensor(gp[:, b % 2, LO, :], o_all[:, b, :], gp[:, b % 2, HI, :].bitcast(F32),
                                        ALU.subtract).then_inc(g_lo, 1)
                dve.wait_ge(y_ready, b + 1)
                dve.wait_ge(mask_again[b % 2], (b // 2 + 1) * 16)
                if b > 0:
                    dve.wait_ge(x_done, b)
                nc.vector.scalar_tensor_tensor(y[:, :], pj[:, b % 2, :], bo[:, 0:1], mask[:, b % 2, :],
                                               ALU.add, ALU.mult).then_inc(y_used, 1)
                dve.wait_ge(y_used, b + 1)
                nc.vector.tensor_tensor(x[:, b, :], x[:, b, :], y[:, :], ALU.add).then_inc(x_done, 1)
            dve.wait_ge(x_done, NB)
    st.close()



ROUND = 1.5 * 2.0 ** 23


def ffn1_stage(nc, x, h, ident_bf, weight_in, scales_in, bias_in):
    st = Stage(nc, "f1")
    words = st.sb("words", [P, DC, D // 4], I32)
    w = st.sb("w", [P, DC, D], BF16)
    ws = st.sb("ws", [P, D], F16)
    bias = st.sb("bias", [P, D], F16)
    top = st.sb("top", [P, NB])
    scale = st.sb("scale", [P, NB])
    inv = st.sb("inv", [P, NB])
    step = st.sb("step", [P, 2, D])
    q = st.sb("q", [P, NB, D], BF16)
    qt = st.sb("qt", [P, 2, DC, P], BF16)
    y32 = st.sb("y32", [P, 2, D])
    y16 = st.sb("y16", [P, 2, D], F16)
    tp = st.ps("tp", [P, 2, 2 * BANK], BF16)
    acc = st.ps("acc", [P, 2, BANK])
    (loaded, w_ready, own, q_ready, tp_ready, qt_ready, acc_ready, y_ready, x_done) = (st.sem(n) for n in (
        "loaded", "w_ready", "own", "q_ready", "tp_ready", "qt_ready", "acc_ready", "y_ready", "x_done"))
    with nc.Block() as block:
        @block.sync
        def _(sp):
            sp.dma_start(words[:, :, :], weight_in.rearrange("(c p) n -> p c n", p=P)).then_inc(loaded, 16)
            sp.dma_start(ws[:, :], scales_in.rearrange("(o n) -> o n", o=1).broadcast_to([P, D])).then_inc(loaded, 16)
            sp.dma_start(bias[:, :], bias_in.broadcast_to([P, D])).then_inc(loaded, 16)

        @block.scalar
        def _(act):
            act.wait_ge(loaded, 48)
            nc.scalar.activation(w[:, :, :], words[:, :, :].bitcast(I8), ACT.Copy).then_inc(w_ready, 1)
            for b in range(NB):
                act.wait_ge(tp_ready, b + 1)
                if b >= 2:
                    act.wait_ge(acc_ready, b - 1)
                nc.scalar.activation(qt[:, b % 2, :, :].rearrange("p c t -> p (c t)"), tp[:, b % 2, 0:D],
                                     ACT.Copy).then_inc(qt_ready, 1)

        @block.tensor
        def _(pe):
            def transposes(b):
                pe.wait_ge(q_ready, b + 1)
                if b >= 2:
                    pe.wait_ge(qt_ready, b - 1)
                for c in range(DC):
                    ins = nc.tensor.transpose(tp[:, b % 2, c * P:(c + 1) * P], q[:, b, c * P:(c + 1) * P], ident_bf[:, :])
                ins.then_inc(tp_ready, 1)

            transposes(0)
            pe.wait_ge(w_ready, 1)
            for b in range(NB):
                if b + 1 < NB:
                    transposes(b + 1)
                pe.wait_ge(qt_ready, b + 1)
                if b >= 2:
                    pe.wait_ge(y_ready, b - 1)
                for c in range(DC):
                    ins = nc.tensor.matmul(acc[:, b % 2, :], qt[:, b % 2, c, :], w[:, c, :], start=c == 0, stop=c == DC - 1)
                ins.then_inc(acc_ready, 1)

        @block.vector
        def _(dve):
            steps = Steps(dve, own)
            for b in range(NB):
                steps.mark(nc.vector.tensor_reduce(top[:, b:b + 1], h[:, b, :], AX.X, ALU.max, apply_absolute_value=True))
            steps.wait()
            steps.mark(nc.vector.tensor_scalar(scale[:, :], top[:, :], 1.0 / 127.0, 1e-37, ALU.mult, ALU.max))
            steps.wait()
            steps.mark(nc.vector.reciprocal(inv[:, :], scale[:, :]))
            steps.wait()
            for b in range(NB):
                steps.mark(nc.vector.tensor_scalar(step[:, b % 2, :], h[:, b, :], inv[:, b:b + 1], ROUND, ALU.mult, ALU.add))
                steps.wait()
                steps.mark(nc.vector.tensor_scalar(step[:, b % 2, :], step[:, b % 2, :], ROUND, 127.0, ALU.subtract, ALU.min))
                steps.wait()
                nc.vector.tensor_scalar(q[:, b, :], step[:, b % 2, :], -128.0, None, ALU.max).then_inc(q_ready, 1)
            dve.wait_ge(loaded, 48)
            for b in range(NB):
                dve.wait_ge(acc_ready, b + 1)
                nc.vector.tensor_tensor(y32[:, b % 2, :], acc[:, b % 2, :], ws[:, :], ALU.mult).then_inc(y_ready, 1)
                dve.wait_ge(y_ready, b + 1)
                steps.mark(nc.vector.tensor_scalar(y16[:, b % 2, :], y32[:, b % 2, :], scale[:, b:b + 1], None, ALU.mult))
                steps.wait()
                steps.mark(nc.vector.tensor_tensor(y16[:, b % 2, :], y16[:, b % 2, :], bias[:, :], ALU.add))
                steps.wait()
                nc.vector.tensor_tensor(x[:, b, :], x[:, b, :], y16[:, b % 2, :], ALU.add).then_inc(x_done, 1)
            dve.wait_ge(x_done, NB)
    st.close()



NF4_PIECES = 3 * NH2 * D // (P * NF4_COLS)


def nf4_stage(nc, flat_in, rounded):
    st = Stage(nc, "nf4")
    blocks = NF4_COLS // NF4_BLOCK
    code = np.array(NF4_CODE, np.float32)
    bounds = ((code[:-1] + code[1:]) * np.float32(0.5)).astype(np.float32)
    above = np.nextafter(bounds, np.float32(np.inf))
    BIG = 2.0 ** 60
    zero = NF4_CODE.index(0.0)
    negative = [(float(above[i]), float(code[i])) for i in range(zero)]
    positive = [(float(bounds[i]), float(code[i + 1])) for i in range(zero, len(bounds))]
    terms = negative + positive
    w = st.sb("w", [P, 2, NF4_COLS])
    top = st.sb("top", [P, blocks])
    empty = st.sb("empty", [P, blocks])
    inv = st.sb("inv", [P, blocks])
    v = st.sb("v", [P, NF4_COLS])
    t = st.sb("t", [P, 4, NF4_COLS])
    acc = st.sb("acc", [P, 2, 2, NF4_COLS])
    res = st.sb("res", [P, 2, NF4_COLS])
    shifts = st.sb("shifts", [P, len(terms)])
    loaded = [st.sem("loaded0"), st.sem("loaded1")]
    stored = [st.sem("stored0"), st.sem("stored1")]
    own, v_ready, t_ready, t_used, done, shifts_set = (
        st.sem(n) for n in ("own", "v_ready", "t_ready", "t_used", "done", "shifts_set"))
    NT_ = len(terms)
    with nc.Block() as block:
        @block.sync
        def _(sp):
            def load(n, slot):
                sp.dma_start(w[:, slot, :], flat_in[bass.ds(n, 1), :, :].rearrange("o p n -> p (o n)")
                             ).then_inc(loaded[slot], 16)

            def store(n, slot):
                sp.dma_start(rounded[bass.ds(n, 1), :, :].rearrange("o p n -> p (o n)"), res[:, slot, :]
                             ).then_inc(stored[slot], 16)

            load(0, 0)
            load(1, 1)
            with sp.Fori(0, NF4_PIECES // 2 - 1) as g:
                for slot in range(2):
                    sp.wait_ge(done, g * 2 + (slot + 1))
                    store(g * 2 + slot, slot)
                    load(g * 2 + (slot + 2), slot)
            for slot in range(2):
                sp.wait_ge(done, NF4_PIECES - 1 + slot)
                store(NF4_PIECES - 2 + slot, slot)
            for slot in range(2):
                sp.wait_ge(stored[slot], NF4_PIECES // 2 * 16)

        @block.gpsimd
        def _(pool):
            for i, (bound, _) in enumerate(terms):
                nc.gpsimd.memset(shifts[:, i:i + 1], -bound * BIG).then_inc(shifts_set, 1)

        @block.scalar
        def _(act):
            act.wait_ge(shifts_set, NT_)
            with act.Fori(0, NF4_PIECES) as n:
                act.wait_ge(v_ready, n + 1)
                for i in range(NT_):
                    act.wait_ge(t_used, n * NT_ + (i + (2 if i < NT_ % 4 else 1)))
                    nc.scalar.activation(t[:, i % 4, :], v[:, :], ACT.Identity, bias=shifts[:, i:i + 1], scale=BIG
                                         ).then_inc(t_ready, 1)

        @block.vector
        def _(dve):
            dve.sem_inc(t_used, 4)

            def piece(n, slot, turn, wait_store, after_first=True):
                steps = Steps(dve, own, n * 5)
                wb = w[:, slot, :].rearrange("p (b i) -> p b i", i=NF4_BLOCK)
                vb = v[:, :].rearrange("p (b i) -> p b i", i=NF4_BLOCK)
                dve.wait_ge(loaded[slot], turn * 16)
                if after_first:
                    dve.wait_ge(done, n)
                steps.mark(nc.vector.tensor_reduce(top[:, :], wb, AX.X, ALU.max, apply_absolute_value=True))
                steps.wait()
                steps.mark(nc.vector.tensor_scalar(empty[:, :], top[:, :], 0.0, None, ALU.is_equal))
                steps.wait()
                steps.mark(nc.vector.tensor_tensor(empty[:, :], empty[:, :], top[:, :], ALU.add))
                steps.wait()
                steps.mark(nc.vector.reciprocal(inv[:, :], empty[:, :]))
                steps.wait()
                nc.vector.tensor_tensor(vb, wb, inv[:, :, None].broadcast_to([P, blocks, NF4_BLOCK]),
                                        ALU.mult).then_inc(v_ready, 1)
                for i, (_, c) in enumerate(terms):
                    below = i < zero
                    acc_i, prev = acc[:, 0 if below else 1, i % 2, :], acc[:, 0 if below else 1, (i + 1) % 2, :]
                    dve.wait_ge(t_ready, n * NT_ + (i + 1))
                    if i in (0, zero):
                        ins = nc.vector.tensor_scalar(acc_i, t[:, i % 4, :], c, 0.0, ALU.max if below else ALU.min,
                                                      ALU.min if below else ALU.max)
                    else:
                        dve.wait_ge(t_used, n * NT_ + (i + 4))
                        ins = nc.vector.scalar_tensor_tensor(acc_i, t[:, i % 4, :], c, prev,
                                                             ALU.max if below else ALU.min, ALU.min if below else ALU.max)
                    ins.then_inc(t_used, 1)
                dve.wait_ge(t_used, n * NT_ + (NT_ + 4))
                steps.mark(nc.vector.tensor_tensor(v[:, :], acc[:, 0, (zero - 1) % 2, :], acc[:, 1, (NT_ - 1) % 2, :], ALU.add))
                steps.wait()
                if wait_store is not None:
                    dve.wait_ge(stored[slot], wait_store)
                nc.vector.tensor_tensor(res[:, slot, :].rearrange("p (b i) -> p b i", i=NF4_BLOCK), vb,
                                        top[:, :, None].broadcast_to([P, blocks, NF4_BLOCK]), ALU.mult).then_inc(done, 1)

            piece(0, 0, 1, None, after_first=False)
            piece(1, 1, 1, None)
            with dve.Fori(1, NF4_PIECES // 2) as g:
                for slot in range(2):
                    piece(g * 2 + slot, slot, g + 1, g * 16)
    st.close()


def ffn2_stage(nc, x, ident, h_t, rounded):
    st = Stage(nc, "f2")
    w1, w2 = (rounded[i * NH2:(i + 1) * NH2, :] for i in range(2))
    w3 = rounded[2 * NH2:3 * NH2, :].rearrange("r c -> (r c)").rearrange("(d h) -> d h", h=NH2)
    REST = NH2 - (HC2 - 1) * P
    rows = st.sb("rows", [P, 2, 2, D])
    cols = st.sb("cols", [P, 2, DC, P])
    wt = st.sb("wt", [P, 2, 2, DC, P], F32R)
    w3t = st.sb("w3t", [P, 2, 2, D], F32R)
    gate = st.sb("gate", [P, 2, BANK])
    a32 = st.sb("a32", [P, 2, BANK])
    a = st.sb("a", [P, 2, 2, NT], F32R)
    ptr = st.ps("ptr", [P, 2, BANK])
    pg = st.ps("pg", [P, 2, BANK])
    pd = st.ps("pd", [P, 2, BANK])
    loaded = [st.sem("loaded0"), st.sem("loaded1")]
    (tr_ready, tr_hi, tr_used, g_ready, silu_done, a_done, g_used, a_hi, a_lo, d_ready, d_used, own) = (
        st.sem(n) for n in ("tr_ready", "tr_hi", "tr_used", "g_ready", "silu_done", "a_done", "g_used",
                            "a_hi", "a_lo", "d_ready", "d_used", "own"))
    turns = [(n, min(n * P, NH2 - P)) for n in range(HC2)]
    with nc.Block() as block:
        @block.sync
        def _(sp):
            def load(start, slot):
                sp.dma_start(rows[:, slot, 0, :], w1[bass.ds(start, P), :]).then_inc(loaded[slot], 16)
                sp.dma_start(rows[:, slot, 1, :], w2[bass.ds(start, P), :]).then_inc(loaded[slot], 16)
                sp.dma_start(cols[:, slot, :, :], w3[:, bass.ds(start, P)].rearrange("(c p) h -> p c h", p=P)
                             ).then_inc(loaded[slot], 16)

            load(0, 0)
            load(P, 1)
            for n, start in turns[2:]:
                sp.wait_ge(tr_ready, 3 * (n - 1))
                load(start, n % 2)

        @block.tensor
        def _(pe):
            def down(n):
                pe.wait_ge(a_lo, 2 * (n + 1))
                for b in range(NB):
                    k = n * NB + b
                    if k >= 2:
                        pe.wait_ge(d_used, k - 1)
                    ins = mm3(nc, pd[:, b % 2, :], lambda p: a[:, n % 2, p, b * P:(b + 1) * P],
                              lambda p: w3t[:, n % 2, p, :])
                    ins.then_inc(d_ready, 1)

            for n, start in turns:
                pe.wait_ge(loaded[n % 2], (n // 2 + 1) * 48)
                for which in range(3):
                    k = 3 * n + which
                    if k >= 2:
                        pe.wait_ge(tr_used, k - 1)
                    for c in range(DC):
                        src = rows[:, n % 2, which, c * P:(c + 1) * P] if which < 2 else cols[:, n % 2, c, :]
                        ins = nc.tensor.transpose(ptr[:, k % 2, c * P:(c + 1) * P], src, ident[:, :])
                    ins.then_inc(tr_ready, 1)
                if n > 0:
                    down(n - 1)
                for half in range(2):
                    k = 2 * n + half
                    if k >= 1:
                        pe.wait_ge(g_used, k)
                    pe.wait_ge(tr_used, 3 * n + 2)
                    for which in range(2):
                        for c in range(DC):
                            ins = mm3(nc, pg[:, which, :], lambda p: wt[:, which, p, c, :],
                                      lambda p: h_t[:, p, c, half * BANK:(half + 1) * BANK], c == 0, c == DC - 1)
                    ins.then_inc(g_ready, 1)
            down(HC2 - 1)

        def tr_dst(n, which, part):
            if which < 2:
                return wt[:, which, part, :, :].rearrange("p c h -> p (c h)")
            return w3t[:, n % 2, part, :]

        @block.scalar
        def _(act):
            for n, start in turns:
                for which in range(3):
                    k = 3 * n + which
                    act.wait_ge(tr_ready, k + 1)
                    if which < 2 and n > 0:
                        act.wait_ge(g_ready, 2 * n)
                    if which == 2 and n >= 2:
                        act.wait_ge(d_ready, NB * (n - 1))
                    nc.scalar.activation(tr_dst(n, which, HI), ptr[:, k % 2, :], ACT.Copy).then_inc(tr_hi, 1)
                for half in range(2):
                    k = 2 * n + half
                    act.wait_ge(g_ready, k + 1)
                    if k >= 2:
                        act.wait_ge(a_done, k - 1)
                    nc.scalar.activation(gate[:, half, :], pg[:, 0, :], ACT.Silu).then_inc(silu_done, 1)
                    act.wait_ge(a_done, k + 1)
                    if n >= 2:
                        act.wait_ge(d_ready, NB * (n - 1))
                    nc.scalar.activation(a[:, n % 2, HI, half * BANK:(half + 1) * BANK], a32[:, half, :],
                                         ACT.Copy).then_inc(a_hi, 1)

        @block.vector
        def _(dve):
            def down(n):
                for b in range(NB):
                    k = n * NB + b
                    dve.wait_ge(d_ready, k + 1)
                    if k >= NB:
                        dve.wait_ge(d_used, k - NB + 1)
                    nc.vector.tensor_tensor(x[:, b, :], pd[:, b % 2, :], x[:, b, :], ALU.add).then_inc(d_used, 1)

            for n, start in turns:
                for which in range(3):
                    k = 3 * n + which
                    dve.wait_ge(tr_hi, k + 1)
                    ins = nc.vector.tensor_tensor(tr_dst(n, which, LO), ptr[:, k % 2, :],
                                                  tr_dst(n, which, HI).bitcast(F32), ALU.subtract)
                    if which == 2 and n == HC2 - 1:
                        for part in (HI, LO):
                            ins.then_inc(own, 1)
                            dve.wait_ge(own, part + 1)
                            ins = nc.vector.memset(w3t[0:P - REST, n % 2, part, :].bitcast(F32), 0.0)
                    ins.then_inc(tr_used, 1)
                if n > 0:
                    down(n - 1)
                for half in range(2):
                    k = 2 * n + half
                    dve.wait_ge(silu_done, k + 1)
                    if n > 0:
                        dve.wait_ge(a_lo, k - 1)
                    nc.vector.tensor_tensor(a32[:, half, :], pg[:, 1, :], gate[:, half, :], ALU.mult).then_inc(a_done, 1)
                    dve.wait_ge(a_done, k + 1)
                    dve.sem_inc(g_used, 1)
                    dve.wait_ge(a_hi, k + 1)
                    cols_ = slice(half * BANK, (half + 1) * BANK)
                    nc.vector.tensor_tensor(a[:, n % 2, LO, cols_], a32[:, half, :], a[:, n % 2, HI, cols_].bitcast(F32),
                                            ALU.subtract).then_inc(a_lo, 1)
            down(HC2 - 1)
            dve.wait_ge(d_used, NB * HC2)
    st.close()



E3, R3, RD3 = 64, 8, 16
TAKEN = -3.0e38


def ffn3_stage(nc, x, ident, h_t, a_in, b_in, router_in, keys_in):
    st = Stage(nc, "f3")
    raw = st.sb("raw", [P, 2, DC, D])
    wa = st.sb("wa", [P, 2, DC, D], F32R)
    wb = st.sb("wb", [P, 2, DC, D], F32R)
    raw_r = st.sb("raw_r", [P, DC, RD3])
    router = st.sb("router", [P, 2, DC, RD3], F32R)
    raw_k = st.sb("raw_k", [RD3, E3])
    keys = st.sb("keys", [RD3, 2, E3], F32R)
    q = st.sb("q", [RD3, 2, NT], F32R)
    s = st.sb("s", [P, NB, E3])
    left = st.sb("left", [P, NB, E3])
    left2 = st.sb("left2", [P, NB, E3])
    best = st.sb("best", [P, NB, 16])
    shift = st.sb("shift", [P, NB])
    total = st.sb("total", [P, NB])
    inv = st.sb("inv", [P, NB])
    zg = st.sb("zg", [P, 2, D])
    zt = st.sb("zt", [P, 2, 2, DC, P], F32R)
    pq = st.ps("pq", [P, BANK])
    ps_ = st.ps("ps", [P, BANK])
    pz = st.ps("pz", [P, 2, BANK])
    ptr = st.ps("ptr", [P, 2, BANK])
    po = st.ps("po", [P, 2, BANK])
    (small_loaded, a_loaded, b_loaded, own, small_split, a_split, b_split, q_ready, q_hi, q_lo, s_ready, shift_ready,
     exp_done, z_ready, z_used, tr_ready, tr_hi, tr_used, o_ready, x_done) = (st.sem(n) for n in (
         "small_loaded", "a_loaded", "b_loaded", "own", "small_split", "a_split", "b_split", "q_ready", "q_hi", "q_lo",
         "s_ready", "shift_ready", "exp_done", "z_ready", "z_used", "tr_ready", "tr_hi", "tr_used", "o_ready", "x_done"))
    with nc.Block() as block:
        @block.sync
        def _(sp):
            with nc.allow_non_contiguous_dma(reason="small weights"):
                sp.dma_start(raw_r[:, :, :], router_in.rearrange("(c p) n -> p c n", p=P)).then_inc(small_loaded, 16)
            sp.dma_start(raw_k[:, :], keys_in).then_inc(small_loaded, 16)
            sp.dma_start(raw[:, 0, :, :], a_in.rearrange("(c p) n -> p c n", p=P)).then_inc(a_loaded, 16)
            sp.dma_start(raw[:, 1, :, :], b_in.rearrange("(c p) n -> p c n", p=P)).then_inc(b_loaded, 16)

        @block.gpsimd
        def _(pool):
            for i, (w, loaded, split) in enumerate(((wa, a_loaded, a_split), (wb, b_loaded, b_split))):
                pool.wait_ge(loaded, 16)
                nc.gpsimd.tensor_scalar(w[:, HI, :, :], raw[:, i, :, :], 1.0, 0.0, ALU.mult, ALU.add).then_inc(split, 1)
                pool.wait_ge(split, 1)
                nc.gpsimd.tensor_tensor(w[:, LO, :, :], raw[:, i, :, :], w[:, HI, :, :].bitcast(F32),
                                        ALU.subtract).then_inc(split, 1)

        @block.tensor
        def _(pe):
            pe.wait_ge(small_split, 2)
            for half in range(2):
                if half:
                    pe.wait_ge(q_lo, 1)
                for c in range(DC):
                    ins = mm3(nc, pq[0:RD3, :], lambda p: router[:, p, c, :],
                              lambda p: h_t[:, p, c, half * BANK:(half + 1) * BANK], c == 0, c == DC - 1)
                ins.then_inc(q_ready, 1)
            pe.wait_ge(q_lo, 2)
            for b in range(NB):
                ins = mm3(nc, ps_[:, b * E3:(b + 1) * E3], lambda p: q[:, p, b * P:(b + 1) * P], lambda p: keys[:, p, :])
            ins.then_inc(s_ready, 1)

            def low(b):
                if b >= 2:
                    pe.wait_ge(z_used, b - 1)
                for c in range(DC):
                    ins = mm3(nc, pz[:, b % 2, :], lambda p: h_t[:, p, c, b * P:(b + 1) * P],
                              lambda p: wa[:, p, c, :], c == 0, c == DC - 1)
                ins.then_inc(z_ready, 1)

            pe.wait_ge(a_split, 2)
            low(0)
            low(1)
            for b in range(NB):
                pe.wait_ge(z_used, b + 1)
                if b >= 2:
                    pe.wait_ge(tr_used, b - 1)
                for c in range(DC):
                    ins = nc.tensor.transpose(ptr[:, b % 2, c * P:(c + 1) * P], zg[:, b % 2, c * P:(c + 1) * P], ident[:, :])
                ins.then_inc(tr_ready, 1)
                if b + 2 < NB:
                    low(b + 2)
                if b == 0:
                    pe.wait_ge(b_split, 2)
                pe.wait_ge(tr_used, b + 1)
                if b >= 2:
                    pe.wait_ge(x_done, b - 1)
                for c in range(DC):
                    ins = mm3(nc, po[:, b % 2, :], lambda p: zt[:, b % 2, p, c, :], lambda p: wb[:, p, c, :],
                              c == 0, c == DC - 1)
                ins.then_inc(o_ready, 1)

        @block.scalar
        def _(act):
            for half in range(2):
                act.wait_ge(q_ready, half + 1)
                nc.scalar.activation(q[:, HI, half * BANK:(half + 1) * BANK], pq[0:RD3, :], ACT.Copy).then_inc(q_hi, 1)
            act.wait_ge(shift_ready, 1)
            for b in range(NB):
                nc.scalar.activation(s[:, b, :], s[:, b, :], ACT.Exp, bias=shift[:, b:b + 1]).then_inc(exp_done, 1)
            for b in range(NB):
                act.wait_ge(tr_ready, b + 1)
                if b >= 2:
                    act.wait_ge(o_ready, b - 1)
                nc.scalar.activation(zt[:, b % 2, HI, :, :].rearrange("p c t -> p (c t)"), ptr[:, b % 2, :],
                                     ACT.Copy).then_inc(tr_hi, 1)

        @block.vector
        def _(dve):
            steps = Steps(dve, own)
            dve.wait_ge(small_loaded, 32)
            steps.mark(nc.vector.tensor_copy(router[:, HI, :, :], raw_r[:, :, :]))
            steps.mark(nc.vector.tensor_copy(keys[:, HI, :], raw_k[:, :]))
            steps.wait()
            nc.vector.tensor_tensor(router[:, LO, :, :], raw_r[:, :, :], router[:, HI, :, :].bitcast(F32),
                                    ALU.subtract).then_inc(small_split, 1)
            nc.vector.tensor_tensor(keys[:, LO, :], raw_k[:, :], keys[:, HI, :].bitcast(F32), ALU.subtract).then_inc(small_split, 1)
            for half in range(2):
                dve.wait_ge(q_hi, half + 1)
                cols = slice(half * BANK, (half + 1) * BANK)
                nc.vector.tensor_tensor(q[:, LO, cols], pq[0:RD3, :], q[:, HI, cols].bitcast(F32), ALU.subtract).then_inc(q_lo, 1)
            dve.wait_ge(s_ready, 1)
            steps.mark(nc.vector.tensor_copy(s[:, :, :].rearrange("p b e -> p (b e)"), ps_[:, :]))
            steps.wait()
            for b in range(NB):
                steps.mark(nc.vector.max(best[:, b, 0:8], s[:, b, :]))
            steps.wait()
            for b in range(NB):
                steps.mark(nc.vector.match_replace(left[:, b, :], best[:, b, 0:8], s[:, b, :], TAKEN))
            steps.mark(nc.vector.tensor_scalar(shift[:, :], best[:, :, 0], -1.0, None, ALU.mult))
            steps.wait()
            for b in range(NB):
                steps.mark(nc.vector.max(best[:, b, 8:16], left[:, b, :]))
            steps.wait()
            for b in range(NB):
                steps.mark(nc.vector.match_replace(left2[:, b, :], best[:, b, 8:16], left[:, b, :], TAKEN))
            steps.wait()
            steps.mark(nc.vector.tensor_scalar(left[:, :, :], left2[:, :, :], TAKEN, None, ALU.is_equal))
            steps.wait()
            dve.sem_inc(shift_ready, 1)
            dve.wait_ge(exp_done, NB)
            steps.mark(nc.vector.tensor_tensor(s[:, :, :], s[:, :, :], left[:, :, :], ALU.mult))
            steps.wait()
            steps.mark(nc.vector.reduce_sum(total[:, :], s[:, :, :], AX.X))
            steps.wait()
            steps.mark(nc.vector.tensor_scalar(total[:, :], total[:, :], 0.5, None, ALU.mult))
            steps.wait()
            steps.mark(nc.vector.reciprocal(inv[:, :], total[:, :]))
            steps.wait()
            steps.mark(nc.vector.tensor_tensor(s[:, :, :], s[:, :, :], inv[:, :, None].broadcast_to([P, NB, E3]), ALU.mult))
            steps.wait()

            def gated(b):
                dve.wait_ge(z_ready, b + 1)
                if b >= 2:
                    dve.wait_ge(tr_ready, b - 1)
                nc.vector.tensor_tensor(zg[:, b % 2, :].rearrange("p (e r) -> p e r", r=R3),
                                        pz[:, b % 2, :].rearrange("p (e r) -> p e r", r=R3),
                                        s[:, b, :, None].broadcast_to([P, E3, R3]), ALU.mult).then_inc(z_used, 1)

            gated(0)
            gated(1)
            for b in range(NB):
                dve.wait_ge(tr_hi, b + 1)
                nc.vector.tensor_tensor(zt[:, b % 2, LO, :, :].rearrange("p c t -> p (c t)"), ptr[:, b % 2, :],
                                        zt[:, b % 2, HI, :, :].rearrange("p c t -> p (c t)").bitcast(F32),
                                        ALU.subtract).then_inc(tr_used, 1)
                if b + 2 < NB:
                    gated(b + 2)
                dve.wait_ge(o_ready, b + 1)
                nc.vector.tensor_tensor(x[:, b, :], po[:, b % 2, :], x[:, b, :], ALU.add).then_inc(x_done, 1)
            dve.wait_ge(x_done, NB)
    st.close()


def store_stage(nc, x, out):
    st = Stage(nc, "store")
    stored = st.sem("stored")
    with nc.Block() as block:
        @block.sync
        def _(sp):
            sp.dma_start(out.rearrange("b t d -> t b d"), x[:, :, :]).then_inc(stored, 16)
            sp.wait_ge(stored, 16)
    st.close()


PLAN0 = Plan("a0", hpg=2, own_kv=True)
PLAN2 = Plan("a2", hpg=4, rope=True)
PLAN3 = Plan("a3", hpg=4, kvb=2, qknorm=True)


def pieces(plan, wq_t, wk_t, wv_t, wo_t):
    def columns(w, n):
        return w[:, n * P:(n + 1) * P].reshape(DC, P, P).transpose(1, 0, 2).reshape(P, D)

    out = []
    for key in plan.all_w():
        kind, n = key[0], key[1]
        if kind == "q":
            out.append(columns(wq_t, n % H))
        elif kind == "o":
            out.append(wo_t[n * P:(n + 1) * P, :])
        else:
            out.append(columns(wk_t if kind == "k" else wv_t, n * plan.kvh + key[2]))
    return np.stack(out)


def rope_tables():
    inv_freq = (1.0 / np.float32(10000.0) ** (np.arange(0, P, 2, dtype=np.float32) / np.float32(P))).astype(np.float32)
    freqs = np.arange(MAX_POS, dtype=np.float32)[:, None] * inv_freq[None, :]
    both = np.concatenate([freqs, freqs], axis=1)
    sin = np.sin(both)
    sin[:, :P // 2] *= -1
    return np.stack([np.cos(both), sin]).astype(np.float32)


def program(nc, ins, out):
    rounded = nc.dram_tensor("nf4_rounded", (NF4_PIECES, P, NF4_COLS), F32, kind="Internal").ap()
    rounded_rows = rounded.rearrange("a p n -> (a p n)").rearrange("(r c) -> r c", c=D)
    with ExitStack() as ctx:
        def sb(name, shape, dt=F32):
            return ctx.enter_context(nc.sbuf_tensor(name, shape, dt))

        x = sb("x", [P, NB, D])
        ident = sb("ident", [P, P])
        nf4_stage(nc, ins["nf4"], rounded)
        ctx_t = sb("ctx_t", [P, 2, DC, NT], F32R)
        load_stage(nc, x, ident, ctx_t, ins["x"], ins["ident"], ins["ctxt"])
        with nc.sbuf_tensor("h_t0", [P, 2, DC, NT], F32R) as h_t:
            norm_stage(nc, "n0", x, ident, h_t, ins["ln_w"])
            attention_stage(nc, PLAN0, x, ident, ctx_t, h_t, ins["a0_w"], ins["mask_bool"], ins["pos_bias"])
            norm_stage(nc, "n1", x, ident, h_t)
            ffn0_stage(nc, x, ident, h_t, ins["w_base"], ins["f0_side"], ins["lora_b"], ins["b_base"], ins["b_router"])
        with nc.sbuf_tensor("h_nat", [P, NB, D], F32) as h:
            norm_natural_stage(nc, "n2", x, h)
            patch_attention_stage(nc, x, h, ident, ins["ctx"], ins["mask_f"], ins["a1_wqk"], ins["a1_wv"], ins["a1_wo"],
                                  ins["a1_bqk"], ins["a1_flag"], ins["a1_bv"], ins["a1_bo"])
            norm_natural_stage(nc, "n3", x, h)
            with nc.sbuf_tensor("ident_bf", [P, P], BF16) as ident_bf:
                made = Stage(nc, "ib")
                done = made.sem("done")
                with nc.Block() as block:
                    @block.vector
                    def _(dve):
                        nc.vector.tensor_copy(ident_bf[:, :], ident[:, :]).then_inc(done, 1)
                        dve.wait_ge(done, 1)
                made.close()
                ffn1_stage(nc, x, h, ident_bf, ins["f1_w"], ins["f1_scale"], ins["f1_bias"])
        with nc.sbuf_tensor("h_t1", [P, 2, DC, NT], F32R) as h_t:
            with nc.sbuf_tensor("cos", [P, NT], F32) as cos, nc.sbuf_tensor("sin", [P, NT], F32) as sin:
                rope_stage(nc, cos, sin, ins["pos"], ins["iota"], ins["rope"])
                norm_stage(nc, "n4", x, ident, h_t)
                attention_stage(nc, PLAN2, x, ident, ctx_t, h_t, ins["a2_w"], ins["mask_i"], rope_sb=(cos, sin))
            norm_stage(nc, "n5", x, ident, h_t)
            ffn2_stage(nc, x, ident, h_t, rounded_rows)
            norm_stage(nc, "n6", x, ident, h_t)
            attention_stage(nc, PLAN3, x, ident, ctx_t, h_t, ins["a3_w"], kq_norm_in=ins["a3_norm"])
            norm_stage(nc, "n7", x, ident, h_t)
            ffn3_stage(nc, x, ident, h_t, ins["f3_a"], ins["f3_b"], ins["f3_router"], ins["f3_keys"])
        store_stage(nc, x, out)


def host_layout(i):
    c = np.ascontiguousarray

    def spread(w):
        out = np.zeros((w.shape[1], 2, 4, ROWS), w.dtype)
        out[:, :, :, :DH] = w.T.reshape(w.shape[1], 2, 4, DH)
        return out.reshape(w.shape[1], 2 * P)

    flag = np.zeros((4, ROWS), np.float32)
    flag[:, DH] = 1
    bqk = np.concatenate([spread(i["L1_xattn_bq"][:, None]), spread(i["L1_xattn_bk"][:, None])], 1)
    lora_a = i["L0_ffn_lora_A"].transpose(1, 0, 2).reshape(D, E0 * R0)
    return {
        "x": i["x"], "ctx": i["ctx_4096"], "ctxt": c(i["ctx_4096"].reshape(NT, D).T), "ident": np.eye(P, dtype=np.float32),
        "mask_bool": c(i["mask_BxSxS2_bk0"]).view(np.int32), "mask_i": i["mask_BxSxS2_ik0"],
        "mask_f": c(i["mask_Bx1x4096_ff1"].reshape(NB, D)), "pos": i["pos_BxS2"],
        "pos_bias": i["L0_xattn_position_bias"], "ln_w": c(i["L0_xattn_ln_weight"].reshape(DC, P).T),
        "a0_w": pieces(PLAN0, i["L0_xattn_w_q"].T, i["L0_xattn_w_k"].T, i["L0_xattn_w_v"].T, i["L0_xattn_w_out"].T),
        "w_base": c(i["L0_ffn_W_base"].T), "f0_side": np.concatenate([lora_a, i["L0_ffn_W_router"].T], 1),
        "lora_b": c(i["L0_ffn_lora_B"].reshape(E0 * R0, D)), "b_base": i["L0_ffn_b_base"], "b_router": i["L0_ffn_b_router"],
        "a1_wqk": np.concatenate([spread(i["L1_xattn_Wq"]), spread(i["L1_xattn_Wk"])], 1),
        "a1_wv": c(i["L1_xattn_Wv"].T), "a1_wo": c(i["L1_xattn_Wo"].T), "a1_bqk": c(bqk.reshape(4, P).T),
        "a1_flag": c(flag.reshape(P, 1)), "a1_bv": i["L1_xattn_bv"], "a1_bo": i["L1_xattn_bo"],
        "f1_w": c(i["L1_ffn_weight"].T).view(np.int32), "f1_scale": i["L1_ffn_weight_scales"], "f1_bias": i["L1_ffn_bias"],
        "iota": c(np.arange(MAX_POS, dtype=np.float32).reshape(DC, P).T), "rope": rope_tables(),
        "a2_w": pieces(PLAN2, i["L2_xattn_Wq"], i["L2_xattn_Wk"], i["L2_xattn_Wv"], i["L2_xattn_Wo"]),
        "nf4": np.concatenate([i[f"L2_ffn_w{n}"].reshape(-1, P, NF4_COLS) for n in (1, 2, 3)]),
        "a3_w": pieces(PLAN3, i["L3_xattn_Wq"], i["L3_xattn_Wk"], i["L3_xattn_Wv"], i["L3_xattn_Wo"]),
        "a3_norm": np.stack([i["L3_xattn_q_norm_w"], i["L3_xattn_k_norm_w"]], 1),
        "f3_a": c(i["L3_ffn_A_w"].T), "f3_b": c(i["L3_ffn_B_w"].T), "f3_router": c(i["L3_ffn_Wq_w"].T),
        "f3_keys": c(i["L3_ffn_keys"].T),
    }


def kernel(**inputs):
    import concourse.bacc as bacc
    from concourse.bass_utils import run_bass_kernel_spmd

    nc = bacc.Bacc("TRN2", target_bir_lowering=False, num_devices=1)
    arrays, ins = {}, {}
    for name, a in host_layout({k: np.asarray(v) for k, v in inputs.items()}).items():
        arrays[f"in_{name}"] = np.ascontiguousarray(a)
        ins[name] = nc.dram_tensor(f"in_{name}", a.shape, mybir.dt.from_np(a.dtype), kind="ExternalInput").ap()
    out = nc.dram_tensor("out", (NB, P, D), F32, kind="ExternalOutput").ap()
    program(nc, ins, out)
    return run_bass_kernel_spmd(nc, [arrays], core_ids=[0]).results[0]["out"]
```

```python
import math
from contextlib import ExitStack

import numpy as np

import concourse.bass as bass
from concourse import mybir

F32 = mybir.dt.float32
F32R = mybir.dt.float32r
BF16 = mybir.dt.bfloat16
F16 = mybir.dt.float16
I32 = mybir.dt.int32
I8 = mybir.dt.int8
U8 = mybir.dt.uint8
ALU = mybir.AluOpType
ACT = mybir.ActivationFunctionType
AX = mybir.AxisListType

P = 128
NB = 8
D = 512
DC = D // P
NT = NB * P
BANK = 512
H = 32
HI, LO = 0, 1
PASSES = ((HI, HI), (HI, LO), (LO, HI))
NEG = -1.0e30
NH2 = 1376
HC2 = -(-NH2 // P)
NF4_BLOCK = 64
NF4_CODE = [-1.0, -0.6961928009986877, -0.5250730514526367, -0.39491748809814453,
            -0.28444138169288635, -0.18477343022823334, -0.09105003625154495, 0.0,
            0.07958029955625534, 0.16093020141124725, 0.24611230194568634, 0.33791524171829224,
            0.44070982933044434, 0.5626170039176941, 0.7229568362236023, 1.0]


class Steps:

    def __init__(self, engine, sem, base=0):
        self.engine, self.sem, self.base, self.n = engine, sem, base, 0

    def mark(self, ins):
        ins.then_inc(self.sem, 1)
        self.n += 1

    def wait(self):
        self.engine.wait_ge(self.sem, self.base + self.n)


class Stage:

    def __init__(self, nc, name):
        self.nc, self.name, self.ctx, self.sems = nc, name, ExitStack(), []

    def sem(self, name):
        s = self.nc.alloc_semaphore(name=f"{self.name}_{name}")
        self.sems.append(s)
        return s

    def sb(self, name, shape, dt=F32):
        return self.ctx.enter_context(self.nc.sbuf_tensor(f"{self.name}_{name}", shape, dt))

    def ps(self, name, shape, dt=F32):
        return self.ctx.enter_context(self.nc.psum_tensor(f"{self.name}_{name}", shape, dt))

    def close(self):
        self.ctx.close()
        self.nc.clear_and_free_semaphores(self.sems)
        self.nc.all_engine_barrier()


def mm3(nc, out, lhs, rhs, first=True, last=True):
    for i, (a, b) in enumerate(PASSES):
        ins = nc.tensor.matmul(out, lhs(a), rhs(b), start=first and i == 0, stop=last and i == 2)
    return ins



def load_stage(nc, x, ident, ctx_t, x_in, ident_in, ctxt_in):
    st = Stage(nc, "load")
    raw = st.sb("ctx_raw", [P, DC, NT])
    loaded, ctx_loaded = st.sem("loaded"), st.sem("ctx_loaded")
    hi_done, lo_done = st.sem("hi_done"), st.sem("lo_done")
    with nc.Block() as block:
        @block.sync
        def _(sp):
            sp.dma_start(raw[:, :, :], ctxt_in.rearrange("(c p) t -> p c t", p=P)).then_inc(ctx_loaded, 16)
            sp.dma_start(x[:, :, :], x_in.rearrange("b t d -> t b d")).then_inc(loaded, 16)
            sp.dma_start(ident[:, :], ident_in).then_inc(loaded, 16)
            sp.wait_ge(loaded, 32)

        @block.scalar
        def _(act):
            act.wait_ge(ctx_loaded, 16)
            for c in range(DC):
                nc.scalar.activation(ctx_t[:, HI, c, :], raw[:, c, :], ACT.Copy).then_inc(hi_done, 1)

        @block.vector
        def _(dve):
            for c in range(DC):
                dve.wait_ge(hi_done, c + 1)
                nc.vector.tensor_tensor(ctx_t[:, LO, c, :], raw[:, c, :],
                                        ctx_t[:, HI, c, :].bitcast(F32), ALU.subtract).then_inc(lo_done, 1)
            dve.wait_ge(lo_done, DC)
    st.close()



class Norm:

    def __init__(self, st, space):
        space = space[:, 0:11 * NB].rearrange("p (i b) -> p i b", b=NB)
        self.stats = space[:, 0:6, :].rearrange("p i b -> p (i b)").rearrange("p (b i) -> p b i", i=6)
        self.mv = space[:, 6:8, :].rearrange("p i b -> p (i b)").rearrange("p (b i) -> p b i", i=2)
        self.var, self.rstd, self.half = space[:, 8, :], space[:, 9, :], space[:, 10, :]
        self.var_ready, self.rstd_ready = st.sem("var_ready"), st.sem("rstd_ready")
        self.half_set = st.sem("half_set")

    def stats_on_vector(self, nc, steps, x):
        for b in range(NB):
            steps.mark(nc.vector.bn_stats(self.stats[:, b, :], x[:, b, :]))
        steps.wait()
        for b in range(NB):
            steps.mark(nc.vector.bn_aggr(self.mv[:, b, :], self.stats[:, b, :]))
        steps.wait()
        nc.vector.tensor_scalar(self.var, self.mv[:, :, 1], 1e-5, None, ALU.add).then_inc(self.var_ready, 1)

    def set_half(self, nc):
        nc.gpsimd.memset(self.half, -0.5).then_inc(self.half_set, 1)

    def rstd_on_gpsimd(self, nc, pool):
        pool.wait_ge(self.half_set, 1)
        pool.wait_ge(self.var_ready, 1)
        nc.gpsimd.tensor_tensor(self.rstd, self.var, self.half, ALU.pow).then_inc(self.rstd_ready, 1)

    def apply(self, nc, b, out, x):
        return nc.vector.tensor_scalar(out, x[:, b, :], self.mv[:, b, 0:1], self.rstd[:, b:b + 1],
                                       ALU.subtract, ALU.mult)


class TransposedNorm:

    def __init__(self, nc, st, x, ident, h_t, banks, space, h, lnw_in=None, h2=None, sq=None):
        self.nc, self.x, self.ident, self.h_t, self.lnw_in, self.h, self.h2, self.sq = nc, x, ident, h_t, lnw_in, h, h2, sq
        self.tp = [bank.rearrange("p (c n) -> p c n", c=DC) for bank in banks]
        self.norm = Norm(st, space)
        self.rms = lnw_in is not None
        self.src = h2 if self.rms else h
        self.h_ready, self.tp_ready, self.hi_done, self.lo_done, self.own = (
            st.sem(n) for n in ("h_ready", "tp_ready", "hi_done", "lo_done", "norm_own"))
        if self.rms:
            self.ssq, self.ms, self.r2, self.lnw = (space[:, (i + 11) * NB:(i + 11) * NB + n]
                                                    for i, n in enumerate((NB, NB, NB, DC)))
            self.lnw_loaded, self.ssq_ready, self.ms_ready, self.r2_ready, self.ln_ready = (
                st.sem(n) for n in ("lnw_loaded", "ssq_ready", "rms_ready", "r2_ready", "ln_ready"))

    def on_sync(self, sp):
        if self.rms:
            with self.nc.allow_non_contiguous_dma(reason="512 weights"):
                sp.dma_start(self.lnw, self.lnw_in).then_inc(self.lnw_loaded, 16)

    def on_gpsimd(self, pool):
        self.norm.set_half(self.nc)
        self.norm.rstd_on_gpsimd(self.nc, pool)
        if self.rms:
            pool.wait_ge(self.ms_ready, 1)
            self.nc.gpsimd.tensor_tensor(self.r2, self.ms, self.norm.half, ALU.pow
                                         ).then_inc(self.r2_ready, 1)

    def on_vector(self, dve):
        nc, x, h, norm, rms = self.nc, self.x, self.h, self.norm, self.rms
        norm.stats_on_vector(nc, Steps(dve, self.own), x)
        dve.wait_ge(norm.rstd_ready, 1)
        if rms:
            for b in range(NB):
                norm.apply(nc, b, h[:, b, :], x).then_inc(self.ln_ready, 1)
            dve.wait_ge(self.ssq_ready, NB)
            nc.vector.tensor_scalar(self.ms, self.ssq, 1.0 / D, 1e-5, ALU.mult, ALU.add).then_inc(self.ms_ready, 1)
            for b in range(NB):
                dve.wait_ge(self.ln_ready, b + 1)
                nc.vector.tensor_tensor(x[:, b, :], x[:, b, :], h[:, b, :], ALU.add)
            dve.wait_ge(self.r2_ready, 1)
            for b in range(NB):
                nc.vector.tensor_scalar(self.h2[:, b, :], h[:, b, :], self.r2[:, b:b + 1], None, ALU.mult
                                        ).then_inc(self.h_ready, 1)
            dve.wait_ge(self.lnw_loaded, 16)
        else:
            for b in range(NB):
                norm.apply(nc, b, h[:, b, :], x).then_inc(self.h_ready, 1)
        for b in range(NB):
            dve.wait_ge(self.hi_done, b + 1)
            tile = self.tp[b % 4]
            dst = self.h_t[:, LO, :, b * P:(b + 1) * P]
            hi = self.h_t[:, HI, :, b * P:(b + 1) * P].bitcast(F32)
            if rms:
                for c in range(DC):
                    ins = nc.vector.scalar_tensor_tensor(dst[:, c, :], tile[:, c, :], self.lnw[:, c:c + 1],
                                                         hi[:, c, :], ALU.mult, ALU.subtract)
            else:
                ins = nc.vector.tensor_tensor(dst, tile, hi, ALU.subtract)
            ins.then_inc(self.lo_done, 1)
        dve.wait_ge(self.lo_done, NB)

    def on_tensor(self, pe):
        for b in range(NB):
            pe.wait_ge(self.h_ready, b + 1)
            if b >= 4:
                pe.wait_ge(self.lo_done, b - 3)
            for c in range(DC):
                ins = self.nc.tensor.transpose(self.tp[b % 4][:, c, :], self.src[:, b, c * P:(c + 1) * P], self.ident[:, :])
            ins.then_inc(self.tp_ready, 1)
        pe.wait_ge(self.lo_done, NB)

    def on_scalar(self, act):
        nc = self.nc
        if self.rms:
            for b in range(NB):
                act.wait_ge(self.ln_ready, b + 1)
                if b >= 2:
                    act.wait_ge(self.ssq_ready, b - 1)
                nc.scalar.activation(self.sq[:, b % 2, :], self.h[:, b, :], ACT.Square,
                                     accum_out=self.ssq[:, b:b + 1]).then_inc(self.ssq_ready, 1)
            act.wait_ge(self.lnw_loaded, 16)
        for b in range(NB):
            act.wait_ge(self.tp_ready, b + 1)
            tile = self.tp[b % 4]
            dst = self.h_t[:, HI, :, b * P:(b + 1) * P]
            if self.rms:
                for c in range(DC):
                    ins = nc.scalar.activation(dst[:, c, :], tile[:, c, :], ACT.Copy, scale=self.lnw[:, c:c + 1])
            else:
                ins = nc.scalar.activation(dst, tile, ACT.Copy)
            ins.then_inc(self.hi_done, 1)



class Place:

    def __init__(self, g, per, n):
        self.before = g * per + n if n or not isinstance(g, int) else g * per
        self.through = g * per + (n + 1)
        self.slot = n % 2
        self.turn = g * (per // 2) + (n // 2 + 1)
        self.filled = n >= 2 or not isinstance(g, int) or g > 0
        self.last_but_one = g * per + (n - 1) if self.filled else None


class Plan:

    def __init__(self, name, hpg, own_kv=False, kvb=1, rope=False, qknorm=False, out_every=2, scale=1.0):
        self.name, self.hpg, self.own_kv, self.kvb = name, hpg, own_kv, kvb
        self.rope, self.qknorm, self.out_every, self.scale = rope, qknorm, out_every, scale
        self.groups = H // hpg
        self.kvh = hpg if own_kv else 1
        self.keys = kvb * P
        self.vcols = self.kvh * P
        self.v_per = BANK // self.vcols
        self.v_tiles = NB * kvb // self.v_per
        self.s_tiles = NB * self.keys // BANK
        self.b_per_s = NB // self.s_tiles

    def q_keys(self, head):
        return [("q", head, 0), ("q", head, 1)]

    def k_keys(self):
        if self.qknorm:
            return [("kt", t) for t in range(4)]
        return [("k", h, half) for h in range(self.kvh) for half in range(2)]

    def v_keys(self):
        return [] if self.qknorm else [("v", t) for t in range(self.v_tiles)]

    def joint_keys(self, ss=()):
        kv, kt = [("kv", n) for n in range(8)], [("kt", t) for t in range(4)]
        return list(ss) + kv[0:4] + kt[0:1] + kv[4:6] + kt[1:2] + kv[6:8] + kt[2:3] + kt[3:4]

    def in_segment(self, j, last):
        return not (last and j + 2 >= self.hpg), not (last and j == self.hpg - 1), not last and j == self.hpg - 1

    def first_a(self):
        order = []
        for head in (0, 1):
            order += self.q_keys(head) + ([("ss", head)] if self.qknorm else [])
        return order + (self.joint_keys() if self.qknorm else self.k_keys() + self.v_keys())

    def segment_a(self, j, last=False):
        q_next, _, kv_next = self.in_segment(j, last)
        q = self.q_keys(j + 2) if q_next else []
        out = [("o", j, b) for b in range(NB)] if (j + 1) % self.out_every == 0 else []
        ss = [("ss", j + 2)] if q_next and self.qknorm else []
        if not kv_next:
            return q + ss + out
        if self.qknorm:
            return q + self.joint_keys(ss)[:-1] + out[:2] + self.joint_keys()[-1:] + out[2:]
        return q[:1] + self.k_keys() + q[1:] + out + self.v_keys()

    def a_order(self, last=False):
        return [key for j in range(self.hpg) for key in self.segment_a(j, last)]

    def hi_of(self, order):
        return [k for k in order if k[0] not in ("o", "ss") and not (self.rope and k[0] in "qk")]

    def ms_of(self, order):
        return [("kn", k[1] // 2) if k[0] == "kv" else k for k in order
                if k[0] == "ss" or (k[0] == "kv" and k[1] % 2 == 1)]

    def rot_of(self, order):
        return [k for k in order if k[0] in ("q", "k")]

    def first_w(self):
        kv = [(kind, 0, i) for kind in "kv" for i in range(self.kvh)]
        return [("q", 0), ("q", 1)] + kv + [("q", 2)]

    def segment_w(self, j, last=False):
        q = [("q", j + 3)] if not (last and j + 3 >= self.hpg) else []
        out = [("o", j)] + q if (j + 1) % self.out_every == 0 else q + [("o", j)]
        if not last and j < 2:
            out += [("kv"[j], 1, i) for i in range(self.kvh)]
        return out

    def w_order(self, last=False):
        return [w for j in range(self.hpg) for w in self.segment_w(j, last)]

    def all_w(self):
        order = self.first_w()
        for g in range(self.groups):
            for kind, n, *slot in self.w_order(g == self.groups - 1):
                order.append((kind, g + n, *slot) if slot else (kind, g * self.hpg + n))
        return order


NF4_BLOCKS = 3 * NH2 * D // (P * NF4_BLOCK)
NF4_STEPS = 17


class Share:

    def __init__(self, first, sizes, left, at):
        self.first, self.sizes, self.left, self.at = first, sizes, left, at
        assert sum(map(sum, at.values())) == NF4_STEPS * len(sizes) and left <= sizes[0]

    def end(self, groups):
        return self.first + (groups - 1) * sum(self.sizes) + self.left


SHARE0 = Share(0, (5, 5), 5, {
    "weights": (0, 0), "exps": (1, 0), "queries": (0, 0), "weighed": (1, 0),
    "queries_1": (2, 2), "keys": (0, 12), "outputs": (0, 8), "values": (0, 8)})
SHARE2 = Share(SHARE0.end(16), (7, 7), 5, {
    "weights": (0, 0, 0, 0), "exps": (0, 0, 0, 0), "queries": (0, 0, 0, 0), "weighed": (0, 0, 0, 0),
    "queries_1": (1, 2, 1, 2), "keys": (0, 0, 0, 4), "outputs": (0, 8, 0, 8), "values": (0, 0, 0, 8)})
assert SHARE2.end(8) == NF4_BLOCKS


class Rounding:

    SCALE = 2.0 ** 60
    zero = NF4_CODE.index(0.0)

    def __init__(self, nc, st, flat_in, rounded, share, groups):
        code = np.array(NF4_CODE, np.float32)
        bounds = ((code[:-1] + code[1:]) * np.float32(0.5)).astype(np.float32)
        above = np.nextafter(bounds, np.float32(np.inf))
        self.terms = [(float(above[i]), float(code[i])) if i < self.zero else (float(bounds[i]), float(code[i + 1]))
                      for i in range(15)]
        self.nc, self.flat_in, self.rounded, self.groups, self.share = nc, flat_in, rounded, groups, share
        self.sizes, self.per_group = share.sizes, sum(share.sizes)
        cols = self.sizes[0] * NF4_BLOCK
        self.w = st.sb("nf_w", [P, cols])
        self.t = st.sb("nf_t", [P, 2, cols], BF16)
        self.acc = st.sb("nf_acc", [P, cols])
        self.top = st.sb("nf_top", [P, self.sizes[0]])
        self.inv = st.sb("nf_inv", [P, self.sizes[0]])
        self.shifts = st.sb("nf_shifts", [P, 15])
        (self.loaded, self.stored, self.shifts_set, self.own, self.v_ready, self.t_ready, self.t_used, self.done) = (
            st.sem(n) for n in ("nf_loaded", "nf_stored", "nf_shifts_set", "nf_own", "nf_v_ready", "nf_t_ready",
                                "nf_t_used", "nf_done"))

    def piece(self, g, n, last):
        before = sum(self.sizes[:n])
        column = g * (self.per_group * NF4_BLOCK) + (self.share.first + before) * NF4_BLOCK
        return g * len(self.sizes) + n, column, self.share.left if last else self.sizes[n]

    def set_up_on_gpsimd(self):
        for i, (bound, _) in enumerate(self.terms):
            self.nc.gpsimd.memset(self.shifts[:, i:i + 1], -bound * self.SCALE).then_inc(self.shifts_set, 1)

    def set_up_on_vector(self, dve):
        dve.sem_inc(self.t_used, 2)
        dve.sem_inc(self.done, 1)

    def load(self, act, column, blocks):
        cols = blocks * NF4_BLOCK
        act.dma_start(self.w[:, 0:cols], self.flat_in[:, bass.ds(column, cols)]).then_inc(self.loaded, 16)

    def set_up_on_scalar(self, act):
        act.wait_ge(self.shifts_set, 15)
        act.dma_start(self.acc[:, 0:NF4_BLOCK], self.flat_in[:, 0:NF4_BLOCK]).then_inc(self.stored, 16)
        self.load(act, self.share.first * NF4_BLOCK, self.sizes[0])

    def store(self, act, number, column, blocks):
        cols = blocks * NF4_BLOCK
        act.wait_ge(self.done, number + 2)
        act.dma_start(self.rounded[:, bass.ds(column, cols)], self.acc[:, 0:cols]).then_inc(self.stored, 16)

    def on_scalar(self, act, g, last, first, end):
        for step in range(first, end):
            n, i = step // NF4_STEPS, step % NF4_STEPS
            number, column, blocks = self.piece(g, n, last)
            m = g * (15 * len(self.sizes)) + (15 * n + i - 1)
            cols = blocks * NF4_BLOCK
            if i == 0:
                continue
            if i == NF4_STEPS - 1:
                if last:
                    self.store(act, number, column, blocks)
                    continue
                act.wait_ge(self.t_ready, m)
                if n + 1 < len(self.sizes):
                    self.load(act, self.piece(g, n + 1, False)[1], self.sizes[n + 1])
                else:
                    self.load(act, self.piece(g + 1, 0, False)[1], self.sizes[0])
                self.store(act, number, column, blocks)
                continue
            if i == 1:
                act.wait_ge(self.v_ready, number + 1)
            act.wait_ge(self.t_used, m + 1)
            self.nc.scalar.activation(self.t[:, (15 * n + i - 1) % 2, 0:cols], self.w[:, 0:cols], ACT.Identity,
                                      bias=self.shifts[:, i - 1:i], scale=self.SCALE).then_inc(self.t_ready, 1)

    def on_vector(self, dve, g, last, first, end):
        nc = self.nc
        for step in range(first, end):
            n, i = step // NF4_STEPS, step % NF4_STEPS
            number, _, blocks = self.piece(g, n, last)
            m = g * (15 * len(self.sizes)) + (15 * n + i - 1)
            cols = blocks * NF4_BLOCK
            top, inv, acc = self.top[:, 0:blocks], self.inv[:, 0:blocks], self.acc[:, 0:cols]
            w_blocks = self.w[:, 0:cols].rearrange("p (b i) -> p b i", i=NF4_BLOCK)
            if i == 0:
                steps = Steps(dve, self.own, number * 4)
                dve.wait_ge(self.loaded, number * 16 + 16)
                dve.wait_ge(self.done, number + 1)
                steps.mark(nc.vector.tensor_reduce(top, w_blocks, AX.X, ALU.max, apply_absolute_value=True))
                steps.wait()
                steps.mark(nc.vector.tensor_scalar(inv, top, 0.0, None, ALU.is_equal))
                steps.wait()
                steps.mark(nc.vector.tensor_tensor(inv, inv, top, ALU.add))
                steps.wait()
                steps.mark(nc.vector.reciprocal(inv, inv))
                steps.wait()
                nc.vector.tensor_tensor(w_blocks, w_blocks, inv[:, :, None].broadcast_to([P, blocks, NF4_BLOCK]),
                                        ALU.mult).then_inc(self.v_ready, 1)
                continue
            if i == NF4_STEPS - 1:
                dve.wait_ge(self.t_used, m + 2)
                acc_blocks = acc.rearrange("p (b i) -> p b i", i=NF4_BLOCK)
                nc.vector.tensor_tensor(acc_blocks, acc_blocks, top[:, :, None].broadcast_to([P, blocks, NF4_BLOCK]),
                                        ALU.mult).then_inc(self.done, 1)
                continue
            below = i - 1 < self.zero
            c = self.terms[i - 1][1]
            inner, outer = (ALU.max, ALU.min) if below else (ALU.min, ALU.max)
            dve.wait_ge(self.t_ready, m + 1)
            t = self.t[:, (15 * n + i - 1) % 2, 0:cols]
            if i == 1:
                dve.wait_ge(self.stored, number * 16 + 16)
                ins = nc.vector.tensor_scalar(acc, t, c, 0.0, inner, outer)
            else:
                dve.wait_ge(self.t_used, m + 2)
                ins = nc.vector.scalar_tensor_tensor(acc, t, c, acc, inner, outer)
            ins.then_inc(self.t_used, 1)

    def finish(self, act):
        act.wait_ge(self.stored, (len(self.sizes) * (self.groups - 1) + 2) * 16)


class SideSteps:

    def __init__(self, emit, engine, g, last):
        self.emit, self.engine, self.g, self.last, self.at = emit, engine, g, last, 0

    def __call__(self, count):
        end = self.at + count
        limit = NF4_STEPS if self.last else end
        self.emit(self.engine, self.g, self.last, min(self.at, limit), min(end, limit))
        self.at = end


def attention_stage(nc, plan, x, ident, ctx_t, h_t, pieces_in, mask_in=None, bias_in=None, rope_sb=None, kq_norm_in=None,
                    nf4=None, lnw_in=None):
    st = Stage(nc, plan.name)
    hpg, keys, kvh, kvb = plan.hpg, plan.keys, plan.kvh, plan.kvb
    rope, qknorm = plan.rope, plan.qknorm
    masked, biased = mask_in is not None, bias_in is not None
    bps, NS, NG = plan.b_per_s, plan.s_tiles, plan.groups

    raw = st.sb("raw", [P, 2, D])
    wq = st.sb("wq", [P, 2, 2, DC, P], F32R)
    wo = st.sb("wo", [P, 2, 2, D], F32R)
    if qknorm:
        wkv = st.sb("wkv", [P, 2, DC, 2, P], F32R)
    else:
        wk = st.sb("wk", [P, kvh, 2, DC, P], F32R)
        wv = st.sb("wv", [P, 2, DC, kvh, P], F32R)
    early = Stage(nc, plan.name + "_norm")
    norm_space = [early.sb("space", [P, 15 * NB]), early.sb("h", [P, NB, D])]
    if lnw_in is not None:
        norm_space += [lnw_in, early.sb("h2", [P, NB, D]), early.sb("sq", [P, 2, D])]
    early.ctx.close()
    qt = st.sb("qt", [P, 2, 2, NT], F32R)
    kt = st.sb("kt", [P, kvh, 2, NB * keys], F32R)
    v = st.sb("v", [P, 2, NB * kvb, plan.vcols], F32R)
    prob = st.sb("prob", [P, 2, NB, keys])
    pt = st.sb("pt", [P, 2, 2, BANK], F32R)
    ot = st.sb("ot", [P, plan.out_every, 2, NT], F32R)
    top = st.sb("top", [P, 2, NB])
    shift = st.sb("shift", [P, 2, NB])
    total = st.sb("total", [P, 2, NB])
    inv = st.sb("inv", [P, 2, NB])
    if masked:
        neg = st.sb("neg", [P, NB, P], BF16)
        words = prob[:, 1, :, 0:mask_in.shape[2]].bitcast(I32)
        mask = words if mask_in.shape[2] == P else words.bitcast(U8)
        mask_loaded, s_used = st.sem("mask_loaded"), st.sem("s_used")
    if biased:
        bias_raw = st.sb("bias_raw", [P, 2, P])
        bias = st.sb("bias", [P, NB, P])
        valid = st.sb("valid", [P, 2, NB])
        bias_loaded = [st.sem("bias_loaded0"), st.sem("bias_loaded1")]
        bias_ready = st.sem("bias_ready")
    if rope:
        cos, sin = rope_sb
        rot = st.sb("rot", [P, 4, 2, BANK])
        rot_ready, rot_sum, rot_hi, rot_lo = (st.sem(n) for n in ("rot_ready", "rot_sum", "rot_hi", "rot_lo"))
    if qknorm:
        q2 = st.sb("q2", [P, NT])
        k2 = q2[:, 0:BANK].rearrange("p (t i n) -> p t i n", t=2, i=2)
        kn = st.sb("kn", [P, 2, 4, P])
        kss = st.sb("kss", [P, 4, 4])
        kms = st.sb("kms", [P, 4, 4])
        krs = st.sb("krs", [P, 4, 4])
        qms = st.sb("qms", [P, 2, NB])
        qsc = st.sb("qsc", [P, 2, NB])
        half_ = st.sb("half", [P, NB])
        ones = st.sb("ones", [P, 1])
        kqw = st.sb("kqw", [P, 2])
        kw = st.sb("kw", [P, 1])
        kqw_loaded, sq_done, ms_ready, rs_ready, kn_ready = (
            st.sem(n) for n in ("kqw_loaded", "sq_done", "ms_ready", "rs_ready", "kn_ready"))
    pa = st.ps("pa", [P, 2, BANK])
    pscore = st.ps("pscore", [P, 2, BANK])
    ptr = st.ps("ptr", [P, 2, BANK])
    pout = st.ps("pout", [P, 2, BANK])

    raw_loaded = [st.sem("raw_loaded0"), st.sem("raw_loaded1")]
    (split_done, a_ready, a_hi, a_used, s_ready, shift_ready, exp_done, inv_ready, norm_done,
     t_ready, t_hi, t_used, o_ready, o_hi, o_used, own, pool_set, pool_own) = (st.sem(n) for n in (
         "split_done", "a_ready", "a_hi", "a_used", "s_ready", "shift_ready", "exp_done",
         "inv_ready", "norm_done", "t_ready", "t_hi", "t_used", "o_ready", "o_hi", "o_used", "own",
         "pool_set", "pool_own"))
    piece_seen = st.sem("piece_seen")
    s_free = s_used if masked else exp_done
    rounding = Rounding(nc, st, *nf4, NG) if nf4 else None
    norm = TransposedNorm(nc, st, x, ident, h_t, [t[:, n, :] for t in (pscore, ptr) for n in range(2)], *norm_space)

    def side_steps(engine, emit_name, g, last):
        if rounding is None:
            return lambda point, j, calls=1: None
        steps = SideSteps(rounding.on_scalar if emit_name == "scalar" else rounding.on_vector, engine, g, last)
        return lambda point, j, calls=1: steps(NF4_STEPS if point == "rest" else rounding.share.at[point][j] // calls)
    n_first_a, n_group_a = len(plan.first_a()), len(plan.a_order())
    assert n_first_a % 2 == 0 and n_group_a % 2 == 0 and len(plan.w_order()) % 2 == 0
    n_first_w, n_group_w = len(plan.first_w()), len(plan.w_order())
    n_first_ms, n_group_ms = len(plan.ms_of(plan.first_a())), len(plan.ms_of(plan.a_order()))
    n_first_rot, n_group_rot = len(plan.rot_of(plan.first_a())), len(plan.rot_of(plan.a_order()))
    n_set = 1 + (3 if qknorm else 0)

    class Orders:

        def __init__(self, g=None, last=False):
            first = g is None
            self.a_keys = plan.first_a() if first else plan.a_order(last)
            w_keys = plan.first_w() if first else plan.w_order(last)
            at = 0 if first else g

            def places(keys, first_n, group_n):
                return {k: Place(at, group_n, i + (0 if first else first_n)) for i, k in enumerate(keys)}

            fa, ga = plan.first_a(), plan.a_order()
            self.a = places(self.a_keys, len(fa), len(ga))
            self.hi = places(plan.hi_of(self.a_keys), len(plan.hi_of(fa)), len(plan.hi_of(ga)))
            self.ms = places(plan.ms_of(self.a_keys), len(plan.ms_of(fa)), len(plan.ms_of(ga)))
            self.rot = places(plan.rot_of(self.a_keys), len(plan.rot_of(fa)), len(plan.rot_of(ga)))
            self.w = places(w_keys, n_first_w, n_group_w)

    def body(engine, emit):
        with engine.Fori(0, NG - 1) as g:
            emit(g, False)
        emit(NG - 1, True)

    with nc.Block() as block:
        @block.sync
        def _(sp):
            norm.on_sync(sp)
            if qknorm:
                with nc.allow_non_contiguous_dma(reason="256 weights"):
                    sp.dma_start(kqw[:, :], kq_norm_in).then_inc(kqw_loaded, 16)
            if masked:
                sp.dma_start(words, mask_in.rearrange("b q k -> q b k")).then_inc(mask_loaded, 16)

            def load_piece(place):
                if place.filled:
                    sp.wait_ge(split_done, place.last_but_one)
                sp.dma_start(raw[:, place.slot, :], pieces_in[bass.ds(place.before, 1), :, :].rearrange("o p n -> p (o n)")
                             ).then_inc(raw_loaded[place.slot], 16)

            def load_bias(head, slot):
                sp.dma_start(bias_raw[:, slot, :], bias_in[bass.ds(head, 1), :, :].rearrange("o q k -> q (o k)")
                             ).then_inc(bias_loaded[slot], 16)

            for place in Orders().w.values():
                load_piece(place)
            if biased:
                load_bias(0, 0)
                load_bias(1, 1)

            def group(g, last):
                w = Orders(g, last).w
                for j in range(hpg):
                    for key in plan.segment_w(j, last):
                        load_piece(w[key])
                    if biased and plan.in_segment(j, last)[0]:
                        sp.wait_ge(bias_ready, g * hpg + (j + 1))
                        load_bias(g * hpg + (j + 2), j % 2)

            body(sp, group)

        @block.gpsimd
        def _(pool):
            def split_piece(key, place, steps):
                src = raw[:, place.slot, :]
                kind, n = key[0], key[-1]
                dst = {"q": lambda p: wq[:, n % 2, p, :, :], "o": lambda p: wo[:, n % 2, p, :],
                       "k": lambda p: wkv[:, p, :, 0, :] if qknorm else wk[:, n, p, :, :],
                       "v": lambda p: wkv[:, p, :, 1, :] if qknorm else wv[:, p, :, n, :]}[kind]
                if kind != "o":
                    src = src.rearrange("p (c n) -> p c n", c=DC)
                pool.wait_ge(raw_loaded[place.slot], place.turn * 16)
                pool.sem_inc(piece_seen, 1)
                steps.mark(nc.gpsimd.tensor_scalar(dst(HI), src, 1.0, 0.0, ALU.mult, ALU.add))
                steps.wait()
                nc.gpsimd.tensor_tensor(dst(LO), src, dst(HI).bitcast(F32), ALU.subtract).then_inc(split_done, 1)

            def make_bias(slot, turn, used=None):
                pool.wait_ge(bias_loaded[slot], turn * 16)
                if used is not None:
                    pool.wait_ge(s_used, used)
                nc.gpsimd.tensor_tensor(bias[:, :, :], neg[:, :, :],
                                        bias_raw[:, slot, None, :].broadcast_to([P, NB, P]),
                                        ALU.add).then_inc(bias_ready, 1)

            def norm_weights(slot, head, halves=(0, 1)):
                if NS == 2:
                    pool.wait_ge(inv_ready, head + 1)
                for half in halves:
                    if NS == 4:
                        pool.wait_ge(inv_ready, head * 2 + (half + 1))
                    bs = slice(half * NB // 2, (half + 1) * NB // 2)
                    nc.gpsimd.tensor_tensor(prob[:, slot, bs, :], prob[:, slot, bs, :],
                                            inv[:, slot, bs, None].broadcast_to([P, NB // 2, keys]),
                                            ALU.mult).then_inc(norm_done, 1)

            def sum_rotated(key, place):
                tile = key[2] + (2 if key[0] == "k" else 0)
                pool.wait_ge(rot_ready, place.through)
                nc.gpsimd.tensor_tensor(rot[:, tile, 0, :], rot[:, tile, 0, :], rot[:, tile, 1, :],
                                        ALU.add).then_inc(rot_sum, 1)

            def inverse_root(key, place):
                pool.wait_ge(ms_ready, place.through)
                if key[0] == "ss":
                    src, dst = qms[:, key[1] % 2, :], qsc[:, key[1] % 2, :]
                    nc.gpsimd.tensor_tensor(dst, src, half_[:, :], ALU.pow).then_inc(rs_ready, 1)
                else:
                    src, dst = kms[:, key[1], :], krs[:, key[1], :]
                    nc.gpsimd.tensor_tensor(dst, src, half_[:, 0:4], ALU.pow).then_inc(rs_ready, 1)

            norm.on_gpsimd(pool)
            if qknorm:
                nc.gpsimd.memset(half_[:, :], -0.5).then_inc(pool_set, 1)
                nc.gpsimd.memset(ones[:, :], 1.0).then_inc(pool_set, 1)
                pool.wait_ge(kqw_loaded, 16)
                nc.gpsimd.tensor_tensor(kw[:, :], kqw[:, 0:1], kqw[:, 1:2], ALU.mult).then_inc(pool_set, 1)
            if not masked:
                nc.gpsimd.memset(inv[:, :, :], 0.0).then_inc(pool_set, 1)
            else:
                pool.wait_ge(mask_loaded, 16)
                nc.gpsimd.tensor_scalar(neg[:, :, :], mask, 0.0, NEG, ALU.is_equal, ALU.mult).then_inc(pool_set, 1)
            if rounding:
                rounding.set_up_on_gpsimd()
            pool.wait_ge(pool_set, n_set)
            steps = Steps(pool, pool_own)
            o = Orders()
            for key, place in o.w.items():
                if key == ("q", 2):
                    pool.wait_ge(a_ready, o.a["q", 0, 1].through)
                split_piece(key, place, steps)
            if biased:
                make_bias(0, 1)
                make_bias(1, 1, NS)
            if rope:
                for key, place in o.rot.items():
                    sum_rotated(key, place)
            if qknorm:
                for key, place in o.ms.items():
                    inverse_root(key, place)
            norm_weights(0, 0)

            def group(g, last):
                o = Orders(g, last)
                steps = Steps(pool, pool_own, g * n_group_w + n_first_w)
                for j in range(hpg):
                    q_next, score_next, kv_next = plan.in_segment(j, last)
                    tiles = plan.segment_a(j, last)
                    rotated = plan.rot_of(tiles) if rope else []
                    for key in rotated[:1]:
                        sum_rotated(key, o.rot[key])
                    early = score_next and NS == 2 and not kv_next
                    before = 1 if rope and (j + 1) % plan.out_every == 0 else 0 if rope else 2
                    pieces = plan.segment_w(j, last)
                    for n, key in enumerate(pieces + [None]):
                        if early and n == min(before, len(pieces)):
                            norm_weights((j + 1) % 2, g * hpg + (j + 1))
                        if n == min(before, len(pieces)):
                            for tile in rotated[1:]:
                                sum_rotated(tile, o.rot[tile])
                        if key is None:
                            break
                        if key[0] == "o" and plan.out_every == 2 and j % 2 == 0:
                            if j > 0:
                                pool.wait_ge(a_ready, o.a["o", j - 1, NB - 1].through)
                            elif not (isinstance(g, int) and g == 0):
                                pool.wait_ge(a_ready, g * n_group_a + (n_first_a - len(plan.v_keys())))
                        if key[0] == "q" and j > 0:
                            pool.wait_ge(a_ready, o.a["q", j + 1, 1].through)
                        split_piece(key, o.w[key], steps)
                    halves = (0, 1)
                    if score_next and NS == 4 and not kv_next:
                        norm_weights((j + 1) % 2, g * hpg + (j + 1), (0,))
                        halves = (1,)
                    for key in plan.ms_of(tiles):
                        inverse_root(key, o.ms[key])
                    if score_next and not early:
                        norm_weights((j + 1) % 2, g * hpg + (j + 1), halves)
                    if biased and q_next:
                        make_bias(j % 2, g * (hpg // 2) + (j // 2 + 2), (g * hpg + (j + 2)) * NS)

            body(pool, group)

        @block.tensor
        def _(pe):
            def tile_of_a(place):
                if place.filled:
                    pe.wait_ge(a_used, place.last_but_one)
                return pa[:, place.slot, :]

            def query_half(o, head, half):
                out = tile_of_a(o.a["q", head, half])
                for c in range(DC):
                    ins = mm3(nc, out, lambda p: wq[:, head % 2, p, c, :],
                              lambda p: h_t[:, p, c, half * BANK:(half + 1) * BANK], c == 0, c == DC - 1)
                ins.then_inc(a_ready, 1)

            def query_squares(o, head, count):
                out = tile_of_a(o.a["ss", head])
                pe.wait_ge(sq_done, count)
                for b in range(NB):
                    ins = nc.tensor.matmul(out[:, b:b + 1], q2[:, b * P:(b + 1) * P], ones[:, :], start=True, stop=True)
                ins.then_inc(a_ready, 1)

            def keys_of(o):
                for key in plan.k_keys():
                    out = tile_of_a(o.a[key])
                    _, h, half = key
                    for c in range(DC):
                        ins = mm3(nc, out, lambda p: wk[:, h, p, c, :],
                                  lambda p: ctx_t[:, p, c, half * BANK:(half + 1) * BANK], c == 0, c == DC - 1)
                    ins.then_inc(a_ready, 1)

            def keys_and_values(o, key):
                out = tile_of_a(o.a[key])
                for i, src in enumerate((ctx_t, h_t)):
                    for c in range(DC):
                        ins = mm3(nc, out[:, i * 2 * P:(i + 1) * 2 * P], lambda p: src[:, p, c, key[1] * P:(key[1] + 1) * P],
                                  lambda p: wkv[:, p, c, :, :].rearrange("p w n -> p (w n)"), c == 0, c == DC - 1)
                ins.then_inc(a_ready, 1)

            def turned_keys(o, key, kn_before):
                out = tile_of_a(o.a[key])
                pe.wait_ge(kn_ready, kn_before + (key[1] + 1))
                for i in range(4):
                    ins = nc.tensor.transpose(out[:, i * P:(i + 1) * P], kn[:, key[1] % 2, i, :], ident[:, :])
                ins.then_inc(a_ready, 1)

            def values(o):
                for key in plan.v_keys():
                    out = tile_of_a(o.a[key])
                    for i in range(plan.v_per):
                        n = key[1] * plan.v_per + i
                        b, src = n // kvb, (ctx_t, h_t)[n % kvb]
                        for c in range(DC):
                            ins = mm3(nc, out[:, i * plan.vcols:(i + 1) * plan.vcols],
                                      lambda p: src[:, p, c, b * P:(b + 1) * P],
                                      lambda p: wv[:, p, c, :, :], c == 0, c == DC - 1)
                    ins.then_inc(a_ready, 1)

            def score_tiles(slot, kv_head, head, tiles):
                for t in tiles:
                    if not (isinstance(head, int) and head * NS + t < 2):
                        pe.wait_ge(s_free, head * NS + (t - 1))
                    for i in range(bps):
                        b = t * bps + i
                        ins = mm3(nc, pscore[:, t % 2, i * keys:(i + 1) * keys],
                                  lambda p: qt[:, slot, p, b * P:(b + 1) * P],
                                  lambda p: kt[:, kv_head, p, b * keys:(b + 1) * keys])
                    ins.then_inc(s_ready, 1)

            def transpose(j, head, t):
                pe.wait_ge(norm_done, head * 2 + (t * 2 // NS + 1))
                flat = prob[:, j % 2, :, :].rearrange("p b k -> p (b k)")
                pe.wait_ge(t_used, head * NS + (t + 1))
                for i in range(4):
                    ins = nc.tensor.transpose(ptr[:, t % 2, i * P:(i + 1) * P],
                                              flat[:, t * BANK + i * P:t * BANK + (i + 1) * P], ident[:, :])
                ins.then_inc(t_ready, 1)

            def weighed(j, head, n):
                col = (j if plan.own_kv else 0) * P
                pe.wait_ge(o_used, head * 2 + (n + 1))
                for t in range(n * NS // 2, (n + 1) * NS // 2):
                    pe.wait_ge(t_used, head * NS + (t + 3))
                    for i in range(bps):
                        b = t * bps + i
                        for s in range(kvb):
                            cols = slice((i * kvb + s) * P, (i * kvb + s + 1) * P)
                            ins = mm3(nc, pout[:, n, (b % 4) * P:(b % 4 + 1) * P],
                                      lambda p: v[:, p, b * kvb + s, col:col + P],
                                      lambda p: pt[:, t % 2, p, cols], s == 0, s == kvb - 1)
                ins.then_inc(o_ready, 1)

            def output_tiles(o, j, batches):
                heads = range(j - plan.out_every + 1, j + 1)
                for b in batches:
                    out = tile_of_a(o.a["o", j, b])
                    for i in heads:
                        ins = mm3(nc, out, lambda p: ot[:, i % plan.out_every, p, b * P:(b + 1) * P],
                                  lambda p: wo[:, i % 2, p, :], i == heads[0], i == heads[-1])
                    ins.then_inc(a_ready, 1)

            def parts_ready(o, key):
                if rope:
                    pe.wait_ge(rot_lo, o.rot[key].through)
                else:
                    pe.wait_ge(a_used, o.a[key].through)

            norm.on_tensor(pe)
            o = Orders()
            if qknorm:
                pe.wait_ge(pool_set, n_set)
            for head in (0, 1):
                pe.wait_ge(split_done, o.w["q", head].through)
                query_half(o, head, 0)
                query_half(o, head, 1)
                if qknorm:
                    query_squares(o, head, 2 * (head + 1))
            pe.wait_ge(split_done, o.w["k", 0, kvh - 1].through)
            if qknorm:
                pe.wait_ge(split_done, o.w["v", 0, 0].through)
                for key in plan.joint_keys():
                    keys_and_values(o, key) if key[0] == "kv" else turned_keys(o, key, 0)
                for t in range(NS):
                    parts_ready(o, ("kt", t))
                    score_tiles(0, 0, 0, (t,))
            else:
                keys_of(o)
                parts_ready(o, plan.k_keys()[-1])
                score_tiles(0, 0, 0, range(NS))
                pe.wait_ge(split_done, o.w["v", 0, kvh - 1].through)
                values(o)

            def group(g, last):
                o = Orders(g, last)
                for j in range(hpg):
                    head = g * hpg + j
                    q_next, score_next, kv_next = plan.in_segment(j, last)
                    out_now = (j + 1) % plan.out_every == 0
                    early_half = rope and not out_now
                    kv_head = (j + 1) % hpg if plan.own_kv else 0

                    def scores(tiles):
                        score_tiles((j + 1) % 2, kv_head, head + 1, tiles)

                    transpose(j, head, 0)
                    transpose(j, head, 1)
                    if j == 0:
                        pe.wait_ge(a_used, g * n_group_a + n_first_a)
                        if rope:
                            pe.wait_ge(rot_lo, g * n_group_rot + n_first_rot)
                    if score_next and not kv_next:
                        if j > 0:
                            parts_ready(o, ("q", j + 1, 1))
                        scores((0, 1))
                    if q_next:
                        pe.wait_ge(split_done, o.w["q", j + 2].through if j else g * n_group_w + n_first_w)
                        query_half(o, j + 2, 0)
                        if early_half:
                            query_half(o, j + 2, 1)
                    weighed(j, head, 0)
                    if NS == 4:
                        transpose(j, head, 2)
                        transpose(j, head, 3)
                        if score_next and not kv_next:
                            scores((2, 3))
                        if q_next:
                            query_half(o, j + 2, 1)
                        weighed(j, head, 1)
                    else:
                        weighed(j, head, 1)
                        if kv_next:
                            pe.wait_ge(split_done, o.w["k", 1, kvh - 1].through)
                            keys_of(o)
                        if q_next and not early_half:
                            query_half(o, j + 2, 1)
                        if kv_next:
                            parts_ready(o, plan.k_keys()[-1])
                            scores((0, 1))
                    count = g * (2 * hpg) + (4 + 2 * (j + 1))
                    if qknorm and kv_next:
                        pe.wait_ge(split_done, o.w["v", 1, 0].through)
                        for key in plan.joint_keys([("ss", j + 2)])[:-1]:
                            if key[0] == "kv":
                                keys_and_values(o, key)
                            elif key[0] == "kt":
                                turned_keys(o, key, (g + 1) * 4)
                            else:
                                query_squares(o, j + 2, count)
                            if key == ("kt", 2):
                                parts_ready(o, ("kt", 1))
                                scores((0, 1))
                    elif qknorm and q_next:
                        query_squares(o, j + 2, count)
                    if out_now:
                        pe.wait_ge(split_done, o.w["o", j].through)
                        pe.wait_ge(o_used, (head + 1) * 2 + 2)
                        if qknorm and kv_next:
                            output_tiles(o, j, (0, 1))
                            turned_keys(o, ("kt", 3), (g + 1) * 4)
                            output_tiles(o, j, (2, 3))
                            parts_ready(o, ("kt", 3))
                            scores((2, 3))
                            output_tiles(o, j, range(4, NB))
                        else:
                            output_tiles(o, j, range(NB))
                    if kv_next and not qknorm:
                        pe.wait_ge(split_done, o.w["v", 1, kvh - 1].through)
                        values(o)

            body(pe, group)

        @block.scalar
        def _(act):
            def hi(o, key, dst, **scale):
                act.wait_ge(a_ready, o.a[key].through)
                nc.scalar.activation(dst, pa[:, o.a[key].slot, :], ACT.Copy, **scale).then_inc(a_hi, 1)

            def query_hi(o, head, half):
                cols, key = slice(half * BANK, (half + 1) * BANK), ("q", head, half)
                if rope:
                    rotated_hi(o, key, qt[:, head % 2, HI, cols])
                    return
                if qknorm:
                    act.wait_ge(a_ready, o.a[key].through)
                    nc.scalar.activation(q2[:, cols], pa[:, o.a[key].slot, :], ACT.Square).then_inc(sq_done, 1)
                hi(o, key, qt[:, head % 2, HI, cols])

            def rotated_hi(o, key, dst):
                tile = key[2] + (2 if key[0] == "k" else 0)
                act.wait_ge(rot_sum, o.rot[key].through)
                nc.scalar.activation(dst, rot[:, tile, 0, :], ACT.Copy).then_inc(rot_hi, 1)

            def keys_hi(o, side=None):
                for key in plan.k_keys():
                    if side:
                        side("keys", hpg - 1, len(plan.k_keys()))
                    dst = kt[:, key[1], HI, key[2] * BANK:(key[2] + 1) * BANK]
                    (rotated_hi if rope else hi)(o, key, dst)

            def joint_hi(o, key):
                n = key[1]
                if key[0] == "kt":
                    hi(o, key, kt[:, 0, HI, n * BANK:(n + 1) * BANK], scale=kw[:, :])
                    return
                act.wait_ge(a_ready, o.a[key].through)
                src = pa[:, o.a[key].slot, :].rearrange("p (i w n) -> p i w n", i=2, w=2)
                nc.scalar.activation(k2[:, n % 2], src[:, :, 0, :], ACT.Square)
                nc.scalar.activation(kn[:, n // 2 % 2, n % 2 * 2:n % 2 * 2 + 2, :], src[:, :, 0, :], ACT.Copy)
                nc.scalar.activation(v[:, HI, 2 * n:2 * n + 2, :], src[:, :, 1, :], ACT.Copy).then_inc(a_hi, 1)

            def values_hi(o, side=None):
                for key in plan.v_keys():
                    if side:
                        side("values", hpg - 1, len(plan.v_keys()))
                    blocks = slice(key[1] * plan.v_per, (key[1] + 1) * plan.v_per)
                    hi(o, key, v[:, HI, blocks, :].rearrange("p b n -> p (b n)"))

            def exps(slot, head, tiles):
                if masked:
                    act.wait_ge(shift_ready, head + 1)
                for t in tiles:
                    if not masked:
                        act.wait_ge(shift_ready, head * NS + (t + 1))
                    for i in range(bps):
                        b = t * bps + i
                        src, scale = prob[:, slot, b, :], plan.scale
                        if not masked:
                            src, scale = pscore[:, t % 2, i * keys:(i + 1) * keys], qsc[:, slot, b:b + 1]
                        ins = nc.scalar.activation(prob[:, slot, b, :], src, ACT.Exp, bias=shift[:, slot, b:b + 1],
                                                   scale=scale, accum_out=total[:, slot, b:b + 1])
                    if not masked or t == NS - 1:
                        ins.then_inc(exp_done, 1)

            def weight_hi(head, t):
                act.wait_ge(t_ready, head * NS + (t + 1))
                nc.scalar.activation(pt[:, t % 2, HI, :], ptr[:, t % 2, :], ACT.Copy).then_inc(t_hi, 1)

            def weighed_hi(j, head, n):
                act.wait_ge(o_ready, head * 2 + (n + 1))
                nc.scalar.activation(ot[:, j % plan.out_every, HI, n * BANK:(n + 1) * BANK], pout[:, n, :],
                                     ACT.Copy).then_inc(o_hi, 1)

            norm.on_scalar(act)
            if qknorm:
                act.wait_ge(pool_set, n_set)
            if rounding:
                rounding.set_up_on_scalar(act)
            o = Orders()
            for head in (0, 1):
                query_hi(o, head, 0)
                query_hi(o, head, 1)
            if qknorm:
                for key in plan.joint_keys():
                    joint_hi(o, key)
            else:
                keys_hi(o)
            exps(0, 0, range(NS))
            values_hi(o)

            def group(g, last):
                o = Orders(g, last)
                side = side_steps(act, "scalar", g, last)
                for j in range(hpg):
                    head = g * hpg + j
                    q_next, score_next, kv_next = plan.in_segment(j, last)
                    side("weights", j)
                    weight_hi(head, 0)
                    weight_hi(head, 1)
                    if NS == 4:
                        if score_next and not kv_next:
                            exps((j + 1) % 2, head + 1, (0, 1))
                        if q_next:
                            query_hi(o, j + 2, 0)
                        weighed_hi(j, head, 0)
                        weight_hi(head, 2)
                        weight_hi(head, 3)
                        if score_next and not kv_next:
                            exps((j + 1) % 2, head + 1, (2, 3))
                        if q_next:
                            query_hi(o, j + 2, 1)
                        weighed_hi(j, head, 1)
                        if kv_next:
                            for key in plan.joint_keys():
                                joint_hi(o, key)
                                if key == ("kt", 2):
                                    exps((j + 1) % 2, head + 1, (0, 1))
                            exps((j + 1) % 2, head + 1, (2, 3))
                        continue
                    if not kv_next:
                        side("exps", j)
                    if score_next and not kv_next:
                        exps((j + 1) % 2, head + 1, (0, 1))
                    side("queries", j)
                    if q_next and (kv_next or not rope):
                        query_hi(o, j + 2, 0)
                    side("weighed", j)
                    weighed_hi(j, head, 0)
                    weighed_hi(j, head, 1)
                    if q_next and rope and not kv_next:
                        query_hi(o, j + 2, 0)
                    if kv_next:
                        keys_hi(o, side)
                    side("queries_1", j)
                    if q_next:
                        query_hi(o, j + 2, 1)
                    if kv_next:
                        side("exps", j)
                        exps((j + 1) % 2, head + 1, (0, 1))
                    if (j + 1) % plan.out_every == 0:
                        for _ in range(4):
                            side("outputs", j, 4)
                    if kv_next:
                        values_hi(o, side)
                if rounding and last:
                    side("rest", 0)
                    rounding.finish(act)

            body(act, group)

        @block.vector
        def _(dve):
            def lo(o, key, dst, hi_part, scale=None):
                dve.wait_ge(a_hi, o.hi[key].through)
                src = pa[:, o.a[key].slot, :]
                if scale is None:
                    nc.vector.tensor_tensor(dst, src, hi_part.bitcast(F32), ALU.subtract).then_inc(a_used, 1)
                else:
                    nc.vector.scalar_tensor_tensor(dst, src, scale, hi_part.bitcast(F32), ALU.mult,
                                                   ALU.subtract).then_inc(a_used, 1)

            def rotate(o, key):
                half = key[2]
                tile, cols = half + (2 if key[0] == "k" else 0), slice(half * BANK, (half + 1) * BANK)
                src = pa[:, o.a[key].slot, :]
                dve.wait_ge(a_ready, o.a[key].through)
                parts = o.rot[key[0], key[1], 0].before
                if not isinstance(parts, int) or parts:
                    dve.wait_ge(rot_lo, parts)
                nc.vector.tensor_tensor(rot[:, tile, 0, :], src, cos[:, cols], ALU.mult)
                nc.vector.tensor_tensor(rot[0:64, tile, 1, :], src[64:128, :], sin[0:64, cols], ALU.mult)
                ins = nc.vector.tensor_tensor(rot[64:128, tile, 1, :], src[0:64, :], sin[64:128, cols], ALU.mult)
                ins.then_inc(rot_ready, 1)
                dve.wait_ge(rot_ready, o.rot[key].through)
                dve.sem_inc(a_used, 1)

            def rotated_lo(o, key, dst, hi_part):
                tile = key[2] + (2 if key[0] == "k" else 0)
                dve.wait_ge(rot_hi, o.rot[key].through)
                nc.vector.tensor_tensor(dst, rot[:, tile, 0, :], hi_part.bitcast(F32), ALU.subtract).then_inc(rot_lo, 1)

            def query_lo(o, head, half):
                if rope:
                    rotate(o, ("q", head, half))
                else:
                    cols = slice(half * BANK, (half + 1) * BANK)
                    lo(o, ("q", head, half), qt[:, head % 2, LO, cols], qt[:, head % 2, HI, cols])

            def rotated_query_lo(o, head, half):
                cols = slice(half * BANK, (half + 1) * BANK)
                rotated_lo(o, ("q", head, half), qt[:, head % 2, LO, cols], qt[:, head % 2, HI, cols])

            def keys_lo(o, side=None):
                if rope:
                    for key in plan.k_keys():
                        rotate(o, key)
                for key in plan.k_keys():
                    if side:
                        side("keys", hpg - 1, len(plan.k_keys()))
                    cols = slice(key[2] * BANK, (key[2] + 1) * BANK)
                    (rotated_lo if rope else lo)(o, key, kt[:, key[1], LO, cols], kt[:, key[1], HI, cols])

            def joint_lo(o, key, steps):
                n = key[1]
                if key[0] == "kt":
                    cols = slice(n * BANK, (n + 1) * BANK)
                    lo(o, key, kt[:, 0, LO, cols], kt[:, 0, HI, cols], kw[:, :])
                    return
                dve.wait_ge(a_hi, o.hi[key].through)
                steps.mark(nc.vector.reduce_sum(kss[:, n // 2, n % 2 * 2:n % 2 * 2 + 2], k2[:, n % 2], AX.X))
                src = pa[:, o.a[key].slot, :].rearrange("p (i w n) -> p i w n", i=2, w=2)
                nc.vector.tensor_tensor(v[:, LO, 2 * n:2 * n + 2, :], src[:, :, 1, :],
                                        v[:, HI, 2 * n:2 * n + 2, :].bitcast(F32), ALU.subtract).then_inc(a_used, 1)
                if n % 2 == 1:
                    t = n // 2
                    steps.wait()
                    nc.vector.tensor_scalar(kms[:, t, :], kss[:, t, :], 1.0 / P, 1e-6, ALU.mult, ALU.add).then_inc(ms_ready, 1)

            def norm_keys(o, t):
                dve.wait_ge(rs_ready, o.ms["kn", t].through)
                nc.vector.tensor_tensor(kn[:, t % 2, :, :], kn[:, t % 2, :, :],
                                        krs[:, t, :, None].broadcast_to([P, 4, P]), ALU.mult).then_inc(kn_ready, 1)

            def values_lo(o, side=None):
                for key in plan.v_keys():
                    if side:
                        side("values", hpg - 1, len(plan.v_keys()))
                    blocks = slice(key[1] * plan.v_per, (key[1] + 1) * plan.v_per)
                    lo(o, key, v[:, LO, blocks, :].rearrange("p b n -> p (b n)"),
                       v[:, HI, blocks, :].rearrange("p b n -> p (b n)"))

            def shifts(slot, head, tiles, steps):
                if not masked:
                    for t in tiles:
                        bs = slice(t * bps, (t + 1) * bps)
                        dve.wait_ge(s_ready, head * NS + (t + 1))
                        steps.mark(nc.vector.reduce_max(top[:, slot, bs], pscore[:, t % 2, :].rearrange("p (b k) -> p b k", k=keys), AX.X))
                        steps.wait()
                        nc.vector.scalar_tensor_tensor(shift[:, slot, bs], top[:, slot, bs], -1.0, qsc[:, slot, bs],
                                                       ALU.mult, ALU.mult).then_inc(shift_ready, 1)
                    return
                if biased:
                    dve.wait_ge(bias_ready, head + 1)
                for t in range(NS):
                    bs = slice(t * bps, (t + 1) * bps)
                    dve.wait_ge(s_ready, head * NS + (t + 1))
                    add = bias[:, bs, :] if biased else neg[:, bs, :]
                    nc.vector.tensor_tensor(prob[:, slot, bs, :], pscore[:, t % 2, :].rearrange("p (b k) -> p b k", k=keys),
                                            add, ALU.add).then_inc(s_used, 1)
                dve.wait_ge(s_used, head * NS + NS)
                steps.mark(nc.vector.reduce_max(top[:, slot, :], prob[:, slot, :, :], AX.X))
                steps.wait()
                if biased:
                    steps.mark(nc.vector.tensor_scalar(valid[:, slot, :], top[:, slot, :], NEG / 2, None, ALU.is_gt))
                nc.vector.tensor_scalar(shift[:, slot, :], top[:, slot, :], -plan.scale, None, ALU.mult).then_inc(shift_ready, 1)

            def inverse(slot, head, steps, halves=(0, 1)):
                if NS == 4:
                    for half in halves:
                        bs = slice(half * 4, half * 4 + 4)
                        dve.wait_ge(exp_done, head * NS + 2 * (half + 1))
                        nc.vector.reciprocal(inv[:, slot, bs], total[:, slot, bs]).then_inc(inv_ready, 1)
                    return
                dve.wait_ge(exp_done, head + 1)
                if not biased:
                    nc.vector.reciprocal(inv[:, slot, :], total[:, slot, :]).then_inc(inv_ready, 1)
                    return
                steps.mark(nc.vector.reciprocal(inv[:, slot, :], total[:, slot, :]))
                steps.wait()
                nc.vector.tensor_tensor(inv[:, slot, :], inv[:, slot, :], valid[:, slot, :], ALU.mult).then_inc(inv_ready, 1)

            def weight_lo(head, t):
                dve.wait_ge(t_hi, head * NS + (t + 1))
                nc.vector.tensor_tensor(pt[:, t % 2, LO, :], ptr[:, t % 2, :], pt[:, t % 2, HI, :].bitcast(F32),
                                        ALU.subtract).then_inc(t_used, 1)

            def weighed_lo(j, head, n):
                dve.wait_ge(o_hi, head * 2 + (n + 1))
                cols = slice(n * BANK, (n + 1) * BANK)
                nc.vector.tensor_tensor(ot[:, j % plan.out_every, LO, cols], pout[:, n, :],
                                        ot[:, j % plan.out_every, HI, cols].bitcast(F32),
                                        ALU.subtract).then_inc(o_used, 1)

            def add_output(o, j, batches):
                for b in batches:
                    dve.wait_ge(a_ready, o.a["o", j, b].through)
                    nc.vector.tensor_tensor(x[:, b, :], pa[:, o.a["o", j, b].slot, :], x[:, b, :],
                                            ALU.add).then_inc(a_used, 1)

            def query_scale(o, head):
                key = ("ss", head)
                dve.wait_ge(a_ready, o.a[key].through)
                nc.vector.tensor_scalar(qms[:, head % 2, :], pa[:, o.a[key].slot, 0:NB], P * 1e-6, None, ALU.add
                                        ).then_inc(ms_ready, 1)
                dve.wait_ge(ms_ready, o.ms[key].through)
                dve.sem_inc(a_used, 1)

            NORMED_AFTER = {("kv", 2): 0, ("kv", 4): 1, ("kv", 6): 2, ("kt", 2): 3}

            norm.on_vector(dve)
            dve.sem_inc(t_used, 2)
            dve.sem_inc(o_used, 2)
            if rounding:
                rounding.set_up_on_vector(dve)
            if masked or qknorm:
                dve.wait_ge(pool_set, n_set)
            o = Orders()
            steps = Steps(dve, own)
            for head in (0, 1):
                for half in range(2):
                    query_lo(o, head, half)
                    if rope:
                        rotated_query_lo(o, head, half)
                if qknorm:
                    query_scale(o, head)
            if qknorm:
                for key in plan.joint_keys():
                    joint_lo(o, key, steps)
                    if key in NORMED_AFTER:
                        norm_keys(o, NORMED_AFTER[key])
                dve.wait_ge(rs_ready, n_first_ms)
            else:
                keys_lo(o)
            shifts(0, 0, range(NS), steps)
            inverse(0, 0, steps)
            values_lo(o)
            own_first = steps.n
            own_group = hpg * ((3 if biased else 1) if masked else NS) + (8 if qknorm else 0)

            def group(g, last):
                o = Orders(g, last)
                side = side_steps(dve, "vector", g, last)
                steps = Steps(dve, own, g * own_group + own_first)
                for j in range(hpg):
                    head = g * hpg + j
                    q_next, score_next, kv_next = plan.in_segment(j, last)
                    out_now = (j + 1) % plan.out_every == 0

                    def next_shifts(tiles):
                        shifts((j + 1) % 2, head + 1, tiles, steps)

                    side("weights", j)
                    weight_lo(head, 0)
                    weight_lo(head, 1)
                    if score_next and qknorm:
                        dve.wait_ge(rs_ready, o.ms["ss", j + 1].through if j else g * n_group_ms + n_first_ms)
                    if score_next and not kv_next:
                        next_shifts((0, 1))
                    if kv_next and rounding:
                        side("queries", j)
                    if q_next and (rope or NS == 4 or kv_next):
                        query_lo(o, j + 2, 0)
                    if not kv_next:
                        side("exps", j)
                    if score_next and NS == 2 and not kv_next:
                        inverse((j + 1) % 2, head + 1, steps)
                    if not (kv_next and rounding):
                        side("queries", j)
                    if q_next and not (rope or NS == 4 or kv_next):
                        query_lo(o, j + 2, 0)
                    if q_next and rope and not out_now:
                        query_lo(o, j + 2, 1)
                    side("weighed", j)
                    weighed_lo(j, head, 0)
                    if NS == 4:
                        weight_lo(head, 2)
                        weight_lo(head, 3)
                        if score_next and not kv_next:
                            inverse((j + 1) % 2, head + 1, steps, (0,))
                            next_shifts((2, 3))
                        if q_next:
                            query_lo(o, j + 2, 1)
                        weighed_lo(j, head, 1)
                        if kv_next:
                            for key in plan.joint_keys([("ss", j + 2)])[:-1]:
                                query_scale(o, j + 2) if key[0] == "ss" else joint_lo(o, key, steps)
                                if key in NORMED_AFTER:
                                    norm_keys(o, NORMED_AFTER[key])
                            next_shifts((0, 1))
                            inverse((j + 1) % 2, head + 1, steps, (0,))
                        elif q_next:
                            query_scale(o, j + 2)
                        if score_next and not out_now:
                            inverse((j + 1) % 2, head + 1, steps, (1,))
                    else:
                        weighed_lo(j, head, 1)
                        if kv_next:
                            if rope:
                                rotated_query_lo(o, j + 2, 0)
                            keys_lo(o, side)
                        side("queries_1", j)
                        if q_next and not (rope and not out_now):
                            query_lo(o, j + 2, 1)
                        if kv_next:
                            next_shifts((0, 1))
                            side("exps", j)
                        elif q_next and rope:
                            rotated_query_lo(o, j + 2, 0)
                    if out_now:
                        dve.wait_ge(a_used, o.a["o", j, 0].before)
                        if NS == 4 and kv_next:
                            add_output(o, j, (0, 1))
                            joint_lo(o, ("kt", 3), steps)
                            add_output(o, j, (2, 3))
                            next_shifts((2, 3))
                        else:
                            add_output(o, j, range(4))
                        if q_next and rope:
                            rotated_query_lo(o, j + 2, 1)
                        if score_next and (NS == 4 or kv_next):
                            inverse((j + 1) % 2, head + 1, steps, (1,) if NS == 4 else (0, 1))
                        for b in range(4, NB):
                            add_output(o, j, (b,))
                            side("outputs", j, 4)
                    elif q_next and rope:
                        rotated_query_lo(o, j + 2, 1)
                    if kv_next:
                        values_lo(o, side)
                if rounding and last:
                    side("rest", 0)
                assert last or steps.n == own_group, (steps.n, own_group)

            body(dve, group)
            dve.wait_ge(a_used, (NG - 1) * n_group_a + n_first_a + len(plan.a_order(True)))
    st.close()



MAX_POS = 512
ROOT_SCALE = float(P) ** -0.25


def rope_stage(nc, cos, sin, pos_in, iota_in, tables_in):
    st = Stage(nc, "rope")
    pos_i = st.sb("pos_i", [P, NT], I32)
    pos = st.sb("pos", [P, NT])
    below = st.sb("below", [P, NT])
    iota = st.sb("iota", [P, DC])
    hot = st.sb("hot", [P, DC, NT], F32R)
    tab = st.sb("tab", [P, DC, 2, P])
    pair = st.sb("pair", [P, 2, DC, 2, P], F32R)
    acc = st.ps("acc", [P, 2, 2, BANK])
    loaded, own, split_done, hot_ready, made, copied = (
        st.sem(n) for n in ("loaded", "own", "split_done", "hot_ready", "made", "copied"))
    with nc.Block() as block:
        @block.sync
        def _(sp):
            sp.dma_start(pos_i[:, :], pos_in.rearrange("(o b) t -> o (b t)", o=1).broadcast_to([P, NT])
                         ).then_inc(loaded, 16)
            sp.dma_start(iota[:, :], iota_in).then_inc(loaded, 16)
            for w in range(2):
                sp.dma_start(tab[:, :, w, :], tables_in[w].rearrange("(c p) d -> p c d", p=P)).then_inc(loaded, 16)

        @block.vector
        def _(dve):
            steps = Steps(dve, own)
            dve.wait_ge(loaded, 64)
            steps.mark(nc.vector.tensor_scalar(below[:, :], pos_i[:, :], 0.0, float(MAX_POS), ALU.is_lt, ALU.mult))
            steps.mark(nc.vector.tensor_copy(pos[:, :], pos_i[:, :]))
            steps.wait()
            steps.mark(nc.vector.tensor_tensor(pos[:, :], pos[:, :], below[:, :], ALU.add))
            steps.wait()
            steps.mark(nc.vector.tensor_scalar(pos[:, :], pos[:, :], 0.0, MAX_POS - 1.0, ALU.max, ALU.min))
            steps.mark(nc.vector.tensor_copy(pair[:, HI, :, :, :], tab[:, :, :, :]))
            steps.wait()
            nc.vector.tensor_tensor(pair[:, LO, :, :, :], tab[:, :, :, :], pair[:, HI, :, :, :].bitcast(F32),
                                    ALU.subtract).then_inc(split_done, 1)
            for c in range(DC):
                nc.vector.tensor_scalar(hot[:, c, :], pos[:, :], iota[:, c:c + 1], None,
                                        ALU.is_equal).then_inc(hot_ready, 1)
            for w, dst in enumerate((cos, sin)):
                for half in range(2):
                    dve.wait_ge(made, 2 * w + half + 1)
                    nc.vector.tensor_scalar(dst[:, half * BANK:(half + 1) * BANK], acc[:, w, half, :], ROOT_SCALE, None,
                                            ALU.mult).then_inc(copied, 1)
            dve.wait_ge(copied, 4)

        @block.tensor
        def _(pe):
            pe.wait_ge(split_done, 1)
            pe.wait_ge(hot_ready, DC)
            for w in range(2):
                for half in range(2):
                    for c in range(DC):
                        for part in (HI, LO):
                            ins = nc.tensor.matmul(acc[:, w, half, :], pair[:, part, c, w, :],
                                                   hot[:, c, half * BANK:(half + 1) * BANK],
                                                   start=c == 0 and part == HI, stop=c == DC - 1 and part == LO)
                    ins.then_inc(made, 1)
    st.close()



E0, R0 = 8, 16


def ffn0_stage(nc, x, ident, h_t, base_in, side_in, lora_b_in, b_base_in, b_router_in):
    st = Stage(nc, "f0")
    SIDE = E0 * R0 + E0
    raw = st.sb("raw", [P, DC, D])
    base = st.sb("base", [P, 2, DC, D], F32R)
    raw_side = st.sb("raw_side", [P, DC, SIDE])
    side = st.sb("side", [P, 2, DC, SIDE], F32R)
    raw_b = st.sb("raw_b", [P, D])
    lora_b = st.sb("lora_b", [P, 2, D], F32R)
    b_base = st.sb("b_base", [P, D])
    b_router = st.sb("b_router", [P, E0])
    low = st.sb("low", [P, NB, E0 * R0])
    z = st.sb("z", [P, NB, E0])
    zs = st.sb("zs", [P, NB, E0])
    cum = st.sb("cum", [P, NB, E0])
    rank = st.sb("rank", [P, E0])
    sup = st.sb("sup", [P, NB, E0])
    count = st.sb("count", [P, NB])
    tau = st.sb("tau", [P, NB])
    rcount = st.sb("rcount", [P, NB])
    gated = st.sb("gated", [P, 2, NB, P], F32R)
    p_side = st.ps("p_side", [P, 2, BANK])
    p_tr = st.ps("p_tr", [P, 2, BANK])
    p_out = st.ps("p_out", [P, 2, BANK])
    (loaded, loaded_side, side_split, base_split, side_ready, side_used, own, gate_ready, tr_ready, tr_hi, tr_lo,
     out_ready, out_used, ranked) = (st.sem(n) for n in (
         "loaded", "loaded_side", "side_split", "base_split", "side_ready", "side_used", "own", "gate_ready",
         "tr_ready", "tr_hi", "tr_lo", "out_ready", "out_used", "ranked"))
    norm = TransposedNorm(nc, st, x, ident, h_t, [t[:, n, :] for t in (p_side, p_tr) for n in range(2)],
                          st.sb("norm_space", [P, 11 * NB]), st.sb("norm_h", [P, NB, D]))
    with nc.Block() as block:
        @block.sync
        def _(sp):
            sp.dma_start(raw_side[:, :, :], side_in.rearrange("(c p) n -> p c n", p=P)).then_inc(loaded_side, 16)
            sp.dma_start(b_router[:, :], b_router_in.rearrange("(o n) -> o n", o=1).broadcast_to([P, E0])
                         ).then_inc(loaded_side, 16)
            sp.dma_start(raw[:, :, :], base_in.rearrange("(c p) n -> p c n", p=P)).then_inc(loaded, 16)
            sp.dma_start(raw_b[:, :], lora_b_in).then_inc(loaded, 16)
            sp.dma_start(b_base[:, :], b_base_in.rearrange("(o n) -> o n", o=1).broadcast_to([P, D])).then_inc(loaded, 16)

        @block.gpsimd
        def _(pool):
            norm.on_gpsimd(pool)
            for e in range(E0):
                nc.gpsimd.memset(rank[:, e:e + 1], float(e + 1)).then_inc(ranked, 1)
            pool.wait_ge(loaded, 48)
            nc.gpsimd.tensor_scalar(base[:, HI, :, :], raw[:, :, :], 1.0, 0.0, ALU.mult, ALU.add).then_inc(base_split, 1)
            nc.gpsimd.tensor_scalar(lora_b[:, HI, :], raw_b[:, :], 1.0, 0.0, ALU.mult, ALU.add).then_inc(base_split, 1)
            pool.wait_ge(base_split, 2)
            nc.gpsimd.tensor_tensor(base[:, LO, :, :], raw[:, :, :], base[:, HI, :, :].bitcast(F32),
                                    ALU.subtract).then_inc(base_split, 1)
            nc.gpsimd.tensor_tensor(lora_b[:, LO, :], raw_b[:, :], lora_b[:, HI, :].bitcast(F32),
                                    ALU.subtract).then_inc(base_split, 1)

        @block.tensor
        def _(pe):
            norm.on_tensor(pe)
            pe.wait_ge(side_split, 1)
            for b in range(NB):
                if b >= 2:
                    pe.wait_ge(side_used, b - 1)
                for c in range(DC):
                    ins = mm3(nc, p_side[:, b % 2, 0:SIDE], lambda p: h_t[:, p, c, b * P:(b + 1) * P],
                              lambda p: side[:, p, c, :], c == 0, c == DC - 1)
                ins.then_inc(side_ready, 1)
            pe.wait_ge(base_split, 4)
            for b in range(NB):
                if b >= 2:
                    pe.wait_ge(out_used, b - 1)
                for c in range(DC):
                    mm3(nc, p_out[:, b % 2, :], lambda p: h_t[:, p, c, b * P:(b + 1) * P],
                        lambda p: base[:, p, c, :], c == 0, False)
                if b % 4 == 0:
                    pe.wait_ge(gate_ready, 1)
                    for i in range(4):
                        ins = nc.tensor.transpose(p_tr[:, b // 4, i * P:(i + 1) * P], low[:, b + i, :], ident[:, :])
                    ins.then_inc(tr_ready, 1)
                    pe.wait_ge(tr_lo, b // 4 + 1)
                ins = mm3(nc, p_out[:, b % 2, :], lambda p: gated[:, p, b, :], lambda p: lora_b[:, p, :], False, True)
                ins.then_inc(out_ready, 1)

        @block.scalar
        def _(act):
            norm.on_scalar(act)
            for t in range(2):
                act.wait_ge(tr_ready, t + 1)
                nc.scalar.activation(gated[:, HI, 4 * t:4 * t + 4, :].rearrange("p b n -> p (b n)"), p_tr[:, t, :],
                                     ACT.Copy).then_inc(tr_hi, 1)

        @block.vector
        def _(dve):
            norm.on_vector(dve)
            steps = Steps(dve, own)
            dve.wait_ge(loaded_side, 32)
            steps.mark(nc.vector.tensor_copy(side[:, HI, :, :], raw_side[:, :, :]))
            steps.wait()
            nc.vector.tensor_tensor(side[:, LO, :, :], raw_side[:, :, :], side[:, HI, :, :].bitcast(F32),
                                    ALU.subtract).then_inc(side_split, 1)
            for b in range(NB):
                dve.wait_ge(side_ready, b + 1)
                steps.mark(nc.vector.tensor_tensor(z[:, b, :], p_side[:, b % 2, E0 * R0:SIDE], b_router[:, :], ALU.add))
                nc.vector.tensor_copy(low[:, b, :], p_side[:, b % 2, 0:E0 * R0]).then_inc(side_used, 1)
            steps.wait()
            for b in range(NB):
                steps.mark(nc.vector.max(zs[:, b, :], z[:, b, :]))
            steps.wait()
            steps.mark(nc.vector.tensor_copy(cum[:, :, 0:1], zs[:, :, 0:1]))
            for e in range(1, E0):
                steps.wait()
                steps.mark(nc.vector.tensor_tensor(cum[:, :, e:e + 1], cum[:, :, e - 1:e], zs[:, :, e:e + 1], ALU.add))
            dve.wait_ge(ranked, E0)
            ranks = rank[:, None, :].broadcast_to([P, NB, E0])
            steps.mark(nc.vector.tensor_tensor(sup[:, :, :], zs[:, :, :], ranks, ALU.mult))
            steps.wait()
            steps.mark(nc.vector.tensor_scalar(sup[:, :, :], sup[:, :, :], 1.0, None, ALU.add))
            steps.wait()
            steps.mark(nc.vector.tensor_tensor(sup[:, :, :], sup[:, :, :], cum[:, :, :], ALU.is_gt))
            steps.wait()
            steps.mark(nc.vector.reduce_sum(count[:, :], sup[:, :, :], AX.X))
            steps.wait()
            steps.mark(nc.vector.tensor_tensor(sup[:, :, :], ranks, count[:, :, None].broadcast_to([P, NB, E0]), ALU.is_equal))
            steps.mark(nc.vector.reciprocal(rcount[:, :], count[:, :]))
            steps.wait()
            steps.mark(nc.vector.tensor_tensor(sup[:, :, :], sup[:, :, :], cum[:, :, :], ALU.mult))
            steps.wait()
            steps.mark(nc.vector.reduce_sum(tau[:, :], sup[:, :, :], AX.X))
            steps.wait()
            steps.mark(nc.vector.scalar_tensor_tensor(tau[:, :], tau[:, :], -1.0, rcount[:, :], ALU.add, ALU.mult))
            steps.wait()
            steps.mark(nc.vector.tensor_tensor(z[:, :, :], z[:, :, :], tau[:, :, None].broadcast_to([P, NB, E0]), ALU.subtract))
            steps.wait()
            steps.mark(nc.vector.tensor_scalar(z[:, :, :], z[:, :, :], 0.0, None, ALU.max))
            steps.wait()
            dve.wait_ge(side_used, NB)
            lowr = low[:, :, :].rearrange("p b (e r) -> p (b e) r", r=R0)
            gate = z[:, :, :].rearrange("p b e -> p (b e)")[:, :, None].broadcast_to([P, NB * E0, R0])
            nc.vector.tensor_tensor(lowr, lowr, gate, ALU.mult).then_inc(gate_ready, 1)
            dve.wait_ge(loaded, 48)
            for b in range(NB):
                steps.mark(nc.vector.tensor_tensor(x[:, b, :], x[:, b, :], b_base[:, :], ALU.add))
            for t in range(2):
                dve.wait_ge(tr_hi, t + 1)
                dst = gated[:, LO, 4 * t:4 * t + 4, :].rearrange("p b n -> p (b n)")
                hi = gated[:, HI, 4 * t:4 * t + 4, :].rearrange("p b n -> p (b n)")
                nc.vector.tensor_tensor(dst, p_tr[:, t, :], hi.bitcast(F32), ALU.subtract).then_inc(tr_lo, 1)
                steps.wait()
                for b in range(4 * t, 4 * t + 4):
                    dve.wait_ge(out_ready, b + 1)
                    nc.vector.tensor_tensor(x[:, b, :], p_out[:, b % 2, :], x[:, b, :], ALU.add).then_inc(out_used, 1)
            dve.wait_ge(out_used, NB)
    st.close()



DK = 64
PH = 8
DH = DK // PH
ROWS = 32
VC = 10


def norm_natural_stage(nc, name, x, h):
    st = Stage(nc, name)
    norm = Norm(st, st.sb("space", [P, 11 * NB]))
    own, done = st.sem("own"), st.sem("done")
    with nc.Block() as block:
        @block.gpsimd
        def _(pool):
            norm.set_half(nc)
            norm.rstd_on_gpsimd(nc, pool)

        @block.vector
        def _(dve):
            norm.stats_on_vector(nc, Steps(dve, own), x)
            dve.wait_ge(norm.rstd_ready, 1)
            for b in range(NB):
                norm.apply(nc, b, h[:, b, :], x).then_inc(done, 1)
            dve.wait_ge(done, NB)
    st.close()


def patch_attention_stage(nc, x, h, ident, ctx_in, mask_in, wqk_in, wv_in, wo_in, bqk_in, flag_in, bv_in, bo_in):
    st = Stage(nc, "a1")
    NP = D // P
    raw_w = st.sb("raw_w", [P, 4 * P + DK])
    w = st.sb("w", [P, 2, 4 * P + DK], F32R)
    raw_o = st.sb("raw_o", [DK, P])
    wo = st.sb("wo", [DK, 2, P], F32R)
    bqk = st.sb("bqk", [P, 4])
    flag = st.sb("flag", [P, 1])
    bv = st.sb("bv", [P, DK])
    bo = st.sb("bo", [P, 1])
    mask = st.sb("mask", [P, 2, D])
    keep = st.sb("keep", [P, D])
    gone = st.sb("gone", [P, D])
    hp = st.sb("hp", [P, 2, D], F32R)
    ctx = st.sb("ctx", [P, 2, D])
    cp = st.sb("cp", [P, 2, D], F32R)
    k32 = st.sb("k32", [P, 2, 2, D])
    qp = st.sb("qp", [P, 2, 2, 2, D], F32R)
    kd = st.sb("kd", [P, 2, 2, 2, 4, P], F32R)
    v32 = st.sb("v32", [P, NP, DK])
    vp = st.sb("vp", [P, 2, 2, NP, PH, VC], F32R)
    top = st.sb("top", [P, 2, PH])
    e = st.sb("e", [P, 2, PH, P])
    ep = st.sb("ep", [P, 2, 2, 4, P], F32R)
    rs = st.sb("rs", [P, PH])
    o32 = st.sb("o32", [P, 2, DK])
    o_all = st.sb("o_all", [DK, NB, D])
    gp = st.sb("gp", [DK, 2, 2, D], F32R)
    y = st.sb("y", [P, D])
    pj = st.ps("pj", [P, 2, BANK])
    psc = st.ps("psc", [P, 2, BANK])
    ptr = st.ps("ptr", [P, 2, BANK])
    pov = st.ps("pov", [P, BANK])
    pot = st.ps("pot", [P, BANK])
    names = ("w_loaded w_split own split_hi split pj_ready pj_used q_hi k_ready kd_hi kd_lo v_ready vp_hi vp_ready "
             "mask_ready sc_ready sc_used e_ready exp_done tr_ready tr_hi tr_used pv_ready o_ready o_seen ot_ready "
             "ot_copied g_ready g_hi g_lo y_ready y_used x_done zeros_set pool_own kd_part mask_seen").split()
    (w_loaded, w_split, own, split_hi, split, pj_ready, pj_used, q_hi, k_ready, kd_hi, kd_lo, v_ready, vp_hi, vp_ready,
     mask_ready, sc_ready, sc_used, e_ready, exp_done, tr_ready, tr_hi, tr_used, pv_ready, o_ready, o_seen, ot_ready,
     ot_copied, g_ready, g_hi, g_lo, y_ready, y_used, x_done, zeros_set, pool_own, kd_part, mask_seen) = (st.sem(n) for n in names)
    loaded = [st.sem("loaded0"), st.sem("loaded1")]
    mask_again = [st.sem("mask_again0"), st.sem("mask_again1")]
    INV = 1.0 / math.sqrt(DH)
    PJ = 5
    LAST = NB * NP - 1

    def wait(engine, sem, value):
        if not (isinstance(value, int) and value <= 0):
            engine.wait_ge(sem, value)

    def body(engine, patch):
        with engine.Fori(0, NB // 2 - 1) as g:
            for slot in range(2):
                for s in range(NP):
                    patch(g * 2 + slot, slot, s, True, True)
        for slot in range(2):
            for s in range(NP):
                patch(NB - 2 + slot, slot, s, slot == 0, False)

    def rows(i):
        return slice(ROWS * i, ROWS * (i + 1))

    def slots(slot, s, ahead):
        return (slot + (s + ahead) // NP) % 2, (s + ahead) % NP

    with nc.Block() as block:
        @block.sync
        def _(sp):
            sp.dma_start(raw_w[:, 0:4 * P], wqk_in).then_inc(w_loaded, 16)
            sp.dma_start(raw_w[:, 4 * P:], wv_in).then_inc(w_loaded, 16)
            sp.dma_start(raw_o[:, :], wo_in).then_inc(w_loaded, 16)
            with nc.allow_non_contiguous_dma(reason="a few columns"):
                sp.dma_start(bqk[:, :], bqk_in).then_inc(w_loaded, 16)
                sp.dma_start(flag[:, :], flag_in).then_inc(w_loaded, 16)
                sp.dma_start(bo[:, :], bo_in.rearrange("(p o) -> p o", o=1)).then_inc(w_loaded, 16)
            sp.dma_start(bv[:, :], bv_in.rearrange("(o n) -> o n", o=1).broadcast_to([P, DK])).then_inc(w_loaded, 16)

            def load_mask(b, slot, sem):
                sp.dma_start(mask[:, slot, :], mask_in[bass.ds(b, 1), :].broadcast_to([P, D])).then_inc(sem, 16)

            def load(b, slot):
                load_mask(b, slot, loaded[slot])
                sp.dma_start(ctx[:, slot, :], ctx_in[bass.ds(b, 1), :, :].rearrange("o p n -> p (o n)")
                             ).then_inc(loaded[slot], 16)

            load(0, 0)
            load(1, 1)
            with sp.Fori(0, NB // 2 - 1) as g:
                for slot in range(2):
                    sp.wait_ge(split, g * 4 + (2 * slot + 2))
                    sp.wait_ge(mask_ready, g * 2 + (slot + 1))
                    load(g * 2 + (slot + 2), slot)
            for b in range(NB):
                sp.wait_ge(mask_ready, NB)
                if b >= 2:
                    sp.wait_ge(y_used, b - 1)
                load_mask(b, b % 2, mask_again[b % 2])

        @block.gpsimd
        def _(pool):
            nc.gpsimd.memset(kd[:, :, :, :, :, :].bitcast(F32), 0.0).then_inc(zeros_set, 1)
            nc.gpsimd.memset(vp[:, :, HI, :, :, DH:VC].bitcast(F32), 1.0).then_inc(zeros_set, 1)
            nc.gpsimd.memset(vp[:, :, LO, :, :, DH:VC].bitcast(F32), 0.0).then_inc(zeros_set, 1)

            def masks(b, slot, turn):
                pool.wait_ge(loaded[slot], turn * 32)
                wait(pool, k_ready, b)
                pool.sem_inc(mask_seen, 1)
                steps = Steps(pool, pool_own, b * 2)
                steps.mark(nc.gpsimd.tensor_scalar(keep[:, :], mask[:, slot, :], 0.0, 1.0, ALU.is_gt, ALU.mult))
                steps.wait()
                pool.sem_inc(mask_seen, 1)
                steps.mark(nc.gpsimd.tensor_scalar(gone[:, :], keep[:, :], 0.0, NEG, ALU.is_equal, ALU.mult))
                steps.wait()
                nc.gpsimd.tensor_tensor(gone[:, :], gone[:, :], flag[:, 0:1].broadcast_to([P, D]),
                                        ALU.mult).then_inc(mask_ready, 1)

            def keys_lo(n, pslot, bslot, s):
                pool.wait_ge(kd_hi, n + 1)
                for i in range(4):
                    nc.gpsimd.tensor_tensor(
                        kd[rows(i), pslot, LO, :, i, :], k32[rows(i), bslot, :, s * P:(s + 1) * P],
                        kd[rows(i), pslot, HI, :, i, :].bitcast(F32), ALU.subtract).then_inc(kd_part, 1)
                    pool.wait_ge(kd_part, n * 4 + (i + 1))
                pool.sem_inc(kd_lo, 1)

            def values_lo(b, slot):
                pool.wait_ge(vp_hi, b + 1)
                nc.gpsimd.tensor_tensor(
                    vp[:, slot, LO, :, :, 0:DH].rearrange("p s h d -> p (s h) d"),
                    v32[:, :, :].rearrange("p s (h d) -> p (s h) d", d=DH),
                    vp[:, slot, HI, :, :, 0:DH].rearrange("p s h d -> p (s h) d").bitcast(F32),
                    ALU.subtract).then_inc(vp_ready, 1)

            pool.wait_ge(w_loaded, 7 * 16)
            masks(0, 0, 1)
            keys_lo(0, 0, 0, 0)
            keys_lo(1, 1, 0, 1)
            values_lo(0, 0)
            keys_lo(2, 0, 0, 2)
            masks(1, 1, 1)

            def patch(b, slot, s, has1):
                if has1 or s + 3 < NP:
                    bslot, ahead = slots(slot, s, 3)
                    keys_lo(b * NP + (s + 3), (s + 1) % 2, bslot, ahead)
                if s == 2 and has1:
                    values_lo(b + 1, 1 - slot)

            with pool.Fori(0, NB // 2 - 1) as g:
                for slot in range(2):
                    for s in range(NP):
                        patch(g * 2 + slot, slot, s, True)
                    masks(g * 2 + (slot + 2), slot, g + 2)
            for slot in range(2):
                for s in range(NP):
                    patch(NB - 2 + slot, slot, s, slot == 0)

        @block.tensor
        def _(pe):
            def project(b, slot, tiles):
                for i in tiles:
                    if i == 0:
                        pe.wait_ge(split, b * 2 + 2)
                    wait(pe, pj_used, b * PJ + (i - 1 if i else 0))
                    if i < 4:
                        t = (i + 2) % 4
                        mm3(nc, pj[:, i % 2, :], lambda p: w[:, p, t * P:(t + 1) * P], lambda p: hp[:, p, :]
                            ).then_inc(pj_ready, 1)
                        continue
                    for s in range(NP):
                        ins = mm3(nc, pj[:, 0, s * DK:(s + 1) * DK], lambda p: cp[:, p, s * P:(s + 1) * P],
                                  lambda p: w[:, p, 4 * P:])
                    ins.then_inc(pj_ready, 1)

            def scores(n, pslot, bslot, s):
                pe.wait_ge(kd_lo, n + 1)
                for t in range(2):
                    wait(pe, sc_used, n * 2 + (t - 1))
                    mm3(nc, psc[:, t, :], lambda p: qp[:, bslot, p, t, s * P:(s + 1) * P],
                        lambda p: kd[:, pslot, p, t, :, :].rearrange("p i j -> p (i j)")).then_inc(sc_ready, 1)

            def transposes(n, pslot):
                pe.wait_ge(exp_done, n + 1)
                for t in range(2):
                    pe.wait_ge(tr_used, n * 2 + (t + 1))
                    for i in range(4):
                        ins = nc.tensor.transpose(ptr[:, t, i * P:(i + 1) * P], e[:, pslot, 4 * t + i, :], ident[:, :])
                    ins.then_inc(tr_ready, 1)

            def patch(b, slot, s, has1, has2):
                n = b * NP + s
                if has1 or s + 2 < NP:
                    bslot, ahead = slots(slot, s, 2)
                    if ahead == 0:
                        pe.wait_ge(pj_used, b * PJ + (PJ + 4))
                    scores(n + 2, s % 2, bslot, ahead)
                if s == 0:
                    pe.wait_ge(vp_ready, b + 1)
                pe.wait_ge(o_ready, n + 1)
                for t in range(2):
                    pe.wait_ge(tr_used, n * 2 + (t + 3))
                    for i in range(4):
                        head = 4 * t + i
                        ins = mm3(nc, pov[:, head * VC:(head + 1) * VC], lambda p: ep[:, p, t, i, :],
                                  lambda p: vp[:, slot, p, s, head, :])
                ins.then_inc(pv_ready, 1)
                if has1 and s < 3:
                    project(b + 1, 1 - slot, ((0, 1), (2, 3), (4,))[s])
                if has1 or s + 1 < NP:
                    transposes(n + 1, (s + 1) % 2)
                if s == 0:
                    pe.wait_ge(ot_copied, b + 1)
                pe.wait_ge(o_ready, n + 2)
                pe.sem_inc(o_seen, 1)
                ins = nc.tensor.transpose(pot[0:DK, s * P:(s + 1) * P], o32[:, s % 2, :], ident[:, :])
                if s == NP - 1:
                    ins.then_inc(ot_ready, 1)

            pe.wait_ge(w_split, 2)
            pe.wait_ge(zeros_set, 3)
            project(0, 0, range(PJ))
            pe.wait_ge(pj_used, 4)
            scores(0, 0, 0, 0)
            scores(1, 1, 0, 1)
            transposes(0, 0)
            body(pe, patch)
            for b in range(NB):
                pe.wait_ge(g_lo, b + 1)
                if b >= 2:
                    pe.wait_ge(y_used, b - 1)
                mm3(nc, pj[:, b % 2, :], lambda p: wo[:, p, :], lambda p: gp[:, b % 2, p, :]).then_inc(y_ready, 1)

        @block.scalar
        def _(act):
            def split_his(b, slot):
                wait(act, pj_ready, b * PJ)
                nc.scalar.activation(hp[:, HI, :], h[:, bass.ds(b, 1), :].rearrange("p o n -> p (o n)"),
                                     ACT.Copy).then_inc(split_hi, 1)
                nc.scalar.activation(cp[:, HI, :], ctx[:, slot, :], ACT.Copy).then_inc(split_hi, 1)

            def queries_hi(b, slot):
                for t in range(2):
                    act.wait_ge(pj_ready, b * PJ + (t + 3))
                    nc.scalar.activation(qp[:, slot, HI, t, :], pj[:, t, :], ACT.Identity, bias=bqk[:, t:t + 1]).then_inc(q_hi, 1)

            def keys_hi(n, pslot, bslot, s, b):
                act.wait_ge(k_ready, b + 1)
                wait(act, sc_ready, n * 2 - 2)
                for i in range(4):
                    ins = nc.scalar.activation(kd[rows(i), pslot, HI, :, i, :], k32[rows(i), bslot, :, s * P:(s + 1) * P],
                                               ACT.Copy)
                ins.then_inc(kd_hi, 1)

            def values_hi(b, slot):
                act.wait_ge(v_ready, b + 1)
                nc.scalar.activation(vp[:, slot, HI, :, :, 0:DH].rearrange("p s h d -> p (s h) d"),
                                     v32[:, :, :].rearrange("p s (h d) -> p (s h) d", d=DH), ACT.Copy).then_inc(vp_hi, 1)

            def exp(n, pslot):
                act.wait_ge(e_ready, n + 1)
                sl = e[:, pslot, :, :].rearrange("p h j -> p (h j)")
                nc.scalar.activation(sl, sl, ACT.Exp, scale=INV).then_inc(exp_done, 1)

            def weights_hi(n):
                for t in range(2):
                    act.wait_ge(tr_ready, n * 2 + (t + 1))
                    nc.scalar.activation(ep[:, HI, t, :, :].rearrange("p i j -> p (i j)"), ptr[:, t, :], ACT.Copy).then_inc(tr_hi, 1)

            def patch(b, slot, s, has1, has2):
                n = b * NP + s
                if has1 or s + 3 < NP:
                    bslot, ahead = slots(slot, s, 3)
                    keys_hi(n + 3, (s + 1) % 2, bslot, ahead, b + (s + 3) // NP)
                if has1 or s + 2 < NP:
                    exp(n + 2, s % 2)
                if has1 and s == 1:
                    queries_hi(b + 1, 1 - slot)
                if has1 and s == 2:
                    values_hi(b + 1, 1 - slot)
                if has1 or s + 1 < NP:
                    weights_hi(n + 1)
                if s == 3:
                    if has2:
                        act.wait_ge(loaded[slot], load_turn[0] * 32)
                        split_his(b + 2, slot)
                    act.wait_ge(ot_ready, b + 1)
                    nc.scalar.activation(o_all[:, bass.ds(b, 1), :].rearrange("p o n -> p (o n)"), pot[0:DK, :],
                                         ACT.Copy).then_inc(ot_copied, 1)

            load_turn = [1]
            act.wait_ge(zeros_set, 3)
            act.wait_ge(loaded[0], 32)
            split_his(0, 0)
            act.wait_ge(w_split, 2)
            keys_hi(0, 0, 0, 0, 0)
            keys_hi(1, 1, 0, 1, 0)
            queries_hi(0, 0)
            values_hi(0, 0)
            exp(0, 0)
            keys_hi(2, 0, 0, 2, 0)
            exp(1, 1)
            weights_hi(0)
            act.wait_ge(loaded[1], 32)
            split_his(1, 1)
            with act.Fori(0, NB // 2 - 1) as g:
                load_turn[0] = g + 2
                for slot in range(2):
                    for s in range(NP):
                        patch(g * 2 + slot, slot, s, True, True)
            for slot in range(2):
                for s in range(NP):
                    patch(NB - 2 + slot, slot, s, slot == 0, False)
            act.wait_ge(ot_copied, NB + 1)
            for b in range(NB):
                nc.scalar.activation(o_all[:, b, :], o_all[:, b, :], ACT.Gelu).then_inc(g_ready, 1)
                if b >= 2:
                    act.wait_ge(y_ready, b - 1)
                act.wait_ge(g_ready, b + 1)
                nc.scalar.activation(gp[:, b % 2, HI, :], o_all[:, b, :], ACT.Copy).then_inc(g_hi, 1)

        @block.vector
        def _(dve):
            dve.sem_inc(tr_used, 2)
            dve.sem_inc(o_ready, 1)
            dve.sem_inc(ot_copied, 1)
            steps = Steps(dve, own)
            dve.wait_ge(w_loaded, 7 * 16)
            steps.mark(nc.vector.tensor_copy(w[:, HI, :], raw_w[:, :]))
            steps.mark(nc.vector.tensor_copy(wo[:, HI, :], raw_o[:, :]))
            steps.mark(nc.vector.tensor_scalar(bqk[:, 0:2], bqk[:, 0:2], flag[:, 0:1], None, ALU.add))
            steps.wait()
            nc.vector.tensor_tensor(w[:, LO, :], raw_w[:, :], w[:, HI, :].bitcast(F32), ALU.subtract).then_inc(w_split, 1)
            nc.vector.tensor_tensor(wo[:, LO, :], raw_o[:, :], wo[:, HI, :].bitcast(F32), ALU.subtract).then_inc(w_split, 1)

            def split_los(b, slot):
                for i, (dst, src) in enumerate(((hp, h[:, bass.ds(b, 1), :].rearrange("p o n -> p (o n)")), (cp, ctx[:, slot, :]))):
                    dve.wait_ge(split_hi, b * 2 + (i + 1))
                    nc.vector.tensor_tensor(dst[:, LO, :], src, dst[:, HI, :].bitcast(F32), ALU.subtract).then_inc(split, 1)

            def keys(b, slot, steps):
                dve.wait_ge(mask_ready, b + 1)
                wait(dve, kd_lo, b * NP - NP)
                for t in range(2):
                    dve.wait_ge(pj_ready, b * PJ + (t + 1))
                    ins = nc.vector.scalar_tensor_tensor(k32[:, slot, t, :], pj[:, t, :], bqk[:, 2 + t:3 + t], keep[:, :],
                                                         ALU.add, ALU.mult)
                    ins.then_inc(pj_used, 1)
                dve.wait_ge(pj_used, b * PJ + 2)
                nc.vector.tensor_tensor(k32[:, slot, :, :], k32[:, slot, :, :], gone[:, None, :].broadcast_to([P, 2, D]),
                                        ALU.add).then_inc(k_ready, 1)

            def queries_lo(b, slot):
                for t in range(2):
                    dve.wait_ge(q_hi, b * 2 + (t + 1))
                    nc.vector.scalar_tensor_tensor(qp[:, slot, LO, t, :], pj[:, t, :], bqk[:, t:t + 1],
                                                   qp[:, slot, HI, t, :].bitcast(F32), ALU.add, ALU.subtract).then_inc(pj_used, 1)

            def values(b):
                dve.wait_ge(pj_ready, b * PJ + 5)
                wait(dve, vp_ready, b)
                vt = pj[:, 0, 0:NP * DK].rearrange("p (s n) -> p s n", n=DK)
                nc.vector.tensor_tensor(v32[:, :, :], vt, bv[:, None, :].broadcast_to([P, NP, DK]), ALU.add).then_inc(v_ready, 1)
                dve.wait_ge(v_ready, b + 1)
                dve.sem_inc(pj_used, 1)

            def shifted(n, pslot, steps):
                for t in range(2):
                    dve.wait_ge(sc_ready, n * 2 + (t + 1))
                    ins = nc.vector.reduce_max(top[:, pslot, 4 * t:4 * t + 4],
                                               psc[:, t, :].rearrange("p (i j) -> p i j", j=P), AX.X)
                steps.mark(ins)
                steps.wait()
                for t in range(2):
                    nc.vector.tensor_tensor(e[:, pslot, 4 * t:4 * t + 4, :],
                                            psc[:, t, :].rearrange("p (i j) -> p i j", j=P),
                                            top[:, pslot, 4 * t:4 * t + 4, None].broadcast_to([P, 4, P]),
                                            ALU.subtract).then_inc(sc_used, 1)
                dve.wait_ge(sc_used, n * 2 + 2)
                dve.sem_inc(e_ready, 1)

            def weights_lo(n):
                for t in range(2):
                    dve.wait_ge(tr_hi, n * 2 + (t + 1))
                    nc.vector.tensor_tensor(ep[:, LO, t, :, :].rearrange("p i j -> p (i j)"), ptr[:, t, :],
                                            ep[:, HI, t, :, :].rearrange("p i j -> p (i j)").bitcast(F32),
                                            ALU.subtract).then_inc(tr_used, 1)

            split_los(0, 0)
            keys(0, 0, steps)
            queries_lo(0, 0)
            values(0)
            shifted(0, 0, steps)
            shifted(1, 1, steps)
            weights_lo(0)
            split_los(1, 1)
            first = steps.n
            PER = 2 * NP

            def patch(b, slot, s, has1, has2):
                n = b * NP + s
                steps = Steps(dve, own, b * PER + (first + 2 * s - (1 if not has1 and s == NP - 1 else 0)))
                if has1 or s + 2 < NP:
                    shifted(n + 2, s % 2, steps)
                dve.wait_ge(pv_ready, n + 1)
                ov = pov[:, 0:PH * VC].rearrange("p (h c) -> p h c", c=VC)
                steps.mark(nc.vector.reciprocal(rs[:, :], ov[:, :, DH]))
                steps.wait()
                nc.vector.tensor_tensor(o32[:, s % 2, :].rearrange("p (h d) -> p h d", d=DH), ov[:, :, 0:DH],
                                        rs[:, :, None].broadcast_to([P, PH, DH]), ALU.mult).then_inc(o_ready, 1)
                if has1 and s == 0:
                    keys(b + 1, 1 - slot, steps)
                if has1 and s == 1:
                    queries_lo(b + 1, 1 - slot)
                if has1 and s == 2:
                    values(b + 1)
                if has1 or s + 1 < NP:
                    weights_lo(n + 1)
                if has2 and s == 3:
                    split_los(b + 2, slot)

            body(dve, patch)
            for b in range(NB):
                dve.wait_ge(g_hi, b + 1)
                nc.vector.tensor_tensor(gp[:, b % 2, LO, :], o_all[:, b, :], gp[:, b % 2, HI, :].bitcast(F32),
                                        ALU.subtract).then_inc(g_lo, 1)
                dve.wait_ge(y_ready, b + 1)
                dve.wait_ge(mask_again[b % 2], (b // 2 + 1) * 16)
                if b > 0:
                    dve.wait_ge(x_done, b)
                nc.vector.scalar_tensor_tensor(y[:, :], pj[:, b % 2, :], bo[:, 0:1], mask[:, b % 2, :],
                                               ALU.add, ALU.mult).then_inc(y_used, 1)
                dve.wait_ge(y_used, b + 1)
                nc.vector.tensor_tensor(x[:, b, :], x[:, b, :], y[:, :], ALU.add).then_inc(x_done, 1)
            dve.wait_ge(x_done, NB)
    st.close()



ROUND = 1.5 * 2.0 ** 23


def ffn1_stage(nc, x, h, ident_bf, weight_in, scales_in, bias_in):
    st = Stage(nc, "f1")
    words = st.sb("words", [P, DC, D // 4], I32)
    w = st.sb("w", [P, DC, D], BF16)
    ws = st.sb("ws", [P, D], F16)
    bias = st.sb("bias", [P, D], F16)
    top = st.sb("top", [P, NB])
    scale = st.sb("scale", [P, NB])
    inv = st.sb("inv", [P, NB])
    step = st.sb("step", [P, 2, D])
    q = st.sb("q", [P, NB, D], BF16)
    qt = st.sb("qt", [P, 2, DC, P], BF16)
    y32 = st.sb("y32", [P, 2, D])
    y16 = st.sb("y16", [P, 2, D], F16)
    tp = st.ps("tp", [P, 2, 2 * BANK], BF16)
    acc = st.ps("acc", [P, 2, BANK])
    (loaded, w_ready, own, q_ready, tp_ready, qt_ready, acc_ready, y_ready, x_done) = (st.sem(n) for n in (
        "loaded", "w_ready", "own", "q_ready", "tp_ready", "qt_ready", "acc_ready", "y_ready", "x_done"))
    with nc.Block() as block:
        @block.sync
        def _(sp):
            sp.dma_start(words[:, :, :], weight_in.rearrange("(c p) n -> p c n", p=P)).then_inc(loaded, 16)
            sp.dma_start(ws[:, :], scales_in.rearrange("(o n) -> o n", o=1).broadcast_to([P, D])).then_inc(loaded, 16)
            sp.dma_start(bias[:, :], bias_in.broadcast_to([P, D])).then_inc(loaded, 16)

        @block.scalar
        def _(act):
            act.wait_ge(loaded, 48)
            nc.scalar.activation(w[:, :, :], words[:, :, :].bitcast(I8), ACT.Copy).then_inc(w_ready, 1)
            for b in range(NB):
                act.wait_ge(tp_ready, b + 1)
                if b >= 2:
                    act.wait_ge(acc_ready, b - 1)
                nc.scalar.activation(qt[:, b % 2, :, :].rearrange("p c t -> p (c t)"), tp[:, b % 2, 0:D],
                                     ACT.Copy).then_inc(qt_ready, 1)

        @block.tensor
        def _(pe):
            def transposes(b):
                pe.wait_ge(q_ready, b + 1)
                if b >= 2:
                    pe.wait_ge(qt_ready, b - 1)
                for c in range(DC):
                    ins = nc.tensor.transpose(tp[:, b % 2, c * P:(c + 1) * P], q[:, b, c * P:(c + 1) * P], ident_bf[:, :])
                ins.then_inc(tp_ready, 1)

            transposes(0)
            pe.wait_ge(w_ready, 1)
            for b in range(NB):
                if b + 1 < NB:
                    transposes(b + 1)
                pe.wait_ge(qt_ready, b + 1)
                if b >= 2:
                    pe.wait_ge(y_ready, b - 1)
                for c in range(DC):
                    ins = nc.tensor.matmul(acc[:, b % 2, :], qt[:, b % 2, c, :], w[:, c, :], start=c == 0, stop=c == DC - 1)
                ins.then_inc(acc_ready, 1)

        @block.vector
        def _(dve):
            steps = Steps(dve, own)
            for b in range(NB):
                steps.mark(nc.vector.tensor_reduce(top[:, b:b + 1], h[:, b, :], AX.X, ALU.max, apply_absolute_value=True))
            steps.wait()
            steps.mark(nc.vector.tensor_scalar(scale[:, :], top[:, :], 1.0 / 127.0, 1e-37, ALU.mult, ALU.max))
            steps.wait()
            steps.mark(nc.vector.reciprocal(inv[:, :], scale[:, :]))
            steps.wait()
            for b in range(NB):
                steps.mark(nc.vector.tensor_scalar(step[:, b % 2, :], h[:, b, :], inv[:, b:b + 1], ROUND, ALU.mult, ALU.add))
                steps.wait()
                steps.mark(nc.vector.tensor_scalar(step[:, b % 2, :], step[:, b % 2, :], ROUND, 127.0, ALU.subtract, ALU.min))
                steps.wait()
                nc.vector.tensor_scalar(q[:, b, :], step[:, b % 2, :], -128.0, None, ALU.max).then_inc(q_ready, 1)
            dve.wait_ge(loaded, 48)
            for b in range(NB):
                dve.wait_ge(acc_ready, b + 1)
                nc.vector.tensor_tensor(y32[:, b % 2, :], acc[:, b % 2, :], ws[:, :], ALU.mult).then_inc(y_ready, 1)
                dve.wait_ge(y_ready, b + 1)
                steps.mark(nc.vector.tensor_scalar(y16[:, b % 2, :], y32[:, b % 2, :], scale[:, b:b + 1], None, ALU.mult))
                steps.wait()
                steps.mark(nc.vector.tensor_tensor(y16[:, b % 2, :], y16[:, b % 2, :], bias[:, :], ALU.add))
                steps.wait()
                nc.vector.tensor_tensor(x[:, b, :], x[:, b, :], y16[:, b % 2, :], ALU.add).then_inc(x_done, 1)
            dve.wait_ge(x_done, NB)
    st.close()



def ffn2_stage(nc, x, ident, h_t, rounded):
    st = Stage(nc, "f2")
    w1, w2 = (rounded[i * NH2:(i + 1) * NH2, :] for i in range(2))
    w3 = rounded[2 * NH2:3 * NH2, :].rearrange("r c -> (r c)").rearrange("(d h) -> d h", h=NH2)
    REST = NH2 - (HC2 - 1) * P
    rows = st.sb("rows", [P, 2, 2, D])
    cols = st.sb("cols", [P, 2, DC, P])
    wt = st.sb("wt", [P, 2, 2, DC, P], F32R)
    w3t = st.sb("w3t", [P, 2, 2, D], F32R)
    gate = st.sb("gate", [P, 2, BANK])
    a32 = st.sb("a32", [P, 2, BANK])
    a = st.sb("a", [P, 2, 2, NT], F32R)
    ptr = st.ps("ptr", [P, 2, BANK])
    pg = st.ps("pg", [P, 2, BANK])
    pd = st.ps("pd", [P, 2, BANK])
    loaded = [st.sem("loaded0"), st.sem("loaded1")]
    (tr_ready, tr_hi, tr_used, g_ready, silu_done, a_done, g_used, a_hi, a_lo, d_ready, d_used, own) = (
        st.sem(n) for n in ("tr_ready", "tr_hi", "tr_used", "g_ready", "silu_done", "a_done", "g_used",
                            "a_hi", "a_lo", "d_ready", "d_used", "own"))
    turns = [(n, min(n * P, NH2 - P)) for n in range(HC2)]
    norm = TransposedNorm(nc, st, x, ident, h_t, [t[:, n, :] for t in (ptr, pg) for n in range(2)],
                          st.sb("norm_space", [P, 11 * NB]), st.sb("norm_h", [P, NB, D]))
    with nc.Block() as block:
        @block.sync
        def _(sp):
            def load(start, slot):
                sp.dma_start(rows[:, slot, 0, :], w1[bass.ds(start, P), :]).then_inc(loaded[slot], 16)
                sp.dma_start(rows[:, slot, 1, :], w2[bass.ds(start, P), :]).then_inc(loaded[slot], 16)
                sp.dma_start(cols[:, slot, :, :], w3[:, bass.ds(start, P)].rearrange("(c p) h -> p c h", p=P)
                             ).then_inc(loaded[slot], 16)

            load(0, 0)
            load(P, 1)
            for n, start in turns[2:]:
                sp.wait_ge(tr_ready, 3 * (n - 1))
                load(start, n % 2)

        @block.gpsimd
        def _(pool):
            norm.on_gpsimd(pool)

        @block.tensor
        def _(pe):
            norm.on_tensor(pe)
            def down(n):
                pe.wait_ge(a_lo, 2 * (n + 1))
                for b in range(NB):
                    k = n * NB + b
                    if k >= 2:
                        pe.wait_ge(d_used, k - 1)
                    ins = mm3(nc, pd[:, b % 2, :], lambda p: a[:, n % 2, p, b * P:(b + 1) * P],
                              lambda p: w3t[:, n % 2, p, :])
                    ins.then_inc(d_ready, 1)

            for n, start in turns:
                pe.wait_ge(loaded[n % 2], (n // 2 + 1) * 48)
                for which in range(3):
                    k = 3 * n + which
                    if k >= 2:
                        pe.wait_ge(tr_used, k - 1)
                    for c in range(DC):
                        src = rows[:, n % 2, which, c * P:(c + 1) * P] if which < 2 else cols[:, n % 2, c, :]
                        ins = nc.tensor.transpose(ptr[:, k % 2, c * P:(c + 1) * P], src, ident[:, :])
                    ins.then_inc(tr_ready, 1)
                if n > 0:
                    down(n - 1)
                for half in range(2):
                    k = 2 * n + half
                    if k >= 1:
                        pe.wait_ge(g_used, k)
                    pe.wait_ge(tr_used, 3 * n + 2)
                    for which in range(2):
                        for c in range(DC):
                            ins = mm3(nc, pg[:, which, :], lambda p: wt[:, which, p, c, :],
                                      lambda p: h_t[:, p, c, half * BANK:(half + 1) * BANK], c == 0, c == DC - 1)
                    ins.then_inc(g_ready, 1)
            down(HC2 - 1)

        def tr_dst(n, which, part):
            if which < 2:
                return wt[:, which, part, :, :].rearrange("p c h -> p (c h)")
            return w3t[:, n % 2, part, :]

        @block.scalar
        def _(act):
            norm.on_scalar(act)
            for n, start in turns:
                for which in range(3):
                    k = 3 * n + which
                    act.wait_ge(tr_ready, k + 1)
                    if which < 2 and n > 0:
                        act.wait_ge(g_ready, 2 * n)
                    if which == 2 and n >= 2:
                        act.wait_ge(d_ready, NB * (n - 1))
                    nc.scalar.activation(tr_dst(n, which, HI), ptr[:, k % 2, :], ACT.Copy).then_inc(tr_hi, 1)
                for half in range(2):
                    k = 2 * n + half
                    act.wait_ge(g_ready, k + 1)
                    if k >= 2:
                        act.wait_ge(a_done, k - 1)
                    nc.scalar.activation(gate[:, half, :], pg[:, 0, :], ACT.Silu).then_inc(silu_done, 1)
                    act.wait_ge(a_done, k + 1)
                    if n >= 2:
                        act.wait_ge(d_ready, NB * (n - 1))
                    nc.scalar.activation(a[:, n % 2, HI, half * BANK:(half + 1) * BANK], a32[:, half, :],
                                         ACT.Copy).then_inc(a_hi, 1)

        @block.vector
        def _(dve):
            norm.on_vector(dve)
            def down(n):
                for b in range(NB):
                    k = n * NB + b
                    dve.wait_ge(d_ready, k + 1)
                    if k >= NB:
                        dve.wait_ge(d_used, k - NB + 1)
                    nc.vector.tensor_tensor(x[:, b, :], pd[:, b % 2, :], x[:, b, :], ALU.add).then_inc(d_used, 1)

            for n, start in turns:
                for which in range(3):
                    k = 3 * n + which
                    dve.wait_ge(tr_hi, k + 1)
                    ins = nc.vector.tensor_tensor(tr_dst(n, which, LO), ptr[:, k % 2, :],
                                                  tr_dst(n, which, HI).bitcast(F32), ALU.subtract)
                    if which == 2 and n == HC2 - 1:
                        for part in (HI, LO):
                            ins.then_inc(own, 1)
                            dve.wait_ge(own, part + 1)
                            ins = nc.vector.memset(w3t[0:P - REST, n % 2, part, :].bitcast(F32), 0.0)
                    ins.then_inc(tr_used, 1)
                if n > 0:
                    down(n - 1)
                for half in range(2):
                    k = 2 * n + half
                    dve.wait_ge(silu_done, k + 1)
                    if n > 0:
                        dve.wait_ge(a_lo, k - 1)
                    nc.vector.tensor_tensor(a32[:, half, :], pg[:, 1, :], gate[:, half, :], ALU.mult).then_inc(a_done, 1)
                    dve.wait_ge(a_done, k + 1)
                    dve.sem_inc(g_used, 1)
                    dve.wait_ge(a_hi, k + 1)
                    cols_ = slice(half * BANK, (half + 1) * BANK)
                    nc.vector.tensor_tensor(a[:, n % 2, LO, cols_], a32[:, half, :], a[:, n % 2, HI, cols_].bitcast(F32),
                                            ALU.subtract).then_inc(a_lo, 1)
            down(HC2 - 1)
            dve.wait_ge(d_used, NB * HC2)
    st.close()



E3, R3, RD3 = 64, 8, 16
TAKEN = -3.0e38


def ffn3_stage(nc, x, ident, h_t, a_in, b_in, router_in, keys_in):
    st = Stage(nc, "f3")
    raw = st.sb("raw", [P, 2, DC, D])
    wa = st.sb("wa", [P, 2, DC, D], F32R)
    wb = st.sb("wb", [P, 2, DC, D], F32R)
    raw_r = st.sb("raw_r", [P, DC, RD3])
    router = st.sb("router", [P, 2, DC, RD3], F32R)
    raw_k = st.sb("raw_k", [RD3, E3])
    keys = st.sb("keys", [RD3, 2, E3], F32R)
    q = st.sb("q", [RD3, 2, NT], F32R)
    s = st.sb("s", [P, NB, E3])
    left = st.sb("left", [P, NB, E3])
    left2 = st.sb("left2", [P, NB, E3])
    best = st.sb("best", [P, NB, 16])
    shift = st.sb("shift", [P, NB])
    total = st.sb("total", [P, NB])
    inv = st.sb("inv", [P, NB])
    zg = st.sb("zg", [P, 2, D])
    zt = st.sb("zt", [P, 2, 2, DC, P], F32R)
    pq = st.ps("pq", [P, BANK])
    ps_ = st.ps("ps", [P, BANK])
    pz = st.ps("pz", [P, 2, BANK])
    ptr = st.ps("ptr", [P, 2, BANK])
    po = st.ps("po", [P, 2, BANK])
    (small_loaded, a_loaded, b_loaded, own, small_split, a_split, b_split, q_ready, q_hi, q_lo, s_ready, shift_ready,
     exp_done, z_ready, z_used, tr_ready, tr_hi, tr_used, o_ready, x_done) = (st.sem(n) for n in (
         "small_loaded", "a_loaded", "b_loaded", "own", "small_split", "a_split", "b_split", "q_ready", "q_hi", "q_lo",
         "s_ready", "shift_ready", "exp_done", "z_ready", "z_used", "tr_ready", "tr_hi", "tr_used", "o_ready", "x_done"))
    norm = TransposedNorm(nc, st, x, ident, h_t, [t[:, n, :] for t in (pz, ptr) for n in range(2)],
                          st.sb("norm_space", [P, 11 * NB]), st.sb("norm_h", [P, NB, D]))
    with nc.Block() as block:
        @block.sync
        def _(sp):
            with nc.allow_non_contiguous_dma(reason="small weights"):
                sp.dma_start(raw_r[:, :, :], router_in.rearrange("(c p) n -> p c n", p=P)).then_inc(small_loaded, 16)
            sp.dma_start(raw_k[:, :], keys_in).then_inc(small_loaded, 16)
            sp.dma_start(raw[:, 0, :, :], a_in.rearrange("(c p) n -> p c n", p=P)).then_inc(a_loaded, 16)
            sp.dma_start(raw[:, 1, :, :], b_in.rearrange("(c p) n -> p c n", p=P)).then_inc(b_loaded, 16)

        @block.gpsimd
        def _(pool):
            norm.on_gpsimd(pool)
            for i, (w, loaded, split) in enumerate(((wa, a_loaded, a_split), (wb, b_loaded, b_split))):
                pool.wait_ge(loaded, 16)
                nc.gpsimd.tensor_scalar(w[:, HI, :, :], raw[:, i, :, :], 1.0, 0.0, ALU.mult, ALU.add).then_inc(split, 1)
                pool.wait_ge(split, 1)
                nc.gpsimd.tensor_tensor(w[:, LO, :, :], raw[:, i, :, :], w[:, HI, :, :].bitcast(F32),
                                        ALU.subtract).then_inc(split, 1)

        @block.tensor
        def _(pe):
            norm.on_tensor(pe)
            pe.wait_ge(small_split, 2)
            for half in range(2):
                if half:
                    pe.wait_ge(q_lo, 1)
                for c in range(DC):
                    ins = mm3(nc, pq[0:RD3, :], lambda p: router[:, p, c, :],
                              lambda p: h_t[:, p, c, half * BANK:(half + 1) * BANK], c == 0, c == DC - 1)
                ins.then_inc(q_ready, 1)
            pe.wait_ge(q_lo, 2)
            for b in range(NB):
                ins = mm3(nc, ps_[:, b * E3:(b + 1) * E3], lambda p: q[:, p, b * P:(b + 1) * P], lambda p: keys[:, p, :])
            ins.then_inc(s_ready, 1)

            def low(b):
                if b >= 2:
                    pe.wait_ge(z_used, b - 1)
                for c in range(DC):
                    ins = mm3(nc, pz[:, b % 2, :], lambda p: h_t[:, p, c, b * P:(b + 1) * P],
                              lambda p: wa[:, p, c, :], c == 0, c == DC - 1)
                ins.then_inc(z_ready, 1)

            pe.wait_ge(a_split, 2)
            low(0)
            low(1)
            for b in range(NB):
                pe.wait_ge(z_used, b + 1)
                if b >= 2:
                    pe.wait_ge(tr_used, b - 1)
                for c in range(DC):
                    ins = nc.tensor.transpose(ptr[:, b % 2, c * P:(c + 1) * P], zg[:, b % 2, c * P:(c + 1) * P], ident[:, :])
                ins.then_inc(tr_ready, 1)
                if b + 2 < NB:
                    low(b + 2)
                if b == 0:
                    pe.wait_ge(b_split, 2)
                pe.wait_ge(tr_used, b + 1)
                if b >= 2:
                    pe.wait_ge(x_done, b - 1)
                for c in range(DC):
                    ins = mm3(nc, po[:, b % 2, :], lambda p: zt[:, b % 2, p, c, :], lambda p: wb[:, p, c, :],
                              c == 0, c == DC - 1)
                ins.then_inc(o_ready, 1)

        @block.scalar
        def _(act):
            norm.on_scalar(act)
            for half in range(2):
                act.wait_ge(q_ready, half + 1)
                nc.scalar.activation(q[:, HI, half * BANK:(half + 1) * BANK], pq[0:RD3, :], ACT.Copy).then_inc(q_hi, 1)
            act.wait_ge(shift_ready, 1)
            for b in range(NB):
                nc.scalar.activation(s[:, b, :], s[:, b, :], ACT.Exp, bias=shift[:, b:b + 1]).then_inc(exp_done, 1)
            for b in range(NB):
                act.wait_ge(tr_ready, b + 1)
                if b >= 2:
                    act.wait_ge(o_ready, b - 1)
                nc.scalar.activation(zt[:, b % 2, HI, :, :].rearrange("p c t -> p (c t)"), ptr[:, b % 2, :],
                                     ACT.Copy).then_inc(tr_hi, 1)

        @block.vector
        def _(dve):
            norm.on_vector(dve)
            steps = Steps(dve, own)
            dve.wait_ge(small_loaded, 32)
            steps.mark(nc.vector.tensor_copy(router[:, HI, :, :], raw_r[:, :, :]))
            steps.mark(nc.vector.tensor_copy(keys[:, HI, :], raw_k[:, :]))
            steps.wait()
            nc.vector.tensor_tensor(router[:, LO, :, :], raw_r[:, :, :], router[:, HI, :, :].bitcast(F32),
                                    ALU.subtract).then_inc(small_split, 1)
            nc.vector.tensor_tensor(keys[:, LO, :], raw_k[:, :], keys[:, HI, :].bitcast(F32), ALU.subtract).then_inc(small_split, 1)
            for half in range(2):
                dve.wait_ge(q_hi, half + 1)
                cols = slice(half * BANK, (half + 1) * BANK)
                nc.vector.tensor_tensor(q[:, LO, cols], pq[0:RD3, :], q[:, HI, cols].bitcast(F32), ALU.subtract).then_inc(q_lo, 1)
            dve.wait_ge(s_ready, 1)
            steps.mark(nc.vector.tensor_copy(s[:, :, :].rearrange("p b e -> p (b e)"), ps_[:, :]))
            steps.wait()
            for b in range(NB):
                steps.mark(nc.vector.max(best[:, b, 0:8], s[:, b, :]))
            steps.wait()
            for b in range(NB):
                steps.mark(nc.vector.match_replace(left[:, b, :], best[:, b, 0:8], s[:, b, :], TAKEN))
            steps.mark(nc.vector.tensor_scalar(shift[:, :], best[:, :, 0], -1.0, None, ALU.mult))
            steps.wait()
            for b in range(NB):
                steps.mark(nc.vector.max(best[:, b, 8:16], left[:, b, :]))
            steps.wait()
            for b in range(NB):
                steps.mark(nc.vector.match_replace(left2[:, b, :], best[:, b, 8:16], left[:, b, :], TAKEN))
            steps.wait()
            steps.mark(nc.vector.tensor_scalar(left[:, :, :], left2[:, :, :], TAKEN, None, ALU.is_equal))
            steps.wait()
            dve.sem_inc(shift_ready, 1)
            dve.wait_ge(exp_done, NB)
            steps.mark(nc.vector.tensor_tensor(s[:, :, :], s[:, :, :], left[:, :, :], ALU.mult))
            steps.wait()
            steps.mark(nc.vector.reduce_sum(total[:, :], s[:, :, :], AX.X))
            steps.wait()
            steps.mark(nc.vector.tensor_scalar(total[:, :], total[:, :], 0.5, None, ALU.mult))
            steps.wait()
            steps.mark(nc.vector.reciprocal(inv[:, :], total[:, :]))
            steps.wait()
            steps.mark(nc.vector.tensor_tensor(s[:, :, :], s[:, :, :], inv[:, :, None].broadcast_to([P, NB, E3]), ALU.mult))
            steps.wait()

            def gated(b):
                dve.wait_ge(z_ready, b + 1)
                if b >= 2:
                    dve.wait_ge(tr_ready, b - 1)
                nc.vector.tensor_tensor(zg[:, b % 2, :].rearrange("p (e r) -> p e r", r=R3),
                                        pz[:, b % 2, :].rearrange("p (e r) -> p e r", r=R3),
                                        s[:, b, :, None].broadcast_to([P, E3, R3]), ALU.mult).then_inc(z_used, 1)

            gated(0)
            gated(1)
            for b in range(NB):
                dve.wait_ge(tr_hi, b + 1)
                nc.vector.tensor_tensor(zt[:, b % 2, LO, :, :].rearrange("p c t -> p (c t)"), ptr[:, b % 2, :],
                                        zt[:, b % 2, HI, :, :].rearrange("p c t -> p (c t)").bitcast(F32),
                                        ALU.subtract).then_inc(tr_used, 1)
                if b + 2 < NB:
                    gated(b + 2)
                dve.wait_ge(o_ready, b + 1)
                nc.vector.tensor_tensor(x[:, b, :], po[:, b % 2, :], x[:, b, :], ALU.add).then_inc(x_done, 1)
            dve.wait_ge(x_done, NB)
    st.close()


def store_stage(nc, x, out):
    st = Stage(nc, "store")
    stored = st.sem("stored")
    with nc.Block() as block:
        @block.sync
        def _(sp):
            sp.dma_start(out.rearrange("b t d -> t b d"), x[:, :, :]).then_inc(stored, 16)
            sp.wait_ge(stored, 16)
    st.close()


PLAN0 = Plan("a0", hpg=2, own_kv=True)
PLAN2 = Plan("a2", hpg=4, rope=True)
PLAN3 = Plan("a3", hpg=4, kvb=2, qknorm=True)


def pieces(plan, wq_t, wk_t, wv_t, wo_t):
    def columns(w, n):
        return w[:, n * P:(n + 1) * P].reshape(DC, P, P).transpose(1, 0, 2).reshape(P, D)

    out = []
    for key in plan.all_w():
        kind, n = key[0], key[1]
        if kind == "q":
            out.append(columns(wq_t, n % H))
        elif kind == "o":
            out.append(wo_t[n * P:(n + 1) * P, :])
        else:
            out.append(columns(wk_t if kind == "k" else wv_t, n * plan.kvh + key[2]))
    return np.stack(out)


def rope_tables():
    inv_freq = (1.0 / np.float32(10000.0) ** (np.arange(0, P, 2, dtype=np.float32) / np.float32(P))).astype(np.float32)
    freqs = np.arange(MAX_POS, dtype=np.float32)[:, None] * inv_freq[None, :]
    both = np.concatenate([freqs, freqs], axis=1)
    sin = np.sin(both)
    sin[:, :P // 2] *= -1
    return np.stack([np.cos(both), sin]).astype(np.float32)


def program(nc, ins, out):
    rounded = nc.dram_tensor("nf4_rounded", (P, NF4_BLOCKS * NF4_BLOCK), F32, kind="Internal").ap()
    rounded_rows = rounded.rearrange("p n -> (p n)").rearrange("(r c) -> r c", c=D)
    with ExitStack() as ctx:
        def sb(name, shape, dt=F32):
            return ctx.enter_context(nc.sbuf_tensor(name, shape, dt))

        x = sb("x", [P, NB, D])
        ident = sb("ident", [P, P])
        ctx_t = sb("ctx_t", [P, 2, DC, NT], F32R)
        load_stage(nc, x, ident, ctx_t, ins["x"], ins["ident"], ins["ctxt"])
        with nc.sbuf_tensor("h_t0", [P, 2, DC, NT], F32R) as h_t:
            attention_stage(nc, PLAN0, x, ident, ctx_t, h_t, ins["a0_w"], ins["mask_bool"], ins["pos_bias"],
                            nf4=(ins["nf4"], rounded, SHARE0), lnw_in=ins["ln_w"])
            ffn0_stage(nc, x, ident, h_t, ins["w_base"], ins["f0_side"], ins["lora_b"], ins["b_base"], ins["b_router"])
        with nc.sbuf_tensor("h_nat", [P, NB, D], F32) as h:
            norm_natural_stage(nc, "n2", x, h)
            patch_attention_stage(nc, x, h, ident, ins["ctx"], ins["mask_f"], ins["a1_wqk"], ins["a1_wv"], ins["a1_wo"],
                                  ins["a1_bqk"], ins["a1_flag"], ins["a1_bv"], ins["a1_bo"])
            norm_natural_stage(nc, "n3", x, h)
            with nc.sbuf_tensor("ident_bf", [P, P], BF16) as ident_bf:
                made = Stage(nc, "ib")
                done = made.sem("done")
                with nc.Block() as block:
                    @block.vector
                    def _(dve):
                        nc.vector.tensor_copy(ident_bf[:, :], ident[:, :]).then_inc(done, 1)
                        dve.wait_ge(done, 1)
                made.close()
                ffn1_stage(nc, x, h, ident_bf, ins["f1_w"], ins["f1_scale"], ins["f1_bias"])
        with nc.sbuf_tensor("h_t1", [P, 2, DC, NT], F32R) as h_t:
            with nc.sbuf_tensor("cos", [P, NT], F32) as cos, nc.sbuf_tensor("sin", [P, NT], F32) as sin:
                rope_stage(nc, cos, sin, ins["pos"], ins["iota"], ins["rope"])
                attention_stage(nc, PLAN2, x, ident, ctx_t, h_t, ins["a2_w"], ins["mask_i"], rope_sb=(cos, sin),
                                nf4=(ins["nf4"], rounded, SHARE2))
            ffn2_stage(nc, x, ident, h_t, rounded_rows)
            attention_stage(nc, PLAN3, x, ident, ctx_t, h_t, ins["a3_w"], kq_norm_in=ins["a3_norm"])
            ffn3_stage(nc, x, ident, h_t, ins["f3_a"], ins["f3_b"], ins["f3_router"], ins["f3_keys"])
        store_stage(nc, x, out)


def host_layout(i):
    c = np.ascontiguousarray

    def spread(w):
        out = np.zeros((w.shape[1], 2, 4, ROWS), w.dtype)
        out[:, :, :, :DH] = w.T.reshape(w.shape[1], 2, 4, DH)
        return out.reshape(w.shape[1], 2 * P)

    flag = np.zeros((4, ROWS), np.float32)
    flag[:, DH] = 1
    bqk = np.concatenate([spread(i["L1_xattn_bq"][:, None]), spread(i["L1_xattn_bk"][:, None])], 1)
    nf4 = np.concatenate([i[f"L2_ffn_w{n}"].reshape(-1) for n in (1, 2, 3)]).reshape(P, -1)
    lora_a = i["L0_ffn_lora_A"].transpose(1, 0, 2).reshape(D, E0 * R0)
    return {
        "x": i["x"], "ctx": i["ctx_4096"], "ctxt": c(i["ctx_4096"].reshape(NT, D).T), "ident": np.eye(P, dtype=np.float32),
        "mask_bool": c(i["mask_BxSxS2_bk0"]).view(np.int32), "mask_i": i["mask_BxSxS2_ik0"],
        "mask_f": c(i["mask_Bx1x4096_ff1"].reshape(NB, D)), "pos": i["pos_BxS2"],
        "pos_bias": i["L0_xattn_position_bias"], "ln_w": c(i["L0_xattn_ln_weight"].reshape(DC, P).T),
        "a0_w": pieces(PLAN0, i["L0_xattn_w_q"].T, i["L0_xattn_w_k"].T, i["L0_xattn_w_v"].T, i["L0_xattn_w_out"].T),
        "w_base": c(i["L0_ffn_W_base"].T), "f0_side": np.concatenate([lora_a, i["L0_ffn_W_router"].T], 1),
        "lora_b": c(i["L0_ffn_lora_B"].reshape(E0 * R0, D)), "b_base": i["L0_ffn_b_base"], "b_router": i["L0_ffn_b_router"],
        "a1_wqk": np.concatenate([spread(i["L1_xattn_Wq"]), spread(i["L1_xattn_Wk"])], 1),
        "a1_wv": c(i["L1_xattn_Wv"].T), "a1_wo": c(i["L1_xattn_Wo"].T), "a1_bqk": c(bqk.reshape(4, P).T),
        "a1_flag": c(flag.reshape(P, 1)), "a1_bv": i["L1_xattn_bv"], "a1_bo": i["L1_xattn_bo"],
        "f1_w": c(i["L1_ffn_weight"].T).view(np.int32), "f1_scale": i["L1_ffn_weight_scales"], "f1_bias": i["L1_ffn_bias"],
        "iota": c(np.arange(MAX_POS, dtype=np.float32).reshape(DC, P).T), "rope": rope_tables(),
        "a2_w": pieces(PLAN2, i["L2_xattn_Wq"], i["L2_xattn_Wk"], i["L2_xattn_Wv"], i["L2_xattn_Wo"]),
        "nf4": np.pad(nf4, ((0, 0), (0, SHARE2.sizes[0] * NF4_BLOCK))),
        "a3_w": pieces(PLAN3, i["L3_xattn_Wq"], i["L3_xattn_Wk"], i["L3_xattn_Wv"], i["L3_xattn_Wo"]),
        "a3_norm": np.stack([i["L3_xattn_q_norm_w"], i["L3_xattn_k_norm_w"]], 1),
        "f3_a": c(i["L3_ffn_A_w"].T), "f3_b": c(i["L3_ffn_B_w"].T), "f3_router": c(i["L3_ffn_Wq_w"].T),
        "f3_keys": c(i["L3_ffn_keys"].T),
    }


def kernel(**inputs):
    import concourse.bacc as bacc
    from concourse.bass_utils import run_bass_kernel_spmd

    nc = bacc.Bacc("TRN2", target_bir_lowering=False, num_devices=1)
    arrays, ins = {}, {}
    for name, a in host_layout({k: np.asarray(v) for k, v in inputs.items()}).items():
        arrays[f"in_{name}"] = np.ascontiguousarray(a)
        ins[name] = nc.dram_tensor(f"in_{name}", a.shape, mybir.dt.from_np(a.dtype), kind="ExternalInput").ap()
    out = nc.dram_tensor("out", (NB, P, D), F32, kind="ExternalOutput").ap()
    program(nc, ins, out)
    return run_bass_kernel_spmd(nc, [arrays], core_ids=[0]).results[0]["out"]
```
